# Optimizing a Trainium2 kernel written in Bass

```python
import numpy as np
import jax
import jax.numpy as jnp

def _softmax(x, axis=-1):
    return jax.nn.softmax(x, axis=axis)

def _gelu(x):
    return jax.nn.gelu(x, approximate=True)

def _silu(x):
    return jax.nn.silu(x)

def _sigmoid(x):
    return jax.nn.sigmoid(x)

def _layernorm(x, axis=-1, eps=1e-05):
    m = jnp.mean(x, axis=axis, keepdims=True)
    v = jnp.var(x, axis=axis, keepdims=True)
    return (x - m) / jnp.sqrt(v + eps)

def _scatter_add(tgt, idx, src, axis=0):
    return tgt.at[idx].add(src)

def _segment_sum(src, seg, n):
    return jax.ops.segment_sum(src, seg, n)
kernel_name = 'mk_sandwich_d4_jaxref_r8_0198a7'

def setup_inputs(seed: int=0):
    np.random.seed(seed)
    _w = jnp.asarray

    def _L0_attn_setup():
        import jax, jax.numpy as jnp
        from jax import lax
        import numpy as np
        D = 128
        H = 16
        DK = 64
        DV = 128
        KDIM = H * DK
        VDIM = H * DV
        CONV_K = 4
        B, T = (2, 512)
        EPS = 1e-05

        def _causal_conv_silu(x, w):
            C = x.shape[-1]
            Kw = w.shape[-1]
            xp = jnp.pad(x, ((0, 0), (Kw - 1, 0), (0, 0))).transpose(0, 2, 1)
            y = lax.conv_general_dilated(xp, w[:, None, :], window_strides=(1,), padding='VALID', feature_group_count=C, dimension_numbers=('NCH', 'OIH', 'NCH'))
            return jax.nn.silu(y.transpose(0, 2, 1))

        def _l2norm(x, eps=1e-06):
            return x * lax.rsqrt(jnp.sum(x * x, axis=-1, keepdims=True) + eps)

        def _gated_delta_rule(q, k, v, g, beta):
            scale = q.shape[-1] ** (-0.5)
            qs = jnp.moveaxis(q, 1, 0)
            ks_ = jnp.moveaxis(k, 1, 0)
            vs = jnp.moveaxis(v, 1, 0)
            gs = jnp.moveaxis(g, 1, 0)
            bs = jnp.moveaxis(beta, 1, 0)

            def step(S, inp):
                q_t, k_t, v_t, g_t, b_t = inp
                S = S * jnp.exp(g_t)[..., None, None]
                mem = jnp.einsum('bhk,bhkv->bhv', k_t, S)
                delta = (v_t - mem) * b_t[..., None]
                S = S + jnp.einsum('bhk,bhv->bhkv', k_t, delta)
                o_t = jnp.einsum('bhk,bhkv->bhv', q_t * scale, S)
                return (S, o_t)
            S0 = jnp.zeros((q.shape[0], q.shape[2], q.shape[3], v.shape[3]), q.dtype)
            _, o = lax.scan(step, S0, (qs, ks_, vs, gs, bs))
            return jnp.moveaxis(o, 0, 1)
        key = jax.random.key(seed)
        ks = jax.random.split(key, 14)

        def w(k, shape, s=0.02):
            return jax.random.normal(k, shape, jnp.float32) * s
        return {'x': jax.random.normal(ks[0], (B, T, D), jnp.float32), 'w_q': w(ks[1], (D, KDIM)), 'w_k': w(ks[2], (D, KDIM)), 'w_v': w(ks[3], (D, VDIM)), 'w_a': w(ks[4], (D, H)), 'w_b': w(ks[5], (D, H)), 'w_g': w(ks[6], (D, VDIM)), 'w_out': w(ks[7], (VDIM, D)), 'A_log': jnp.log(jax.random.uniform(ks[8], (H,), jnp.float32, 1.0, 16.0)), 'dt_bias': jax.random.uniform(ks[9], (H,), jnp.float32, -4.0, -1.0), 'conv_q': w(ks[10], (KDIM, CONV_K), 0.1), 'conv_k': w(ks[11], (KDIM, CONV_K), 0.1), 'conv_v': w(ks[12], (VDIM, CONV_K), 0.1), 'norm_w': jnp.ones((DV,), jnp.float32)}
    _L0_attn_in = _L0_attn_setup()

    def _L0_ffn_setup():
        import jax, jax.numpy as jnp
        import numpy as np
        DIM = 128
        DEPTH = 2
        HEADS = 8
        DIM_HEAD = 64
        WINDOW = 64
        INNER = HEADS * DIM_HEAD
        HID = int(DIM * 4 * 2 / 3)
        B, N = (2, 1024)
        QK_SCALE = 8.0

        def shift_token(t):
            t1, t2 = jnp.split(t, 2, axis=-1)
            t2 = jnp.pad(t2, ((0, 0), (1, 0), (0, 0)))[:, :-1]
            return jnp.concatenate([t1, t2], axis=-1)

        def l2norm(t):
            return t / jnp.clip(jnp.linalg.norm(t, axis=-1, keepdims=True), 1e-12)

        def rotate_half(x):
            x1, x2 = jnp.split(x, 2, axis=-1)
            return jnp.concatenate([-x2, x1], axis=-1)

        def rotary_xpos(q, k):
            n = q.shape[-2]
            half_idx = jnp.arange(0, DIM_HEAD, 2, dtype=jnp.float32)
            inv_freq = 1.0 / 10000.0 ** (half_idx / DIM_HEAD)
            t = jnp.arange(n, dtype=jnp.float32)
            freqs = t[:, None] * inv_freq[None, :]
            freqs = jnp.concatenate([freqs, freqs], axis=-1)
            base = (half_idx + 0.4 * DIM_HEAD) / (1.4 * DIM_HEAD)
            power = (t - n // 2) / float(WINDOW // 2)
            scale = base[None, :] ** power[:, None]
            scale = jnp.concatenate([scale, scale], axis=-1)
            cos, sin = (jnp.cos(freqs), jnp.sin(freqs))
            q = q * cos * scale + rotate_half(q) * sin * scale
            k = k * cos / scale + rotate_half(k) * sin / scale
            return (q, k)

        def local_attention(q, k, v):
            b, h, n, d = q.shape
            w = n // WINDOW
            bq = q.reshape(b, h, w, WINDOW, d) * QK_SCALE
            bk = k.reshape(b, h, w, WINDOW, d)
            bv = v.reshape(b, h, w, WINDOW, d)

            def look_around(t):
                p = jnp.pad(t, ((0, 0), (0, 0), (1, 0), (0, 0), (0, 0)))
                return jnp.concatenate([p[:, :, :w], p[:, :, 1:]], axis=3)
            bk, bv = (look_around(bk), look_around(bv))
            bt = jnp.arange(n).reshape(w, WINDOW)
            btp = jnp.pad(bt, ((1, 0), (0, 0)), constant_values=-1)
            btk = jnp.concatenate([btp[:w], btp[1:]], axis=1)
            sim = jnp.einsum('bhwid,bhwjd->bhwij', bq, bk)
            i = bt[:, :, None]
            j = btk[:, None, :]
            mask = (i < j) | (i > j + WINDOW) | (j == -1)
            sim = jnp.where(mask, -jnp.finfo(sim.dtype).max, sim)
            attn = jax.nn.softmax(sim, axis=-1)
            out = jnp.einsum('bhwij,bhwjd->bhwid', attn, bv)
            return out.reshape(b, h, n, d)

        def _layer(x, wqkv, qs, ksc, wo, lg, lb, w1, b1, w2, b2):
            b, n, _ = x.shape
            h = shift_token(x)
            qkv = h @ wqkv
            q, k, v = jnp.split(qkv, 3, axis=-1)
            to_heads = lambda t: t.reshape(b, n, HEADS, DIM_HEAD).transpose(0, 2, 1, 3)
            q, k, v = (to_heads(q), to_heads(k), to_heads(v))
            q = l2norm(q) * qs
            k = l2norm(k) * ksc
            q, k = rotary_xpos(q, k)
            o = local_attention(q, k, v)
            o = o.transpose(0, 2, 1, 3).reshape(b, n, INNER)
            x = x + o @ wo
            h = shift_token(x)
            mu = h.mean(-1, keepdims=True)
            var = h.var(-1, keepdims=True)
            h = (h - mu) / jnp.sqrt(var + 1e-05) * lg + lb
            h = h @ w1 + b1
            a, g = jnp.split(h, 2, axis=-1)
            h = a * jax.nn.gelu(g, approximate=False)
            x = x + h @ w2 + b2
            return x
        key = jax.random.key(seed)
        ks = jax.random.split(key, 6)
        return {'x': jax.random.normal(ks[0], (B, N, DIM), jnp.float32), 'wqkv': jax.random.normal(ks[1], (DEPTH, DIM, 3 * INNER), jnp.float32) * 0.02, 'q_scale': jnp.ones((DEPTH, DIM_HEAD), jnp.float32), 'k_scale': jnp.ones((DEPTH, DIM_HEAD), jnp.float32), 'wo': jax.random.normal(ks[2], (DEPTH, INNER, DIM), jnp.float32) * 0.02, 'ln_g': jnp.ones((DEPTH, DIM), jnp.float32), 'ln_b': jnp.zeros((DEPTH, DIM), jnp.float32), 'w1': jax.random.normal(ks[3], (DEPTH, DIM, 2 * HID), jnp.float32) * 0.02, 'b1': jnp.zeros((DEPTH, 2 * HID), jnp.float32), 'w2': jax.random.normal(ks[4], (DEPTH, HID, DIM), jnp.float32) * 0.02, 'b2': jnp.zeros((DEPTH, DIM), jnp.float32)}
    _L0_ffn_in = _L0_ffn_setup()

    def _L1_attn_setup():
        import jax, jax.numpy as jnp
        import numpy as np
        _J6 = jnp.array([[0, 0, 0, 0, 0, 1], [0, 0, 0, 0, -1, 0], [0, 0, 0, 1, 0, 0], [0, 0, 1, 0, 0, 0], [0, -1, 0, 0, 0, 0], [1, 0, 0, 0, 0, 0]], dtype=jnp.float32)
        _PAIRS = [(0, 1), (0, 2), (0, 3), (1, 2), (1, 3), (2, 3)]
        _H = 16
        _SCALE = 6.0 ** (-0.5)

        def _plucker_lines(p1, p2):
            parts = [p1[..., i] * p2[..., j] - p1[..., j] * p2[..., i] for i, j in _PAIRS]
            lines = jnp.stack(parts, axis=-1)
            n = jnp.linalg.norm(lines, axis=-1, keepdims=True)
            return lines / jnp.maximum(n, 1e-12)
        key = jax.random.key(seed)
        ks = jax.random.split(key, 9)
        B, T, D, H = (2, 256, 128, _H)
        std = 0.02
        return {'x': jax.random.normal(ks[0], (B, T, D), jnp.float32), 'W1_q': jax.random.normal(ks[1], (4 * H, 2 * D), jnp.float32) * std, 'W2_q': jax.random.normal(ks[2], (4 * H, 2 * D), jnp.float32) * std, 'W1_k': jax.random.normal(ks[3], (4 * H, D), jnp.float32) * std, 'W2_k': jax.random.normal(ks[4], (4 * H, D), jnp.float32) * std, 'Wv': jax.random.normal(ks[5], (D, D), jnp.float32) * std, 'bv': jnp.zeros((D,), jnp.float32), 'Wo': jax.random.normal(ks[6], (D, D), jnp.float32) * std, 'bo': jnp.zeros((D,), jnp.float32)}
    _L1_attn_in = _L1_attn_setup()

    def _L1_ffn_setup():
        import jax, jax.numpy as jnp
        import numpy as np
        D_IN, D_HID = (128, 512)

        def _ternary(key, shape):
            return jax.random.randint(key, shape, -1, 2).astype(jnp.float32)

        def _tlin(x, w, s):
            return jnp.einsum('bsi,oi->bso', x, w) * s
        key = jax.random.key(seed)
        ks = jax.random.split(key, 12)
        inv = lambda fan: 1.0 / np.sqrt(fan).astype(np.float32)
        return {'x': jax.random.normal(ks[0], (4, 256, D_IN), dtype=jnp.float32), 'w1_w': _ternary(ks[1], (D_HID, D_IN)), 'w1_s': jax.random.uniform(ks[2], (D_HID,), dtype=jnp.float32) * inv(D_IN), 'w2_w': _ternary(ks[3], (D_HID, D_IN)), 'w2_s': jax.random.uniform(ks[4], (D_HID,), dtype=jnp.float32) * inv(D_IN), 'h1_w': _ternary(ks[5], (D_HID, D_HID)), 'h1_s': jax.random.uniform(ks[6], (D_HID,), dtype=jnp.float32) * inv(D_HID), 'h2_w': _ternary(ks[7], (D_HID, D_HID)), 'h2_s': jax.random.uniform(ks[8], (D_HID,), dtype=jnp.float32) * inv(D_HID), 'w3_w': _ternary(ks[9], (D_IN, D_HID)), 'w3_s': jax.random.uniform(ks[10], (D_IN,), dtype=jnp.float32) * inv(D_HID)}
    _L1_ffn_in = _L1_ffn_setup()

    def _L2_attn_setup():
        import jax, jax.numpy as jnp
        import numpy as np
        H = 16
        D = 64
        BQ = 64
        BKV = 64

        def _flash_tiled(q, k, v, scale):
            B, nh, S, d = q.shape
            nq, nkv = (S // BQ, S // BKV)
            qb = q.reshape(B, nh, nq, BQ, d)
            kb = k.reshape(B, nh, nkv, BKV, d).transpose(2, 0, 1, 3, 4)
            vb = v.reshape(B, nh, nkv, BKV, d).transpose(2, 0, 1, 3, 4)
            o0 = jnp.zeros((B, nh, nq, BQ, d), q.dtype)
            m0 = jnp.full((B, nh, nq, BQ), -jnp.inf, q.dtype)
            l0 = jnp.zeros((B, nh, nq, BQ), q.dtype)

            def step(carry, kv):
                o, m, l = carry
                kj, vj = kv
                s = jnp.einsum('bhnqd,bhkd->bhnqk', qb, kj) * scale
                m_new = jnp.maximum(m, s.max(axis=-1))
                p = jnp.exp(s - m_new[..., None])
                alpha = jnp.exp(m - m_new)
                l_new = alpha * l + p.sum(axis=-1)
                o_new = (alpha[..., None] * o + jnp.einsum('bhnqk,bhkd->bhnqd', p, vj)) / l_new[..., None]
                return ((o_new, m_new, l_new), None)
            (o, _, _), _ = jax.lax.scan(step, (o0, m0, l0), (kb, vb))
            return o.reshape(B, nh, S, d)
        key = jax.random.key(seed)
        ks = jax.random.split(key, 5)
        B, S, dim = (2, 256, 128)
        x = jax.random.normal(ks[0], (B, S, dim), dtype=jnp.float32)
        Wq = jax.random.normal(ks[1], (dim, H * D), dtype=jnp.float32) * 0.02
        Wk = jax.random.normal(ks[2], (dim, H * D), dtype=jnp.float32) * 0.02
        Wv = jax.random.normal(ks[3], (dim, H * D), dtype=jnp.float32) * 0.02
        Wo = jax.random.normal(ks[4], (H * D, dim), dtype=jnp.float32) * 0.02
        return {'x': x, 'Wq': Wq, 'Wk': Wk, 'Wv': Wv, 'Wo': Wo}
    _L2_attn_in = _L2_attn_setup()

    def _L2_ffn_setup():
        import jax, jax.numpy as jnp
        import numpy as np
        B, S, D, E, K = (4, 256, 128, 8, 2)
        EPS, W_THRES, TEMP = (0.0001, 0.1, 1.0)
        key = jax.random.key(seed)
        k1, k2, k3, k4, k5 = jax.random.split(key, 5)
        x = jax.random.normal(k1, (B, S, D), dtype=jnp.float32)
        gate_W = jax.random.normal(k2, (D, E), dtype=jnp.float32) * 0.02
        gate_b = jnp.zeros((E,), dtype=jnp.float32)
        expert_W = jax.random.normal(k3, (E, D, D), dtype=jnp.float32) * 0.02
        expert_b = jnp.zeros((E, D), dtype=jnp.float32)
        return {'x': x, 'gate_W': gate_W, 'gate_b': gate_b, 'expert_W': expert_W, 'expert_b': expert_b}
    _L2_ffn_in = _L2_ffn_setup()

    def _L3_attn_setup():
        import jax, jax.numpy as jnp
        import numpy as np
        D = 128
        E = 2 * D
        N = 64
        R = D // 16
        K = 4
        BATCH, L = (2, 256)
        LN_EPS = 1e-05

        def _layernorm(x, w, b):
            mu = x.mean(-1, keepdims=True)
            var = ((x - mu) ** 2).mean(-1, keepdims=True)
            return (x - mu) * jax.lax.rsqrt(var + LN_EPS) * w + b

        def _silu(x):
            return x * jax.nn.sigmoid(x)

        def _mamba(x, W_in, conv_w, conv_b, W_xp, W_dt, dt_b, A_log, Dp, W_out):
            Bsz = x.shape[0]
            xz = x @ W_in.T
            xp, z = jnp.split(xz, 2, axis=-1)
            xc = jax.lax.conv_general_dilated(xp.transpose(0, 2, 1), conv_w[:, None, :], window_strides=(1,), padding=[(K - 1, 0)], dimension_numbers=('NCH', 'OIH', 'NCH'), feature_group_count=E)
            xc = _silu(xc.transpose(0, 2, 1) + conv_b)
            x_dbl = xc @ W_xp.T
            dt_lo, Bm, Cm = (x_dbl[..., :R], x_dbl[..., R:R + N], x_dbl[..., R + N:])
            dt = jax.nn.softplus(dt_lo @ W_dt.T + dt_b)
            A = -jnp.exp(A_log)

            def step(h, inp):
                xt, dtt, Bt, Ct = inp
                dA = jnp.exp(dtt[:, :, None] * A)
                h = dA * h + (dtt * xt)[:, :, None] * Bt[:, None, :]
                y = jnp.einsum('ben,bn->be', h, Ct)
                return (h, y)
            h0 = jnp.zeros((Bsz, E, N), x.dtype)
            xs = (xc.transpose(1, 0, 2), dt.transpose(1, 0, 2), Bm.transpose(1, 0, 2), Cm.transpose(1, 0, 2))
            _, ys = jax.lax.scan(step, h0, xs)
            y = ys.transpose(1, 0, 2) + xc * Dp
            y = y * _silu(z)
            return y @ W_out.T
        key = jax.random.key(seed)
        ks = jax.random.split(key, 20)
        s_in = 0.02

        def mamba_params(k):
            kk = jax.random.split(k, 8)
            a_init = jnp.log(jnp.broadcast_to(jnp.arange(1, N + 1, dtype=jnp.float32), (E, N)))
            return dict(W_in=jax.random.normal(kk[0], (2 * E, D), jnp.float32) * s_in, conv_w=jax.random.normal(kk[1], (E, K), jnp.float32) * 0.1, conv_b=jnp.zeros((E,), jnp.float32), W_xp=jax.random.normal(kk[2], (R + 2 * N, E), jnp.float32) * s_in, W_dt=jax.random.normal(kk[3], (E, R), jnp.float32) * 0.1, dt_b=jnp.log(jnp.expm1(jax.random.uniform(kk[4], (E,), jnp.float32, 0.001, 0.1))), A_log=a_init, D=jnp.ones((E,), jnp.float32), W_out=jax.random.normal(kk[5], (D, E), jnp.float32) * s_in)
        p1 = mamba_params(ks[1])
        p2 = mamba_params(ks[2])
        inp = {'x': jax.random.normal(ks[0], (BATCH, L, D), jnp.float32), 'ln1_w': jnp.ones((D,), jnp.float32), 'ln1_b': jnp.zeros((D,), jnp.float32), 'ln2_w': jnp.ones((D,), jnp.float32), 'ln2_b': jnp.zeros((D,), jnp.float32)}
        for pre, p in (('m1_', p1), ('m2_', p2)):
            for k2, v in p.items():
                inp[pre + k2] = v
        return inp
    _L3_attn_in = _L3_attn_setup()

    def _L3_ffn_setup():
        import jax, jax.numpy as jnp
        import numpy as np
        DIM = 128
        HIDDEN = 384
        SCALE = 1.0 / 127.0

        def _dequant(w_int, dtype):
            return w_int.astype(dtype) * jnp.asarray(SCALE, dtype)
        key = jax.random.key(seed)
        k_x, k_g, k_u, k_d = jax.random.split(key, 4)
        x = jax.random.normal(k_x, (4, 256, DIM), dtype=jnp.float32)
        w_gate = jax.random.randint(k_g, (HIDDEN, DIM), -127, 128, dtype=jnp.int32)
        w_up = jax.random.randint(k_u, (HIDDEN, DIM), -127, 128, dtype=jnp.int32)
        w_down = jax.random.randint(k_d, (DIM, HIDDEN), -127, 128, dtype=jnp.int32)
        return {'x': x, 'w_gate': w_gate, 'w_up': w_up, 'w_down': w_down}
    _L3_ffn_in = _L3_ffn_setup()
    _d = {'L0_attn_x': _L0_attn_in['x'], 'L0_attn_w_q': _L0_attn_in['w_q'], 'L0_attn_w_k': _L0_attn_in['w_k'], 'L0_attn_w_v': _L0_attn_in['w_v'], 'L0_attn_w_a': _L0_attn_in['w_a'], 'L0_attn_w_b': _L0_attn_in['w_b'], 'L0_attn_w_g': _L0_attn_in['w_g'], 'L0_attn_w_out': _L0_attn_in['w_out'], 'L0_attn_A_log': _L0_attn_in['A_log'], 'L0_attn_dt_bias': _L0_attn_in['dt_bias'], 'L0_attn_conv_q': _L0_attn_in['conv_q'], 'L0_attn_conv_k': _L0_attn_in['conv_k'], 'L0_attn_conv_v': _L0_attn_in['conv_v'], 'L0_attn_norm_w': _L0_attn_in['norm_w'], 'L0_ffn_wqkv': _L0_ffn_in['wqkv'], 'L0_ffn_q_scale': _L0_ffn_in['q_scale'], 'L0_ffn_k_scale': _L0_ffn_in['k_scale'], 'L0_ffn_wo': _L0_ffn_in['wo'], 'L0_ffn_ln_g': _L0_ffn_in['ln_g'], 'L0_ffn_ln_b': _L0_ffn_in['ln_b'], 'L0_ffn_w1': _L0_ffn_in['w1'], 'L0_ffn_b1': _L0_ffn_in['b1'], 'L0_ffn_w2': _L0_ffn_in['w2'], 'L0_ffn_b2': _L0_ffn_in['b2'], 'L1_attn_W1_q': _L1_attn_in['W1_q'], 'L1_attn_W2_q': _L1_attn_in['W2_q'], 'L1_attn_W1_k': _L1_attn_in['W1_k'], 'L1_attn_W2_k': _L1_attn_in['W2_k'], 'L1_attn_Wv': _L1_attn_in['Wv'], 'L1_attn_bv': _L1_attn_in['bv'], 'L1_attn_Wo': _L1_attn_in['Wo'], 'L1_attn_bo': _L1_attn_in['bo'], 'L1_ffn_w1_w': _L1_ffn_in['w1_w'], 'L1_ffn_w1_s': _L1_ffn_in['w1_s'], 'L1_ffn_w2_w': _L1_ffn_in['w2_w'], 'L1_ffn_w2_s': _L1_ffn_in['w2_s'], 'L1_ffn_h1_w': _L1_ffn_in['h1_w'], 'L1_ffn_h1_s': _L1_ffn_in['h1_s'], 'L1_ffn_h2_w': _L1_ffn_in['h2_w'], 'L1_ffn_h2_s': _L1_ffn_in['h2_s'], 'L1_ffn_w3_w': _L1_ffn_in['w3_w'], 'L1_ffn_w3_s': _L1_ffn_in['w3_s'], 'L2_attn_Wq': _L2_attn_in['Wq'], 'L2_attn_Wk': _L2_attn_in['Wk'], 'L2_attn_Wv': _L2_attn_in['Wv'], 'L2_attn_Wo': _L2_attn_in['Wo'], 'L2_ffn_gate_W': _L2_ffn_in['gate_W'], 'L2_ffn_gate_b': _L2_ffn_in['gate_b'], 'L2_ffn_expert_W': _L2_ffn_in['expert_W'], 'L2_ffn_expert_b': _L2_ffn_in['expert_b'], 'L3_attn_ln1_w': _L3_attn_in['ln1_w'], 'L3_attn_ln1_b': _L3_attn_in['ln1_b'], 'L3_attn_ln2_w': _L3_attn_in['ln2_w'], 'L3_attn_ln2_b': _L3_attn_in['ln2_b'], 'L3_attn_m1_W_in': _L3_attn_in['m1_W_in'], 'L3_attn_m1_conv_w': _L3_attn_in['m1_conv_w'], 'L3_attn_m1_conv_b': _L3_attn_in['m1_conv_b'], 'L3_attn_m1_W_xp': _L3_attn_in['m1_W_xp'], 'L3_attn_m1_W_dt': _L3_attn_in['m1_W_dt'], 'L3_attn_m1_dt_b': _L3_attn_in['m1_dt_b'], 'L3_attn_m1_A_log': _L3_attn_in['m1_A_log'], 'L3_attn_m1_D': _L3_attn_in['m1_D'], 'L3_attn_m1_W_out': _L3_attn_in['m1_W_out'], 'L3_attn_m2_W_in': _L3_attn_in['m2_W_in'], 'L3_attn_m2_conv_w': _L3_attn_in['m2_conv_w'], 'L3_attn_m2_conv_b': _L3_attn_in['m2_conv_b'], 'L3_attn_m2_W_xp': _L3_attn_in['m2_W_xp'], 'L3_attn_m2_W_dt': _L3_attn_in['m2_W_dt'], 'L3_attn_m2_dt_b': _L3_attn_in['m2_dt_b'], 'L3_attn_m2_A_log': _L3_attn_in['m2_A_log'], 'L3_attn_m2_D': _L3_attn_in['m2_D'], 'L3_attn_m2_W_out': _L3_attn_in['m2_W_out'], 'L3_ffn_w_gate': _L3_ffn_in['w_gate'], 'L3_ffn_w_up': _L3_ffn_in['w_up'], 'L3_ffn_w_down': _L3_ffn_in['w_down']}
    _x0 = _d['L0_attn_x']
    _d['L0_attn_x'] = jax.random.normal(jax.random.fold_in(jax.random.key(seed), 1), (8, 256, 128), dtype=_x0.dtype)
    del _x0
    return _d

def reference(L0_attn_x, L0_attn_w_q, L0_attn_w_k, L0_attn_w_v, L0_attn_w_a, L0_attn_w_b, L0_attn_w_g, L0_attn_w_out, L0_attn_A_log, L0_attn_dt_bias, L0_attn_conv_q, L0_attn_conv_k, L0_attn_conv_v, L0_attn_norm_w, L0_ffn_wqkv, L0_ffn_q_scale, L0_ffn_k_scale, L0_ffn_wo, L0_ffn_ln_g, L0_ffn_ln_b, L0_ffn_w1, L0_ffn_b1, L0_ffn_w2, L0_ffn_b2, L1_attn_W1_q, L1_attn_W2_q, L1_attn_W1_k, L1_attn_W2_k, L1_attn_Wv, L1_attn_bv, L1_attn_Wo, L1_attn_bo, L1_ffn_w1_w, L1_ffn_w1_s, L1_ffn_w2_w, L1_ffn_w2_s, L1_ffn_h1_w, L1_ffn_h1_s, L1_ffn_h2_w, L1_ffn_h2_s, L1_ffn_w3_w, L1_ffn_w3_s, L2_attn_Wq, L2_attn_Wk, L2_attn_Wv, L2_attn_Wo, L2_ffn_gate_W, L2_ffn_gate_b, L2_ffn_expert_W, L2_ffn_expert_b, L3_attn_ln1_w, L3_attn_ln1_b, L3_attn_ln2_w, L3_attn_ln2_b, L3_attn_m1_W_in, L3_attn_m1_conv_w, L3_attn_m1_conv_b, L3_attn_m1_W_xp, L3_attn_m1_W_dt, L3_attn_m1_dt_b, L3_attn_m1_A_log, L3_attn_m1_D, L3_attn_m1_W_out, L3_attn_m2_W_in, L3_attn_m2_conv_w, L3_attn_m2_conv_b, L3_attn_m2_W_xp, L3_attn_m2_W_dt, L3_attn_m2_dt_b, L3_attn_m2_A_log, L3_attn_m2_D, L3_attn_m2_W_out, L3_ffn_w_gate, L3_ffn_w_up, L3_ffn_w_down):

    def _L0_attn_ref(x, w_q, w_k, w_v, w_a, w_b, w_g, w_out, A_log, dt_bias, conv_q, conv_k, conv_v, norm_w):
        import jax, jax.numpy as jnp
        from jax import lax
        import numpy as np
        D = 128
        H = 16
        DK = 64
        DV = 128
        KDIM = H * DK
        VDIM = H * DV
        CONV_K = 4
        B, T = (2, 512)
        EPS = 1e-05

        def _causal_conv_silu(x, w):
            C = x.shape[-1]
            Kw = w.shape[-1]
            xp = jnp.pad(x, ((0, 0), (Kw - 1, 0), (0, 0))).transpose(0, 2, 1)
            y = lax.conv_general_dilated(xp, w[:, None, :], window_strides=(1,), padding='VALID', feature_group_count=C, dimension_numbers=('NCH', 'OIH', 'NCH'))
            return jax.nn.silu(y.transpose(0, 2, 1))

        def _l2norm(x, eps=1e-06):
            return x * lax.rsqrt(jnp.sum(x * x, axis=-1, keepdims=True) + eps)

        def _gated_delta_rule(q, k, v, g, beta):
            scale = q.shape[-1] ** (-0.5)
            qs = jnp.moveaxis(q, 1, 0)
            ks_ = jnp.moveaxis(k, 1, 0)
            vs = jnp.moveaxis(v, 1, 0)
            gs = jnp.moveaxis(g, 1, 0)
            bs = jnp.moveaxis(beta, 1, 0)

            def step(S, inp):
                q_t, k_t, v_t, g_t, b_t = inp
                S = S * jnp.exp(g_t)[..., None, None]
                mem = jnp.einsum('bhk,bhkv->bhv', k_t, S)
                delta = (v_t - mem) * b_t[..., None]
                S = S + jnp.einsum('bhk,bhv->bhkv', k_t, delta)
                o_t = jnp.einsum('bhk,bhkv->bhv', q_t * scale, S)
                return (S, o_t)
            S0 = jnp.zeros((q.shape[0], q.shape[2], q.shape[3], v.shape[3]), q.dtype)
            _, o = lax.scan(step, S0, (qs, ks_, vs, gs, bs))
            return jnp.moveaxis(o, 0, 1)
        Bx, Tx, _ = x.shape
        q = x @ w_q
        k = x @ w_k
        v = x @ w_v
        beta = jax.nn.sigmoid(x @ w_b) * 2.0
        g = -jnp.exp(A_log) * jax.nn.softplus(x @ w_a + dt_bias)
        q = _causal_conv_silu(q, conv_q)
        k = _causal_conv_silu(k, conv_k)
        v = _causal_conv_silu(v, conv_v)
        q = q.reshape(Bx, Tx, H, DK)
        k = k.reshape(Bx, Tx, H, DK)
        v = v.reshape(Bx, Tx, H, DV)
        q = _l2norm(q)
        k = _l2norm(k)
        o = _gated_delta_rule(q, k, v, g, beta)
        g_gate = (x @ w_g).reshape(Bx, Tx, H, DV)
        rms = o * lax.rsqrt(jnp.mean(o * o, axis=-1, keepdims=True) + EPS)
        y = rms * norm_w * jax.nn.silu(g_gate)
        return y.reshape(Bx, Tx, VDIM) @ w_out

    def _L0_ffn_ref(x, wqkv, q_scale, k_scale, wo, ln_g, ln_b, w1, b1, w2, b2):
        import jax, jax.numpy as jnp
        import numpy as np
        DIM = 128
        DEPTH = 2
        HEADS = 8
        DIM_HEAD = 64
        WINDOW = 64
        INNER = HEADS * DIM_HEAD
        HID = int(DIM * 4 * 2 / 3)
        B, N = (2, 1024)
        QK_SCALE = 8.0

        def shift_token(t):
            t1, t2 = jnp.split(t, 2, axis=-1)
            t2 = jnp.pad(t2, ((0, 0), (1, 0), (0, 0)))[:, :-1]
            return jnp.concatenate([t1, t2], axis=-1)

        def l2norm(t):
            return t / jnp.clip(jnp.linalg.norm(t, axis=-1, keepdims=True), 1e-12)

        def rotate_half(x):
            x1, x2 = jnp.split(x, 2, axis=-1)
            return jnp.concatenate([-x2, x1], axis=-1)

        def rotary_xpos(q, k):
            n = q.shape[-2]
            half_idx = jnp.arange(0, DIM_HEAD, 2, dtype=jnp.float32)
            inv_freq = 1.0 / 10000.0 ** (half_idx / DIM_HEAD)
            t = jnp.arange(n, dtype=jnp.float32)
            freqs = t[:, None] * inv_freq[None, :]
            freqs = jnp.concatenate([freqs, freqs], axis=-1)
            base = (half_idx + 0.4 * DIM_HEAD) / (1.4 * DIM_HEAD)
            power = (t - n // 2) / float(WINDOW // 2)
            scale = base[None, :] ** power[:, None]
            scale = jnp.concatenate([scale, scale], axis=-1)
            cos, sin = (jnp.cos(freqs), jnp.sin(freqs))
            q = q * cos * scale + rotate_half(q) * sin * scale
            k = k * cos / scale + rotate_half(k) * sin / scale
            return (q, k)

        def local_attention(q, k, v):
            b, h, n, d = q.shape
            w = n // WINDOW
            bq = q.reshape(b, h, w, WINDOW, d) * QK_SCALE
            bk = k.reshape(b, h, w, WINDOW, d)
            bv = v.reshape(b, h, w, WINDOW, d)

            def look_around(t):
                p = jnp.pad(t, ((0, 0), (0, 0), (1, 0), (0, 0), (0, 0)))
                return jnp.concatenate([p[:, :, :w], p[:, :, 1:]], axis=3)
            bk, bv = (look_around(bk), look_around(bv))
            bt = jnp.arange(n).reshape(w, WINDOW)
            btp = jnp.pad(bt, ((1, 0), (0, 0)), constant_values=-1)
            btk = jnp.concatenate([btp[:w], btp[1:]], axis=1)
            sim = jnp.einsum('bhwid,bhwjd->bhwij', bq, bk)
            i = bt[:, :, None]
            j = btk[:, None, :]
            mask = (i < j) | (i > j + WINDOW) | (j == -1)
            sim = jnp.where(mask, -jnp.finfo(sim.dtype).max, sim)
            attn = jax.nn.softmax(sim, axis=-1)
            out = jnp.einsum('bhwij,bhwjd->bhwid', attn, bv)
            return out.reshape(b, h, n, d)

        def _layer(x, wqkv, qs, ksc, wo, lg, lb, w1, b1, w2, b2):
            b, n, _ = x.shape
            h = shift_token(x)
            qkv = h @ wqkv
            q, k, v = jnp.split(qkv, 3, axis=-1)
            to_heads = lambda t: t.reshape(b, n, HEADS, DIM_HEAD).transpose(0, 2, 1, 3)
            q, k, v = (to_heads(q), to_heads(k), to_heads(v))
            q = l2norm(q) * qs
            k = l2norm(k) * ksc
            q, k = rotary_xpos(q, k)
            o = local_attention(q, k, v)
            o = o.transpose(0, 2, 1, 3).reshape(b, n, INNER)
            x = x + o @ wo
            h = shift_token(x)
            mu = h.mean(-1, keepdims=True)
            var = h.var(-1, keepdims=True)
            h = (h - mu) / jnp.sqrt(var + 1e-05) * lg + lb
            h = h @ w1 + b1
            a, g = jnp.split(h, 2, axis=-1)
            h = a * jax.nn.gelu(g, approximate=False)
            x = x + h @ w2 + b2
            return x
        for l in range(DEPTH):
            x = _layer(x, wqkv[l], q_scale[l], k_scale[l], wo[l], ln_g[l], ln_b[l], w1[l], b1[l], w2[l], b2[l])
        return x

    def _L1_attn_ref(x, W1_q, W2_q, W1_k, W2_k, Wv, bv, Wo, bo):
        import jax, jax.numpy as jnp
        import numpy as np
        _J6 = jnp.array([[0, 0, 0, 0, 0, 1], [0, 0, 0, 0, -1, 0], [0, 0, 0, 1, 0, 0], [0, 0, 1, 0, 0, 0], [0, -1, 0, 0, 0, 0], [1, 0, 0, 0, 0, 0]], dtype=jnp.float32)
        _PAIRS = [(0, 1), (0, 2), (0, 3), (1, 2), (1, 3), (2, 3)]
        _H = 16
        _SCALE = 6.0 ** (-0.5)

        def _plucker_lines(p1, p2):
            parts = [p1[..., i] * p2[..., j] - p1[..., j] * p2[..., i] for i, j in _PAIRS]
            lines = jnp.stack(parts, axis=-1)
            n = jnp.linalg.norm(lines, axis=-1, keepdims=True)
            return lines / jnp.maximum(n, 1e-12)
        B, T, D = x.shape
        H = _H
        dh = D // H
        x_prev = jnp.pad(x[:, :-1, :], ((0, 0), (1, 0), (0, 0)))
        bg = jnp.concatenate([x, x_prev], axis=-1)
        q1 = (bg @ W1_q.T).reshape(B, T, H, 4)
        q2 = (bg @ W2_q.T).reshape(B, T, H, 4)
        k1 = (x @ W1_k.T).reshape(B, T, H, 4)
        k2 = (x @ W2_k.T).reshape(B, T, H, 4)
        q = _plucker_lines(q1, q2).transpose(0, 2, 1, 3)
        k = _plucker_lines(k1, k2).transpose(0, 2, 1, 3)
        Jk = k @ _J6.T
        logits = jnp.einsum('bhtc,bhsc->bhts', q, Jk) * _SCALE
        causal = jnp.tril(jnp.ones((T, T), dtype=bool))
        logits = jnp.where(causal[None, None], logits, -jnp.inf)
        attn = jax.nn.softmax(logits, axis=-1)
        v = (x @ Wv.T + bv).reshape(B, T, H, dh).transpose(0, 2, 1, 3)
        o = jnp.einsum('bhts,bhsd->bhtd', attn, v)
        o = o.transpose(0, 2, 1, 3).reshape(B, T, D)
        return o @ Wo.T + bo

    def _L1_ffn_ref(x, w1_w, w1_s, w2_w, w2_s, h1_w, h1_s, h2_w, h2_s, w3_w, w3_s):
        import jax, jax.numpy as jnp
        import numpy as np
        D_IN, D_HID = (128, 512)

        def _ternary(key, shape):
            return jax.random.randint(key, shape, -1, 2).astype(jnp.float32)

        def _tlin(x, w, s):
            return jnp.einsum('bsi,oi->bso', x, w) * s
        h = jax.nn.silu(_tlin(x, w1_w, w1_s)) * _tlin(x, w2_w, w2_s)
        h = jax.nn.gelu(_tlin(h, h1_w, h1_s), approximate=False)
        h = jax.nn.gelu(_tlin(h, h2_w, h2_s), approximate=False)
        return _tlin(h, w3_w, w3_s)

    def _L2_attn_ref(x, Wq, Wk, Wv, Wo):
        import jax, jax.numpy as jnp
        import numpy as np
        H = 16
        D = 64
        BQ = 64
        BKV = 64

        def _flash_tiled(q, k, v, scale):
            B, nh, S, d = q.shape
            nq, nkv = (S // BQ, S // BKV)
            qb = q.reshape(B, nh, nq, BQ, d)
            kb = k.reshape(B, nh, nkv, BKV, d).transpose(2, 0, 1, 3, 4)
            vb = v.reshape(B, nh, nkv, BKV, d).transpose(2, 0, 1, 3, 4)
            o0 = jnp.zeros((B, nh, nq, BQ, d), q.dtype)
            m0 = jnp.full((B, nh, nq, BQ), -jnp.inf, q.dtype)
            l0 = jnp.zeros((B, nh, nq, BQ), q.dtype)

            def step(carry, kv):
                o, m, l = carry
                kj, vj = kv
                s = jnp.einsum('bhnqd,bhkd->bhnqk', qb, kj) * scale
                m_new = jnp.maximum(m, s.max(axis=-1))
                p = jnp.exp(s - m_new[..., None])
                alpha = jnp.exp(m - m_new)
                l_new = alpha * l + p.sum(axis=-1)
                o_new = (alpha[..., None] * o + jnp.einsum('bhnqk,bhkd->bhnqd', p, vj)) / l_new[..., None]
                return ((o_new, m_new, l_new), None)
            (o, _, _), _ = jax.lax.scan(step, (o0, m0, l0), (kb, vb))
            return o.reshape(B, nh, S, d)
        B, S, dim = x.shape
        scale = D ** (-0.5)
        q = (x @ Wq).reshape(B, S, H, D).transpose(0, 2, 1, 3)
        k = (x @ Wk).reshape(B, S, H, D).transpose(0, 2, 1, 3)
        v = (x @ Wv).reshape(B, S, H, D).transpose(0, 2, 1, 3)
        o = _flash_tiled(q, k, v, scale)
        out = o.transpose(0, 2, 1, 3).reshape(B, S, H * D)
        return out @ Wo

    def _L2_ffn_ref(x, gate_W, gate_b, expert_W, expert_b):
        import jax, jax.numpy as jnp
        import numpy as np
        B, S, D, E, K = (4, 256, 128, 8, 2)
        EPS, W_THRES, TEMP = (0.0001, 0.1, 1.0)
        scores = jnp.maximum((x @ gate_W + gate_b) / TEMP, EPS)
        p = jax.nn.softmax(scores, axis=-1)
        _, topk_idx = jax.lax.top_k(p, K)
        topk_mask = jax.nn.one_hot(topk_idx, E, dtype=p.dtype).sum(-2) > 0
        w = jnp.maximum(p, W_THRES)
        w_gather = jnp.take_along_axis(w, topk_idx, axis=-1)
        total = jax.lax.stop_gradient(w_gather.sum(-1, keepdims=True))
        w = w / total
        comb = jnp.where(topk_mask, w, jnp.zeros_like(w))
        y = jnp.einsum('bsd,edf->bsef', x, expert_W) + expert_b
        out = jnp.einsum('bsef,bse->bsf', y, comb) / K
        return out

    def _L3_attn_ref(x, ln1_w, ln1_b, ln2_w, ln2_b, m1_W_in, m1_conv_w, m1_conv_b, m1_W_xp, m1_W_dt, m1_dt_b, m1_A_log, m1_D, m1_W_out, m2_W_in, m2_conv_w, m2_conv_b, m2_W_xp, m2_W_dt, m2_dt_b, m2_A_log, m2_D, m2_W_out):
        import jax, jax.numpy as jnp
        import numpy as np
        D = 128
        E = 2 * D
        N = 64
        R = D // 16
        K = 4
        BATCH, L = (2, 256)
        LN_EPS = 1e-05

        def _layernorm(x, w, b):
            mu = x.mean(-1, keepdims=True)
            var = ((x - mu) ** 2).mean(-1, keepdims=True)
            return (x - mu) * jax.lax.rsqrt(var + LN_EPS) * w + b

        def _silu(x):
            return x * jax.nn.sigmoid(x)

        def _mamba(x, W_in, conv_w, conv_b, W_xp, W_dt, dt_b, A_log, Dp, W_out):
            Bsz = x.shape[0]
            xz = x @ W_in.T
            xp, z = jnp.split(xz, 2, axis=-1)
            xc = jax.lax.conv_general_dilated(xp.transpose(0, 2, 1), conv_w[:, None, :], window_strides=(1,), padding=[(K - 1, 0)], dimension_numbers=('NCH', 'OIH', 'NCH'), feature_group_count=E)
            xc = _silu(xc.transpose(0, 2, 1) + conv_b)
            x_dbl = xc @ W_xp.T
            dt_lo, Bm, Cm = (x_dbl[..., :R], x_dbl[..., R:R + N], x_dbl[..., R + N:])
            dt = jax.nn.softplus(dt_lo @ W_dt.T + dt_b)
            A = -jnp.exp(A_log)

            def step(h, inp):
                xt, dtt, Bt, Ct = inp
                dA = jnp.exp(dtt[:, :, None] * A)
                h = dA * h + (dtt * xt)[:, :, None] * Bt[:, None, :]
                y = jnp.einsum('ben,bn->be', h, Ct)
                return (h, y)
            h0 = jnp.zeros((Bsz, E, N), x.dtype)
            xs = (xc.transpose(1, 0, 2), dt.transpose(1, 0, 2), Bm.transpose(1, 0, 2), Cm.transpose(1, 0, 2))
            _, ys = jax.lax.scan(step, h0, xs)
            y = ys.transpose(1, 0, 2) + xc * Dp
            y = y * _silu(z)
            return y @ W_out.T
        xn = _layernorm(x, ln1_w, ln1_b)
        x1 = _mamba(xn, m1_W_in, m1_conv_w, m1_conv_b, m1_W_xp, m1_W_dt, m1_dt_b, m1_A_log, m1_D, m1_W_out)
        xr = jnp.flip(xn, axis=1)
        x2 = jnp.flip(_mamba(xr, m2_W_in, m2_conv_w, m2_conv_b, m2_W_xp, m2_W_dt, m2_dt_b, m2_A_log, m2_D, m2_W_out), axis=1)
        x_mamba = _layernorm(x1 + x2, ln2_w, ln2_b)
        return x_mamba + xn

    def _L3_ffn_ref(x, w_gate, w_up, w_down):
        import jax, jax.numpy as jnp
        import numpy as np
        DIM = 128
        HIDDEN = 384
        SCALE = 1.0 / 127.0

        def _dequant(w_int, dtype):
            return w_int.astype(dtype) * jnp.asarray(SCALE, dtype)
        wg = _dequant(w_gate, x.dtype)
        wu = _dequant(w_up, x.dtype)
        wd = _dequant(w_down, x.dtype)
        gate = jnp.einsum('bsd,hd->bsh', x, wg)
        up = jnp.einsum('bsd,hd->bsh', x, wu)
        h = jax.nn.silu(gate) * up
        return jnp.einsum('bsh,dh->bsd', h, wd)
    x = L0_attn_x
    x = x + _layernorm(_L0_attn_ref(_layernorm(x, axis=-1), L0_attn_w_q, L0_attn_w_k, L0_attn_w_v, L0_attn_w_a, L0_attn_w_b, L0_attn_w_g, L0_attn_w_out, L0_attn_A_log, L0_attn_dt_bias, L0_attn_conv_q, L0_attn_conv_k, L0_attn_conv_v, L0_attn_norm_w), axis=-1)
    x = x + _layernorm(_L0_ffn_ref(_layernorm(x, axis=-1), L0_ffn_wqkv, L0_ffn_q_scale, L0_ffn_k_scale, L0_ffn_wo, L0_ffn_ln_g, L0_ffn_ln_b, L0_ffn_w1, L0_ffn_b1, L0_ffn_w2, L0_ffn_b2), axis=-1)
    x = x + _layernorm(_L1_attn_ref(_layernorm(x, axis=-1), L1_attn_W1_q, L1_attn_W2_q, L1_attn_W1_k, L1_attn_W2_k, L1_attn_Wv, L1_attn_bv, L1_attn_Wo, L1_attn_bo), axis=-1)
    x = x + _layernorm(_L1_ffn_ref(_layernorm(x, axis=-1), L1_ffn_w1_w, L1_ffn_w1_s, L1_ffn_w2_w, L1_ffn_w2_s, L1_ffn_h1_w, L1_ffn_h1_s, L1_ffn_h2_w, L1_ffn_h2_s, L1_ffn_w3_w, L1_ffn_w3_s), axis=-1)
    x = x + _layernorm(_L2_attn_ref(_layernorm(x, axis=-1), L2_attn_Wq, L2_attn_Wk, L2_attn_Wv, L2_attn_Wo), axis=-1)
    x = x + _layernorm(_L2_ffn_ref(_layernorm(x, axis=-1), L2_ffn_gate_W, L2_ffn_gate_b, L2_ffn_expert_W, L2_ffn_expert_b), axis=-1)
    x = x + _layernorm(_L3_attn_ref(_layernorm(x, axis=-1), L3_attn_ln1_w, L3_attn_ln1_b, L3_attn_ln2_w, L3_attn_ln2_b, L3_attn_m1_W_in, L3_attn_m1_conv_w, L3_attn_m1_conv_b, L3_attn_m1_W_xp, L3_attn_m1_W_dt, L3_attn_m1_dt_b, L3_attn_m1_A_log, L3_attn_m1_D, L3_attn_m1_W_out, L3_attn_m2_W_in, L3_attn_m2_conv_w, L3_attn_m2_conv_b, L3_attn_m2_W_xp, L3_attn_m2_W_dt, L3_attn_m2_dt_b, L3_attn_m2_A_log, L3_attn_m2_D, L3_attn_m2_W_out), axis=-1)
    x = x + _layernorm(_L3_ffn_ref(_layernorm(x, axis=-1), L3_ffn_w_gate, L3_ffn_w_up, L3_ffn_w_down), axis=-1)
    return x

_drawn_inputs = setup_inputs


def setup_inputs(seed=0):
    import zlib

    import numpy as np

    out = dict(_drawn_inputs(seed))
    spreads = {'L0_attn_norm_w': (1.0, 0.2),
     'L0_ffn_q_scale': (1.0, 0.6),
     'L0_ffn_k_scale': (1.0, 0.6),
     'L0_ffn_ln_g': (1.0, 0.6),
     'L0_ffn_ln_b': (0.0, 0.769),
     'L0_ffn_b1': (0.0, 0.387),
     'L0_ffn_b2': (0.0, 0.1),
     'L1_attn_bv': (0.0, 0.1),
     'L1_attn_bo': (0.0, 0.1),
     'L2_ffn_gate_b': (0.0, 0.1),
     'L2_ffn_expert_b': (0.0, 0.1),
     'L3_attn_ln1_w': (1.0, 0.2),
     'L3_attn_ln1_b': (0.0, 0.317),
     'L3_attn_ln2_w': (1.0, 0.561),
     'L3_attn_ln2_b': (0.0, 0.352),
     'L3_attn_m1_conv_b': (0.0, 0.1),
     'L3_attn_m1_D': (1.0, 0.6),
     'L3_attn_m2_conv_b': (0.0, 0.1),
     'L3_attn_m2_D': (1.0, 0.6)}
    factors = {'L1_attn_W1_q': 3.532,
     'L1_attn_W2_q': 3.626,
     'L1_attn_W1_k': 4.429,
     'L1_attn_W2_k': 3.112,
     'L3_attn_m1_W_xp': 8.0,
     'L3_attn_m1_W_dt': 8.0,
     'L3_attn_m1_dt_b': 8.0,
     'L3_attn_m1_A_log': 8.0,
     'L3_attn_m2_W_xp': 8.0,
     'L3_attn_m2_W_dt': 8.0,
     'L3_attn_m2_dt_b': 8.0,
     'L3_attn_m2_A_log': 8.0}
    for name, (base, spread) in spreads.items():
        noise = np.random.default_rng([zlib.crc32(name.encode()), seed]).standard_normal(out[name].shape)
        drawn = base * np.exp(spread * noise) if base else spread * noise
        out[name] = jnp.asarray(drawn.astype(out[name].dtype))
    for name, factor in factors.items():
        out[name] = (out[name] * factor).astype(out[name].dtype)
    return out
```

```python
from contextlib import ExitStack

import concourse.bass as bass
from concourse import mybir

F32 = mybir.dt.float32
BF16 = mybir.dt.bfloat16
I32 = mybir.dt.int32
ALU = mybir.AluOpType
ACT = mybir.ActivationFunctionType
AXX = mybir.AxisListType.X

P = 128
B, T, D = 8, 256, 128
NT = B * T // P
TPB = T // P
PAD = 4
LNEPS = 1e-5


class Core:

    def __init__(self, nc, dram, ctx):
        self.nc, self.dram, self.parts, self.cleared = nc, dram, 0, []
        sb = lambda name, shape, dt=F32: ctx.enter_context(nc.sbuf_tensor(name, shape, dt))
        self.banks = ctx.enter_context(nc.psum_tensor("banks", [P, 8, 512], F32))
        self.bank = [self.banks[:, i, :] for i in range(8)]
        self.X = sb("residual", [P, NT, D])
        self.Y = sb("block_out", [P, NT, D])
        self.HT = sb("norm_featmajor", [P, B, PAD + T])
        self.H = sb("norm", [P, NT, D])
        self.ident = sb("ident", [P, P])


class Part:

    def __init__(self, k):
        self.k, self.nc, self.ctx, self.sems = k, k.nc, ExitStack(), []
        k.parts += 1
        self.id = k.parts

    def __enter__(self):
        return self

    def sb(self, name, shape, dt=F32):
        return self.ctx.enter_context(self.nc.sbuf_tensor(f"{name}_{self.id}", shape, dt))

    def sem(self, name):
        self.sems.append(self.nc.alloc_semaphore(f"{name}_{self.id}"))
        return self.sems[-1]

    def __exit__(self, *a):
        if a[0] is None:
            for s in self.k.cleared:
                self.nc.release_semaphore(s)
            for s in self.sems:
                self.nc.gpsimd.sem_clear(s)
            self.k.cleared = self.sems
        return self.ctx.__exit__(*a)


def over(ap, n):
    return ap.unsqueeze(len(ap.shape)).to_broadcast([*ap.shape, n])


def across(ap, n):
    return ap.unsqueeze(1).to_broadcast([ap.shape[0], n, *ap.shape[1:]])


def load_residual(k):
    nc = k.nc
    with Part(k) as p:
        loaded = p.sem("loaded")
        with nc.Block() as block:
            @block.sync
            def _(sp):
                sp.dma_start(k.X[:], k.dram["x"]).then_inc(loaded, 16)
                sp.dma_start(k.ident[:], k.dram["ident"]).then_inc(loaded, 16)
                sp.wait_ge(loaded, 32)

            @block.vector
            def _(dve):
                nc.vector.memset(k.HT[:], 0.0)


def store_residual(k):
    nc = k.nc
    with Part(k) as p:
        stored = p.sem("stored")
        with nc.Block() as block:
            @block.sync
            def _(sp):
                sp.dma_start(k.dram["out"], k.X[:]).then_inc(stored, 16)
                sp.wait_ge(stored, 16)


def layer_norm_steps(nc, dve, src, dst, stats, mv, rstd, var_ready, rstd_ready):
    for t in range(NT):
        nc.vector.bn_stats(stats[:, t, :], src[:, t, :])
    dve.drain()
    for t in range(NT):
        nc.vector.bn_aggr(mv[:, t, :], stats[:, t, :])
    dve.drain()
    nc.vector.tensor_scalar_add(rstd[:], mv[:, :, 1], LNEPS).then_inc(var_ready, 1)
    dve.wait_ge(*rstd_ready)
    for t in range(NT):
        nc.vector.tensor_scalar(dst[:, t, :], src[:, t, :], mv[:, t, 0:1], rstd[:, t:t + 1],
                                ALU.subtract, ALU.mult)
    dve.drain()


def normalise(k, add_y=False, make_ht=True, src=None, affine=None, norm=True):
    nc = k.nc
    src = k.X if src is None else src
    rounds = int(add_y) + int(make_ht and norm)
    with Part(k) as p:
        stats = p.sb("stats", [P, NT, 6])
        mv = p.sb("meanvar", [P, NT, 2])
        rstd = p.sb("rstd", [P, NT])
        half = p.sb("minus_half", [P, NT])
        H = k.H
        var_ready, rstd_ready = p.sem("var"), p.sem("rstd")
        h_ready, turned = p.sem("h"), p.sem("turned")
        turn_from = H if norm else src
        with nc.Block() as block:
            @block.gpsimd
            def _(pool):
                nc.gpsimd.memset(half[:], -0.5)
                pool.drain()
                for r in range(rounds):
                    pool.wait_ge(var_ready, r + 1)
                    nc.gpsimd.tensor_tensor(rstd[:], rstd[:], half[:], ALU.pow).then_inc(rstd_ready, 1)

            @block.vector
            def _(dve):
                r = 0
                if add_y:
                    r += 1
                    layer_norm_steps(nc, dve, k.Y, H, stats, mv, rstd, var_ready, (rstd_ready, r))
                    nc.vector.tensor_add(k.X[:], k.X[:], H[:])
                    dve.drain()
                if make_ht and norm:
                    r += 1
                    layer_norm_steps(nc, dve, src, H, stats, mv, rstd, var_ready, (rstd_ready, r))
                    if affine is not None:
                        nc.vector.tensor_tensor(H[:], H[:], across(affine[:, 0, :], NT), ALU.mult)
                        dve.drain()
                        nc.vector.tensor_tensor(H[:], H[:], across(affine[:, 1, :], NT), ALU.add)
                        dve.drain()
                nc.vector.engine_nop().then_inc(h_ready, 1)

            if make_ht:
                @block.tensor
                def _(pe):
                    pe.wait_ge(h_ready, 1)
                    for t in range(NT):
                        i = nc.tensor.transpose(k.bank[t // 4][:, t % 4 * P:(t % 4 + 1) * P], turn_from[:, t, :], k.ident[:])
                        if t % 4 == 3:
                            i.then_inc(turned, 1)

                @block.scalar
                def _(act):
                    for g in range(4):
                        act.wait_ge(turned, g + 1)
                        nc.scalar.activation(k.HT[:, 2 * g:2 * g + 2, PAD:PAD + T],
                                             k.bank[g][:].rearrange("p (b t) -> p b t", b=2), ACT.Copy)
                    act.drain()


def ffn_ternary(k):
    nc, HID, CH = k.nc, 512, 512
    KB, NCH = HID // P, B * T // CH
    bpc = CH // T
    with Part(k) as p:
        w12 = p.sb("w12", [P, 2, HID])
        wh = p.sb("wh", [P, 2, KB, HID])
        w3 = p.sb("w3", [P, KB, D])
        sc = p.sb("scales", [P, 4, KB])
        s3 = p.sb("s3", [P, D])
        gate = p.sb("gate", [P, KB, CH])
        hid = [p.sb(f"hid{i}", [P, KB, CH]) for i in range(3)]
        loaded, w3_loaded = p.sem("loaded"), p.sem("w3_loaded")
        pair, gated, prod = p.sem("pair"), p.sem("gated"), p.sem("prod")
        lin = [p.sem("lin1"), p.sem("lin2")]
        gelu = [p.sem("gelu1"), p.sem("gelu2")]
        down, out = p.sem("down"), p.sem("out")
        with nc.Block() as block:
            @block.sync
            def _(sp):
                sp.dma_start(w12[:], k.dram["l1f_w12"]).then_inc(loaded, 16)
                sp.dma_start(sc[:], k.dram["l1f_sc"]).then_inc(loaded, 16)
                sp.dma_start(wh[:], k.dram["l1f_wh"]).then_inc(loaded, 16)
                sp.dma_start(w3[:], k.dram["l1f_w3"]).then_inc(w3_loaded, 16)
                sp.dma_start(s3[:], k.dram["l1f_s3"].partition_broadcast(P)).then_inc(w3_loaded, 16)

            @block.tensor
            def _(pe):
                pe.wait_ge(loaded, 48)
                pe.wait_ge(w3_loaded, 32)
                with pe.Fori(0, NCH) as c:
                    x = k.HT[:, bass.ds(c * bpc, bpc), PAD:PAD + T]
                    pe.wait_ge(out, c + 1)
                    for ob in range(KB):
                        for j in range(2):
                            i = nc.tensor.matmul(k.bank[4 * j + ob][:].rearrange("p (b t) -> p b t", b=bpc),
                                                 w12[:, j, ob * P:(ob + 1) * P], x, start=True, stop=True)
                        i.then_inc(pair, 1)
                    for l in range(2):
                        pe.wait_ge(*((prod, c * KB + KB) if l == 0 else (gelu[0], c * KB + KB)))
                        for ob in range(KB):
                            for kb in range(KB):
                                i = nc.tensor.matmul(k.bank[4 * l + ob][:], wh[:, l, kb, ob * P:(ob + 1) * P],
                                                     hid[l][:, kb, :], start=kb == 0, stop=kb == KB - 1)
                            i.then_inc(lin[l], 1)
                    pe.wait_ge(gelu[1], c * KB + KB)
                    for tt in range(CH // P):
                        for kb in range(KB):
                            i = nc.tensor.matmul(k.bank[0][:, tt * D:(tt + 1) * D], hid[2][:, kb, tt * P:(tt + 1) * P],
                                                 w3[:, kb, :], start=kb == 0, stop=kb == KB - 1)
                    i.then_inc(down, 1)

            @block.scalar
            def _(act):
                act.wait_ge(loaded, 48)
                with act.Fori(0, NCH) as c:
                    for ob in range(KB):
                        act.wait_ge(pair, c * KB + ob + 1)
                        nc.scalar.activation(gate[:, ob, :], k.bank[ob][:], ACT.Silu,
                                             scale=sc[:, 0, ob:ob + 1]).then_inc(gated, 1)
                    for l in range(2):
                        for ob in range(KB):
                            act.wait_ge(lin[l], c * KB + ob + 1)
                            nc.scalar.activation(hid[l + 1][:, ob, :], k.bank[4 * l + ob][:], ACT.Gelu,
                                                 scale=sc[:, 2 + l, ob:ob + 1]).then_inc(gelu[l], 1)

            @block.vector
            def _(dve):
                dve.sem_inc(out, 1)
                dve.wait_ge(w3_loaded, 32)
                dve.wait_ge(loaded, 48)
                with dve.Fori(0, NCH) as c:
                    for ob in range(KB):
                        dve.wait_ge(gated, c * KB + ob + 1)
                        nc.vector.scalar_tensor_tensor(out=hid[0][:, ob, :], in0=k.bank[4 + ob][:],
                                                       scalar=sc[:, 1, ob:ob + 1], in1=gate[:, ob, :],
                                                       op0=ALU.mult, op1=ALU.mult).then_inc(prod, 1)
                    dve.wait_ge(down, c + 1)
                    nc.vector.tensor_tensor(k.Y[:, bass.ds(c * (CH // P), CH // P), :],
                                            k.bank[0][:].rearrange("p (t d) -> p t d", d=D),
                                            across(s3[:], CH // P), ALU.mult).then_inc(out, 1)


def ffn_int8(k):
    nc, HID, CH = k.nc, 384, 512
    KB, NCH = HID // P, B * T // CH
    bpc = CH // T
    NW = 2 * HID + KB * D
    with Part(k) as p:
        wi = p.sb("w_int", [P, NW], I32)
        w = p.sb("w", [P, NW])
        gate = p.sb("gate", [P, KB, CH])
        hid = p.sb("hid", [P, KB, CH])
        loaded, scaled = p.sem("loaded"), p.sem("scaled")
        pair, gated, prod, down, out = p.sem("pair"), p.sem("gated"), p.sem("prod"), p.sem("down"), p.sem("out")
        with nc.Block() as block:
            @block.sync
            def _(sp):
                sp.dma_start(wi[:, 0:2 * HID], k.dram["l3f_wgu"]).then_inc(loaded, 16)
                sp.dma_start(wi[:, 2 * HID:], k.dram["l3f_wd"]).then_inc(loaded, 16)

            @block.tensor
            def _(pe):
                pe.wait_ge(scaled, 1)
                with pe.Fori(0, NCH) as c:
                    x = k.HT[:, bass.ds(c * bpc, bpc), PAD:PAD + T]
                    pe.wait_ge(out, c + 1)
                    for ob in range(KB):
                        for j in range(2):
                            i = nc.tensor.matmul(k.bank[KB * j + ob][:].rearrange("p (b t) -> p b t", b=bpc),
                                                 w[:, j * HID + ob * P:j * HID + (ob + 1) * P], x,
                                                 start=True, stop=True)
                        i.then_inc(pair, 1)
                    pe.wait_ge(prod, c * KB + KB)
                    for tt in range(CH // P):
                        for kb in range(KB):
                            i = nc.tensor.matmul(k.bank[6][:, tt * D:(tt + 1) * D], hid[:, kb, tt * P:(tt + 1) * P],
                                                 w[:, 2 * HID + kb * D:2 * HID + (kb + 1) * D],
                                                 start=kb == 0, stop=kb == KB - 1)
                    i.then_inc(down, 1)

            @block.scalar
            def _(act):
                with act.Fori(0, NCH) as c:
                    for ob in range(KB):
                        act.wait_ge(pair, c * KB + ob + 1)
                        nc.scalar.activation(gate[:, ob, :], k.bank[ob][:], ACT.Silu).then_inc(gated, 1)

            @block.vector
            def _(dve):
                dve.sem_inc(out, 1)
                dve.wait_ge(loaded, 32)
                nc.vector.tensor_scalar(w[:], wi[:], 1.0 / 127.0, None, ALU.mult).then_inc(scaled, 1)
                with dve.Fori(0, NCH) as c:
                    for ob in range(KB):
                        dve.wait_ge(gated, c * KB + ob + 1)
                        nc.vector.tensor_tensor(hid[:, ob, :], k.bank[KB + ob][:], gate[:, ob, :],
                                                ALU.mult).then_inc(prod, 1)
                    dve.wait_ge(down, c + 1)
                    nc.vector.tensor_copy(k.Y[:, bass.ds(c * (CH // P), CH // P), :],
                                          k.bank[6][:].rearrange("p (t d) -> p t d", d=D)).then_inc(out, 1)


def ffn_experts(k):
    nc, E, TOPK, EPS, THRES = k.nc, 8, 2, 1e-4, 0.1
    with Part(k) as p:
        gw, gb = p.sb("gate_w", [P, E]), p.sb("gate_b", [P, E])
        ew, eb = p.sb("expert_w", [P, E * D]), p.sb("expert_b", [1, E * D])
        iota, ones = p.sb("iota", [P, E]), p.sb("ones", [1, P])
        xb = p.sb("x_batch", [P, 2, T])
        S, M, W, V = (p.sb(n, [P, NT, E]) for n in ("score", "mask", "weight", "tmp"))
        r = p.sb("row", [P, NT])
        loaded, xb_ready = p.sem("loaded"), p.sem("xb_ready")
        gates, exped, clipped = p.sem("gates"), p.sem("exped"), p.sem("clipped")
        experts, mixed, ones_ready = p.sem("experts"), p.sem("mixed"), p.sem("ones")
        sc3 = k.bank[0][:, 0:NT * E].rearrange("p (t e) -> p t e", e=E)
        with nc.Block() as block:
            @block.sync
            def _(sp):
                sp.dma_start(gw[:], k.dram["l2f_gw"]).then_inc(loaded, 16)
                sp.dma_start(gb[:], k.dram["l2f_gb"].partition_broadcast(P)).then_inc(loaded, 16)
                sp.dma_start(ew[:], k.dram["l2f_ew"]).then_inc(loaded, 16)
                sp.dma_start(eb[:], k.dram["l2f_eb"]).then_inc(loaded, 16)
                sp.dma_start(iota[:], k.dram["iota8"].partition_broadcast(P)).then_inc(loaded, 16)

            @block.gpsimd
            def _(pool):
                nc.gpsimd.memset(ones[:], 1.0).then_inc(ones_ready, 1)

            @block.tensor
            def _(pe):
                pe.wait_ge(loaded, 80)
                pe.wait_ge(ones_ready, 1)
                for t in range(NT):
                    i = nc.tensor.matmul(sc3[:, t, :], k.HT[:, t // TPB, PAD + t % TPB * P:PAD + (t % TPB + 1) * P],
                                         gw[:], start=True, stop=True)
                i.then_inc(gates, 1)
                with pe.Fori(0, B // 2) as bb:
                    pe.wait_ge(xb_ready, bb + 1)
                    for s in range(2):
                        for t in range(TPB):
                            u = 2 * s + t
                            pe.wait_ge(mixed, bb * 4 + u + 1)
                            for h in range(2):
                                o = k.bank[2 * u + h][:]
                                nc.tensor.matmul(o, ones[:], eb[:, h * 512:(h + 1) * 512], start=True, stop=False)
                                i = nc.tensor.matmul(o, xb[:, s, t * P:(t + 1) * P], ew[:, h * 512:(h + 1) * 512],
                                                     start=False, stop=True)
                            i.then_inc(experts, 1)

            @block.scalar
            def _(act):
                act.wait_ge(clipped, 1)
                nc.scalar.activation(W[:], S[:], ACT.Exp).then_inc(exped, 1)

            @block.vector
            def _(dve):
                v = nc.vector
                dve.sem_inc(mixed, 4)
                dve.wait_ge(loaded, 80)
                dve.wait_ge(gates, 1)
                v.tensor_tensor(S[:], sc3, across(gb[:], NT), ALU.add)
                dve.drain()
                v.tensor_scalar_max(S[:], S[:], EPS)
                dve.drain()
                v.tensor_reduce(r[:], S[:], AXX, ALU.max)
                dve.drain()
                v.tensor_tensor(S[:], S[:], over(r[:], E), ALU.subtract).then_inc(clipped, 1)
                dve.wait_ge(exped, 1)
                v.tensor_reduce(r[:], W[:], AXX, ALU.add)
                dve.drain()
                v.reciprocal(r[:], r[:])
                dve.drain()
                v.tensor_tensor(W[:], W[:], over(r[:], E), ALU.mult)
                dve.drain()
                v.tensor_copy(S[:], W[:])
                v.memset(M[:], 0.0)
                for _ in range(TOPK):
                    dve.drain()
                    v.tensor_reduce(r[:], S[:], AXX, ALU.max)
                    dve.drain()
                    v.tensor_tensor(V[:], S[:], over(r[:], E), ALU.is_equal)
                    dve.drain()
                    v.scalar_tensor_tensor(out=V[:], in0=V[:], scalar=-100.0, in1=across(iota[:], NT),
                                           op0=ALU.mult, op1=ALU.add)
                    dve.drain()
                    v.tensor_reduce(r[:], V[:], AXX, ALU.min)
                    dve.drain()
                    v.tensor_tensor(V[:], V[:], over(r[:], E), ALU.is_equal)
                    dve.drain()
                    v.tensor_add(M[:], M[:], V[:])
                    v.scalar_tensor_tensor(out=S[:], in0=V[:], scalar=-2.0, in1=S[:], op0=ALU.mult, op1=ALU.add)
                dve.drain()
                v.scalar_tensor_tensor(out=W[:], in0=W[:], scalar=THRES, in1=M[:], op0=ALU.max, op1=ALU.mult)
                dve.drain()
                v.tensor_reduce(r[:], W[:], AXX, ALU.add)
                dve.drain()
                v.reciprocal(r[:], r[:])
                dve.drain()
                v.scalar_tensor_tensor(out=W[:], in0=W[:], scalar=1.0 / TOPK, in1=over(r[:], E),
                                       op0=ALU.mult, op1=ALU.mult)
                dve.drain()
                with dve.Fori(0, B // 2) as bb:
                    v.tensor_copy(xb[:], k.HT[:, bass.ds(bb * 2, 2), PAD:PAD + T]).then_inc(xb_ready, 1)
                    for s in range(2):
                        for t in range(TPB):
                            u = 2 * s + t
                            dve.wait_ge(experts, bb * 4 + u + 1)
                            y = k.Y[:, bb * 4 + u, :]
                            for e in range(E):
                                o = k.bank[2 * u + e // 4][:, e % 4 * D:(e % 4 + 1) * D]
                                c = W[:, bb * 4 + u, e:e + 1]
                                if e == 0:
                                    i = v.tensor_scalar(y, o, c, None, ALU.mult)
                                else:
                                    i = v.scalar_tensor_tensor(out=y, in0=o, scalar=c, in1=y,
                                                               op0=ALU.mult, op1=ALU.add)
                                if e < E - 1:
                                    dve.drain()
                            i.then_inc(mixed, 1)


def lay_out_flash(i, d, np):
    for n in "qkv":
        d[f"l2a_w{n}"] = i[f"L2_attn_W{n}"]
    d["l2a_wo"] = by_blocks(i["L2_attn_Wo"])
    d["l2a_forget"] = np.tile(np.array([-3e38, 0, 0, 0], np.float32), 4)
    d["l2a_keep"] = np.tile(np.array([0, 1, 1, 1], np.float32), 4)


def flash_attn(k):
    nc, H, DK, NJ = k.nc, 16, 64, 4
    C = H * DK
    CB = C // P
    HG = 4
    units = [(g, t) for g in range(H // HG) for t in range(TPB)]
    NU = len(units)
    with Part(k) as p:
        w = {n: p.sb("w" + n, [P, C]) for n in "qkv"}
        wo = p.sb("wo", [P, CB, D])
        forget, keep = p.sb("forget", [P, 16]), p.sb("keep", [P, 16])
        xb = p.sb("x_batch", [P, T])
        qk = p.sb("qk_featmajor", [P, 2, CB, T])
        v = p.sb("v", [P, TPB, C])
        S = p.sb("probs", [P, 2, HG, T])
        SW = p.sb("weighted", [P, 2, HG, T])
        PT = p.sb("weighted_keymajor", [P, 2, HG * TPB, P])
        O = p.sb("heads_out", [P, TPB, C])
        OT = p.sb("heads_out_featmajor", [P, CB, T])
        bm, m, al, ls, rs, f = (p.sb(n, [P, 2, 16]) for n in ("bm", "m", "alpha", "l", "rowsum", "f"))
        loaded, xb_ready = p.sem("loaded"), p.sem("xb_ready")
        proj, proj_act, proj_dve = p.sem("proj"), p.sem("proj_act"), p.sem("proj_dve")
        scores, shifted, exped = p.sem("scores"), p.sem("shifted"), p.sem("exped")
        w_ready, weighted, turned, pt_ready = p.sem("w_ready"), p.sem("weighted"), p.sem("turned"), p.sem("pt_ready")
        heads, heads_out = p.sem("heads"), p.sem("heads_out")
        o_turned, ot_act, ot_dve, final, done = p.sem("o_turned"), p.sem("ot_act"), p.sem("ot_dve"), p.sem("final"), p.sem("done")

        qk_flat = qk[:].rearrange("p a c t -> p (a c t)")
        v_flat = v[:].rearrange("p a c -> p (a c)")
        dest = [qk_flat[:, n * 512:(n + 1) * 512] for n in range(8)] + \
               [v_flat[:, n * 512:(n + 1) * 512] for n in range(4)]

        def project(pe, b):
            pe.wait_ge(xb_ready, b + 1)
            for n in range(12):
                o = k.bank[n % 6][:]
                if n >= 6:
                    sem = proj_act if n % 2 == 0 else proj_dve
                    pe.wait_ge(sem, b * 6 + (n - 6) // 2 + 1)
                if n < 8:
                    for h in range(2):
                        c = n % 4 * 2 + h
                        i = nc.tensor.matmul(o[:, h * T:(h + 1) * T], w["qk"[n // 4]][:, c * P:(c + 1) * P], xb[:],
                                             start=True, stop=True)
                else:
                    t, h = (n - 8) // 2, (n - 8) % 2
                    i = nc.tensor.matmul(o, xb[:, t * P:(t + 1) * P], w["v"][:, h * 512:(h + 1) * 512],
                                         start=True, stop=True)
                i.then_inc(proj, 1)
            pe.wait_ge(proj_act, b * 6 + 6)
            pe.wait_ge(proj_dve, b * 6 + 6)

        with nc.Block() as block:
            @block.sync
            def _(sp):
                for n in "qkv":
                    sp.dma_start(w[n][:], k.dram[f"l2a_w{n}"]).then_inc(loaded, 16)
                sp.dma_start(forget[:], k.dram["l2a_forget"].partition_broadcast(P)).then_inc(loaded, 16)
                sp.dma_start(keep[:], k.dram["l2a_keep"].partition_broadcast(P)).then_inc(loaded, 16)
                sp.dma_start(wo[:], k.dram["l2a_wo"]).then_inc(loaded, 16)

            @block.tensor
            def _(pe):
                pe.wait_ge(loaded, 96)

                def score(b, u):
                    g, t = units[u]
                    s = u % 2
                    pe.wait_ge(shifted, b * NU + u + 1)
                    for h in range(HG):
                        c, r = (g * HG + h) // 2, (g * HG + h) % 2 * DK
                        i = nc.tensor.matmul(k.bank[2 * s + h % 2][:, h // 2 * T:(h // 2 + 1) * T],
                                             qk[r:r + DK, 0, c, t * P:(t + 1) * P], qk[r:r + DK, 1, c, :],
                                             start=True, stop=True)
                    i.then_inc(scores, 1)

                def turn(b, u):
                    s = u % 2
                    pe.wait_ge(weighted, b * NU + u + 1)
                    pe.wait_ge(pt_ready, b * NU + u + 1)
                    for h in range(HG):
                        for kt in range(TPB):
                            n = h * TPB + kt
                            i = nc.tensor.transpose(k.bank[4 + n // 4][:, n % 4 * P:(n % 4 + 1) * P],
                                                    SW[:, s, h, kt * P:(kt + 1) * P], k.ident[:])
                    i.then_inc(turned, 1)

                def values(b, u):
                    g, t = units[u]
                    s = u % 2
                    pe.wait_ge(pt_ready, b * NU + u + 2)
                    pe.wait_ge(heads_out, b * NU + u + 1)
                    for h in range(HG):
                        hd = g * HG + h
                        at = h % 2 * 2 + h // 2
                        for kt in range(TPB):
                            i = nc.tensor.matmul(k.bank[6][:, h * DK:(h + 1) * DK], PT[:, s, at * TPB + kt, :],
                                                 v[:, kt, hd * DK:(hd + 1) * DK], start=kt == 0, stop=kt == TPB - 1)
                    i.then_inc(heads, 1)

                with pe.Fori(0, B) as b:
                    project(pe, b)
                    score(b, 0)
                    for u in range(NU):
                        if u + 1 < NU:
                            score(b, u + 1)
                        turn(b, u)
                        values(b, u)
                    pe.wait_ge(heads_out, b * NU + NU + 1)
                    for c in range(CB):
                        for t in range(TPB):
                            n = c * TPB + t
                            i = nc.tensor.transpose(k.bank[n // 4][:, n % 4 * P:(n % 4 + 1) * P],
                                                    O[:, t, c * P:(c + 1) * P], k.ident[:])
                            if n % 4 == 3:
                                i.then_inc(o_turned, 1)
                    pe.wait_ge(ot_act, b * 2 + 2)
                    pe.wait_ge(ot_dve, b * 2 + 2)
                    for t in range(TPB):
                        for c in range(CB):
                            i = nc.tensor.matmul(k.bank[6][:, t * D:(t + 1) * D], OT[:, c, t * P:(t + 1) * P],
                                                 wo[:, c, :], start=c == 0, stop=c == CB - 1)
                    i.then_inc(final, 1)

            @block.scalar
            def _(act):
                act.sem_inc(pt_ready, 1)
                act.sem_inc(heads_out, 1)

                def evacuate(b, u):
                    s = u % 2
                    act.wait_ge(turned, b * NU + u + 1)
                    for h in range(2):
                        i = nc.scalar.activation(PT[:, s, 4 * h:4 * h + 4, :],
                                                 k.bank[4 + h][:].rearrange("p (a q) -> p a q", q=P), ACT.Copy)
                    i.then_inc(pt_ready, 1)

                def out(b, u):
                    g, t = units[u]
                    act.wait_ge(heads, b * NU + u + 1)
                    nc.scalar.activation(O[:, t, g * HG * DK:(g + 1) * HG * DK], k.bank[6][:, 0:HG * DK],
                                         ACT.Copy).then_inc(heads_out, 1)

                with act.Fori(0, B) as b:
                    for n in range(0, 12, 2):
                        act.wait_ge(proj, b * 12 + n + 1)
                        nc.scalar.activation(dest[n], k.bank[n % 6][:], ACT.Copy).then_inc(proj_act, 1)
                    for u in range(NU):
                        s = u % 2
                        act.wait_ge(shifted, b * NU + u + 3)
                        nc.scalar.activation(al[:, s, :], al[:, s, :], ACT.Exp, scale=DK ** -0.5)
                        nc.scalar.activation(S[:, s], S[:, s], ACT.Exp, scale=DK ** -0.5).then_inc(exped, 1)
                        if u > 0:
                            evacuate(b, u - 1)
                            out(b, u - 1)
                    evacuate(b, NU - 1)
                    out(b, NU - 1)
                    for n in range(0, 4, 2):
                        act.wait_ge(o_turned, b * 4 + n + 1)
                        nc.scalar.activation(OT[:, 2 * n:2 * n + 2, :], k.bank[n][:].rearrange("p (c t) -> p c t", t=T),
                                             ACT.Copy).then_inc(ot_act, 1)

            @block.gpsimd
            def _(pool):
                with pool.Fori(0, B) as b:
                    for u in range(NU):
                        s = u % 2
                        pool.wait_ge(w_ready, b * NU + u + 1)
                        nc.gpsimd.tensor_tensor(SW[:, s].rearrange("p h (j t) -> p (h j) t", j=NJ),
                                                S[:, s].rearrange("p h (j t) -> p (h j) t", j=NJ),
                                                over(f[:, s, :], T // NJ), ALU.mult).then_inc(weighted, 1)

            @block.vector
            def _(dve):
                vv = nc.vector
                dve.sem_inc(shifted, 2)
                dve.wait_ge(loaded, 96)

                def shift(b, u):
                    s = u % 2
                    dve.wait_ge(scores, b * NU + u + 1)
                    for h in range(2):
                        vv.tensor_reduce(bm[:, s, 8 * h:8 * h + 8], k.bank[2 * s + h][:].rearrange("p (a t) -> p a t", a=8),
                                         AXX, ALU.max)
                    dve.drain()
                    vv.tensor_tensor_scan(m[:, s, :], forget[:], bm[:, s, :], 0.0, ALU.add, ALU.max)
                    dve.drain()
                    vv.tensor_tensor(al[:, s, 1:16], m[:, s, 0:15], m[:, s, 1:16], ALU.subtract)
                    dve.drain()
                    vv.memset(al[:, s, 0:1], 0.0)
                    dve.drain()
                    vv.tensor_tensor(al[:, s, :], al[:, s, :], keep[:], ALU.mult)
                    if u >= 2:
                        dve.wait_ge(weighted, b * NU + u - 1)
                    for h in range(2):
                        i = vv.tensor_tensor(S[:, s, 2 * h:2 * h + 2, :].rearrange("p h (j t) -> p (h j) t", j=NJ),
                                             k.bank[2 * s + h][:].rearrange("p (a t) -> p a t", a=8),
                                             over(m[:, s, 8 * h:8 * h + 8], T // NJ), ALU.subtract)
                    i.then_inc(shifted, 1)

                def weigh(b, u):
                    s = u % 2
                    dve.wait_ge(exped, b * NU + u + 1)
                    vv.tensor_reduce(rs[:, s, :], S[:, s].rearrange("p h (j t) -> p (h j) t", j=NJ), AXX, ALU.add)
                    vv.tensor_tensor(al[:, s, :], al[:, s, :], keep[:], ALU.mult)
                    dve.drain()
                    vv.tensor_tensor_scan(ls[:, s, :], al[:, s, :], rs[:, s, :], 0.0, ALU.mult, ALU.add)
                    dve.drain()
                    vv.reciprocal(f[:, s, :], ls[:, s, :])
                    dve.drain()
                    f4 = f[:, s, :].rearrange("p (h j) -> p h j", j=NJ)
                    a4 = al[:, s, :].rearrange("p (h j) -> p h j", j=NJ)
                    vv.tensor_tensor(f4[:, :, 0:3], f4[:, :, 0:3], a4[:, :, 1:4], ALU.mult)
                    for j in (2, 1, 0):
                        dve.drain()
                        i = vv.tensor_tensor(f4[:, :, j], f4[:, :, j], f4[:, :, j + 1], ALU.mult)
                    i.then_inc(w_ready, 1)

                with dve.Fori(0, B) as b:
                    vv.tensor_copy(xb[:], k.HT[:, bass.ds(b, 1), PAD:PAD + T].rearrange("p a t -> p (a t)")).then_inc(xb_ready, 1)
                    for n in range(1, 12, 2):
                        dve.wait_ge(proj, b * 12 + n + 1)
                        vv.tensor_copy(dest[n], k.bank[n % 6][:]).then_inc(proj_dve, 1)
                    shift(b, 0)
                    for u in range(NU):
                        if u + 1 < NU:
                            shift(b, u + 1)
                        weigh(b, u)
                    for n in range(1, 4, 2):
                        dve.wait_ge(o_turned, b * 4 + n + 1)
                        vv.tensor_copy(OT[:, 2 * n:2 * n + 2, :],
                                       k.bank[n][:].rearrange("p (c t) -> p c t", t=T)).then_inc(ot_dve, 1)
                    dve.wait_ge(final, b + 1)
                    vv.tensor_copy(k.Y[:, bass.ds(b * TPB, TPB), :],
                                   k.bank[6][:, 0:TPB * D].rearrange("p (t d) -> p t d", d=D)).then_inc(done, 1)


def lay_out_plucker(i, d, np):
    wq = [i["L1_attn_W1_q"].T, i["L1_attn_W2_q"].T]
    d["l1a_wx"] = np.concatenate([wq[0][:D], wq[1][:D], i["L1_attn_W1_k"].T, i["L1_attn_W2_k"].T,
                                  i["L1_attn_Wv"].T], 1)
    d["l1a_wprev"] = np.concatenate([wq[0][D:], wq[1][D:]], 1)
    d["l1a_wo"] = i["L1_attn_Wo"].T
    d["l1a_bias"] = np.stack([i["L1_attn_bv"], i["L1_attn_bo"]])
    d["causal"] = np.triu(np.ones((P, P), np.float32))


def plucker_attn(k):
    nc, H, LC = k.nc, 16, 6
    DH, SLOT = D // H, 32
    G = H // 4
    PAIRS = [(0, slice(1, 4), slice(0, 3)), (1, slice(2, 4), slice(3, 5)), (2, slice(3, 4), slice(5, 6))]
    JSIGN = [1.0, -1.0, 1.0, 1.0, -1.0, 1.0]
    with Part(k) as p:
        wx, wprev, wo = p.sb("wx", [P, 4 * 64 + D]), p.sb("wprev", [P, 2 * 64]), p.sb("wo", [P, D])
        bias = p.sb("bias", [P, 2, D])
        causal = p.sb("causal", [P, P])
        xb = p.sb("x_batch", [P, 1 + T])
        pts = p.sb("points", [P, TPB, 2, 2, H, 4])
        v = p.sb("v_and_one", [P, TPB, H, DH + 1])
        ln, ln2 = p.sb("lines", [P, TPB * 2, H, LC]), p.sb("lines2", [P, TPB * 2, H, LC])
        nrm, half = p.sb("norms", [P, TPB * 2, H]), p.sb("minus_half", [P, TPB * 2, H])
        qk = p.sb("lines_padded", [P, 2, TPB, H, SLOT])
        qkT = p.sb("lines_featmajor", [P, 2, G, T])
        E = p.sb("probs", [P, 2, 4, T + P])
        rsum = p.sb("rsum", [P, TPB, H])
        O = p.sb("heads_out", [P, TPB, H, DH])
        OT = p.sb("heads_out_featmajor", [P, T])
        loaded, xb_ready, proj, pts_ready = p.sem("loaded"), p.sem("xb_ready"), p.sem("proj"), p.sem("pts_ready")
        sq_ready, norm_ready, lines_ready = p.sem("sq_ready"), p.sem("norm_ready"), p.sem("lines_ready")
        turned, t_act, t_dve = p.sem("turned"), p.sem("t_act"), p.sem("t_dve")
        scores, exped, masked, heads = p.sem("scores"), p.sem("exped"), p.sem("masked"), p.sem("heads")
        o_ready, o_turned, ot_ready, final, done = (p.sem(n) for n in ("o_ready", "o_turned", "ot_ready", "final", "done"))
        zeroed = p.sem("zeroed")
        oview = k.bank[6][:, 0:TPB * H * (DH + 1)].rearrange("p (t h c) -> p t h c", t=TPB, h=H)
        with nc.Block() as block:
            @block.sync
            def _(sp):
                sp.dma_start(wx[:], k.dram["l1a_wx"]).then_inc(loaded, 16)
                sp.dma_start(wprev[:], k.dram["l1a_wprev"]).then_inc(loaded, 16)
                sp.dma_start(wo[:], k.dram["l1a_wo"]).then_inc(loaded, 16)
                sp.dma_start(bias[:], k.dram["l1a_bias"].partition_broadcast(P)).then_inc(loaded, 16)
                sp.dma_start(causal[:], k.dram["causal"]).then_inc(loaded, 16)

            @block.tensor
            def _(pe):
                pe.wait_ge(loaded, 80)

                def out_of(pe, b, g):
                    s = g % 2
                    pe.wait_ge(masked, b * G + g + 1)
                    for r in range(4):
                        h = 4 * g + r
                        nc.tensor.matmul(oview[:, 0, h, :], E[:, s, r, 0:P], v[:, 0, h, :], start=True, stop=True)
                        nc.tensor.matmul(oview[:, 1, h, :], E[:, s, r, P:2 * P], v[:, 0, h, :], start=True, stop=False)
                        i = nc.tensor.matmul(oview[:, 1, h, :], E[:, s, r, T:T + P], v[:, 1, h, :], start=False, stop=True)
                    i.then_inc(heads, 1)

                with pe.Fori(0, B) as b:
                    pe.wait_ge(xb_ready, b + 1)
                    for t in range(TPB):
                        o = k.bank[4 + t]
                        nc.tensor.matmul(o[:, 0:384], xb[:, 1 + t * P:1 + (t + 1) * P], wx[:], start=True, stop=False)
                        i = nc.tensor.matmul(o[:, 0:128], xb[:, t * P:(t + 1) * P], wprev[:], start=False, stop=True)
                    i.then_inc(proj, 1)
                    pe.wait_ge(lines_ready, b + 1)
                    for n in range(4):
                        for g in range(G):
                            i = nc.tensor.transpose(k.bank[n][:, g * P:(g + 1) * P],
                                                    qk[:, n // 2, n % 2, 4 * g:4 * g + 4, :].rearrange("p h c -> p (h c)"),
                                                    k.ident[:])
                        i.then_inc(turned, 1)
                    pe.wait_ge(t_act, b * 2 + 2)
                    pe.wait_ge(t_dve, b * 2 + 2)
                    for g in range(G):
                        if g > 0:
                            pe.wait_ge(exped, b * G + g)
                        for kt in range(TPB):
                            for r in range(4):
                                rows = slice(SLOT * r, SLOT * (r + 1))
                                i = nc.tensor.matmul(k.bank[r][:, kt * T:kt * T + (T - kt * P)],
                                                     qkT[rows, 1, g, kt * P:(kt + 1) * P], qkT[rows, 0, g, kt * P:T],
                                                     start=True, stop=True)
                        i.then_inc(scores, 1)
                        if g > 0:
                            out_of(pe, b, g - 1)
                    out_of(pe, b, G - 1)
                    pe.wait_ge(o_ready, b + 1)
                    for t in range(TPB):
                        i = nc.tensor.transpose(k.bank[7][:, t * P:(t + 1) * P],
                                                O[:, t].rearrange("p h c -> p (h c)"), k.ident[:])
                    i.then_inc(o_turned, 1)
                    pe.wait_ge(ot_ready, b + 1)
                    for t in range(TPB):
                        i = nc.tensor.matmul(k.bank[7][:, 256 + t * D:256 + (t + 1) * D], OT[:, t * P:(t + 1) * P], wo[:],
                                             start=True, stop=True)
                    i.then_inc(final, 1)

            @block.scalar
            def _(act):
                with act.Fori(0, B) as b:
                    for n in (0, 2):
                        act.wait_ge(turned, b * 4 + n + 1)
                        nc.scalar.activation(qkT[:, n // 2, :, 0:P], k.bank[n].rearrange("p (g t) -> p g t", g=G),
                                             ACT.Copy).then_inc(t_act, 1)
                    for g in range(G):
                        s = g % 2
                        act.wait_ge(scores, b * G + g + 1)
                        if g > 1:
                            act.wait_ge(heads, b * G + g - 1)
                        nc.scalar.activation(E[:, s], k.banks[:, 0:4, 0:T + P], ACT.Exp, scale=LC ** -0.5).then_inc(exped, 1)
                    act.wait_ge(o_turned, b + 1)
                    nc.scalar.activation(OT[:], k.bank[7][:, 0:T], ACT.Copy).then_inc(ot_ready, 1)

            @block.gpsimd
            def _(pool):
                nc.gpsimd.memset(half[:], -0.5)
                nc.gpsimd.memset(qk[:], 0.0)
                nc.gpsimd.memset(v[:], 1.0).then_inc(zeroed, 1)
                pool.wait_ge(loaded, 80)
                pool.drain()
                with pool.Fori(0, B) as b:
                    pool.wait_ge(sq_ready, b + 1)
                    nc.gpsimd.tensor_tensor(nrm[:], nrm[:], half[:], ALU.pow).then_inc(norm_ready, 1)
                    for g in range(G):
                        s = g % 2
                        pool.wait_ge(exped, b * G + g + 1)
                        for c in (0, T):
                            i = nc.gpsimd.tensor_tensor(E[:, s, :, c:c + P], E[:, s, :, c:c + P], across(causal[:], 4),
                                                        ALU.mult)
                        i.then_inc(masked, 1)

            @block.vector
            def _(dve):
                vv = nc.vector
                dve.wait_ge(loaded, 80)
                dve.wait_ge(zeroed, 1)
                with dve.Fori(0, B) as b:
                    vv.tensor_copy(xb[:], k.HT[:, bass.ds(b, 1), PAD - 1:PAD + T].rearrange("p a t -> p (a t)")).then_inc(xb_ready, 1)
                    dve.wait_ge(proj, b + 1)
                    for t in range(TPB):
                        vv.tensor_copy(pts[:, t].rearrange("p a b h c -> p (a b h c)"), k.bank[4 + t][:, 0:256])
                        vv.tensor_tensor(v[:, t, :, 0:DH], k.bank[4 + t][:, 256:384].rearrange("p (h c) -> p h c", h=H),
                                         bias[:, 0, :].rearrange("p (h c) -> p h c", h=H), ALU.add)
                    dve.drain()
                    pv = pts[:].rearrange("p t a b h c -> p (t a) b h c")
                    for i0, js, cs in PAIRS:
                        n = js.stop - js.start
                        one = [pv[:, :, a, :, i0:i0 + 1].to_broadcast([P, 4, H, n]) for a in range(2)]
                        many = [pv[:, :, a, :, js] for a in range(2)]
                        vv.tensor_tensor(ln[:, :, :, cs], one[0], many[1], ALU.mult)
                        vv.tensor_tensor(ln2[:, :, :, cs], one[1], many[0], ALU.mult)
                    dve.drain()
                    vv.tensor_tensor(ln[:], ln[:], ln2[:], ALU.subtract)
                    dve.drain()
                    vv.tensor_tensor(ln2[:], ln[:], ln[:], ALU.mult)
                    dve.drain()
                    vv.tensor_reduce(nrm[:], ln2[:], AXX, ALU.add)
                    dve.drain()
                    vv.tensor_scalar_max(nrm[:], nrm[:], 1e-24).then_inc(sq_ready, 1)
                    dve.wait_ge(norm_ready, b + 1)
                    lq = ln[:].rearrange("p (t a) h c -> p t a h c", a=2)
                    nq = nrm[:].rearrange("p (t a) h -> p t a h", a=2)
                    for t in range(TPB):
                        vv.tensor_tensor(qk[:, 0, t, :, 0:LC], lq[:, t, 0], over(nq[:, t, 0, :], LC), ALU.mult)
                    for c in range(LC):
                        i = vv.scalar_tensor_tensor(out=qk[:, 1, :, :, c], in0=lq[:, :, 1, :, 5 - c], scalar=JSIGN[c],
                                                    in1=nq[:, :, 1, :], op0=ALU.mult, op1=ALU.mult)
                    i.then_inc(lines_ready, 1)
                    for n in (1, 3):
                        dve.wait_ge(turned, b * 4 + n + 1)
                        vv.tensor_copy(qkT[:, n // 2, :, P:T], k.bank[n].rearrange("p (g t) -> p g t", g=G)).then_inc(t_dve, 1)
                    dve.wait_ge(heads, b * G + G)
                    vv.reciprocal(rsum[:], oview[:, :, :, DH])
                    dve.drain()
                    for t in range(TPB):
                        i = vv.tensor_tensor(O[:, t], oview[:, t, :, 0:DH], over(rsum[:, t, :], DH), ALU.mult)
                    i.then_inc(o_ready, 1)
                    dve.wait_ge(final, b + 1)
                    vv.tensor_tensor(k.Y[:, bass.ds(b * TPB, TPB), :], k.bank[7][:, 256:512].rearrange("p (t d) -> p t d", d=D),
                                     across(bias[:, 1, :], TPB), ALU.add).then_inc(done, 1)


def lay_out_window(i, d, np):
    half = 32
    swap = lambda a: np.concatenate([a[..., half:], a[..., :half]], -1)
    HID = 341
    for l in range(2):
        d[f"l0f_wqkv{l}"] = i["L0_ffn_wqkv"][l]
        qk = np.stack([i["L0_ffn_q_scale"][l], i["L0_ffn_k_scale"][l]])
        d[f"l0f_qks{l}"] = np.stack([qk, swap(qk)], 1)
        d[f"l0f_wo{l}"] = by_blocks(i["L0_ffn_wo"][l])
        d[f"l0f_ln{l}"] = np.stack([i["L0_ffn_ln_g"][l], i["L0_ffn_ln_b"][l]])
        pad = lambda a: np.concatenate([a, np.zeros((3 * P - HID,) + a.shape[1:], a.dtype)])
        w1, b1 = i["L0_ffn_w1"][l], i["L0_ffn_b1"][l]
        d[f"l0f_w1{l}"] = np.stack([pad(w1[:, n * HID:(n + 1) * HID].T).T for n in range(2)], 1)
        d[f"l0f_b1{l}"] = np.stack([pad(b1[n * HID:(n + 1) * HID]).reshape(3, P).T for n in range(2)], 1)
        d[f"l0f_w2{l}"] = by_blocks(pad(i["L0_ffn_w2"][l]))
        d[f"l0f_b2{l}"] = i["L0_ffn_b2"][l]
    hi = np.arange(0, 64, 2, dtype=np.float32)
    inv = (np.float32(1.0) / np.float32(10000.0) ** (hi / np.float32(64))).astype(np.float32)
    t = np.arange(T, dtype=np.float32)
    fr = (t[:, None] * inv[None, :]).astype(np.float32)
    base = ((hi + np.float32(0.4 * 64)) / np.float32(1.4 * 64)).astype(np.float32)
    power = ((t - T // 2) / np.float32(32.0)).astype(np.float32)
    sc = (base[None, :] ** power[:, None]).astype(np.float32)
    tw = lambda a: np.concatenate([a, a], -1)
    cos, sin, sc = tw(np.cos(fr)), tw(np.sin(fr)), tw(sc)
    sin[:, :half] *= -1
    tab = np.stack([cos * sc, sin * sc, cos / sc, sin / sc], 1).reshape(T, 2, 2, 64)
    d["l0f_rot"] = tab.reshape(TPB, P, 2, 2, 64).transpose(1, 0, 2, 3, 4)
    q, j0, j1 = np.arange(P), np.arange(P), np.arange(64, 256)
    ok = lambda q, j: (q[:, None] >= j[None, :]) & (q[:, None] <= j[None, :] + 64)
    band = np.concatenate([ok(q, j0), ok(q + P, j1)], 1)
    d["l0f_band"] = np.where(band, 0.0, -1e30).astype(np.float32)
    d["l0f_shift"] = np.stack([np.eye(P, k=1, dtype=np.float32), np.zeros((P, P), np.float32)], 1)
    d["l0f_shift"][P - 1, 1, 0] = 1.0


def window_attn(k):
    nc = k.nc
    with Part(k) as p:
        with nc.Block() as block:
            @block.vector
            def _(dve):
                nc.vector.tensor_copy(k.Y[:], k.H[:])
    for l in range(2):
        if l:
            normalise(k, src=k.Y, norm=False)
        window_attention_layer(k, l)
        with Part(k) as p:
            shifted = p.sb("shifted", [P, NT, D])
            affine = p.sb("affine", [P, 2, D])
            shift_tokens(k, p, shifted, affine, l)
            normalise(k, src=shifted, affine=affine)
        window_ffn_layer(k, l)


def shift_tokens(k, p, shifted, affine, l):
    nc, HALF = k.nc, D // 2
    mats = p.sb("shift", [P, 2, P])
    loaded, moved = p.sem("loaded"), p.sem("moved")
    with nc.Block() as block:
        @block.sync
        def _(sp):
            sp.dma_start(mats[:], k.dram["l0f_shift"]).then_inc(loaded, 16)
            sp.dma_start(affine[:], k.dram[f"l0f_ln{l}"].partition_broadcast(P)).then_inc(loaded, 16)
            sp.wait_ge(loaded, 32)

        @block.tensor
        def _(pe):
            pe.wait_ge(loaded, 32)
            for n in range(2):
                o = k.bank[n].rearrange("p (b t d) -> p b t d", t=TPB, d=HALF)
                y = k.Y[:, 8 * n:8 * n + 8, HALF:].rearrange("p (b t) d -> p b t d", t=TPB)
                nc.tensor.matmul(k.bank[n].rearrange("p (b d) -> p b d", d=HALF), mats[:, 0, :], k.Y[:, 8 * n:8 * n + 8, HALF:],
                                 start=True, stop=False)
                nc.tensor.matmul(o[:, :, 1, :], mats[:, 1, :], y[:, :, 0, :], start=False, stop=True).then_inc(moved, 1)

        @block.vector
        def _(dve):
            nc.vector.tensor_copy(shifted[:, :, 0:HALF], k.Y[:, :, 0:HALF])
            for n in range(2):
                dve.wait_ge(moved, n + 1)
                nc.vector.tensor_copy(shifted[:, 8 * n:8 * n + 8, HALF:], k.bank[n].rearrange("p (a d) -> p a d", d=HALF))


def window_attention_layer(k, l):
    nc, H, DK, HALF = k.nc, 8, 64, 32
    CB, HG, NU, W0, W1 = H * DK // P, 4, 2, P, 192
    with Part(k) as p:
        wqkv, wo = p.sb("wqkv", [P, 3 * 512]), p.sb("wo", [P, CB, D])
        qks, rot, tab = p.sb("qk_scales", [P, 2, 2, DK]), p.sb("rotary", [P, TPB, 2, 2, DK]), p.sb("table", [P, TPB, 2, 2, DK])
        band = p.sb("band", [P, W0 + W1])
        xb = p.sb("x_batch", [P, T])
        sq = p.sb("squares", [P, TPB, 2, 512])
        ss, half = p.sb("norms", [P, TPB, 2, H]), p.sb("minus_half", [P, TPB * 2 * H])
        qn, qr, qk = (p.sb(n, [P, TPB, 2, H, DK]) for n in ("qk_normed", "qk_turned_part", "qk_rotated"))
        v = p.sb("v", [P, TPB, 512])
        qkT = p.sb("qk_featmajor", [P, 2, CB, T])
        S = p.sb("scores", [P, 2, HG, W0 + W1])
        E = p.sb("probs", [P, 2, HG, W0 + T])
        mx, rs = p.sb("rowmax", [P, 2, HG, TPB]), p.sb("rowsum", [P, 2, HG, TPB])
        ET = p.sb("probs_keymajor", [P, HG * 3, P])
        O = p.sb("heads_out", [P, TPB, 512])
        OT = p.sb("heads_out_featmajor", [P, CB, T])
        names = ("loaded", "zeroed", "xb_ready", "proj", "squared", "ss_ready", "norm_ready", "normed", "turned_part",
                 "rotated", "turned", "t_act", "t_dve", "scores", "maxed", "exped", "p_turned", "pt_act", "pt_dve", "heads",
                 "heads_out", "o_turned", "ot_ready", "final", "v_ready", "s_read")
        q = {n: p.sem(n) for n in names}
        hout = k.bank[7].rearrange("p (t h d) -> p t h d", t=TPB, h=HG)
        with nc.Block() as block:
            @block.sync
            def _(sp):
                sp.dma_start(wqkv[:], k.dram[f"l0f_wqkv{l}"]).then_inc(q["loaded"], 16)
                sp.dma_start(wo[:], k.dram[f"l0f_wo{l}"]).then_inc(q["loaded"], 16)
                sp.dma_start(qks[:], k.dram[f"l0f_qks{l}"].partition_broadcast(P)).then_inc(q["loaded"], 16)
                sp.dma_start(rot[:], k.dram["l0f_rot"]).then_inc(q["loaded"], 16)
                sp.dma_start(band[:], k.dram["l0f_band"]).then_inc(q["loaded"], 16)

            @block.tensor
            def _(pe):
                pe.wait_ge(q["loaded"], 80)

                def score(b, u):
                    for h in range(HG):
                        hd = HG * u + h
                        rows, c = slice(hd % 2 * DK, (hd % 2 + 1) * DK), hd // 2
                        nc.tensor.matmul(k.bank[h][:, 0:W0], qkT[rows, 0, c, 0:P], qkT[rows, 1, c, 0:P], start=True, stop=True)
                        nc.tensor.matmul(k.bank[h][:, W0:W0 + W1], qkT[rows, 0, c, P:T], qkT[rows, 1, c, DK:T],
                                         start=True, stop=True).then_inc(q["scores"], 1)

                def heads_of(b, u):
                    pe.wait_ge(q["exped"], b * NU + u + 1)
                    for n in range(HG * 3):
                        i = nc.tensor.transpose(k.bank[4 + n // 4][:, n % 4 * P:(n % 4 + 1) * P],
                                                E[:, u, n // 3, n % 3 * P:(n % 3 + 1) * P], k.ident[:])
                        if n % 4 == 3:
                            i.then_inc(q["p_turned"], 1)
                    pe.wait_ge(q["pt_act"], (b * NU + u) * 2 + 2)
                    pe.wait_ge(q["pt_dve"], b * NU + u + 1)
                    pe.wait_ge(q["heads_out"], b * NU + u + 1)
                    for h in range(HG):
                        vh = slice((HG * u + h) * DK, (HG * u + h + 1) * DK)
                        nc.tensor.matmul(hout[:, 0, h, :], ET[:, 3 * h, :], v[:, 0, vh], start=True, stop=True)
                        nc.tensor.matmul(hout[:, 1, h, :], ET[:, 3 * h + 1, :], v[:, 0, vh], start=True, stop=False)
                        i = nc.tensor.matmul(hout[:, 1, h, :], ET[:, 3 * h + 2, :], v[:, 1, vh], start=False, stop=True)
                    i.then_inc(q["heads"], 1)

                with pe.Fori(0, B) as b:
                    pe.wait_ge(q["xb_ready"], b + 1)
                    for t in range(TPB):
                        for n in range(3):
                            i = nc.tensor.matmul(k.bank[3 * t + n][:], xb[:, t * P:(t + 1) * P], wqkv[:, n * 512:(n + 1) * 512],
                                                 start=True, stop=True)
                    i.then_inc(q["proj"], 1)
                    pe.wait_ge(q["rotated"], b + 1)
                    pe.wait_ge(q["v_ready"], b + 1)
                    for n in range(4):
                        for c in range(CB):
                            i = nc.tensor.transpose(k.bank[n][:, c * P:(c + 1) * P],
                                                    qk[:, n % 2, n // 2].rearrange("p h d -> p (h d)")[:, c * P:(c + 1) * P],
                                                    k.ident[:])
                        i.then_inc(q["turned"], 1)
                    pe.wait_ge(q["t_act"], b * 2 + 2)
                    pe.wait_ge(q["t_dve"], b * 2 + 2)
                    score(b, 0)
                    pe.wait_ge(q["s_read"], b * NU + 1)
                    score(b, 1)
                    heads_of(b, 0)
                    heads_of(b, 1)
                    pe.wait_ge(q["heads_out"], b * NU + NU + 1)
                    for n in range(CB * TPB):
                        c, t = n // TPB, n % TPB
                        i = nc.tensor.transpose(k.bank[n // 4][:, n % 4 * P:(n % 4 + 1) * P], O[:, t, c * P:(c + 1) * P],
                                                k.ident[:])
                    i.then_inc(q["o_turned"], 1)
                    pe.wait_ge(q["ot_ready"], b + 1)
                    for t in range(TPB):
                        for c in range(CB):
                            i = nc.tensor.matmul(k.bank[2][:, t * D:(t + 1) * D], OT[:, c, t * P:(t + 1) * P], wo[:, c, :],
                                                 start=c == 0, stop=c == CB - 1)
                    i.then_inc(q["final"], 1)

            @block.scalar
            def _(act):
                with act.Fori(0, B) as b:
                    act.wait_ge(q["proj"], b + 1)
                    for t in range(TPB):
                        nc.scalar.activation(sq[:, t], k.banks[:, 3 * t:3 * t + 2, :], ACT.Square).then_inc(q["squared"], 1)
                    for t in range(TPB):
                        i = nc.scalar.activation(v[:, t], k.bank[3 * t + 2], ACT.Copy)
                    i.then_inc(q["v_ready"], 1)
                    for n in (0, 2):
                        act.wait_ge(q["turned"], b * 4 + n + 1)
                        nc.scalar.activation(qkT[:, n // 2, :, 0:P], k.bank[n].rearrange("p (c t) -> p c t", c=CB),
                                             ACT.Copy).then_inc(q["t_act"], 1)
                    for u in range(NU):
                        act.wait_ge(q["maxed"], b * NU + u + 1)
                        for h in range(HG):
                            for t in range(TPB):
                                src = S[:, u, h, 0:W0] if t == 0 else S[:, u, h, W0:]
                                dst = E[:, u, h, 0:W0] if t == 0 else E[:, u, h, W0 + T - W1:]
                                i = nc.scalar.activation(dst, src, ACT.Exp, scale=8.0, bias=mx[:, u, h, t:t + 1],
                                                         accum_out=rs[:, u, h, t:t + 1])
                        i.then_inc(q["exped"], 1)
                    for u in range(NU):
                        for n in (0, 1):
                            act.wait_ge(q["p_turned"], (b * NU + u) * 3 + n + 1)
                            nc.scalar.activation(ET[:, 4 * n:4 * n + 4, :], k.bank[4 + n].rearrange("p (a t) -> p a t", t=P),
                                                 ACT.Copy).then_inc(q["pt_act"], 1)
                    act.wait_ge(q["o_turned"], b + 1)
                    for n in range(2):
                        i = nc.scalar.activation(OT[:, 2 * n:2 * n + 2, :], k.bank[n].rearrange("p (c t) -> p c t", t=T), ACT.Copy)
                    i.then_inc(q["ot_ready"], 1)

            @block.gpsimd
            def _(pool):
                g = nc.gpsimd
                g.memset(half[:], -0.5)
                g.memset(E[:], 0.0).then_inc(q["zeroed"], 1)
                pool.wait_ge(q["loaded"], 80)
                for t in range(TPB):
                    for a in range(2):
                        g.tensor_tensor(tab[:, t, a], rot[:, t, a], qks[:, a], ALU.mult)
                pool.drain()
                with pool.Fori(0, B) as b:
                    pool.wait_ge(q["ss_ready"], b + 1)
                    flat = ss[:].rearrange("p t a h -> p (t a h)")
                    g.tensor_tensor(flat, flat, half[:], ALU.pow).then_inc(q["norm_ready"], 1)
                    for t in range(TPB):
                        pool.wait_ge(q["normed"], b * TPB + t + 1)
                        for a in range(2):
                            g.tensor_tensor(qk[:, t, a], qn[:, t, a], across(tab[:, t, a, 0, :], H), ALU.mult).then_inc(q["turned_part"], 1)

            @block.vector
            def _(dve):
                vv = nc.vector
                dve.sem_inc(q["heads_out"], 1)
                dve.wait_ge(q["zeroed"], 1)
                dve.wait_ge(q["loaded"], 80)
                with dve.Fori(0, B) as b:
                    x = lambda lo, at: k.HT[lo:lo + 64, bass.ds(b, 1), at:at + T].rearrange("p a t -> p (a t)")
                    vv.tensor_copy(xb[0:64, :], x(0, PAD))
                    vv.tensor_copy(xb[64:128, :], x(64, PAD - 1))
                    dve.drain()
                    vv.engine_nop().then_inc(q["xb_ready"], 1)
                    for t in range(TPB):
                        dve.wait_ge(q["squared"], b * TPB + t + 1)
                        vv.tensor_reduce(ss[:, t], sq[:, t].rearrange("p a (h d) -> p a h d", d=DK), AXX, ALU.add)
                    dve.drain()
                    vv.tensor_scalar_max(ss[:], ss[:], 1e-24).then_inc(q["ss_ready"], 1)
                    dve.wait_ge(q["norm_ready"], b + 1)
                    for t in range(TPB):
                        for a in range(2):
                            i = vv.tensor_tensor(qn[:, t, a], k.bank[3 * t + a].rearrange("p (h d) -> p h d", d=DK),
                                                 over(ss[:, t, a, :], DK), ALU.mult)
                        i.then_inc(q["normed"], 1)
                    dve.drain()
                    for t in range(TPB):
                        for a in range(2):
                            for lo in (0, HALF):
                                vv.tensor_tensor(qr[:, t, a, :, lo:lo + HALF], qn[:, t, a, :, HALF - lo:DK - lo],
                                                 across(tab[:, t, a, 1, lo:lo + HALF], H), ALU.mult)
                    dve.drain()
                    for t in range(TPB):
                        for a in range(2):
                            dve.wait_ge(q["turned_part"], (b * TPB + t) * 2 + a + 1)
                            i = vv.tensor_add(qk[:, t, a], qk[:, t, a], qr[:, t, a])
                    i.then_inc(q["rotated"], 1)
                    for n in (1, 3):
                        dve.wait_ge(q["turned"], b * 4 + n + 1)
                        vv.tensor_copy(qkT[:, n // 2, :, P:T], k.bank[n].rearrange("p (c t) -> p c t", c=CB)).then_inc(q["t_dve"], 1)
                    for u in range(NU):
                        for h in range(HG):
                            dve.wait_ge(q["scores"], (b * NU + u) * HG + h + 1)
                            i = vv.tensor_tensor(S[:, u, h, :], k.bank[h][:, 0:W0 + W1], band[:], ALU.add)
                        i.then_inc(q["s_read"], 1)
                        dve.drain()
                        vv.tensor_reduce(mx[:, u, :, 0], S[:, u, :, 0:W0], AXX, ALU.max)
                        vv.tensor_reduce(mx[:, u, :, 1], S[:, u, :, W0:], AXX, ALU.max)
                        dve.drain()
                        vv.tensor_scalar(mx[:, u], mx[:, u], -8.0, None, ALU.mult).then_inc(q["maxed"], 1)
                    for u in range(NU):
                        dve.wait_ge(q["p_turned"], (b * NU + u) * 3 + 3)
                        vv.tensor_copy(ET[:, 8:12, :], k.bank[6].rearrange("p (a t) -> p a t", t=P)).then_inc(q["pt_dve"], 1)
                        dve.wait_ge(q["heads"], b * NU + u + 1)
                        vv.reciprocal(rs[:, u], rs[:, u])
                        dve.drain()
                        for t in range(TPB):
                            i = vv.tensor_tensor(O[:, t, u * 256:(u + 1) * 256].rearrange("p (h d) -> p h d", d=DK),
                                                 hout[:, t], over(rs[:, u, :, t], DK), ALU.mult)
                        i.then_inc(q["heads_out"], 1)
                    dve.wait_ge(q["final"], b + 1)
                    y = k.Y[:, bass.ds(b * TPB, TPB), :]
                    vv.tensor_tensor(y, k.bank[2][:, 0:TPB * D].rearrange("p (t d) -> p t d", d=D), y, ALU.add)
                    dve.drain()


def window_ffn_layer(k, l):
    nc, KB, CH = k.nc, 3, 512
    NCH, bpc = B * T // CH, CH // T
    with Part(k) as p:
        w1, b1 = p.sb("w1", [P, 2, KB * P]), p.sb("b1", [P, 2, KB])
        w2, b2 = p.sb("w2", [P, KB, D]), p.sb("b2", [P, D])
        gate, hid = p.sb("gate", [P, KB, CH]), p.sb("hid", [P, KB, CH])
        loaded, pair, gated, prod, down, out = (p.sem(n) for n in ("loaded", "pair", "gated", "prod", "down", "out"))
        with nc.Block() as block:
            @block.sync
            def _(sp):
                sp.dma_start(w1[:], k.dram[f"l0f_w1{l}"]).then_inc(loaded, 16)
                sp.dma_start(b1[:], k.dram[f"l0f_b1{l}"]).then_inc(loaded, 16)
                sp.dma_start(w2[:], k.dram[f"l0f_w2{l}"]).then_inc(loaded, 16)
                sp.dma_start(b2[:], k.dram[f"l0f_b2{l}"].partition_broadcast(P)).then_inc(loaded, 16)

            @block.tensor
            def _(pe):
                pe.wait_ge(loaded, 64)
                with pe.Fori(0, NCH) as c:
                    x = k.HT[:, bass.ds(c * bpc, bpc), PAD:PAD + T]
                    pe.wait_ge(out, c + 1)
                    for ob in range(KB):
                        for j in range(2):
                            i = nc.tensor.matmul(k.bank[KB * j + ob].rearrange("p (b t) -> p b t", b=bpc),
                                                 w1[:, j, ob * P:(ob + 1) * P], x, start=True, stop=True)
                        i.then_inc(pair, 1)
                    pe.wait_ge(prod, c * KB + KB)
                    for tt in range(CH // P):
                        for kb in range(KB):
                            i = nc.tensor.matmul(k.bank[6][:, tt * D:(tt + 1) * D], hid[:, kb, tt * P:(tt + 1) * P],
                                                 w2[:, kb, :], start=kb == 0, stop=kb == KB - 1)
                    i.then_inc(down, 1)

            @block.scalar
            def _(act):
                act.wait_ge(loaded, 64)
                with act.Fori(0, NCH) as c:
                    for ob in range(KB):
                        act.wait_ge(pair, c * KB + ob + 1)
                        nc.scalar.activation(gate[:, ob, :], k.bank[KB + ob], ACT.Gelu, bias=b1[:, 1, ob:ob + 1]).then_inc(gated, 1)

            @block.vector
            def _(dve):
                dve.sem_inc(out, 1)
                dve.wait_ge(loaded, 64)
                nc.vector.tensor_tensor(k.Y[:], k.Y[:], across(b2[:], NT), ALU.add)
                dve.drain()
                with dve.Fori(0, NCH) as c:
                    for ob in range(KB):
                        dve.wait_ge(gated, c * KB + ob + 1)
                        nc.vector.scalar_tensor_tensor(out=hid[:, ob, :], in0=k.bank[ob], scalar=b1[:, 0, ob:ob + 1],
                                                       in1=gate[:, ob, :], op0=ALU.add, op1=ALU.mult).then_inc(prod, 1)
                    dve.wait_ge(down, c + 1)
                    y = k.Y[:, bass.ds(c * (CH // P), CH // P), :]
                    nc.vector.tensor_tensor(y, k.bank[6].rearrange("p (t d) -> p t d", d=D), y, ALU.add).then_inc(out, 1)


def lay_out_delta(i, d, np):
    for n in "qkv":
        d[f"l0a_w{n}"] = i[f"L0_attn_w_{n}"]
        d[f"l0a_conv{n}"] = i[f"L0_attn_conv_{n}"].T
    d["l0a_wg"] = i["L0_attn_w_g"]
    d["l0a_wab"] = np.concatenate([i["L0_attn_w_a"], i["L0_attn_w_b"]], 1)
    d["l0a_wout"] = by_blocks(i["L0_attn_w_out"])
    d["l0a_alog_dt"] = np.stack([i["L0_attn_A_log"], i["L0_attn_dt_bias"]])
    d["l0a_normw"] = i["L0_attn_norm_w"]
    r = np.arange(P)
    row, col = r[:, None], r[None, :]
    f = lambda a: a.astype(np.float32)
    d["l0a_tri"] = np.stack([f(row <= col), f(row > col), f(row >= col)], 1)
    lev = []
    for e in range(7):
        s = 1 << e
        lev.append(f((row // (2 * s) == col // (2 * s)) & (row // s % 2 == 1) & (col // s % 2 == 0)) + f(row == col))
    d["l0a_level"] = np.stack(lev + [lev[0].T], 1)


def gated_delta(k):
    nc, H, DK, DV, HG = k.nc, 16, 64, 128, 4
    NG = H // HG
    KD, VD = H * DK, H * DV
    NLEV = 7
    TH = NT * H
    with Part(k) as p:
        wq, wk, wv = p.sb("wq", [P, 4, KD]), p.sb("wk", [P, 4, KD]), p.sb("wv", [P, 4, VD])
        wg, wout = p.sb("wg", [P, VD]), p.sb("wout", [P, H, D])
        tri, lev, nw = p.sb("tri", [P, 3, P]), p.sb("levels", [P, NLEV + 1, P]), p.sb("norm_w", [P, DV])
        g, nbeta, lam, dlast = (p.sb(n, [P, TH]) for n in ("g", "minus_beta", "lam", "decay_to_end"))
        half = p.sb("minus_half", [P, 2 * 2 * HG])
        delta_prologue(k, p, dict(wq=wq, wk=wk, wv=wv, wg=wg, wout=wout, tri=tri, lev=lev, nw=nw, g=g, nbeta=nbeta,
                                  lam=lam, dlast=dlast))
        xb = p.sb("x_batch", [P, 3 + T])
        C2 = lambda name, shape, parts=P: p.sb(name, [parts, TPB, *shape])
        qk, v, gate = C2("qk", [2 * HG, DK]), C2("v", [HG, DV]), C2("gate", [HG, DV])
        sq = C2("squares", [2 * HG, DK])
        ss, os_ = C2("qk_norms", [2 * HG]), C2("o_norms", [HG])
        qkT = p.sb("qk_featmajor", [DK, TPB, 2 * HG, P])
        G2 = lambda name: C2(name, [HG, P])
        rD, Dm, Ds, A, AT, Pm, PT, Tm, TT, Yp = (G2(n) for n in ("g_masked", "decay", "decay_strict", "A", "A_turned",
                                                                 "QK", "QK_turned", "inv", "inv_turned", "step"))
        delta, wdelta, S = G2("delta"), p.sb("delta_decayed", [P, HG, DV]), p.sb("state", [DK, HG, DV])
        lamq, O, yT = p.sb("lam_qs", [P, HG, DV]), G2("o"), G2("y_featmajor")
        names = ("xb", "proj", "qk_silu", "v_silu", "gate_silu", "ss", "ssr", "qkn", "turned", "qkT", "rD", "Dps", "Dexp", "Dm",
                 "Ds", "G", "A0", "A", "P", "APt", "AT", "PTr", "T1", "Yps", "Yp", "TTps", "Tps", "T", "TT", "bv", "gatew",
                 "dps", "delta", "wdelta", "Sps", "S", "KS", "R1", "Ops", "O", "osq", "osum", "orstd", "y", "yT_ps", "yT", "fin", "done", "through_pe", "through_pool")
        q = {n: p.sem(n) for n in names}
        flat = lambda a: a.rearrange("p h t -> p (h t)")

        with nc.Block() as block:
            @block.tensor
            def _(pe):
                mm, tr = nc.tensor.matmul, nc.tensor.transpose
                with pe.Fori(0, B) as b:
                    with pe.Fori(0, NG) as hg:
                        it = b * NG + hg
                        w = lambda n, per, j: pe.wait_ge(q[n], it * per + j)
                        w("xb", 1, 1)
                        w("done", 1, 1)
                        for c in range(TPB):
                            for n, ww in enumerate((wq, wk)):
                                for j in range(4):
                                    mm(k.bank[c][:, n * 256:(n + 1) * 256], xb[:, c * P + j:c * P + j + P],
                                       ww[:, j, bass.ds(hg * 256, 256)], start=j == 0, stop=j == 3)
                            for j in range(4):
                                mm(k.bank[2 + c], xb[:, c * P + j:c * P + j + P], wv[:, j, bass.ds(hg * 512, 512)],
                                   start=j == 0, stop=j == 3)
                            mm(k.bank[4 + c], xb[:, 3 + c * P:3 + c * P + P], wg[:, bass.ds(hg * 512, 512)],
                               start=True, stop=True).then_inc(q["proj"], 1)
                        for c in range(TPB):
                            w("rD", 2, c + 1)
                            mm(k.bank[6 + c], tri[:, 0, :], flat(rD[:, c]), start=True, stop=True).then_inc(q["Dps"], 1)
                        for c in range(TPB):
                            w("qkn", 2, c + 1)
                            w("v_silu", 2, c + 1)
                            pe.sem_inc(q["through_pe"], 1)
                            for n in range(2 * HG):
                                i = tr(k.bank[2 * (n // HG) + c][0:DK, n % HG * P:(n % HG + 1) * P], qk[:, c, n, :], k.ident[:])
                            i.then_inc(q["turned"], 1)
                        for c in range(TPB):
                            w("qkT", 2, c + 1)
                            w("gate_silu", 2, c + 1)
                            w("Dexp", 2, c + 1)
                            for h in range(HG):
                                mm(k.bank[4 + c][:, h * P:(h + 1) * P], qkT[:, c, HG + h, :], qkT[:, c, HG + h, :], start=True, stop=True)
                            for h in range(HG):
                                i = mm(k.bank[6 + c][:, h * P:(h + 1) * P], qkT[:, c, h, :], qkT[:, c, HG + h, :], start=True, stop=True)
                            i.then_inc(q["G"], 1)
                        for c in range(TPB):
                            w("A", 2, c + 1)
                            for h in range(HG):
                                tr(k.bank[c][:, h * P:(h + 1) * P], A[:, c, h, :], k.ident[:])
                            w("P", 2, c + 1)
                            for h in range(HG):
                                i = tr(k.bank[2 + c][:, h * P:(h + 1) * P], Pm[:, c, h, :], k.ident[:])
                            i.then_inc(q["APt"], 1)
                        for l in range(1, NLEV):
                            for c in range(TPB):
                                if l == 1:
                                    w("T1", 2, c + 1)
                                    w("PTr", 2, c + 1)
                                else:
                                    w("T", 2 * (NLEV - 2), 2 * (l - 2) + c + 1)
                                for h in range(HG):
                                    i = mm(k.bank[c][:, h * P:(h + 1) * P], AT[:, c, h, :], Tm[:, c, h, :], start=True, stop=True)
                                i.then_inc(q["Yps"], 1)
                            for c in range(TPB):
                                w("Yp", 2 * (NLEV - 1), 2 * (l - 1) + c + 1)
                                if l > 1:
                                    w("TT", 2 * (NLEV - 1), 2 * (l - 2) + c + 1)
                                if l < NLEV - 1:
                                    for h in range(HG):
                                        i = mm(k.bank[2 + c][:, h * P:(h + 1) * P], TT[:, c, h, :], Yp[:, c, h, :], start=True, stop=True)
                                    i.then_inc(q["Tps"], 1)
                                for h in range(HG):
                                    i = mm(k.bank[4 + c][:, h * P:(h + 1) * P], Yp[:, c, h, :], TT[:, c, h, :], start=True, stop=True)
                                i.then_inc(q["TTps"], 1)
                        wTT = lambda c: w("TT", 2 * (NLEV - 1), 2 * (NLEV - 2) + c + 1)
                        wTT(0)
                        w("bv", 2, 2)
                        for h in range(HG):
                            i = mm(k.bank[6][:, h * DV:(h + 1) * DV], TT[:, 0, h, :], v[:, 0, h, :], start=True, stop=True)
                        i.then_inc(q["dps"], 1)
                        w("wdelta", 1, 1)
                        for h in range(HG):
                            i = mm(k.bank[7][0:DK, h * DV:(h + 1) * DV], qk[:, 0, HG + h, :], wdelta[:, h, :], start=True, stop=True)
                        i.then_inc(q["Sps"], 1)
                        for h in range(HG):
                            i = mm(k.bank[0][:, h * DV:(h + 1) * DV], PT[:, 0, h, :], delta[:, 0, h, :], start=True, stop=True)
                        i.then_inc(q["Ops"], 1)
                        w("S", 1, 1)
                        for h in range(HG):
                            i = mm(k.bank[1][:, h * DV:(h + 1) * DV], qkT[:, 1, HG + h, :], S[:, h, :], start=True, stop=True)
                        i.then_inc(q["KS"], 1)
                        for h in range(HG):
                            i = mm(k.bank[2][:, h * DV:(h + 1) * DV], qkT[:, 1, h, :], S[:, h, :], start=True, stop=True)
                        i.then_inc(q["KS"], 1)
                        wTT(1)
                        w("R1", 1, 1)
                        for h in range(HG):
                            i = mm(k.bank[6][:, h * DV:(h + 1) * DV], TT[:, 1, h, :], v[:, 1, h, :], start=True, stop=True)
                        i.then_inc(q["dps"], 1)
                        w("delta", 2, 2)
                        for h in range(HG):
                            i = mm(k.bank[3][:, h * DV:(h + 1) * DV], PT[:, 1, h, :], delta[:, 1, h, :], start=True, stop=True)
                        i.then_inc(q["Ops"], 1)
                        for c in range(TPB):
                            w("y", 2, c + 1)
                            for h in range(HG):
                                i = tr(k.bank[4 + c][:, h * P:(h + 1) * P], O[:, c, h, :], k.ident[:])
                            i.then_inc(q["yT_ps"], 1)
                        for c in range(TPB):
                            w("yT", 2, c + 1)
                            for h in range(HG):
                                i = mm(k.bank[c][:, 0:D], yT[:, c, h, :], wout[:, bass.ds(hg * HG + h, 1), :].rearrange("p a d -> p (a d)"),
                                       start=h == 0, stop=h == HG - 1)
                            i.then_inc(q["fin"], 1)

            @block.scalar
            def _(act):
                def copy(dst, src):
                    return nc.scalar.activation(dst, src, ACT.Copy)

                with act.Fori(0, B) as b:
                    with act.Fori(0, NG) as hg:
                        it = b * NG + hg
                        w = lambda n, per, j: act.wait_ge(q[n], it * per + j)
                        for c in range(TPB):
                            w("proj", 2, c + 1)
                            nc.scalar.activation(qk[:, c].rearrange("p h d -> p (h d)"), k.bank[c], ACT.Silu).then_inc(q["qk_silu"], 1)
                            nc.scalar.activation(flat(v[:, c]), k.bank[2 + c], ACT.Silu).then_inc(q["v_silu"], 1)
                            nc.scalar.activation(flat(gate[:, c]), k.bank[4 + c], ACT.Silu).then_inc(q["gate_silu"], 1)
                        for c in range(TPB):
                            w("Dps", 2, c + 1)
                            nc.scalar.activation(flat(Dm[:, c]), k.bank[6 + c], ACT.Exp).then_inc(q["Dexp"], 1)
                        for c in range(TPB):
                            w("turned", 2, c + 1)
                            copy(flat(qkT[:, c, 0:HG]), k.bank[c][0:DK, :])
                            copy(flat(qkT[:, c, HG:]), k.bank[2 + c][0:DK, :]).then_inc(q["qkT"], 1)
                        for c in range(TPB):
                            w("APt", 2, c + 1)
                            copy(flat(AT[:, c]), k.bank[c]).then_inc(q["AT"], 1)
                            copy(flat(PT[:, c]), k.bank[2 + c]).then_inc(q["PTr"], 1)
                        for l in range(1, NLEV):
                            for c in range(TPB):
                                if l < NLEV - 1:
                                    w("Tps", 2 * (NLEV - 2), 2 * (l - 1) + c + 1)
                                    w("TTps", 2 * (NLEV - 1), 2 * (l - 1) + c + 1)
                                    copy(flat(Tm[:, c]), k.bank[2 + c]).then_inc(q["T"], 1)
                                w("TTps", 2 * (NLEV - 1), 2 * (l - 1) + c + 1)
                                copy(flat(TT[:, c]), k.bank[4 + c]).then_inc(q["TT"], 1)
                        w("dps", 2, 1)
                        copy(flat(delta[:, 0]), k.bank[6]).then_inc(q["delta"], 1)
                        w("Sps", 1, 1)
                        copy(flat(S[:]), k.bank[7][0:DK, :]).then_inc(q["S"], 1)
                        w("dps", 2, 2)
                        copy(flat(delta[:, 1]), k.bank[6]).then_inc(q["delta"], 1)
                        for c in range(TPB):
                            w("O", 2, c + 1)
                            nc.scalar.activation(sq[:, c].rearrange("p h d -> p (h d)"), flat(O[:, c]), ACT.Square).then_inc(q["osq"], 1)
                        for c in range(TPB):
                            w("yT_ps", 2, c + 1)
                            copy(flat(yT[:, c]), k.bank[4 + c]).then_inc(q["yT"], 1)

            @block.gpsimd
            def _(pool):
                tt = nc.gpsimd.tensor_tensor
                nc.gpsimd.memset(half[:], -0.5)
                pool.drain()
                pool.sem_inc(q["done"], 1)
                with pool.Fori(0, B) as b:
                    with pool.Fori(0, NG) as hg:
                        it = b * NG + hg
                        w = lambda n, per, j: pool.wait_ge(q[n], it * per + j)
                        col = lambda a, c: a[:, bass.ds(b * (TPB * H) + hg * HG + c * H, HG)]
                        w("done", 1, 1)
                        pool.sem_inc(q["through_pool"], 1)
                        for c in range(TPB):
                            tt(rD[:, c], across(tri[:, 1, :], HG), over(col(g, c), P), ALU.mult).then_inc(q["rD"], 1)
                        for c in range(TPB):
                            tt(Ds[:, c], across(tri[:, 1, :], HG), over(col(nbeta, c), P), ALU.mult)
                        w("ss", 1, 1)
                        flatss = ss[:].rearrange("p c h -> p (c h)")
                        tt(flatss, flatss, half[:], ALU.pow).then_inc(q["ssr"], 1)
                        pool.drain()
                        for c in range(TPB):
                            w("Dexp", 2, c + 1)
                            tt(Ds[:, c], Dm[:, c], Ds[:, c], ALU.mult).then_inc(q["Ds"], 1)
                            pool.drain()
                            tt(Dm[:, c], Dm[:, c], across(tri[:, 2, :], HG), ALU.mult).then_inc(q["Dm"], 1)
                        for c in range(TPB):
                            w("A0", 2, c + 1)
                            tt(A[:, c], A[:, c], across(k.ident[:], HG), ALU.add).then_inc(q["A"], 1)
                        for c in range(TPB):
                            w("v_silu", 2, c + 1)
                            pool.sem_inc(q["through_pool"], 1)
                            tt(v[:, c], v[:, c], over(col(nbeta, c), DV), ALU.mult).then_inc(q["bv"], 1)
                            w("gate_silu", 2, c + 1)
                            tt(gate[:, c], gate[:, c], across(nw[:], HG), ALU.mult).then_inc(q["gatew"], 1)
                        w("osum", 1, 1)
                        flato = os_[:].rearrange("p c h -> p (c h)")
                        tt(flato, flato, half[:, 0:2 * HG], ALU.pow).then_inc(q["orstd"], 1)

            @block.vector
            def _(dve):
                vv = nc.vector
                tt = vv.tensor_tensor
                vv.memset(k.Y[:], 0.0)
                vv.memset(xb[:], 0.0)
                dve.drain()
                with dve.Fori(0, B) as b:
                    dve.wait_ge(q["done"], b * NG + 1)
                    vv.tensor_copy(xb[:], k.HT[:, bass.ds(b, 1), PAD - 3:].rearrange("p a t -> p (a t)"))
                    dve.drain()
                    with dve.Fori(0, NG) as hg:
                        it = b * NG + hg
                        w = lambda n, per, j: dve.wait_ge(q[n], it * per + j)
                        col = lambda a, c: a[:, bass.ds(b * (TPB * H) + hg * HG + c * H, HG)]
                        bank3 = lambda n: k.bank[n].rearrange("p (h t) -> p h t", h=HG)
                        vv.engine_nop().then_inc(q["xb"], 1)
                        for c in range(TPB):
                            w("qk_silu", 2, c + 1)
                            tt(sq[:, c], qk[:, c], qk[:, c], ALU.mult)
                            dve.drain()
                            vv.tensor_reduce(ss[:, c], sq[:, c], AXX, ALU.add)
                        dve.drain()
                        vv.tensor_scalar_add(ss[:], ss[:], 1e-6).then_inc(q["ss"], 1)
                        w("ssr", 1, 1)
                        vv.tensor_scalar(ss[:, :, 0:HG], ss[:, :, 0:HG], DK ** -0.5, None, ALU.mult)
                        dve.drain()
                        for c in range(TPB):
                            tt(qk[:, c], qk[:, c], over(ss[:, c, :], DK), ALU.mult).then_inc(q["qkn"], 1)
                        for c in range(TPB):
                            w("G", 2, c + 1)
                            w("Ds", 2, c + 1)
                            tt(A[:, c], bank3(4 + c), Ds[:, c], ALU.mult).then_inc(q["A0"], 1)
                            w("Dm", 2, c + 1)
                            tt(Pm[:, c], bank3(6 + c), Dm[:, c], ALU.mult).then_inc(q["P"], 1)
                        for c in range(TPB):
                            w("A", 2, c + 1)
                            tt(Tm[:, c], A[:, c], across(lev[:, 0, :], HG), ALU.mult)
                            w("AT", 2, c + 1)
                            tt(TT[:, c], AT[:, c], across(lev[:, NLEV, :], HG), ALU.mult).then_inc(q["T1"], 1)
                        for l in range(1, NLEV):
                            for c in range(TPB):
                                w("Yps", 2 * (NLEV - 1), 2 * (l - 1) + c + 1)
                                tt(Yp[:, c], bank3(c), across(lev[:, l, :], HG), ALU.mult).then_inc(q["Yp"], 1)
                        w("delta", 2, 1)
                        tt(wdelta[:], delta[:, 0], over(col(dlast, 0), DV), ALU.mult).then_inc(q["wdelta"], 1)
                        w("Ops", 2, 1)
                        vv.tensor_copy(O[:, 0], bank3(0)).then_inc(q["O"], 1)
                        w("KS", 2, 1)
                        tt(lamq[:], bank3(1), over(col(lam, 1), DV), ALU.mult)
                        dve.drain()
                        tt(lamq[:], lamq[:], over(col(nbeta, 1), DV), ALU.mult)
                        dve.drain()
                        w("bv", 2, 2)
                        tt(v[:, 1], v[:, 1], lamq[:], ALU.add).then_inc(q["R1"], 1)
                        dve.drain()
                        w("KS", 2, 2)
                        tt(lamq[:], bank3(2), over(col(lam, 1), DV), ALU.mult)
                        dve.drain()
                        w("Ops", 2, 2)
                        tt(O[:, 1], bank3(3), lamq[:], ALU.add).then_inc(q["O"], 1)
                        for c in range(TPB):
                            w("osq", 2, c + 1)
                            vv.tensor_reduce(os_[:, c], sq[:, c].rearrange("p h d -> p (h d)").rearrange("p (h d) -> p h d", h=HG), AXX, ALU.add)
                        dve.drain()
                        vv.tensor_scalar(os_[:], os_[:], 1.0 / DV, 1e-5, ALU.mult, ALU.add).then_inc(q["osum"], 1)
                        w("orstd", 1, 1)
                        vv.tensor_scalar(os_[:], os_[:], -1.0, None, ALU.mult)
                        dve.drain()
                        for c in range(TPB):
                            w("gatew", 2, c + 1)
                            tt(O[:, c], O[:, c], over(os_[:, c, :], DV), ALU.mult)
                            dve.drain()
                            tt(O[:, c], O[:, c], gate[:, c], ALU.mult).then_inc(q["y"], 1)
                        w("fin", 2, 2)
                        y = k.Y[:, bass.ds(b * TPB, TPB), :]
                        tt(y, k.banks[:, 0:2, 0:D], y, ALU.add).then_inc(q["done"], 1)


def delta_prologue(k, p, m):
    nc, H, TH = k.nc, 16, NT * 16
    wab, al = p.sb("wab", [P, 2 * H]), p.sb("alog_dtbias", [P, 2, H])
    with Part(k) as own:
        wide = {n: own.sb("plain_" + n, [P, s]) for n, s in (("q", 1024), ("k", 1024), ("v", 2048))}
        z, e, u, l, r = (own.sb(n, [P, NT, H]) for n in ("z", "e", "u", "l", "r"))
        names = ("small", "taps", "plain", "rest", "ab", "z", "exped", "u", "logged", "alog", "g", "cum", "cum_read")
        q = {n: own.sem(n) for n in names}
        ab = k.bank[0].rearrange("p (t h) -> p t h", h=2 * H)
        g3 = m["g"][:].rearrange("p (t h) -> p t h", h=H)
        with nc.Block() as block:
            @block.sync
            def _(sp):
                sp.dma_start(wab[:], k.dram["l0a_wab"]).then_inc(q["small"], 16)
                sp.dma_start(al[:], k.dram["l0a_alog_dt"].partition_broadcast(P)).then_inc(q["small"], 16)
                sp.dma_start(m["tri"][:], k.dram["l0a_tri"]).then_inc(q["small"], 16)
                for n in "qkv":
                    sp.dma_start(m["w" + n][:], k.dram[f"l0a_conv{n}"].partition_broadcast(P)).then_inc(q["taps"], 16)
                    sp.dma_start(wide[n][:], k.dram[f"l0a_w{n}"]).then_inc(q["plain"], 16)
                sp.dma_start(m["wg"][:], k.dram["l0a_wg"]).then_inc(q["rest"], 16)
                sp.dma_start(m["wout"][:], k.dram["l0a_wout"]).then_inc(q["rest"], 16)
                sp.dma_start(m["lev"][:], k.dram["l0a_level"]).then_inc(q["rest"], 16)
                sp.dma_start(m["nw"][:], k.dram["l0a_normw"].partition_broadcast(P)).then_inc(q["rest"], 16)
                sp.wait_ge(q["rest"], 64)

            @block.tensor
            def _(pe):
                pe.wait_ge(q["small"], 48)
                for t in range(NT):
                    i = nc.tensor.matmul(ab[:, t, :], k.HT[:, t // TPB, PAD + t % TPB * P:PAD + (t % TPB + 1) * P], wab[:],
                                         start=True, stop=True)
                i.then_inc(q["ab"], 1)
                pe.wait_ge(q["g"], 1)
                nc.tensor.matmul(k.bank[1][:, 0:TH], m["tri"][:, 0, :], m["g"][:], start=True, stop=True)
                nc.tensor.matmul(k.bank[2][:, 0:TH], m["tri"][:, 1, :], m["g"][:], start=True, stop=True).then_inc(q["cum"], 1)

            @block.scalar
            def _(act):
                a = nc.scalar.activation
                act.wait_ge(q["small"], 48)
                a(al[:, 0, :], al[:, 0, :], ACT.Exp).then_inc(q["alog"], 1)
                act.wait_ge(q["z"], 1)
                a(e[:], z[:], ACT.Abs)
                act.drain()
                a(e[:], e[:], ACT.Exp, scale=-1.0)
                a(r[:], ab[:, :, H:], ACT.Exp, scale=-1.0).then_inc(q["exped"], 1)
                act.wait_ge(q["u"], 1)
                a(l[:], u[:], ACT.Ln).then_inc(q["logged"], 1)
                act.wait_ge(q["cum"], 1)
                a(m["lam"][:], k.bank[1][:, 0:TH], ACT.Exp)
                a(m["dlast"][:], k.bank[2][:, 0:TH], ACT.Exp)
                act.drain()

            @block.vector
            def _(dve):
                v = nc.vector
                dve.wait_ge(q["ab"], 1)
                dve.wait_ge(q["alog"], 1)
                v.tensor_tensor(z[:], ab[:, :, 0:H], across(al[:, 1, :], NT), ALU.add).then_inc(q["z"], 1)
                dve.wait_ge(q["exped"], 1)
                v.tensor_scalar_add(u[:], e[:], 1.0).then_inc(q["u"], 1)
                v.tensor_scalar_max(z[:], z[:], 0.0)
                v.tensor_scalar_add(r[:], r[:], 1.0)
                dve.drain()
                v.scalar_tensor_tensor(out=e[:], in0=u[:], scalar=-1.0, in1=e[:], op0=ALU.add, op1=ALU.subtract)
                dve.wait_ge(q["logged"], 1)
                dve.drain()
                v.tensor_tensor(l[:], l[:], e[:], ALU.subtract)
                dve.drain()
                v.tensor_add(z[:], z[:], l[:])
                dve.drain()
                v.scalar_tensor_tensor(out=g3, in0=z[:], scalar=-1.0, in1=across(al[:, 0, :], NT), op0=ALU.mult,
                                       op1=ALU.mult).then_inc(q["g"], 1)
                v.reciprocal(r[:], r[:])
                dve.drain()
                v.tensor_scalar(m["nbeta"][:].rearrange("p (t h) -> p t h", h=H), r[:], -2.0, None, ALU.mult)
                dve.wait_ge(q["taps"], 48)
                dve.wait_ge(q["plain"], 48)
                for n in "qkv":
                    w = m["w" + n]
                    v.tensor_tensor(w[:], w[:], across(wide[n][:], 4), ALU.mult)
                dve.drain()


def lay_out_mamba(i, d, np):
    E, N, R = 2 * D, 64, D // 16
    rows = lambda a: a.reshape(2, P, *a.shape[1:]).swapaxes(0, 1)
    d["l3a_ln1"] = np.stack([i["L3_attn_ln1_w"], i["L3_attn_ln1_b"]])
    d["l3a_ln2"] = np.stack([i["L3_attn_ln2_w"], i["L3_attn_ln2_b"]])
    for m in (1, 2):
        g = lambda n: i[f"L3_attn_m{m}_{n}"]
        d[f"l3a_win{m}"] = g("W_in").T
        d[f"l3a_conv{m}"] = np.concatenate([rows(g("conv_w")), rows(g("conv_b"))[:, :, None],
                                            rows(g("dt_b"))[:, :, None], rows(g("D"))[:, :, None]], 2)
        xp = g("W_xp")
        bm, cm = xp[R:R + N], xp[R + N:]
        d[f"l3a_wxp{m}"] = by_blocks(np.concatenate([bm, bm, cm, cm, bm, cm, xp[:R]]).T)
        d[f"l3a_wdt{m}"] = g("W_dt").T
        d[f"l3a_alog{m}"] = rows(g("A_log"))
        d[f"l3a_wout{m}"] = by_blocks(g("W_out").T)
    e = np.eye(N, dtype=np.float32)
    z = np.zeros((N, N), np.float32)
    d["l3a_sel"] = np.stack([np.concatenate([e, e]), np.concatenate([e, z]), np.concatenate([z, e])], 1)




def bi_mamba(k):
    nc = k.nc
    with Part(k) as p:
        affine = p.sb("ln1", [P, 2, D])
        load_one(k, p, affine, k.dram["l3a_ln1"].partition_broadcast(P))
        normalise(k, src=k.H, affine=affine)
    with Part(k) as p:
        mem = mamba_memories(p)
        for m in (1, 2):
            mamba_inputs(k, m, mem)
            mamba_scan(k, m, mem)
            mamba_output(k, m, mem)
    with Part(k) as p:
        affine = p.sb("ln2", [P, 2, D])
        load_one(k, p, affine, k.dram["l3a_ln2"].partition_broadcast(P))
        add_norm_to_input(k, p, affine)


def load_one(k, p, dst, src):
    loaded = p.sem("loaded")
    with k.nc.Block() as block:
        @block.sync
        def _(sp):
            sp.dma_start(dst[:], src).then_inc(loaded, 16)
            sp.wait_ge(loaded, 16)


def add_norm_to_input(k, p, affine):
    nc = k.nc
    stats, mv = p.sb("stats", [P, NT, 6]), p.sb("meanvar", [P, NT, 2])
    rstd, half = p.sb("rstd", [P, NT]), p.sb("minus_half", [P, NT])
    var_ready, rstd_ready = p.sem("var"), p.sem("rstd")
    with nc.Block() as block:
        @block.gpsimd
        def _(pool):
            nc.gpsimd.memset(half[:], -0.5)
            pool.drain()
            pool.wait_ge(var_ready, 1)
            nc.gpsimd.tensor_tensor(rstd[:], rstd[:], half[:], ALU.pow).then_inc(rstd_ready, 1)

        @block.vector
        def _(dve):
            layer_norm_steps(nc, dve, k.Y, k.Y, stats, mv, rstd, var_ready, (rstd_ready, 1))
            nc.vector.tensor_tensor(k.Y[:], k.Y[:], across(affine[:, 0, :], NT), ALU.mult)
            dve.drain()
            nc.vector.tensor_tensor(k.Y[:], k.Y[:], across(affine[:, 1, :], NT), ALU.add)
            dve.drain()
            nc.vector.tensor_add(k.Y[:], k.Y[:], k.H[:])
            dve.drain()


SN, SE = 64, 2
SCH = 512
SNC = B * T // SCH
CPAD = 3


def mamba_memories(p):
    m = {}
    m["xp"] = p.sb("xp_padded", [P, B, CPAD + T])
    m["xc"] = p.sb("xc", [P, SE, B * T])
    m["sz"] = p.sb("silu_z", [P, SE, B * T])
    m["dt"] = p.sb("dt", [P, SE, B * T])
    m["dtx"] = p.sb("dtx", [P, SE, B * T])
    for n in ("hm_b", "hm_c", "lo"):
        m[n] = p.sb("bc_" + n, [P, B * T], BF16)
    m["A"] = p.sb("A", [P, SE, SN])
    m["sel"] = p.sb("selectors", [P, 3, SN], BF16)
    m["self"] = p.sb("selectors_f32", [P, 3, SN])
    m["cw"] = p.sb("conv_and_biases", [P, SE, 7])
    m["wout"] = p.sb("w_out", [P, SE, D])
    return m


def mamba_inputs(k, m, mem):
    nc, R = k.nc, D // 16
    xp, xc, sz, dt, dtx = (mem[n] for n in ("xp", "xc", "sz", "dt", "dtx"))
    cw = mem["cw"]
    with Part(k) as p:
        win, wxp = p.sb("w_in", [P, 4 * P]), p.sb("w_xp", [P, SE, 3 * P + R])
        wdt = p.sb("w_dt", [R, 2 * P])
        dtlo = p.sb("dt_low", [R, B * T])
        tmp = [p.sb(f"tmp{n}", [P, SCH]) for n in range(3)]
        hi, mid = p.sb("high", [P, SCH], BF16), p.sb("middle", [P, SCH], BF16)
        r1, r2 = p.sb("rest1", [P, SCH]), p.sb("rest2", [P, SCH])
        names = ("loaded", "proj", "xp_out", "z_out", "conved", "xc_ready", "bc", "bc_read", "dtlo", "dtlo_ready", "dtp",
                 "absd", "exped", "u_ready", "logged", "dt_done", "src_ready", "a_ready")
        q = {n: p.sem(n) for n in names}
        xsrc = xp[:, :, CPAD:]
        with nc.Block() as block:
            @block.sync
            def _(sp):
                for dst, n in ((win, "win"), (cw, "conv"), (wxp, "wxp"), (wdt, "wdt"), (mem["A"], "alog"), (mem["wout"], "wout")):
                    sp.dma_start(dst[:], k.dram[f"l3a_{n}{m}"]).then_inc(q["loaded"], 16)
                sp.dma_start(mem["self"][:], k.dram["l3a_sel"]).then_inc(q["loaded"], 16)

            @block.tensor
            def _(pe):
                pe.wait_ge(q["loaded"], 112)
                pe.wait_ge(q["src_ready"], 1)
                for blk in (0, 1, 2, 3):
                    if blk == 2:
                        pe.wait_ge(q["xp_out"], 4)
                    if blk == 3:
                        pe.wait_ge(q["xp_out"], 8)
                    for c in range(SNC):
                        nc.tensor.matmul(k.bank[blk % 2 * 4 + c].rearrange("p (b t) -> p b t", b=2), win[:, blk * P:(blk + 1) * P],
                                         k.HT[:, 2 * c:2 * c + 2, PAD:], start=True, stop=True).then_inc(q["proj"], 1)
                pe.wait_ge(q["xc_ready"], 2)
                for c in range(SNC):
                    for n, (lo, w) in enumerate(((0, P), (P, P), (2 * P, P), (3 * P, R))):
                        pe.wait_ge(*((q["z_out"], 4) if c == 0 else (q["bc_read"], 4 * c)))
                        for e in range(SE):
                            i = nc.tensor.matmul(k.bank[n][0:w, :], wxp[:, e, lo:lo + w], xc[:, e, c * SCH:(c + 1) * SCH],
                                                 start=e == 0, stop=e == SE - 1)
                        i.then_inc(q["bc"], 1)
                pe.wait_ge(q["dtlo_ready"], SNC)
                pe.wait_ge(q["z_out"], 8)
                for c in range(SNC):
                    for e in range(SE):
                        if c:
                            pe.wait_ge(q["dt_done"], (c - 1) * SE + e + 1)
                        nc.tensor.matmul(k.bank[4 + e], wdt[:, e * P:(e + 1) * P], dtlo[:, c * SCH:(c + 1) * SCH],
                                         start=True, stop=True).then_inc(q["dtp"], 1)

            @block.scalar
            def _(act):
                act.wait_ge(q["loaded"], 112)
                for blk in (0, 1):
                    if blk == 1:
                        act.wait_ge(q["conved"], 1)
                    for c in range(SNC):
                        act.wait_ge(q["proj"], blk * 4 + c + 1)
                        nc.scalar.activation(xsrc[:, 2 * c:2 * c + 2, :], k.bank[blk * 4 + c].rearrange("p (b t) -> p b t", b=2),
                                             ACT.Copy).then_inc(q["xp_out"], 1)
                for blk in (0, 1):
                    for c in range(SNC):
                        act.wait_ge(q["proj"], 8 + blk * 4 + c + 1)
                        nc.scalar.activation(sz[:, blk, c * SCH:(c + 1) * SCH], k.bank[blk * 4 + c], ACT.Silu).then_inc(q["z_out"], 1)
                for e in range(SE):
                    act.wait_ge(q["conved"], e + 1)
                    nc.scalar.activation(xc[:, e, :], xc[:, e, :], ACT.Silu, bias=cw[:, e, 4:5]).then_inc(q["xc_ready"], 1)
                nc.scalar.activation(mem["A"][:], mem["A"][:], ACT.Exp).then_inc(q["a_ready"], 1)
                for c in range(SNC):
                    for e in range(SE):
                        n = c * SE + e
                        act.wait_ge(q["dtp"], n + 1)
                        if n:
                            act.wait_ge(q["dt_done"], n)
                        nc.scalar.activation(tmp[0][:], k.bank[4 + e], ACT.Abs, bias=cw[:, e, 5:6])
                        act.drain()
                        nc.scalar.activation(tmp[0][:], tmp[0][:], ACT.Exp, scale=-1.0).then_inc(q["exped"], 1)
                        act.wait_ge(q["u_ready"], n + 1)
                        nc.scalar.activation(tmp[2][:], tmp[1][:], ACT.Ln).then_inc(q["logged"], 1)

            @block.vector
            def _(dve):
                v = nc.vector
                if m == 2:
                    v.tensor_copy(dtx[:, 0, :].rearrange("p (b t) -> p b t", b=B), k.HT[:, :, PAD + T - 1:PAD - 1:-1])
                    dve.drain()
                    v.tensor_copy(k.HT[:, :, PAD:], dtx[:, 0, :].rearrange("p (b t) -> p b t", b=B))
                    dve.drain()
                v.memset(xp[:, :, 0:CPAD], 0.0).then_inc(q["src_ready"], 1)
                dve.wait_ge(q["loaded"], 112)
                v.tensor_copy(mem["sel"][:], mem["self"][:])
                dve.drain()
                for e in range(SE):
                    dve.wait_ge(q["xp_out"], 4 * e + 4)
                    o = xc[:, e, :].rearrange("p (b t) -> p b t", b=B)
                    v.tensor_scalar(o, xp[:, :, 0:T], cw[:, e, 0:1], None, ALU.mult)
                    for j in range(1, 4):
                        dve.drain()
                        i = v.scalar_tensor_tensor(out=o, in0=xp[:, :, j:j + T], scalar=cw[:, e, j:j + 1], in1=o,
                                                   op0=ALU.mult, op1=ALU.add)
                    i.then_inc(q["conved"], 1)
                dve.wait_ge(q["a_ready"], 1)
                v.tensor_scalar(mem["A"][:], mem["A"][:], -1.0, None, ALU.mult)
                for c in range(SNC):
                    cols = slice(c * SCH, (c + 1) * SCH)
                    for n, name in enumerate(("hm_b", "hm_c")):
                        dve.wait_ge(q["bc"], c * 4 + n + 1)
                        v.tensor_copy(hi[:], k.bank[n])
                        dve.drain()
                        v.tensor_copy(mem[name][0:64, cols], hi[0:64, :])
                        v.tensor_tensor(mem[name][64:128, cols], k.bank[n][64:128, :], hi[64:128, :], ALU.subtract)
                        dve.drain()
                        v.engine_nop().then_inc(q["bc_read"], 1)
                    dve.wait_ge(q["bc"], c * 4 + 3)
                    v.tensor_copy(hi[:], k.bank[2])
                    dve.drain()
                    v.tensor_tensor(r1[:], k.bank[2], hi[:], ALU.subtract).then_inc(q["bc_read"], 1)
                    dve.drain()
                    v.tensor_copy(mid[:], r1[:])
                    dve.drain()
                    v.tensor_tensor(mem["lo"][:, cols], r1[:], mid[:], ALU.subtract)
                    dve.wait_ge(q["bc"], c * 4 + 4)
                    v.tensor_copy(dtlo[:, cols], k.bank[3][0:R, :]).then_inc(q["bc_read"], 1)
                    dve.drain()
                    v.engine_nop().then_inc(q["dtlo_ready"], 1)
                for c in range(SNC):
                    for e in range(SE):
                        n = c * SE + e
                        o = dt[:, e, c * SCH:(c + 1) * SCH]
                        dve.wait_ge(q["exped"], n + 1)
                        v.tensor_scalar_add(tmp[1][:], tmp[0][:], 1.0).then_inc(q["u_ready"], 1)
                        v.tensor_scalar(o, k.bank[4 + e], cw[:, e, 5:6], 0.0, ALU.add, ALU.max)
                        dve.drain()
                        v.scalar_tensor_tensor(out=r1[:], in0=tmp[1][:], scalar=-1.0, in1=tmp[0][:], op0=ALU.add, op1=ALU.subtract)
                        dve.drain()
                        dve.wait_ge(q["logged"], n + 1)
                        v.tensor_tensor(r2[:], tmp[2][:], r1[:], ALU.subtract)
                        dve.drain()
                        v.tensor_add(o, o, r2[:])
                        dve.drain()
                        v.tensor_tensor(dtx[:, e, c * SCH:(c + 1) * SCH], o, xc[:, e, c * SCH:(c + 1) * SCH],
                                        ALU.mult).then_inc(q["dt_done"], 1)
                dve.drain()
                for e in range(SE):
                    v.tensor_scalar(xc[:, e, :], xc[:, e, :], cw[:, e, 6:7], None, ALU.mult)
                dve.drain()


def mamba_scan(k, m, mem):
    NS = 4
    nc = k.nc
    xc, sz, dt, dtx = (mem[n] for n in ("xc", "sz", "dt", "dtx"))
    with Part(k) as p:
        dA = p.sb("dA", [P, NS, SE, SCH])
        dBx = p.sb("dBx", [P, NS, SE, SCH])
        h = p.sb("h", [P, 2, SE, SCH])
        hc = p.sb("hc", [P, 2, SE, SCH])
        bsb = p.sb("b_row", [P, NS, SCH])
        zero = p.sb("zero", [P, SCH], BF16)
        names = ("zeroed", "b_ready", "c_ready", "bsb_ready", "da_ready", "dbx_ready",
                 "scanned", "through_pool", "hc_ready", "hc_free", "y_ready", "y_read")
        q = {n: p.sem(n) for n in names}
        sel = mem["sel"]
        BBANK, LEAD = (2, 3, 6, 7), NS - 1

        def onto_all(ap):
            return ap.to_broadcast([P, P])

        with nc.Block() as block:
            @block.tensor
            def _(pe):
                pe.wait_ge(q["zeroed"], 1)

                def row(c, n, part, which, bank, free, ready):
                    cols = bass.ds(c * SCH, SCH)
                    pe.wait_ge(q[free], c * SN + n + 1)
                    nc.tensor.matmul(k.bank[bank], onto_all(sel[:, 0, bass.ds(n, 1)]), mem[part][:, cols], start=True, stop=False)
                    nc.tensor.matmul(k.bank[bank], onto_all(sel[:, which, bass.ds(n, 1)]), mem["lo"][:, cols],
                                     start=False, stop=True).then_inc(q[ready], 1)

                def b_row(c, n, s):
                    row(c, n, "hm_b", 1, BBANK[s], "bsb_ready", "b_ready")

                def c_row(c, n, s):
                    row(c, n, "hm_c", 2, 4 + s, "hc_ready", "c_ready")

                def add_up(c, n, s):
                    pe.wait_ge(q["hc_ready"], c * SN + n + 3)
                    for e in range(SE):
                        i = nc.tensor.matmul(k.bank[e], k.ident[:], hc[:, s, e, :], start=False, stop=False)
                    i.then_inc(q["hc_free"], 1)

                with pe.Fori(0, SNC) as c:
                    for n in range(LEAD):
                        b_row(c, n, n)
                    c_row(c, 0, 0)
                    pe.wait_ge(q["y_read"], c + 1)
                    for e in range(SE):
                        nc.tensor.matmul(k.bank[e], zero[:, 0:P], zero[:], start=True, stop=False)

                    def step(n, s):
                        b_row(c, n + LEAD, (s + LEAD) % NS)
                        c_row(c, n + 1, (s + 1) % 2)
                        add_up(c, n, s % 2)

                    with pe.Fori(0, SN // NS - 1) as n4:
                        for s in range(NS):
                            step(n4 * NS + s, s)
                    step(SN - NS, 0)
                    for n in range(SN - LEAD, SN):
                        if n + 1 < SN:
                            c_row(c, n + 1, (n + 1) % 2)
                        add_up(c, n, n % 2)
                    for e in range(SE):
                        i = nc.tensor.matmul(k.bank[e], k.ident[:], xc[:, e, bass.ds(c * SCH, SCH)], start=False, stop=True)
                    i.then_inc(q["y_ready"], 1)

            @block.scalar
            def _(act):
                act.wait_ge(q["zeroed"], 1)
                nc.scalar.activation(bsb[:, 0, 0:1], bsb[:, 0, 0:1], ACT.Exp)
                act.drain()
                with act.Fori(0, SNC) as c:
                    with act.Fori(0, SN // NS) as n4:
                        for s in range(NS):
                            n = n4 * NS + s
                            it = c * SN + n
                            act.wait_ge(q["scanned"], it + 1)
                            for e in range(SE):
                                d3 = dt[:, e, bass.ds(c * SCH, SCH)].rearrange("p (b t) -> p b t", t=T)
                                i = nc.scalar.activation(dA[:, s, e, :].rearrange("p (b t) -> p b t", t=T)[:, :, 1:], d3[:, :, 1:],
                                                         ACT.Exp, scale=mem["A"][:, e, bass.ds(n, 1)])
                            i.then_inc(q["da_ready"], 1)
                            act.wait_ge(q["b_ready"], it + 1)
                            act.wait_ge(q["dbx_ready"], it + 1)
                            nc.scalar.activation(bsb[:, s, :], k.bank[BBANK[s]], ACT.Copy).then_inc(q["bsb_ready"], 1)

            @block.gpsimd
            def _(pool):
                nc.gpsimd.memset(zero[:], 0.0)
                nc.gpsimd.memset(bsb[:], 0.0)
                nc.gpsimd.memset(dA[:], 0.0).then_inc(q["zeroed"], 1)
                for n, slots in (("bsb_ready", NS), ("dbx_ready", NS), ("scanned", NS), ("hc_ready", 2), ("hc_free", 2)):
                    pool.sem_inc(q[n], slots)
                pool.sem_inc(q["y_read"], 1)
                with pool.Fori(0, SNC) as c:
                    with pool.Fori(0, SN // NS) as n4:
                        for s in range(NS):
                            it = c * SN + n4 * NS + s
                            pool.wait_ge(q["bsb_ready"], it + NS + 1)
                            pool.wait_ge(q["scanned"], it + 1)
                            pool.sem_inc(q["through_pool"], 1)
                            nc.gpsimd.tensor_tensor(dBx[:, s], dtx[:, :, bass.ds(c * SCH, SCH)], across(bsb[:, s, :], SE),
                                                    ALU.mult).then_inc(q["dbx_ready"], 1)

            @block.vector
            def _(dve):
                v = nc.vector

                def scan(c, n, s):
                    it = c * SN + n
                    dve.wait_ge(q["da_ready"], it + 1)
                    dve.wait_ge(q["dbx_ready"], it + NS + 1)
                    dve.wait_ge(q["hc_ready"], it + 1)
                    flat = lambda a: a.rearrange("p e t -> p (e t)")
                    v.tensor_tensor_scan(flat(h[:, s % 2]), flat(dA[:, s]), flat(dBx[:, s]), 0.0, ALU.mult,
                                         ALU.add).then_inc(q["scanned"], 1)

                def times_c(c, n, s):
                    it = c * SN + n
                    dve.wait_ge(q["c_ready"], it + 1)
                    dve.wait_ge(q["hc_free"], it + 1)
                    dve.wait_ge(q["scanned"], it + NS + 1)
                    v.tensor_tensor(hc[:, s], h[:, s], across(k.bank[4 + s], SE), ALU.mult).then_inc(q["hc_ready"], 1)

                with dve.Fori(0, SNC) as c:
                    scan(c, 0, 0)
                    with dve.Fori(0, SN // NS - 1) as n4:
                        for s in range(NS):
                            scan(c, n4 * NS + s + 1, (s + 1) % NS)
                            times_c(c, n4 * NS + s, s % 2)
                    for n in range(SN - NS, SN):
                        if n + 1 < SN:
                            scan(c, n + 1, (n + 1) % NS)
                        times_c(c, n, n % 2)
                    dve.wait_ge(q["y_ready"], c + 1)
                    for e in range(SE):
                        z = sz[:, e, bass.ds(c * SCH, SCH)]
                        i = v.tensor_tensor(z, k.bank[e], z, ALU.mult)
                    i.then_inc(q["y_read"], 1)


def mamba_output(k, m, mem):
    nc = k.nc
    sz, xc = mem["sz"], mem["xc"]
    with Part(k) as p:
        gated_ready, out = p.sem("gated_ready"), p.sem("out")
        with nc.Block() as block:
            @block.tensor
            def _(pe):
                pe.wait_ge(gated_ready, 1)
                for t in range(NT):
                    for e in range(SE):
                        i = nc.tensor.matmul(k.bank[t // 4][:, t % 4 * D:(t % 4 + 1) * D], xc[:, e, t * P:(t + 1) * P],
                                             mem["wout"][:, e, :], start=e == 0, stop=e == SE - 1)
                    if t % 4 == 3:
                        i.then_inc(out, 1)

            @block.vector
            def _(dve):
                v = nc.vector
                for e in range(SE):
                    src = sz[:, e, :].rearrange("p (b t) -> p b t", t=T)
                    if m == 2:
                        src = src[:, :, ::-1]
                    v.tensor_copy(xc[:, e, :].rearrange("p (b t) -> p b t", t=T), src)
                dve.drain()
                v.engine_nop().then_inc(gated_ready, 1)
                for g in range(4):
                    dve.wait_ge(out, g + 1)
                    y, o = k.Y[:, 4 * g:4 * g + 4, :], k.bank[g].rearrange("p (t d) -> p t d", d=D)
                    if m == 1:
                        v.tensor_copy(y, o)
                    else:
                        v.tensor_tensor(y, o, y, ALU.add)
                dve.drain()


def blocks():
    return [gated_delta, window_attn, plucker_attn, ffn_ternary, flash_attn, ffn_experts, bi_mamba, ffn_int8]


def build_program(nc, dram, todo=None):
    with ExitStack() as ctx:
        k = Core(nc, dram, ctx)
        load_residual(k)
        todo = blocks() if todo is None else todo
        for n, block in enumerate(todo):
            normalise(k, add_y=n > 0)
            block(k)
        normalise(k, add_y=True, make_ht=False)
        store_residual(k)


def tokens_first(a):
    a = a.reshape(-1, P, a.shape[-1])
    return a.transpose(1, 0, 2)


def by_blocks(a):
    return a.reshape(-1, P, a.shape[-1]).transpose(1, 0, 2)


def laid_out(i):
    import numpy as np
    d = {}
    d["x"] = tokens_first(i["L0_attn_x"].reshape(-1, D))
    d["ident"] = np.eye(P, dtype=np.float32)
    d["iota8"] = np.arange(8, dtype=np.float32)
    d["l1f_w12"] = np.stack([i["L1_ffn_w1_w"].T, i["L1_ffn_w2_w"].T], 1)
    d["l1f_sc"] = np.stack([i[f"L1_ffn_{n}_s"].reshape(4, P).T for n in ("w1", "w2", "h1", "h2")], 1)
    d["l1f_wh"] = np.stack([by_blocks(i[f"L1_ffn_{n}_w"].T) for n in ("h1", "h2")], 1)
    d["l1f_w3"] = by_blocks(i["L1_ffn_w3_w"].T)
    d["l1f_s3"] = i["L1_ffn_w3_s"]
    d["l2f_gw"], d["l2f_gb"] = i["L2_ffn_gate_W"], i["L2_ffn_gate_b"]
    d["l2f_ew"] = i["L2_ffn_expert_W"].transpose(1, 0, 2).reshape(D, -1)
    d["l2f_eb"] = i["L2_ffn_expert_b"].reshape(1, -1)
    d["l3f_wgu"] = np.concatenate([i["L3_ffn_w_gate"].T, i["L3_ffn_w_up"].T], 1)
    d["l3f_wd"] = by_blocks(i["L3_ffn_w_down"].T).reshape(P, -1)
    for lay_out in (lay_out_delta, lay_out_window, lay_out_plucker, lay_out_flash, lay_out_mamba):
        lay_out(i, d, np)
    return {n: np.ascontiguousarray(a) for n, a in d.items()}


def kernel(**inputs):
    import numpy as np
    import concourse.bacc as bacc
    from concourse.bass_utils import run_bass_kernel_spmd

    arrays = laid_out({n: np.asarray(a) for n, a in inputs.items()})
    nc = bacc.Bacc("TRN2", target_bir_lowering=False, num_devices=1)
    dram = {n: nc.dram_tensor(f"in_{n}", a.shape, mybir.dt.from_np(a.dtype), kind="ExternalInput").ap()
            for n, a in arrays.items()}
    dram["out"] = nc.dram_tensor("out_0", (P, NT, D), F32, kind="ExternalOutput").ap()
    build_program(nc, dram)
    r = run_bass_kernel_spmd(nc, [{f"in_{n}": a for n, a in arrays.items()}], core_ids=[0])
    return r.results[0]["out_0"].transpose(1, 0, 2).reshape(B, T, D)
```

```python
from contextlib import ExitStack

import concourse.bass as bass
from concourse import mybir

F32 = mybir.dt.float32
BF16 = mybir.dt.bfloat16
I32 = mybir.dt.int32
ALU = mybir.AluOpType
ACT = mybir.ActivationFunctionType
AXX = mybir.AxisListType.X

P = 128
B, T, D = 8, 256, 128
NT = B * T // P
TPB = T // P
PAD = 4
LNEPS = 1e-5


class Core:

    def __init__(self, nc, dram, ctx):
        self.nc, self.dram, self.parts, self.cleared = nc, dram, 0, []
        sb = lambda name, shape, dt=F32: ctx.enter_context(nc.sbuf_tensor(name, shape, dt))
        self.banks = ctx.enter_context(nc.psum_tensor("banks", [P, 8, 512], F32))
        self.bank = [self.banks[:, i, :] for i in range(8)]
        self.X = sb("residual", [P, NT, D])
        self.Y = sb("block_out", [P, NT, D])
        self.HT = sb("norm_featmajor", [P, B, PAD + T])
        self.H = sb("norm", [P, NT, D])
        self.ident = sb("ident", [P, P])


class Part:

    def __init__(self, k):
        self.k, self.nc, self.ctx, self.sems = k, k.nc, ExitStack(), []
        k.parts += 1
        self.id = k.parts

    def __enter__(self):
        return self

    def sb(self, name, shape, dt=F32):
        return self.ctx.enter_context(self.nc.sbuf_tensor(f"{name}_{self.id}", shape, dt))

    def sem(self, name):
        self.sems.append(self.nc.alloc_semaphore(f"{name}_{self.id}"))
        return self.sems[-1]

    def __exit__(self, *a):
        if a[0] is None:
            for s in self.k.cleared:
                self.nc.release_semaphore(s)
            for s in self.sems:
                self.nc.gpsimd.sem_clear(s)
            self.k.cleared = self.sems
        return self.ctx.__exit__(*a)


def over(ap, n):
    return ap.unsqueeze(len(ap.shape)).to_broadcast([*ap.shape, n])


def across(ap, n):
    return ap.unsqueeze(1).to_broadcast([ap.shape[0], n, *ap.shape[1:]])


def load_residual(k):
    nc = k.nc
    with Part(k) as p:
        loaded = p.sem("loaded")
        with nc.Block() as block:
            @block.sync
            def _(sp):
                sp.dma_start(k.X[:], k.dram["x"]).then_inc(loaded, 16)
                sp.dma_start(k.ident[:], k.dram["ident"]).then_inc(loaded, 16)
                sp.wait_ge(loaded, 32)

            @block.vector
            def _(dve):
                nc.vector.memset(k.HT[:], 0.0)


def store_residual(k):
    nc = k.nc
    with Part(k) as p:
        stored = p.sem("stored")
        with nc.Block() as block:
            @block.sync
            def _(sp):
                sp.dma_start(k.dram["out"], k.X[:]).then_inc(stored, 16)
                sp.wait_ge(stored, 16)


def layer_norm_steps(nc, dve, src, dst, stats, mv, rstd, var_ready, rstd_ready):
    for t in range(NT):
        nc.vector.bn_stats(stats[:, t, :], src[:, t, :])
    dve.drain()
    for t in range(NT):
        nc.vector.bn_aggr(mv[:, t, :], stats[:, t, :])
    dve.drain()
    nc.vector.tensor_scalar_add(rstd[:], mv[:, :, 1], LNEPS).then_inc(var_ready, 1)
    dve.wait_ge(*rstd_ready)
    for t in range(NT):
        nc.vector.tensor_scalar(dst[:, t, :], src[:, t, :], mv[:, t, 0:1], rstd[:, t:t + 1],
                                ALU.subtract, ALU.mult)
    dve.drain()


def normalise(k, add_y=False, make_ht=True, src=None, affine=None, norm=True):
    nc = k.nc
    src = k.X if src is None else src
    rounds = int(add_y) + int(make_ht and norm)
    with Part(k) as p:
        stats = p.sb("stats", [P, NT, 6])
        mv = p.sb("meanvar", [P, NT, 2])
        rstd = p.sb("rstd", [P, NT])
        half = p.sb("minus_half", [P, NT])
        H = k.H
        var_ready, rstd_ready = p.sem("var"), p.sem("rstd")
        h_ready, turned = p.sem("h"), p.sem("turned")
        turn_from = H if norm else src
        with nc.Block() as block:
            @block.gpsimd
            def _(pool):
                nc.gpsimd.memset(half[:], -0.5)
                pool.drain()
                for r in range(rounds):
                    pool.wait_ge(var_ready, r + 1)
                    nc.gpsimd.tensor_tensor(rstd[:], rstd[:], half[:], ALU.pow).then_inc(rstd_ready, 1)

            @block.vector
            def _(dve):
                r = 0
                if add_y:
                    r += 1
                    layer_norm_steps(nc, dve, k.Y, H, stats, mv, rstd, var_ready, (rstd_ready, r))
                    nc.vector.tensor_add(k.X[:], k.X[:], H[:])
                    dve.drain()
                if make_ht and norm:
                    r += 1
                    layer_norm_steps(nc, dve, src, H, stats, mv, rstd, var_ready, (rstd_ready, r))
                    if affine is not None:
                        nc.vector.tensor_tensor(H[:], H[:], across(affine[:, 0, :], NT), ALU.mult)
                        dve.drain()
                        nc.vector.tensor_tensor(H[:], H[:], across(affine[:, 1, :], NT), ALU.add)
                        dve.drain()
                nc.vector.engine_nop().then_inc(h_ready, 1)

            if make_ht:
                @block.tensor
                def _(pe):
                    pe.wait_ge(h_ready, 1)
                    for t in range(NT):
                        i = nc.tensor.transpose(k.bank[t // 4][:, t % 4 * P:(t % 4 + 1) * P], turn_from[:, t, :], k.ident[:])
                        if t % 4 == 3:
                            i.then_inc(turned, 1)

                @block.scalar
                def _(act):
                    for g in range(4):
                        act.wait_ge(turned, g + 1)
                        nc.scalar.activation(k.HT[:, 2 * g:2 * g + 2, PAD:PAD + T],
                                             k.bank[g][:].rearrange("p (b t) -> p b t", b=2), ACT.Copy)
                    act.drain()


def ffn_ternary(k):
    nc, HID, CH = k.nc, 512, 512
    KB, NCH = HID // P, B * T // CH
    bpc = CH // T
    with Part(k) as p:
        w12 = p.sb("w12", [P, 2, HID])
        wh = p.sb("wh", [P, 2, KB, HID])
        w3 = p.sb("w3", [P, KB, D])
        sc = p.sb("scales", [P, 4, KB])
        s3 = p.sb("s3", [P, D])
        gate = p.sb("gate", [P, KB, CH])
        hid = [p.sb(f"hid{i}", [P, KB, CH]) for i in range(3)]
        loaded, w3_loaded = p.sem("loaded"), p.sem("w3_loaded")
        pair, gated, prod = p.sem("pair"), p.sem("gated"), p.sem("prod")
        lin = [p.sem("lin1"), p.sem("lin2")]
        gelu = [p.sem("gelu1"), p.sem("gelu2")]
        down, out = p.sem("down"), p.sem("out")
        with nc.Block() as block:
            @block.sync
            def _(sp):
                sp.dma_start(w12[:], k.dram["l1f_w12"]).then_inc(loaded, 16)
                sp.dma_start(sc[:], k.dram["l1f_sc"]).then_inc(loaded, 16)
                sp.dma_start(wh[:], k.dram["l1f_wh"]).then_inc(loaded, 16)
                sp.dma_start(w3[:], k.dram["l1f_w3"]).then_inc(w3_loaded, 16)
                sp.dma_start(s3[:], k.dram["l1f_s3"].partition_broadcast(P)).then_inc(w3_loaded, 16)

            @block.tensor
            def _(pe):
                pe.wait_ge(loaded, 48)
                pe.wait_ge(w3_loaded, 32)
                with pe.Fori(0, NCH) as c:
                    x = k.HT[:, bass.ds(c * bpc, bpc), PAD:PAD + T]
                    pe.wait_ge(out, c + 1)
                    for ob in range(KB):
                        for j in range(2):
                            i = nc.tensor.matmul(k.bank[4 * j + ob][:].rearrange("p (b t) -> p b t", b=bpc),
                                                 w12[:, j, ob * P:(ob + 1) * P], x, start=True, stop=True)
                        i.then_inc(pair, 1)
                    for l in range(2):
                        pe.wait_ge(*((prod, c * KB + KB) if l == 0 else (gelu[0], c * KB + KB)))
                        for ob in range(KB):
                            for kb in range(KB):
                                i = nc.tensor.matmul(k.bank[4 * l + ob][:], wh[:, l, kb, ob * P:(ob + 1) * P],
                                                     hid[l][:, kb, :], start=kb == 0, stop=kb == KB - 1)
                            i.then_inc(lin[l], 1)
                    pe.wait_ge(gelu[1], c * KB + KB)
                    for tt in range(CH // P):
                        for kb in range(KB):
                            i = nc.tensor.matmul(k.bank[0][:, tt * D:(tt + 1) * D], hid[2][:, kb, tt * P:(tt + 1) * P],
                                                 w3[:, kb, :], start=kb == 0, stop=kb == KB - 1)
                    i.then_inc(down, 1)

            @block.scalar
            def _(act):
                act.wait_ge(loaded, 48)
                with act.Fori(0, NCH) as c:
                    for ob in range(KB):
                        act.wait_ge(pair, c * KB + ob + 1)
                        nc.scalar.activation(gate[:, ob, :], k.bank[ob][:], ACT.Silu,
                                             scale=sc[:, 0, ob:ob + 1]).then_inc(gated, 1)
                    for l in range(2):
                        for ob in range(KB):
                            act.wait_ge(lin[l], c * KB + ob + 1)
                            nc.scalar.activation(hid[l + 1][:, ob, :], k.bank[4 * l + ob][:], ACT.Gelu,
                                                 scale=sc[:, 2 + l, ob:ob + 1]).then_inc(gelu[l], 1)

            @block.vector
            def _(dve):
                dve.sem_inc(out, 1)
                dve.wait_ge(w3_loaded, 32)
                dve.wait_ge(loaded, 48)
                with dve.Fori(0, NCH) as c:
                    for ob in range(KB):
                        dve.wait_ge(gated, c * KB + ob + 1)
                        nc.vector.scalar_tensor_tensor(out=hid[0][:, ob, :], in0=k.bank[4 + ob][:],
                                                       scalar=sc[:, 1, ob:ob + 1], in1=gate[:, ob, :],
                                                       op0=ALU.mult, op1=ALU.mult).then_inc(prod, 1)
                    dve.wait_ge(down, c + 1)
                    nc.vector.tensor_tensor(k.Y[:, bass.ds(c * (CH // P), CH // P), :],
                                            k.bank[0][:].rearrange("p (t d) -> p t d", d=D),
                                            across(s3[:], CH // P), ALU.mult).then_inc(out, 1)


def ffn_int8(k):
    nc, HID, CH = k.nc, 384, 512
    KB, NCH = HID // P, B * T // CH
    bpc = CH // T
    NW = 2 * HID + KB * D
    with Part(k) as p:
        wi = p.sb("w_int", [P, NW], I32)
        w = p.sb("w", [P, NW])
        gate = p.sb("gate", [P, KB, CH])
        hid = p.sb("hid", [P, KB, CH])
        loaded, scaled = p.sem("loaded"), p.sem("scaled")
        pair, gated, prod, down, out = p.sem("pair"), p.sem("gated"), p.sem("prod"), p.sem("down"), p.sem("out")
        with nc.Block() as block:
            @block.sync
            def _(sp):
                sp.dma_start(wi[:, 0:2 * HID], k.dram["l3f_wgu"]).then_inc(loaded, 16)
                sp.dma_start(wi[:, 2 * HID:], k.dram["l3f_wd"]).then_inc(loaded, 16)

            @block.tensor
            def _(pe):
                pe.wait_ge(scaled, 1)
                with pe.Fori(0, NCH) as c:
                    x = k.HT[:, bass.ds(c * bpc, bpc), PAD:PAD + T]
                    pe.wait_ge(out, c + 1)
                    for ob in range(KB):
                        for j in range(2):
                            i = nc.tensor.matmul(k.bank[KB * j + ob][:].rearrange("p (b t) -> p b t", b=bpc),
                                                 w[:, j * HID + ob * P:j * HID + (ob + 1) * P], x,
                                                 start=True, stop=True)
                        i.then_inc(pair, 1)
                    pe.wait_ge(prod, c * KB + KB)
                    for tt in range(CH // P):
                        for kb in range(KB):
                            i = nc.tensor.matmul(k.bank[6][:, tt * D:(tt + 1) * D], hid[:, kb, tt * P:(tt + 1) * P],
                                                 w[:, 2 * HID + kb * D:2 * HID + (kb + 1) * D],
                                                 start=kb == 0, stop=kb == KB - 1)
                    i.then_inc(down, 1)

            @block.scalar
            def _(act):
                with act.Fori(0, NCH) as c:
                    for ob in range(KB):
                        act.wait_ge(pair, c * KB + ob + 1)
                        nc.scalar.activation(gate[:, ob, :], k.bank[ob][:], ACT.Silu).then_inc(gated, 1)

            @block.vector
            def _(dve):
                dve.sem_inc(out, 1)
                dve.wait_ge(loaded, 32)
                nc.vector.tensor_scalar(w[:], wi[:], 1.0 / 127.0, None, ALU.mult).then_inc(scaled, 1)
                with dve.Fori(0, NCH) as c:
                    for ob in range(KB):
                        dve.wait_ge(gated, c * KB + ob + 1)
                        nc.vector.tensor_tensor(hid[:, ob, :], k.bank[KB + ob][:], gate[:, ob, :],
                                                ALU.mult).then_inc(prod, 1)
                    dve.wait_ge(down, c + 1)
                    nc.vector.tensor_copy(k.Y[:, bass.ds(c * (CH // P), CH // P), :],
                                          k.bank[6][:].rearrange("p (t d) -> p t d", d=D)).then_inc(out, 1)


def ffn_experts(k):
    nc, E, TOPK, EPS, THRES = k.nc, 8, 2, 1e-4, 0.1
    with Part(k) as p:
        gw, gb = p.sb("gate_w", [P, E]), p.sb("gate_b", [P, E])
        ew, eb = p.sb("expert_w", [P, E * D]), p.sb("expert_b", [1, E * D])
        iota, ones = p.sb("iota", [P, E]), p.sb("ones", [1, P])
        xb = p.sb("x_batch", [P, 2, T])
        S, M, W, V = (p.sb(n, [P, NT, E]) for n in ("score", "mask", "weight", "tmp"))
        r = p.sb("row", [P, NT])
        loaded, xb_ready = p.sem("loaded"), p.sem("xb_ready")
        gates, exped, clipped = p.sem("gates"), p.sem("exped"), p.sem("clipped")
        experts, mixed, ones_ready = p.sem("experts"), p.sem("mixed"), p.sem("ones")
        sc3 = k.bank[0][:, 0:NT * E].rearrange("p (t e) -> p t e", e=E)
        with nc.Block() as block:
            @block.sync
            def _(sp):
                sp.dma_start(gw[:], k.dram["l2f_gw"]).then_inc(loaded, 16)
                sp.dma_start(gb[:], k.dram["l2f_gb"].partition_broadcast(P)).then_inc(loaded, 16)
                sp.dma_start(ew[:], k.dram["l2f_ew"]).then_inc(loaded, 16)
                sp.dma_start(eb[:], k.dram["l2f_eb"]).then_inc(loaded, 16)
                sp.dma_start(iota[:], k.dram["iota8"].partition_broadcast(P)).then_inc(loaded, 16)

            @block.gpsimd
            def _(pool):
                nc.gpsimd.memset(ones[:], 1.0).then_inc(ones_ready, 1)

            @block.tensor
            def _(pe):
                pe.wait_ge(loaded, 80)
                pe.wait_ge(ones_ready, 1)
                for t in range(NT):
                    i = nc.tensor.matmul(sc3[:, t, :], k.HT[:, t // TPB, PAD + t % TPB * P:PAD + (t % TPB + 1) * P],
                                         gw[:], start=True, stop=True)
                i.then_inc(gates, 1)
                with pe.Fori(0, B // 2) as bb:
                    pe.wait_ge(xb_ready, bb + 1)
                    for s in range(2):
                        for t in range(TPB):
                            u = 2 * s + t
                            pe.wait_ge(mixed, bb * 4 + u + 1)
                            for h in range(2):
                                o = k.bank[2 * u + h][:]
                                nc.tensor.matmul(o, ones[:], eb[:, h * 512:(h + 1) * 512], start=True, stop=False)
                                i = nc.tensor.matmul(o, xb[:, s, t * P:(t + 1) * P], ew[:, h * 512:(h + 1) * 512],
                                                     start=False, stop=True)
                            i.then_inc(experts, 1)

            @block.scalar
            def _(act):
                act.wait_ge(clipped, 1)
                nc.scalar.activation(W[:], S[:], ACT.Exp).then_inc(exped, 1)

            @block.vector
            def _(dve):
                v = nc.vector
                dve.sem_inc(mixed, 4)
                dve.wait_ge(loaded, 80)
                dve.wait_ge(gates, 1)
                v.tensor_tensor(S[:], sc3, across(gb[:], NT), ALU.add)
                dve.drain()
                v.tensor_scalar_max(S[:], S[:], EPS)
                dve.drain()
                v.tensor_reduce(r[:], S[:], AXX, ALU.max)
                dve.drain()
                v.tensor_tensor(S[:], S[:], over(r[:], E), ALU.subtract).then_inc(clipped, 1)
                dve.wait_ge(exped, 1)
                v.tensor_reduce(r[:], W[:], AXX, ALU.add)
                dve.drain()
                v.reciprocal(r[:], r[:])
                dve.drain()
                v.tensor_tensor(W[:], W[:], over(r[:], E), ALU.mult)
                dve.drain()
                v.tensor_copy(S[:], W[:])
                v.memset(M[:], 0.0)
                for _ in range(TOPK):
                    dve.drain()
                    v.tensor_reduce(r[:], S[:], AXX, ALU.max)
                    dve.drain()
                    v.tensor_tensor(V[:], S[:], over(r[:], E), ALU.is_equal)
                    dve.drain()
                    v.scalar_tensor_tensor(out=V[:], in0=V[:], scalar=-100.0, in1=across(iota[:], NT),
                                           op0=ALU.mult, op1=ALU.add)
                    dve.drain()
                    v.tensor_reduce(r[:], V[:], AXX, ALU.min)
                    dve.drain()
                    v.tensor_tensor(V[:], V[:], over(r[:], E), ALU.is_equal)
                    dve.drain()
                    v.tensor_add(M[:], M[:], V[:])
                    v.scalar_tensor_tensor(out=S[:], in0=V[:], scalar=-2.0, in1=S[:], op0=ALU.mult, op1=ALU.add)
                dve.drain()
                v.scalar_tensor_tensor(out=W[:], in0=W[:], scalar=THRES, in1=M[:], op0=ALU.max, op1=ALU.mult)
                dve.drain()
                v.tensor_reduce(r[:], W[:], AXX, ALU.add)
                dve.drain()
                v.reciprocal(r[:], r[:])
                dve.drain()
                v.scalar_tensor_tensor(out=W[:], in0=W[:], scalar=1.0 / TOPK, in1=over(r[:], E),
                                       op0=ALU.mult, op1=ALU.mult)
                dve.drain()
                with dve.Fori(0, B // 2) as bb:
                    v.tensor_copy(xb[:], k.HT[:, bass.ds(bb * 2, 2), PAD:PAD + T]).then_inc(xb_ready, 1)
                    for s in range(2):
                        for t in range(TPB):
                            u = 2 * s + t
                            dve.wait_ge(experts, bb * 4 + u + 1)
                            y = k.Y[:, bb * 4 + u, :]
                            for e in range(E):
                                o = k.bank[2 * u + e // 4][:, e % 4 * D:(e % 4 + 1) * D]
                                c = W[:, bb * 4 + u, e:e + 1]
                                if e == 0:
                                    i = v.tensor_scalar(y, o, c, None, ALU.mult)
                                else:
                                    i = v.scalar_tensor_tensor(out=y, in0=o, scalar=c, in1=y,
                                                               op0=ALU.mult, op1=ALU.add)
                                if e < E - 1:
                                    dve.drain()
                            i.then_inc(mixed, 1)


def lay_out_flash(i, d, np):
    for n in "qkv":
        d[f"l2a_w{n}"] = i[f"L2_attn_W{n}"]
    d["l2a_wo"] = by_blocks(i["L2_attn_Wo"])
    d["l2a_forget"] = np.tile(np.array([-3e38, 0, 0, 0], np.float32), 4)
    d["l2a_keep"] = np.tile(np.array([0, 1, 1, 1], np.float32), 4)


def flash_attn(k):
    nc, H, DK, NJ = k.nc, 16, 64, 4
    C = H * DK
    CB = C // P
    HG = 4
    units = [(g, t) for g in range(H // HG) for t in range(TPB)]
    NU = len(units)
    with Part(k) as p:
        w = {n: p.sb("w" + n, [P, C]) for n in "qkv"}
        wo = p.sb("wo", [P, CB, D])
        forget, keep = p.sb("forget", [P, 16]), p.sb("keep", [P, 16])
        xb = p.sb("x_batch", [P, T])
        qk = p.sb("qk_featmajor", [P, 2, CB, T])
        v = p.sb("v", [P, TPB, C])
        S = p.sb("probs", [P, 2, HG, T])
        SW = p.sb("weighted", [P, 2, HG, T])
        PT = p.sb("weighted_keymajor", [P, 2, HG * TPB, P])
        O = p.sb("heads_out", [P, TPB, C])
        OT = p.sb("heads_out_featmajor", [P, CB, T])
        bm, m, al, ls, rs, f = (p.sb(n, [P, 2, 16]) for n in ("bm", "m", "alpha", "l", "rowsum", "f"))
        loaded, xb_ready = p.sem("loaded"), p.sem("xb_ready")
        proj, proj_act, proj_dve = p.sem("proj"), p.sem("proj_act"), p.sem("proj_dve")
        scores, shifted, exped = p.sem("scores"), p.sem("shifted"), p.sem("exped")
        w_ready, weighted, turned, pt_ready = p.sem("w_ready"), p.sem("weighted"), p.sem("turned"), p.sem("pt_ready")
        heads, heads_out = p.sem("heads"), p.sem("heads_out")
        o_turned, ot_act, ot_dve, final, done = p.sem("o_turned"), p.sem("ot_act"), p.sem("ot_dve"), p.sem("final"), p.sem("done")

        qk_flat = qk[:].rearrange("p a c t -> p (a c t)")
        v_flat = v[:].rearrange("p a c -> p (a c)")
        dest = [qk_flat[:, n * 512:(n + 1) * 512] for n in range(8)] + \
               [v_flat[:, n * 512:(n + 1) * 512] for n in range(4)]

        def project(pe, b):
            pe.wait_ge(xb_ready, b + 1)
            for n in range(12):
                o = k.bank[n % 6][:]
                if n >= 6:
                    sem = proj_act if n % 2 == 0 else proj_dve
                    pe.wait_ge(sem, b * 6 + (n - 6) // 2 + 1)
                if n < 8:
                    for h in range(2):
                        c = n % 4 * 2 + h
                        i = nc.tensor.matmul(o[:, h * T:(h + 1) * T], w["qk"[n // 4]][:, c * P:(c + 1) * P], xb[:],
                                             start=True, stop=True)
                else:
                    t, h = (n - 8) // 2, (n - 8) % 2
                    i = nc.tensor.matmul(o, xb[:, t * P:(t + 1) * P], w["v"][:, h * 512:(h + 1) * 512],
                                         start=True, stop=True)
                i.then_inc(proj, 1)
            pe.wait_ge(proj_act, b * 6 + 6)
            pe.wait_ge(proj_dve, b * 6 + 6)

        with nc.Block() as block:
            @block.sync
            def _(sp):
                for n in "qkv":
                    sp.dma_start(w[n][:], k.dram[f"l2a_w{n}"]).then_inc(loaded, 16)
                sp.dma_start(forget[:], k.dram["l2a_forget"].partition_broadcast(P)).then_inc(loaded, 16)
                sp.dma_start(keep[:], k.dram["l2a_keep"].partition_broadcast(P)).then_inc(loaded, 16)
                sp.dma_start(wo[:], k.dram["l2a_wo"]).then_inc(loaded, 16)

            @block.tensor
            def _(pe):
                pe.wait_ge(loaded, 96)

                def score(b, u):
                    g, t = units[u]
                    s = u % 2
                    pe.wait_ge(shifted, b * NU + u + 1)
                    for h in range(HG):
                        c, r = (g * HG + h) // 2, (g * HG + h) % 2 * DK
                        i = nc.tensor.matmul(k.bank[2 * s + h % 2][:, h // 2 * T:(h // 2 + 1) * T],
                                             qk[r:r + DK, 0, c, t * P:(t + 1) * P], qk[r:r + DK, 1, c, :],
                                             start=True, stop=True)
                    i.then_inc(scores, 1)

                def turn(b, u):
                    s = u % 2
                    pe.wait_ge(weighted, b * NU + u + 1)
                    pe.wait_ge(pt_ready, b * NU + u + 1)
                    for h in range(HG):
                        for kt in range(TPB):
                            n = h * TPB + kt
                            i = nc.tensor.transpose(k.bank[4 + n // 4][:, n % 4 * P:(n % 4 + 1) * P],
                                                    SW[:, s, h, kt * P:(kt + 1) * P], k.ident[:])
                    i.then_inc(turned, 1)

                def values(b, u):
                    g, t = units[u]
                    s = u % 2
                    pe.wait_ge(pt_ready, b * NU + u + 2)
                    pe.wait_ge(heads_out, b * NU + u + 1)
                    for h in range(HG):
                        hd = g * HG + h
                        at = h % 2 * 2 + h // 2
                        for kt in range(TPB):
                            i = nc.tensor.matmul(k.bank[6][:, h * DK:(h + 1) * DK], PT[:, s, at * TPB + kt, :],
                                                 v[:, kt, hd * DK:(hd + 1) * DK], start=kt == 0, stop=kt == TPB - 1)
                    i.then_inc(heads, 1)

                with pe.Fori(0, B) as b:
                    project(pe, b)
                    score(b, 0)
                    for u in range(NU):
                        if u + 1 < NU:
                            score(b, u + 1)
                        turn(b, u)
                        values(b, u)
                    pe.wait_ge(heads_out, b * NU + NU + 1)
                    for c in range(CB):
                        for t in range(TPB):
                            n = c * TPB + t
                            i = nc.tensor.transpose(k.bank[n // 4][:, n % 4 * P:(n % 4 + 1) * P],
                                                    O[:, t, c * P:(c + 1) * P], k.ident[:])
                            if n % 4 == 3:
                                i.then_inc(o_turned, 1)
                    pe.wait_ge(ot_act, b * 2 + 2)
                    pe.wait_ge(ot_dve, b * 2 + 2)
                    for t in range(TPB):
                        for c in range(CB):
                            i = nc.tensor.matmul(k.bank[6][:, t * D:(t + 1) * D], OT[:, c, t * P:(t + 1) * P],
                                                 wo[:, c, :], start=c == 0, stop=c == CB - 1)
                    i.then_inc(final, 1)

            @block.scalar
            def _(act):
                act.sem_inc(pt_ready, 1)
                act.sem_inc(heads_out, 1)

                def evacuate(b, u):
                    s = u % 2
                    act.wait_ge(turned, b * NU + u + 1)
                    for h in range(2):
                        i = nc.scalar.activation(PT[:, s, 4 * h:4 * h + 4, :],
                                                 k.bank[4 + h][:].rearrange("p (a q) -> p a q", q=P), ACT.Copy)
                    i.then_inc(pt_ready, 1)

                def out(b, u):
                    g, t = units[u]
                    act.wait_ge(heads, b * NU + u + 1)
                    nc.scalar.activation(O[:, t, g * HG * DK:(g + 1) * HG * DK], k.bank[6][:, 0:HG * DK],
                                         ACT.Copy).then_inc(heads_out, 1)

                with act.Fori(0, B) as b:
                    for n in range(0, 12, 2):
                        act.wait_ge(proj, b * 12 + n + 1)
                        nc.scalar.activation(dest[n], k.bank[n % 6][:], ACT.Copy).then_inc(proj_act, 1)
                    for u in range(NU):
                        s = u % 2
                        act.wait_ge(shifted, b * NU + u + 3)
                        nc.scalar.activation(al[:, s, :], al[:, s, :], ACT.Exp, scale=DK ** -0.5)
                        nc.scalar.activation(S[:, s], S[:, s], ACT.Exp, scale=DK ** -0.5).then_inc(exped, 1)
                        if u > 0:
                            evacuate(b, u - 1)
                            out(b, u - 1)
                    evacuate(b, NU - 1)
                    out(b, NU - 1)
                    for n in range(0, 4, 2):
                        act.wait_ge(o_turned, b * 4 + n + 1)
                        nc.scalar.activation(OT[:, 2 * n:2 * n + 2, :], k.bank[n][:].rearrange("p (c t) -> p c t", t=T),
                                             ACT.Copy).then_inc(ot_act, 1)

            @block.gpsimd
            def _(pool):
                with pool.Fori(0, B) as b:
                    for u in range(NU):
                        s = u % 2
                        pool.wait_ge(w_ready, b * NU + u + 1)
                        nc.gpsimd.tensor_tensor(SW[:, s].rearrange("p h (j t) -> p (h j) t", j=NJ),
                                                S[:, s].rearrange("p h (j t) -> p (h j) t", j=NJ),
                                                over(f[:, s, :], T // NJ), ALU.mult).then_inc(weighted, 1)

            @block.vector
            def _(dve):
                vv = nc.vector
                dve.sem_inc(shifted, 2)
                dve.wait_ge(loaded, 96)

                def shift(b, u):
                    s = u % 2
                    dve.wait_ge(scores, b * NU + u + 1)
                    for h in range(2):
                        vv.tensor_reduce(bm[:, s, 8 * h:8 * h + 8], k.bank[2 * s + h][:].rearrange("p (a t) -> p a t", a=8),
                                         AXX, ALU.max)
                    dve.drain()
                    vv.tensor_tensor_scan(m[:, s, :], forget[:], bm[:, s, :], 0.0, ALU.add, ALU.max)
                    dve.drain()
                    vv.tensor_tensor(al[:, s, 1:16], m[:, s, 0:15], m[:, s, 1:16], ALU.subtract)
                    dve.drain()
                    vv.memset(al[:, s, 0:1], 0.0)
                    dve.drain()
                    vv.tensor_tensor(al[:, s, :], al[:, s, :], keep[:], ALU.mult)
                    if u >= 2:
                        dve.wait_ge(weighted, b * NU + u - 1)
                    for h in range(2):
                        i = vv.tensor_tensor(S[:, s, 2 * h:2 * h + 2, :].rearrange("p h (j t) -> p (h j) t", j=NJ),
                                             k.bank[2 * s + h][:].rearrange("p (a t) -> p a t", a=8),
                                             over(m[:, s, 8 * h:8 * h + 8], T // NJ), ALU.subtract)
                    i.then_inc(shifted, 1)

                def weigh(b, u):
                    s = u % 2
                    dve.wait_ge(exped, b * NU + u + 1)
                    vv.tensor_reduce(rs[:, s, :], S[:, s].rearrange("p h (j t) -> p (h j) t", j=NJ), AXX, ALU.add)
                    vv.tensor_tensor(al[:, s, :], al[:, s, :], keep[:], ALU.mult)
                    dve.drain()
                    vv.tensor_tensor_scan(ls[:, s, :], al[:, s, :], rs[:, s, :], 0.0, ALU.mult, ALU.add)
                    dve.drain()
                    vv.reciprocal(f[:, s, :], ls[:, s, :])
                    dve.drain()
                    f4 = f[:, s, :].rearrange("p (h j) -> p h j", j=NJ)
                    a4 = al[:, s, :].rearrange("p (h j) -> p h j", j=NJ)
                    vv.tensor_tensor(f4[:, :, 0:3], f4[:, :, 0:3], a4[:, :, 1:4], ALU.mult)
                    for j in (2, 1, 0):
                        dve.drain()
                        i = vv.tensor_tensor(f4[:, :, j], f4[:, :, j], f4[:, :, j + 1], ALU.mult)
                    i.then_inc(w_ready, 1)

                with dve.Fori(0, B) as b:
                    vv.tensor_copy(xb[:], k.HT[:, bass.ds(b, 1), PAD:PAD + T].rearrange("p a t -> p (a t)")).then_inc(xb_ready, 1)
                    for n in range(1, 12, 2):
                        dve.wait_ge(proj, b * 12 + n + 1)
                        vv.tensor_copy(dest[n], k.bank[n % 6][:]).then_inc(proj_dve, 1)
                    shift(b, 0)
                    for u in range(NU):
                        if u + 1 < NU:
                            shift(b, u + 1)
                        weigh(b, u)
                    for n in range(1, 4, 2):
                        dve.wait_ge(o_turned, b * 4 + n + 1)
                        vv.tensor_copy(OT[:, 2 * n:2 * n + 2, :],
                                       k.bank[n][:].rearrange("p (c t) -> p c t", t=T)).then_inc(ot_dve, 1)
                    dve.wait_ge(final, b + 1)
                    vv.tensor_copy(k.Y[:, bass.ds(b * TPB, TPB), :],
                                   k.bank[6][:, 0:TPB * D].rearrange("p (t d) -> p t d", d=D)).then_inc(done, 1)


def lay_out_plucker(i, d, np):
    wq = [i["L1_attn_W1_q"].T, i["L1_attn_W2_q"].T]
    d["l1a_wx"] = np.concatenate([wq[0][:D], wq[1][:D], i["L1_attn_W1_k"].T, i["L1_attn_W2_k"].T,
                                  i["L1_attn_Wv"].T], 1)
    d["l1a_wprev"] = np.concatenate([wq[0][D:], wq[1][D:]], 1)
    d["l1a_wo"] = i["L1_attn_Wo"].T
    d["l1a_bias"] = np.stack([i["L1_attn_bv"], i["L1_attn_bo"]])
    d["causal"] = np.triu(np.ones((P, P), np.float32))


def plucker_attn(k):
    nc, H, LC = k.nc, 16, 6
    DH, SLOT = D // H, 32
    G = H // 4
    PAIRS = [(0, slice(1, 4), slice(0, 3)), (1, slice(2, 4), slice(3, 5)), (2, slice(3, 4), slice(5, 6))]
    JSIGN = [1.0, -1.0, 1.0, 1.0, -1.0, 1.0]
    with Part(k) as p:
        wx, wprev, wo = p.sb("wx", [P, 4 * 64 + D]), p.sb("wprev", [P, 2 * 64]), p.sb("wo", [P, D])
        bias = p.sb("bias", [P, 2, D])
        causal = p.sb("causal", [P, P])
        xb = p.sb("x_batch", [P, 1 + T])
        pts = p.sb("points", [P, TPB, 2, 2, H, 4])
        v = p.sb("v_and_one", [P, TPB, H, DH + 1])
        ln, ln2 = p.sb("lines", [P, TPB * 2, H, LC]), p.sb("lines2", [P, TPB * 2, H, LC])
        nrm, half = p.sb("norms", [P, TPB * 2, H]), p.sb("minus_half", [P, TPB * 2, H])
        qk = p.sb("lines_padded", [P, 2, TPB, H, SLOT])
        qkT = p.sb("lines_featmajor", [P, 2, G, T])
        E = p.sb("probs", [P, 2, 4, T + P])
        rsum = p.sb("rsum", [P, TPB, H])
        O = p.sb("heads_out", [P, TPB, H, DH])
        OT = p.sb("heads_out_featmajor", [P, T])
        loaded, xb_ready, proj, pts_ready = p.sem("loaded"), p.sem("xb_ready"), p.sem("proj"), p.sem("pts_ready")
        sq_ready, norm_ready, lines_ready = p.sem("sq_ready"), p.sem("norm_ready"), p.sem("lines_ready")
        turned, t_act, t_dve = p.sem("turned"), p.sem("t_act"), p.sem("t_dve")
        scores, exped, masked, heads = p.sem("scores"), p.sem("exped"), p.sem("masked"), p.sem("heads")
        o_ready, o_turned, ot_ready, final, done = (p.sem(n) for n in ("o_ready", "o_turned", "ot_ready", "final", "done"))
        zeroed = p.sem("zeroed")
        oview = k.bank[6][:, 0:TPB * H * (DH + 1)].rearrange("p (t h c) -> p t h c", t=TPB, h=H)
        with nc.Block() as block:
            @block.sync
            def _(sp):
                sp.dma_start(wx[:], k.dram["l1a_wx"]).then_inc(loaded, 16)
                sp.dma_start(wprev[:], k.dram["l1a_wprev"]).then_inc(loaded, 16)
                sp.dma_start(wo[:], k.dram["l1a_wo"]).then_inc(loaded, 16)
                sp.dma_start(bias[:], k.dram["l1a_bias"].partition_broadcast(P)).then_inc(loaded, 16)
                sp.dma_start(causal[:], k.dram["causal"]).then_inc(loaded, 16)

            @block.tensor
            def _(pe):
                pe.wait_ge(loaded, 80)

                def out_of(pe, b, g):
                    s = g % 2
                    pe.wait_ge(masked, b * G + g + 1)
                    for r in range(4):
                        h = 4 * g + r
                        nc.tensor.matmul(oview[:, 0, h, :], E[:, s, r, 0:P], v[:, 0, h, :], start=True, stop=True)
                        nc.tensor.matmul(oview[:, 1, h, :], E[:, s, r, P:2 * P], v[:, 0, h, :], start=True, stop=False)
                        i = nc.tensor.matmul(oview[:, 1, h, :], E[:, s, r, T:T + P], v[:, 1, h, :], start=False, stop=True)
                    i.then_inc(heads, 1)

                with pe.Fori(0, B) as b:
                    pe.wait_ge(xb_ready, b + 1)
                    for t in range(TPB):
                        o = k.bank[4 + t]
                        nc.tensor.matmul(o[:, 0:384], xb[:, 1 + t * P:1 + (t + 1) * P], wx[:], start=True, stop=False)
                        i = nc.tensor.matmul(o[:, 0:128], xb[:, t * P:(t + 1) * P], wprev[:], start=False, stop=True)
                    i.then_inc(proj, 1)
                    pe.wait_ge(lines_ready, b + 1)
                    for n in range(4):
                        for g in range(G):
                            i = nc.tensor.transpose(k.bank[n][:, g * P:(g + 1) * P],
                                                    qk[:, n // 2, n % 2, 4 * g:4 * g + 4, :].rearrange("p h c -> p (h c)"),
                                                    k.ident[:])
                        i.then_inc(turned, 1)
                    pe.wait_ge(t_act, b * 2 + 2)
                    pe.wait_ge(t_dve, b * 2 + 2)
                    for g in range(G):
                        if g > 0:
                            pe.wait_ge(exped, b * G + g)
                        for kt in range(TPB):
                            for r in range(4):
                                rows = slice(SLOT * r, SLOT * (r + 1))
                                i = nc.tensor.matmul(k.bank[r][:, kt * T:kt * T + (T - kt * P)],
                                                     qkT[rows, 1, g, kt * P:(kt + 1) * P], qkT[rows, 0, g, kt * P:T],
                                                     start=True, stop=True)
                        i.then_inc(scores, 1)
                        if g > 0:
                            out_of(pe, b, g - 1)
                    out_of(pe, b, G - 1)
                    pe.wait_ge(o_ready, b + 1)
                    for t in range(TPB):
                        i = nc.tensor.transpose(k.bank[7][:, t * P:(t + 1) * P],
                                                O[:, t].rearrange("p h c -> p (h c)"), k.ident[:])
                    i.then_inc(o_turned, 1)
                    pe.wait_ge(ot_ready, b + 1)
                    for t in range(TPB):
                        i = nc.tensor.matmul(k.bank[7][:, 256 + t * D:256 + (t + 1) * D], OT[:, t * P:(t + 1) * P], wo[:],
                                             start=True, stop=True)
                    i.then_inc(final, 1)

            @block.scalar
            def _(act):
                with act.Fori(0, B) as b:
                    for n in (0, 2):
                        act.wait_ge(turned, b * 4 + n + 1)
                        nc.scalar.activation(qkT[:, n // 2, :, 0:P], k.bank[n].rearrange("p (g t) -> p g t", g=G),
                                             ACT.Copy).then_inc(t_act, 1)
                    for g in range(G):
                        s = g % 2
                        act.wait_ge(scores, b * G + g + 1)
                        if g > 1:
                            act.wait_ge(heads, b * G + g - 1)
                        nc.scalar.activation(E[:, s], k.banks[:, 0:4, 0:T + P], ACT.Exp, scale=LC ** -0.5).then_inc(exped, 1)
                    act.wait_ge(o_turned, b + 1)
                    nc.scalar.activation(OT[:], k.bank[7][:, 0:T], ACT.Copy).then_inc(ot_ready, 1)

            @block.gpsimd
            def _(pool):
                nc.gpsimd.memset(half[:], -0.5)
                nc.gpsimd.memset(qk[:], 0.0)
                nc.gpsimd.memset(v[:], 1.0).then_inc(zeroed, 1)
                pool.wait_ge(loaded, 80)
                pool.drain()
                with pool.Fori(0, B) as b:
                    pool.wait_ge(sq_ready, b + 1)
                    nc.gpsimd.tensor_tensor(nrm[:], nrm[:], half[:], ALU.pow).then_inc(norm_ready, 1)
                    for g in range(G):
                        s = g % 2
                        pool.wait_ge(exped, b * G + g + 1)
                        for c in (0, T):
                            i = nc.gpsimd.tensor_tensor(E[:, s, :, c:c + P], E[:, s, :, c:c + P], across(causal[:], 4),
                                                        ALU.mult)
                        i.then_inc(masked, 1)

            @block.vector
            def _(dve):
                vv = nc.vector
                dve.wait_ge(loaded, 80)
                dve.wait_ge(zeroed, 1)
                with dve.Fori(0, B) as b:
                    vv.tensor_copy(xb[:], k.HT[:, bass.ds(b, 1), PAD - 1:PAD + T].rearrange("p a t -> p (a t)")).then_inc(xb_ready, 1)
                    dve.wait_ge(proj, b + 1)
                    for t in range(TPB):
                        vv.tensor_copy(pts[:, t].rearrange("p a b h c -> p (a b h c)"), k.bank[4 + t][:, 0:256])
                        vv.tensor_tensor(v[:, t, :, 0:DH], k.bank[4 + t][:, 256:384].rearrange("p (h c) -> p h c", h=H),
                                         bias[:, 0, :].rearrange("p (h c) -> p h c", h=H), ALU.add)
                    dve.drain()
                    pv = pts[:].rearrange("p t a b h c -> p (t a) b h c")
                    for i0, js, cs in PAIRS:
                        n = js.stop - js.start
                        one = [pv[:, :, a, :, i0:i0 + 1].to_broadcast([P, 4, H, n]) for a in range(2)]
                        many = [pv[:, :, a, :, js] for a in range(2)]
                        vv.tensor_tensor(ln[:, :, :, cs], one[0], many[1], ALU.mult)
                        vv.tensor_tensor(ln2[:, :, :, cs], one[1], many[0], ALU.mult)
                    dve.drain()
                    vv.tensor_tensor(ln[:], ln[:], ln2[:], ALU.subtract)
                    dve.drain()
                    vv.tensor_tensor(ln2[:], ln[:], ln[:], ALU.mult)
                    dve.drain()
                    vv.tensor_reduce(nrm[:], ln2[:], AXX, ALU.add)
                    dve.drain()
                    vv.tensor_scalar_max(nrm[:], nrm[:], 1e-24).then_inc(sq_ready, 1)
                    dve.wait_ge(norm_ready, b + 1)
                    lq = ln[:].rearrange("p (t a) h c -> p t a h c", a=2)
                    nq = nrm[:].rearrange("p (t a) h -> p t a h", a=2)
                    for t in range(TPB):
                        vv.tensor_tensor(qk[:, 0, t, :, 0:LC], lq[:, t, 0], over(nq[:, t, 0, :], LC), ALU.mult)
                    for c in range(LC):
                        i = vv.scalar_tensor_tensor(out=qk[:, 1, :, :, c], in0=lq[:, :, 1, :, 5 - c], scalar=JSIGN[c],
                                                    in1=nq[:, :, 1, :], op0=ALU.mult, op1=ALU.mult)
                    i.then_inc(lines_ready, 1)
                    for n in (1, 3):
                        dve.wait_ge(turned, b * 4 + n + 1)
                        vv.tensor_copy(qkT[:, n // 2, :, P:T], k.bank[n].rearrange("p (g t) -> p g t", g=G)).then_inc(t_dve, 1)
                    dve.wait_ge(heads, b * G + G)
                    vv.reciprocal(rsum[:], oview[:, :, :, DH])
                    dve.drain()
                    for t in range(TPB):
                        i = vv.tensor_tensor(O[:, t], oview[:, t, :, 0:DH], over(rsum[:, t, :], DH), ALU.mult)
                    i.then_inc(o_ready, 1)
                    dve.wait_ge(final, b + 1)
                    vv.tensor_tensor(k.Y[:, bass.ds(b * TPB, TPB), :], k.bank[7][:, 256:512].rearrange("p (t d) -> p t d", d=D),
                                     across(bias[:, 1, :], TPB), ALU.add).then_inc(done, 1)


def lay_out_window(i, d, np):
    half = 32
    swap = lambda a: np.concatenate([a[..., half:], a[..., :half]], -1)
    HID = 341
    for l in range(2):
        d[f"l0f_wqkv{l}"] = i["L0_ffn_wqkv"][l]
        qk = np.stack([i["L0_ffn_q_scale"][l], i["L0_ffn_k_scale"][l]])
        d[f"l0f_qks{l}"] = np.stack([qk, swap(qk)], 1)
        d[f"l0f_wo{l}"] = by_blocks(i["L0_ffn_wo"][l])
        d[f"l0f_ln{l}"] = np.stack([i["L0_ffn_ln_g"][l], i["L0_ffn_ln_b"][l]])
        pad = lambda a: np.concatenate([a, np.zeros((3 * P - HID,) + a.shape[1:], a.dtype)])
        w1, b1 = i["L0_ffn_w1"][l], i["L0_ffn_b1"][l]
        d[f"l0f_w1{l}"] = np.stack([pad(w1[:, n * HID:(n + 1) * HID].T).T for n in range(2)], 1)
        d[f"l0f_b1{l}"] = np.stack([pad(b1[n * HID:(n + 1) * HID]).reshape(3, P).T for n in range(2)], 1)
        d[f"l0f_w2{l}"] = by_blocks(pad(i["L0_ffn_w2"][l]))
        d[f"l0f_b2{l}"] = i["L0_ffn_b2"][l]
    hi = np.arange(0, 64, 2, dtype=np.float32)
    inv = (np.float32(1.0) / np.float32(10000.0) ** (hi / np.float32(64))).astype(np.float32)
    t = np.arange(T, dtype=np.float32)
    fr = (t[:, None] * inv[None, :]).astype(np.float32)
    base = ((hi + np.float32(0.4 * 64)) / np.float32(1.4 * 64)).astype(np.float32)
    power = ((t - T // 2) / np.float32(32.0)).astype(np.float32)
    sc = (base[None, :] ** power[:, None]).astype(np.float32)
    tw = lambda a: np.concatenate([a, a], -1)
    cos, sin, sc = tw(np.cos(fr)), tw(np.sin(fr)), tw(sc)
    sin[:, :half] *= -1
    tab = np.stack([cos * sc, sin * sc, cos / sc, sin / sc], 1).reshape(T, 2, 2, 64)
    d["l0f_rot"] = tab.reshape(TPB, P, 2, 2, 64).transpose(1, 0, 2, 3, 4)
    q, j0, j1 = np.arange(P), np.arange(P), np.arange(64, 256)
    ok = lambda q, j: (q[:, None] >= j[None, :]) & (q[:, None] <= j[None, :] + 64)
    band = np.concatenate([ok(q, j0), ok(q + P, j1)], 1)
    d["l0f_band"] = np.where(band, 0.0, -1e30).astype(np.float32)
    d["l0f_shift"] = np.stack([np.eye(P, k=1, dtype=np.float32), np.zeros((P, P), np.float32)], 1)
    d["l0f_shift"][P - 1, 1, 0] = 1.0


def window_attn(k):
    nc = k.nc
    with Part(k) as p:
        with nc.Block() as block:
            @block.vector
            def _(dve):
                nc.vector.tensor_copy(k.Y[:], k.H[:])
    for l in range(2):
        if l:
            normalise(k, src=k.Y, norm=False)
        window_attention_layer(k, l)
        with Part(k) as p:
            shifted = p.sb("shifted", [P, NT, D])
            affine = p.sb("affine", [P, 2, D])
            shift_tokens(k, p, shifted, affine, l)
            normalise(k, src=shifted, affine=affine)
        window_ffn_layer(k, l)


def shift_tokens(k, p, shifted, affine, l):
    nc, HALF = k.nc, D // 2
    mats = p.sb("shift", [P, 2, P])
    loaded, moved = p.sem("loaded"), p.sem("moved")
    with nc.Block() as block:
        @block.sync
        def _(sp):
            sp.dma_start(mats[:], k.dram["l0f_shift"]).then_inc(loaded, 16)
            sp.dma_start(affine[:], k.dram[f"l0f_ln{l}"].partition_broadcast(P)).then_inc(loaded, 16)
            sp.wait_ge(loaded, 32)

        @block.tensor
        def _(pe):
            pe.wait_ge(loaded, 32)
            for n in range(2):
                o = k.bank[n].rearrange("p (b t d) -> p b t d", t=TPB, d=HALF)
                y = k.Y[:, 8 * n:8 * n + 8, HALF:].rearrange("p (b t) d -> p b t d", t=TPB)
                nc.tensor.matmul(k.bank[n].rearrange("p (b d) -> p b d", d=HALF), mats[:, 0, :], k.Y[:, 8 * n:8 * n + 8, HALF:],
                                 start=True, stop=False)
                nc.tensor.matmul(o[:, :, 1, :], mats[:, 1, :], y[:, :, 0, :], start=False, stop=True).then_inc(moved, 1)

        @block.vector
        def _(dve):
            nc.vector.tensor_copy(shifted[:, :, 0:HALF], k.Y[:, :, 0:HALF])
            for n in range(2):
                dve.wait_ge(moved, n + 1)
                nc.vector.tensor_copy(shifted[:, 8 * n:8 * n + 8, HALF:], k.bank[n].rearrange("p (a d) -> p a d", d=HALF))


def window_attention_layer(k, l):
    nc, H, DK, HALF = k.nc, 8, 64, 32
    CB, HG, NU, W0, W1 = H * DK // P, 4, 2, P, 192
    with Part(k) as p:
        wqkv, wo = p.sb("wqkv", [P, 3 * 512]), p.sb("wo", [P, CB, D])
        qks, rot, tab = p.sb("qk_scales", [P, 2, 2, DK]), p.sb("rotary", [P, TPB, 2, 2, DK]), p.sb("table", [P, TPB, 2, 2, DK])
        band = p.sb("band", [P, W0 + W1])
        xb = p.sb("x_batch", [P, T])
        sq = p.sb("squares", [P, TPB, 2, 512])
        ss, half = p.sb("norms", [P, TPB, 2, H]), p.sb("minus_half", [P, TPB * 2 * H])
        qn, qr, qk = (p.sb(n, [P, TPB, 2, H, DK]) for n in ("qk_normed", "qk_turned_part", "qk_rotated"))
        v = p.sb("v", [P, TPB, 512])
        qkT = p.sb("qk_featmajor", [P, 2, CB, T])
        S = p.sb("scores", [P, 2, HG, W0 + W1])
        E = p.sb("probs", [P, 2, HG, W0 + T])
        mx, rs = p.sb("rowmax", [P, 2, HG, TPB]), p.sb("rowsum", [P, 2, HG, TPB])
        ET = p.sb("probs_keymajor", [P, HG * 3, P])
        O = p.sb("heads_out", [P, TPB, 512])
        OT = p.sb("heads_out_featmajor", [P, CB, T])
        names = ("loaded", "zeroed", "xb_ready", "proj", "squared", "ss_ready", "norm_ready", "normed", "turned_part",
                 "rotated", "turned", "t_act", "t_dve", "scores", "maxed", "exped", "p_turned", "pt_act", "pt_dve", "heads",
                 "heads_out", "o_turned", "ot_ready", "final", "v_ready", "s_read")
        q = {n: p.sem(n) for n in names}
        hout = k.bank[7].rearrange("p (t h d) -> p t h d", t=TPB, h=HG)
        with nc.Block() as block:
            @block.sync
            def _(sp):
                sp.dma_start(wqkv[:], k.dram[f"l0f_wqkv{l}"]).then_inc(q["loaded"], 16)
                sp.dma_start(wo[:], k.dram[f"l0f_wo{l}"]).then_inc(q["loaded"], 16)
                sp.dma_start(qks[:], k.dram[f"l0f_qks{l}"].partition_broadcast(P)).then_inc(q["loaded"], 16)
                sp.dma_start(rot[:], k.dram["l0f_rot"]).then_inc(q["loaded"], 16)
                sp.dma_start(band[:], k.dram["l0f_band"]).then_inc(q["loaded"], 16)

            @block.tensor
            def _(pe):
                pe.wait_ge(q["loaded"], 80)

                def score(b, u):
                    for h in range(HG):
                        hd = HG * u + h
                        rows, c = slice(hd % 2 * DK, (hd % 2 + 1) * DK), hd // 2
                        nc.tensor.matmul(k.bank[h][:, 0:W0], qkT[rows, 0, c, 0:P], qkT[rows, 1, c, 0:P], start=True, stop=True)
                        nc.tensor.matmul(k.bank[h][:, W0:W0 + W1], qkT[rows, 0, c, P:T], qkT[rows, 1, c, DK:T],
                                         start=True, stop=True).then_inc(q["scores"], 1)

                def heads_of(b, u):
                    pe.wait_ge(q["exped"], b * NU + u + 1)
                    for n in range(HG * 3):
                        i = nc.tensor.transpose(k.bank[4 + n // 4][:, n % 4 * P:(n % 4 + 1) * P],
                                                E[:, u, n // 3, n % 3 * P:(n % 3 + 1) * P], k.ident[:])
                        if n % 4 == 3:
                            i.then_inc(q["p_turned"], 1)
                    pe.wait_ge(q["pt_act"], (b * NU + u) * 2 + 2)
                    pe.wait_ge(q["pt_dve"], b * NU + u + 1)
                    pe.wait_ge(q["heads_out"], b * NU + u + 1)
                    for h in range(HG):
                        vh = slice((HG * u + h) * DK, (HG * u + h + 1) * DK)
                        nc.tensor.matmul(hout[:, 0, h, :], ET[:, 3 * h, :], v[:, 0, vh], start=True, stop=True)
                        nc.tensor.matmul(hout[:, 1, h, :], ET[:, 3 * h + 1, :], v[:, 0, vh], start=True, stop=False)
                        i = nc.tensor.matmul(hout[:, 1, h, :], ET[:, 3 * h + 2, :], v[:, 1, vh], start=False, stop=True)
                    i.then_inc(q["heads"], 1)

                with pe.Fori(0, B) as b:
                    pe.wait_ge(q["xb_ready"], b + 1)
                    for t in range(TPB):
                        for n in range(3):
                            i = nc.tensor.matmul(k.bank[3 * t + n][:], xb[:, t * P:(t + 1) * P], wqkv[:, n * 512:(n + 1) * 512],
                                                 start=True, stop=True)
                    i.then_inc(q["proj"], 1)
                    pe.wait_ge(q["rotated"], b + 1)
                    pe.wait_ge(q["v_ready"], b + 1)
                    for n in range(4):
                        for c in range(CB):
                            i = nc.tensor.transpose(k.bank[n][:, c * P:(c + 1) * P],
                                                    qk[:, n % 2, n // 2].rearrange("p h d -> p (h d)")[:, c * P:(c + 1) * P],
                                                    k.ident[:])
                        i.then_inc(q["turned"], 1)
                    pe.wait_ge(q["t_act"], b * 2 + 2)
                    pe.wait_ge(q["t_dve"], b * 2 + 2)
                    score(b, 0)
                    pe.wait_ge(q["s_read"], b * NU + 1)
                    score(b, 1)
                    heads_of(b, 0)
                    heads_of(b, 1)
                    pe.wait_ge(q["heads_out"], b * NU + NU + 1)
                    for n in range(CB * TPB):
                        c, t = n // TPB, n % TPB
                        i = nc.tensor.transpose(k.bank[n // 4][:, n % 4 * P:(n % 4 + 1) * P], O[:, t, c * P:(c + 1) * P],
                                                k.ident[:])
                    i.then_inc(q["o_turned"], 1)
                    pe.wait_ge(q["ot_ready"], b + 1)
                    for t in range(TPB):
                        for c in range(CB):
                            i = nc.tensor.matmul(k.bank[2][:, t * D:(t + 1) * D], OT[:, c, t * P:(t + 1) * P], wo[:, c, :],
                                                 start=c == 0, stop=c == CB - 1)
                    i.then_inc(q["final"], 1)

            @block.scalar
            def _(act):
                with act.Fori(0, B) as b:
                    act.wait_ge(q["proj"], b + 1)
                    for t in range(TPB):
                        nc.scalar.activation(sq[:, t], k.banks[:, 3 * t:3 * t + 2, :], ACT.Square).then_inc(q["squared"], 1)
                    for t in range(TPB):
                        i = nc.scalar.activation(v[:, t], k.bank[3 * t + 2], ACT.Copy)
                    i.then_inc(q["v_ready"], 1)
                    for n in (0, 2):
                        act.wait_ge(q["turned"], b * 4 + n + 1)
                        nc.scalar.activation(qkT[:, n // 2, :, 0:P], k.bank[n].rearrange("p (c t) -> p c t", c=CB),
                                             ACT.Copy).then_inc(q["t_act"], 1)
                    for u in range(NU):
                        act.wait_ge(q["maxed"], b * NU + u + 1)
                        for h in range(HG):
                            for t in range(TPB):
                                src = S[:, u, h, 0:W0] if t == 0 else S[:, u, h, W0:]
                                dst = E[:, u, h, 0:W0] if t == 0 else E[:, u, h, W0 + T - W1:]
                                i = nc.scalar.activation(dst, src, ACT.Exp, scale=8.0, bias=mx[:, u, h, t:t + 1],
                                                         accum_out=rs[:, u, h, t:t + 1])
                        i.then_inc(q["exped"], 1)
                    for u in range(NU):
                        for n in (0, 1):
                            act.wait_ge(q["p_turned"], (b * NU + u) * 3 + n + 1)
                            nc.scalar.activation(ET[:, 4 * n:4 * n + 4, :], k.bank[4 + n].rearrange("p (a t) -> p a t", t=P),
                                                 ACT.Copy).then_inc(q["pt_act"], 1)
                    act.wait_ge(q["o_turned"], b + 1)
                    for n in range(2):
                        i = nc.scalar.activation(OT[:, 2 * n:2 * n + 2, :], k.bank[n].rearrange("p (c t) -> p c t", t=T), ACT.Copy)
                    i.then_inc(q["ot_ready"], 1)

            @block.gpsimd
            def _(pool):
                g = nc.gpsimd
                g.memset(half[:], -0.5)
                g.memset(E[:], 0.0).then_inc(q["zeroed"], 1)
                pool.wait_ge(q["loaded"], 80)
                for t in range(TPB):
                    for a in range(2):
                        g.tensor_tensor(tab[:, t, a], rot[:, t, a], qks[:, a], ALU.mult)
                pool.drain()
                with pool.Fori(0, B) as b:
                    pool.wait_ge(q["ss_ready"], b + 1)
                    flat = ss[:].rearrange("p t a h -> p (t a h)")
                    g.tensor_tensor(flat, flat, half[:], ALU.pow).then_inc(q["norm_ready"], 1)
                    for t in range(TPB):
                        pool.wait_ge(q["normed"], b * TPB + t + 1)
                        for a in range(2):
                            g.tensor_tensor(qk[:, t, a], qn[:, t, a], across(tab[:, t, a, 0, :], H), ALU.mult).then_inc(q["turned_part"], 1)

            @block.vector
            def _(dve):
                vv = nc.vector
                dve.sem_inc(q["heads_out"], 1)
                dve.wait_ge(q["zeroed"], 1)
                dve.wait_ge(q["loaded"], 80)
                with dve.Fori(0, B) as b:
                    x = lambda lo, at: k.HT[lo:lo + 64, bass.ds(b, 1), at:at + T].rearrange("p a t -> p (a t)")
                    vv.tensor_copy(xb[0:64, :], x(0, PAD))
                    vv.tensor_copy(xb[64:128, :], x(64, PAD - 1))
                    dve.drain()
                    vv.engine_nop().then_inc(q["xb_ready"], 1)
                    for t in range(TPB):
                        dve.wait_ge(q["squared"], b * TPB + t + 1)
                        vv.tensor_reduce(ss[:, t], sq[:, t].rearrange("p a (h d) -> p a h d", d=DK), AXX, ALU.add)
                    dve.drain()
                    vv.tensor_scalar_max(ss[:], ss[:], 1e-24).then_inc(q["ss_ready"], 1)
                    dve.wait_ge(q["norm_ready"], b + 1)
                    for t in range(TPB):
                        for a in range(2):
                            i = vv.tensor_tensor(qn[:, t, a], k.bank[3 * t + a].rearrange("p (h d) -> p h d", d=DK),
                                                 over(ss[:, t, a, :], DK), ALU.mult)
                        i.then_inc(q["normed"], 1)
                    dve.drain()
                    for t in range(TPB):
                        for a in range(2):
                            for lo in (0, HALF):
                                vv.tensor_tensor(qr[:, t, a, :, lo:lo + HALF], qn[:, t, a, :, HALF - lo:DK - lo],
                                                 across(tab[:, t, a, 1, lo:lo + HALF], H), ALU.mult)
                    dve.drain()
                    for t in range(TPB):
                        for a in range(2):
                            dve.wait_ge(q["turned_part"], (b * TPB + t) * 2 + a + 1)
                            i = vv.tensor_add(qk[:, t, a], qk[:, t, a], qr[:, t, a])
                    i.then_inc(q["rotated"], 1)
                    for n in (1, 3):
                        dve.wait_ge(q["turned"], b * 4 + n + 1)
                        vv.tensor_copy(qkT[:, n // 2, :, P:T], k.bank[n].rearrange("p (c t) -> p c t", c=CB)).then_inc(q["t_dve"], 1)
                    for u in range(NU):
                        for h in range(HG):
                            dve.wait_ge(q["scores"], (b * NU + u) * HG + h + 1)
                            i = vv.tensor_tensor(S[:, u, h, :], k.bank[h][:, 0:W0 + W1], band[:], ALU.add)
                        i.then_inc(q["s_read"], 1)
                        dve.drain()
                        vv.tensor_reduce(mx[:, u, :, 0], S[:, u, :, 0:W0], AXX, ALU.max)
                        vv.tensor_reduce(mx[:, u, :, 1], S[:, u, :, W0:], AXX, ALU.max)
                        dve.drain()
                        vv.tensor_scalar(mx[:, u], mx[:, u], -8.0, None, ALU.mult).then_inc(q["maxed"], 1)
                    for u in range(NU):
                        dve.wait_ge(q["p_turned"], (b * NU + u) * 3 + 3)
                        vv.tensor_copy(ET[:, 8:12, :], k.bank[6].rearrange("p (a t) -> p a t", t=P)).then_inc(q["pt_dve"], 1)
                        dve.wait_ge(q["heads"], b * NU + u + 1)
                        vv.reciprocal(rs[:, u], rs[:, u])
                        dve.drain()
                        for t in range(TPB):
                            i = vv.tensor_tensor(O[:, t, u * 256:(u + 1) * 256].rearrange("p (h d) -> p h d", d=DK),
                                                 hout[:, t], over(rs[:, u, :, t], DK), ALU.mult)
                        i.then_inc(q["heads_out"], 1)
                    dve.wait_ge(q["final"], b + 1)
                    y = k.Y[:, bass.ds(b * TPB, TPB), :]
                    vv.tensor_tensor(y, k.bank[2][:, 0:TPB * D].rearrange("p (t d) -> p t d", d=D), y, ALU.add)
                    dve.drain()


def window_ffn_layer(k, l):
    nc, KB, CH = k.nc, 3, 512
    NCH, bpc = B * T // CH, CH // T
    with Part(k) as p:
        w1, b1 = p.sb("w1", [P, 2, KB * P]), p.sb("b1", [P, 2, KB])
        w2, b2 = p.sb("w2", [P, KB, D]), p.sb("b2", [P, D])
        gate, hid = p.sb("gate", [P, KB, CH]), p.sb("hid", [P, KB, CH])
        loaded, pair, gated, prod, down, out = (p.sem(n) for n in ("loaded", "pair", "gated", "prod", "down", "out"))
        with nc.Block() as block:
            @block.sync
            def _(sp):
                sp.dma_start(w1[:], k.dram[f"l0f_w1{l}"]).then_inc(loaded, 16)
                sp.dma_start(b1[:], k.dram[f"l0f_b1{l}"]).then_inc(loaded, 16)
                sp.dma_start(w2[:], k.dram[f"l0f_w2{l}"]).then_inc(loaded, 16)
                sp.dma_start(b2[:], k.dram[f"l0f_b2{l}"].partition_broadcast(P)).then_inc(loaded, 16)

            @block.tensor
            def _(pe):
                pe.wait_ge(loaded, 64)
                with pe.Fori(0, NCH) as c:
                    x = k.HT[:, bass.ds(c * bpc, bpc), PAD:PAD + T]
                    pe.wait_ge(out, c + 1)
                    for ob in range(KB):
                        for j in range(2):
                            i = nc.tensor.matmul(k.bank[KB * j + ob].rearrange("p (b t) -> p b t", b=bpc),
                                                 w1[:, j, ob * P:(ob + 1) * P], x, start=True, stop=True)
                        i.then_inc(pair, 1)
                    pe.wait_ge(prod, c * KB + KB)
                    for tt in range(CH // P):
                        for kb in range(KB):
                            i = nc.tensor.matmul(k.bank[6][:, tt * D:(tt + 1) * D], hid[:, kb, tt * P:(tt + 1) * P],
                                                 w2[:, kb, :], start=kb == 0, stop=kb == KB - 1)
                    i.then_inc(down, 1)

            @block.scalar
            def _(act):
                act.wait_ge(loaded, 64)
                with act.Fori(0, NCH) as c:
                    for ob in range(KB):
                        act.wait_ge(pair, c * KB + ob + 1)
                        nc.scalar.activation(gate[:, ob, :], k.bank[KB + ob], ACT.Gelu, bias=b1[:, 1, ob:ob + 1]).then_inc(gated, 1)

            @block.vector
            def _(dve):
                dve.sem_inc(out, 1)
                dve.wait_ge(loaded, 64)
                nc.vector.tensor_tensor(k.Y[:], k.Y[:], across(b2[:], NT), ALU.add)
                dve.drain()
                with dve.Fori(0, NCH) as c:
                    for ob in range(KB):
                        dve.wait_ge(gated, c * KB + ob + 1)
                        nc.vector.scalar_tensor_tensor(out=hid[:, ob, :], in0=k.bank[ob], scalar=b1[:, 0, ob:ob + 1],
                                                       in1=gate[:, ob, :], op0=ALU.add, op1=ALU.mult).then_inc(prod, 1)
                    dve.wait_ge(down, c + 1)
                    y = k.Y[:, bass.ds(c * (CH // P), CH // P), :]
                    nc.vector.tensor_tensor(y, k.bank[6].rearrange("p (t d) -> p t d", d=D), y, ALU.add).then_inc(out, 1)


def lay_out_delta(i, d, np):
    for n in "qkv":
        d[f"l0a_w{n}"] = i[f"L0_attn_w_{n}"]
        d[f"l0a_conv{n}"] = i[f"L0_attn_conv_{n}"].T
    d["l0a_wg"] = i["L0_attn_w_g"]
    d["l0a_wab"] = np.concatenate([i["L0_attn_w_a"], i["L0_attn_w_b"]], 1)
    d["l0a_wout"] = by_blocks(i["L0_attn_w_out"])
    d["l0a_alog_dt"] = np.stack([i["L0_attn_A_log"], i["L0_attn_dt_bias"]])
    d["l0a_normw"] = i["L0_attn_norm_w"]
    r = np.arange(P)
    row, col = r[:, None], r[None, :]
    f = lambda a: a.astype(np.float32)
    d["l0a_tri"] = np.stack([f(row <= col), f(row > col), f(row >= col)], 1)
    lev = []
    for e in range(7):
        s = 1 << e
        lev.append(f((row // (2 * s) == col // (2 * s)) & (row // s % 2 == 1) & (col // s % 2 == 0)) + f(row == col))
    d["l0a_level0"] = np.stack([lev[0], lev[0].T], 1)
    d["l0a_levels"] = np.stack([lev[e][:, r // (1 << e) % 2 == 0] for e in range(1, 7)], 1)


def gated_delta(k):
    nc, H, DK, DV, HG = k.nc, 16, 64, 128, 4
    NG = H // HG
    KD, VD = H * DK, H * DV
    NLEV = 7
    TH = NT * H
    with Part(k) as p:
        wq, wk, wv = p.sb("wq", [P, 4, KD]), p.sb("wk", [P, 4, KD]), p.sb("wv", [P, 4, VD])
        wg, wout = p.sb("wg", [P, VD]), p.sb("wout", [P, H, D])
        tri, lev0, nw = p.sb("tri", [P, 3, P]), p.sb("level0", [P, 2, P]), p.sb("norm_w", [P, DV])
        lev = p.sb("levels", [P, NLEV - 1, P // 2])
        g, nbeta, lam, dlast = (p.sb(n, [P, TH]) for n in ("g", "minus_beta", "lam", "decay_to_end"))
        half = p.sb("minus_half", [P, 2 * HG])
        delta_prologue(k, p, dict(wq=wq, wk=wk, wv=wv, wg=wg, wout=wout, tri=tri, lev=lev, lev0=lev0, nw=nw, g=g, nbeta=nbeta,
                                  lam=lam, dlast=dlast))
        xb = p.sb("x_batch", [P, 3 + T])
        C2 = lambda name, shape, parts=P: p.sb(name, [parts, TPB, *shape])
        qk, v, gate = C2("qk", [2 * HG, DK]), C2("v", [HG, DV]), C2("gate", [HG, DV])
        sq = C2("squares", [2 * HG, DK])
        ss, os_ = C2("qk_norms", [2 * HG]), C2("o_norms", [HG])
        qkT = p.sb("qk_featmajor", [DK, TPB, 2 * HG, P])
        G2 = lambda name: C2(name, [HG, P])
        rD, Dm, Ds, A, AT, Pm, PT, Tm, TT = (G2(n) for n in ("g_masked", "decay", "decay_strict", "A", "A_turned",
                                                             "QK", "QK_turned", "inv", "inv_turned"))
        step = p.sb("steps", [P, NLEV - 1, TPB, HG, P])
        delta, O, yT = Ds, A, PT
        wdelta, lamq, S = Pm[:, 0], Pm[:, 1], k.H[0:DK, 0:HG, :]
        names = ("xb", "qk", "v", "gate", "QS", "qk_silu", "v_silu", "gate_silu", "ss", "ssr", "qkn", "turned", "qkT", "rD", "Dps", "Dexp", "Dm",
                 "Ds", "G", "A0", "A", "P", "APt", "AT", "PTr", "T1", "Yps", "Yp", "TTps", "Tps", "T", "TT", "bv", "gatew",
                 "dps", "delta", "wdelta", "Sps", "S", "KS", "R1", "Ops", "O", "osq", "osum", "orstd", "y", "yT_ps", "yT", "fin", "done", "through_pe", "through_pool")
        q = {n: p.sem(n) for n in names}
        flat = lambda a: a.rearrange("p h t -> p (h t)")

        def cols(a, l, odd):
            return a.rearrange("p (n two s) -> p n two s", two=2, s=1 << l)[:, :, odd, :]

        def packed(c, l):
            return k.bank[c][:, 0:HG * P // 2].rearrange("p (n s) -> p n s", s=1 << l)

        def pairs(eng, pair):
            def batch(b, before, behind):
                pair(b, 0, before, (b, 1))
                with eng.Fori(1, NG - 1) as hg:
                    pair(b, hg, (b, hg - 1), (b, hg + 1))
                pair(b, NG - 1, (b, NG - 2), behind)

            batch(0, None, (1, 0))
            with eng.Fori(1, B - 1) as b:
                batch(b, (b - 1, NG - 1), (b + 1, 0))
            batch(B - 1, (B - 2, NG - 1), None)

        def steps(b, hg, before, behind):
            u = (b * NG + hg) * 2
            yield (u, b, hg, 0), (u + 1, b, hg, 1), before and (u - 1, *before, 1)
            yield (u + 1, b, hg, 1), behind and (u + 2, *behind, 0), (u, b, hg, 0)

        LV = NLEV - 1
        FIRST, FINAL = (0, 0, 0, 0), (2 * B * NG - 1, B - 1, NG - 1, 1)

        with nc.Block() as block:
            @block.tensor
            def _(pe):
                mm, tr = nc.tensor.matmul, nc.tensor.transpose
                w = lambda n, u, per=1, j=1: pe.wait_ge(q[n], u * per + j)
                hd = lambda bank, h: k.bank[bank][:, h * P:(h + 1) * P]

                def project_qk(f, n):
                    u, b, hg, c = f
                    for j in range(4):
                        i = mm(k.bank[4][:, n * 256:(n + 1) * 256], xb[:, c * P + j:c * P + j + P],
                               (wq, wk)[n][:, j, bass.ds(hg * 256, 256)], start=j == 0, stop=j == 3)
                    if n == 1:
                        i.then_inc(q["qk"], 1)

                def project_v(f, taps):
                    u, b, hg, c = f
                    for j in taps:
                        i = mm(k.bank[5], xb[:, c * P + j:c * P + j + P], wv[:, j, bass.ds(hg * 512, 512)],
                               start=j == 0, stop=j == 3)
                    if j == 3:
                        i.then_inc(q["v"], 1)

                def project_gate(f):
                    u, b, hg, c = f
                    mm(k.bank[6], xb[:, 3 + c * P:3 + c * P + P], wg[:, bass.ds(hg * 512, 512)],
                       start=True, stop=True).then_inc(q["gate"], 1)

                def decays(f):
                    w("rD", f[0])
                    mm(k.bank[7], tri[:, 0, :], flat(rD[:, f[3]]), start=True, stop=True).then_inc(q["Dps"], 1)

                def turn_qk(f):
                    u, b, hg, c = f
                    w("v_silu", u)
                    w("qkn", u)
                    pe.sem_inc(q["through_pe"], 1)
                    for n in range(2 * HG):
                        i = tr(k.bank[4 + n // HG][0:DK, n % HG * P:(n % HG + 1) * P], qk[:, c, n, :], k.ident[:])
                    i.then_inc(q["turned"], 1)

                def kk(f):
                    u, b, hg, c = f
                    w("gate_silu", u)
                    w("qkT", u)
                    for h in range(HG):
                        mm(hd(6, h), qkT[:, c, HG + h, :], qkT[:, c, HG + h, :], start=True, stop=True)

                def qk_products(f):
                    u, b, hg, c = f
                    w("Dexp", u)
                    for h in range(HG):
                        i = mm(hd(7, h), qkT[:, c, h, :], qkT[:, c, HG + h, :], start=True, stop=True)
                    i.then_inc(q["G"], 1)

                def turn_ap(f):
                    u, b, hg, c = f
                    w("P", u)
                    w("A", u)
                    for n, a in enumerate((A, Pm)):
                        for h in range(HG):
                            i = tr(hd(4 + n, h), a[:, c, h, :], k.ident[:])
                    i.then_inc(q["APt"], 1)

                def level_step(bk, l):
                    u, b, hg, c = bk
                    if l > 1:
                        w("T", u, LV - 1, l - 1)
                    for h in range(HG):
                        i = mm(k.bank[0][:, h * 64:(h + 1) * 64], AT[:, c, h, :], cols(Tm[:, c, h, :], l, 0), start=True, stop=True)
                    i.then_inc(q["Yps"], 1)

                def level_inverse(bk, l):
                    u, b, hg, c = bk
                    if l > 1:
                        w("TT", u, LV, l - 1)
                    w("Yp", u, LV, l)
                    if l < LV:
                        for h in range(HG):
                            i = mm(k.bank[1][:, h * 64:(h + 1) * 64], TT[:, c, h, :],
                                   cols(step[:, l - 1, c, h, :], l, 0), start=True, stop=True)
                        i.then_inc(q["Tps"], 1)
                    for h in range(HG):
                        i = mm(k.bank[2][:, h * 64:(h + 1) * 64], step[:, l - 1, c, h, :],
                               cols(TT[:, c, h, :], l, 1), start=True, stop=True)
                    i.then_inc(q["TTps"], 1)

                def turn_y(last):
                    u, b, hg, c = last
                    w("y", u)
                    for h in range(HG):
                        i = tr(hd(3, h), O[:, c, h, :], k.ident[:])
                    i.then_inc(q["yT_ps"], 1)

                def out(last):
                    u, b, hg, c = last
                    w("yT", u)
                    for h in range(HG):
                        i = mm(k.bank[3][:, 0:D], yT[:, c, h, :], wout[:, bass.ds(hg * HG + h, 1), :].rearrange("p a d -> p (a d)"),
                               start=h == 0, stop=h == HG - 1)
                    i.then_inc(q["fin"], 1)

                def front_first(f):
                    if f[3] == 0:
                        w("xb", f[1])
                    project_qk(f, 0)

                def pair(b, hg, before, behind):
                    for bk, f, last in steps(b, hg, before, behind):
                        u, _, _, c = bk
                        g = b * NG + hg
                        if f:
                            w("AT", u)
                            front_first(f)
                        w("PTr", u)
                        w("T1", u)
                        level_step(bk, 1)
                        if f:
                            project_qk(f, 1)
                        level_inverse(bk, 1)
                        if f:
                            decays(f)
                        level_step(bk, 2)
                        if f:
                            project_v(f, [0])
                        level_inverse(bk, 2)
                        if last:
                            turn_y(last)
                        level_step(bk, 3)
                        if f:
                            project_v(f, [1])
                        level_inverse(bk, 3)
                        if f:
                            project_v(f, [2, 3])
                        level_step(bk, 4)
                        if f:
                            project_gate(f)
                        level_inverse(bk, 4)
                        if last:
                            out(last)
                        level_step(bk, 5)
                        if last:
                            w("done", u - 1)
                        if c == 1:
                            w("S", g)
                            for h in range(HG):
                                i = mm(hd(3, h), qkT[:, 1, HG + h, :], S[:, h, :], start=True, stop=True)
                            i.then_inc(q["KS"], 1)
                        if f:
                            turn_qk(f)
                        level_inverse(bk, 5)
                        level_step(bk, 6)
                        if f:
                            kk(f)
                        level_inverse(bk, 6)
                        if f:
                            qk_products(f)
                        if c == 1:
                            w("R1", g)
                            for h in range(HG):
                                i = mm(hd(3, h), qkT[:, 1, h, :], S[:, h, :], start=True, stop=True)
                            i.then_inc(q["QS"], 1)
                        else:
                            w("bv", u)
                        w("TT", u, LV, LV)
                        for h in range(HG):
                            i = mm(hd(0, h), TT[:, c, h, :], v[:, c, h, :], start=True, stop=True)
                        i.then_inc(q["dps"], 1)
                        w("delta", u)
                        for h in range(HG):
                            i = mm(hd(1, h), PT[:, c, h, :], delta[:, c, h, :], start=True, stop=True)
                        i.then_inc(q["Ops"], 1)
                        if c == 0:
                            w("wdelta", g)
                            for h in range(HG):
                                i = mm(k.bank[3][0:DK, h * DV:(h + 1) * DV], qk[:, 0, HG + h, :], wdelta[:, h, :], start=True, stop=True)
                            i.then_inc(q["Sps"], 1)
                        else:
                            w("O", u, 1, 3)
                        if f:
                            turn_ap(f)
                        if c == 0:
                            w("S", g)

                f = FIRST
                front_first(f)
                project_qk(f, 1)
                decays(f)
                project_v(f, range(4))
                project_gate(f)
                turn_qk(f)
                kk(f)
                qk_products(f)
                turn_ap(f)
                pairs(pe, pair)
                turn_y(FINAL)
                out(FINAL)

            @block.scalar
            def _(act):
                w = lambda n, u, per=1, j=1: act.wait_ge(q[n], u * per + j)

                def copy(dst, src):
                    return nc.scalar.activation(dst, src, ACT.Copy)

                def silu(f, n, dst, src):
                    w(n, f[0])
                    nc.scalar.activation(dst[:, f[3]].rearrange("p h d -> p (h d)"), k.bank[src], ACT.Silu).then_inc(q[n + "_silu"], 1)

                def exp_decays(f):
                    w("Dps", f[0])
                    nc.scalar.activation(flat(Dm[:, f[3]]), k.bank[7], ACT.Exp).then_inc(q["Dexp"], 1)

                def copy_qkT(f):
                    w("turned", f[0])
                    copy(flat(qkT[:, f[3], 0:HG]), k.bank[4][0:DK, :])
                    copy(flat(qkT[:, f[3], HG:]), k.bank[5][0:DK, :]).then_inc(q["qkT"], 1)

                def copy_ap(f):
                    w("APt", f[0])
                    copy(flat(AT[:, f[3]]), k.bank[4]).then_inc(q["AT"], 1)
                    copy(flat(PT[:, f[3]]), k.bank[5]).then_inc(q["PTr"], 1)

                def copy_y(last):
                    u, b, hg, c = last
                    w("yT_ps", u)
                    copy(flat(yT[:, c]), k.bank[3]).then_inc(q["yT"], 1)

                def pair(b, hg, before, behind):
                    for (u, _, _, c), f, last in steps(b, hg, before, behind):
                        for l in range(1, NLEV):
                            if l < LV:
                                w("Tps", u, LV - 1, l)
                                copy(cols(flat(Tm[:, c]), l, 0), packed(1, l)).then_inc(q["T"], 1)
                            w("TTps", u, LV, l)
                            copy(cols(flat(TT[:, c]), l, 1), packed(2, l)).then_inc(q["TT"], 1)
                            if l == 1 and f:
                                silu(f, "qk", qk, 4)
                            elif l == 2:
                                if f:
                                    exp_decays(f)
                                if last:
                                    copy_y(last)
                            elif l == 4 and f:
                                silu(f, "v", v, 5)
                                silu(f, "gate", gate, 6)
                            elif l == 5 and f:
                                copy_qkT(f)
                        w("dps", u)
                        copy(flat(delta[:, c]), k.bank[0]).then_inc(q["delta"], 1)
                        w("O", u, 1, 3)
                        nc.scalar.activation(sq[:, c].rearrange("p h d -> p (h d)"), flat(O[:, c]), ACT.Square).then_inc(q["osq"], 1)
                        if c == 0:
                            w("Sps", b * NG + hg)
                            copy(flat(S), k.bank[3][0:DK, :]).then_inc(q["S"], 1)
                        if f:
                            copy_ap(f)

                f = FIRST
                silu(f, "qk", qk, 4)
                exp_decays(f)
                silu(f, "v", v, 5)
                silu(f, "gate", gate, 6)
                copy_qkT(f)
                copy_ap(f)
                pairs(act, pair)
                copy_y(FINAL)

            @block.gpsimd
            def _(pool):
                tt = nc.gpsimd.tensor_tensor
                w = lambda n, u, per=1, j=1: pool.wait_ge(q[n], u * per + j)
                nc.gpsimd.memset(half[:], -0.5)
                pool.drain()

                def alone():
                    pool.sem_inc(q["through_pool"], 1)

                def front(f):
                    u, b, hg, c = f
                    col = lambda a: a[:, bass.ds(b * (TPB * H) + hg * HG + c * H, HG)]
                    w("O", u, 1, 1)
                    alone()
                    tt(rD[:, c], across(tri[:, 1, :], HG), over(col(g), P), ALU.mult).then_inc(q["rD"], 1)
                    tt(Ds[:, c], across(tri[:, 1, :], HG), over(col(nbeta), P), ALU.mult)
                    w("ss", u)
                    tt(ss[:, c], ss[:, c], half[:], ALU.pow).then_inc(q["ssr"], 1)
                    pool.drain()
                    w("Dexp", u)
                    tt(Ds[:, c], Dm[:, c], Ds[:, c], ALU.mult).then_inc(q["Ds"], 1)
                    pool.drain()
                    tt(Dm[:, c], Dm[:, c], across(tri[:, 2, :], HG), ALU.mult).then_inc(q["Dm"], 1)
                    w("v_silu", u)
                    alone()
                    tt(v[:, c], v[:, c], over(col(nbeta), DV), ALU.mult).then_inc(q["bv"], 1)
                    w("gate_silu", u)
                    tt(gate[:, c], gate[:, c], across(nw[:], HG), ALU.mult).then_inc(q["gatew"], 1)
                    w("A0", u)
                    tt(A[:, c], A[:, c], across(k.ident[:], HG), ALU.add).then_inc(q["A"], 1)

                def pair(b, hg, before, behind):
                    for (u, _, _, c), f, last in steps(b, hg, before, behind):
                        if f:
                            front(f)
                        w("osum", u)
                        tt(os_[:, c], os_[:, c], half[:, 0:HG], ALU.pow).then_inc(q["orstd"], 1)

                front(FIRST)
                pairs(pool, pair)

            @block.vector
            def _(dve):
                vv = nc.vector
                tt = vv.tensor_tensor
                w = lambda n, u, per=1, j=1: dve.wait_ge(q[n], u * per + j)
                bank3 = lambda n: k.bank[n].rearrange("p (h t) -> p h t", h=HG)
                vv.memset(k.Y[:], 0.0)
                every = LV * TPB * HG
                vv.tensor_copy(step[:].rearrange("p l c h t -> p (l c h) t"), across(k.ident[:], every))
                dve.drain()
                dve.sem_inc(q["O"], 2)

                def load_x(b):
                    vv.tensor_copy(xb[:], k.HT[:, bass.ds(b, 1), PAD - 3:].rearrange("p a t -> p (a t)")).then_inc(q["xb"], 1)

                def square_qk(f):
                    u, b, hg, c = f
                    w("qk_silu", u)
                    tt(sq[:, c], qk[:, c], qk[:, c], ALU.mult)
                    dve.drain()
                    vv.tensor_reduce(ss[:, c], sq[:, c], AXX, ALU.add)
                    dve.drain()
                    vv.tensor_scalar_add(ss[:, c], ss[:, c], 1e-6).then_inc(q["ss"], 1)

                def norm_qk(f):
                    u, b, hg, c = f
                    w("ssr", u)
                    vv.tensor_scalar(ss[:, c, 0:HG], ss[:, c, 0:HG], DK ** -0.5, None, ALU.mult)
                    dve.drain()
                    tt(qk[:, c], qk[:, c], over(ss[:, c, :], DK), ALU.mult).then_inc(q["qkn"], 1)

                def mask_products(f):
                    u, b, hg, c = f
                    w("G", u)
                    w("Ds", u)
                    tt(A[:, c], bank3(6), Ds[:, c], ALU.mult).then_inc(q["A0"], 1)
                    w("Dm", u)
                    tt(Pm[:, c], bank3(7), Dm[:, c], ALU.mult).then_inc(q["P"], 1)

                def level0(f):
                    u, b, hg, c = f
                    w("A", u)
                    tt(Tm[:, c], A[:, c], across(lev0[:, 0, :], HG), ALU.mult)
                    w("AT", u)
                    tt(TT[:, c], AT[:, c], across(lev0[:, 1, :], HG), ALU.mult).then_inc(q["T1"], 1)

                def gate_y(last):
                    u, b, hg, c = last
                    w("orstd", u)
                    vv.tensor_scalar(os_[:, c], os_[:, c], -1.0, None, ALU.mult)
                    dve.drain()
                    tt(O[:, c], O[:, c], over(os_[:, c, :], DV), ALU.mult)
                    dve.drain()
                    w("gatew", u)
                    tt(O[:, c], O[:, c], gate[:, c], ALU.mult).then_inc(q["y"], 1)

                def add_y(last):
                    u, b, hg, c = last
                    w("fin", u)
                    y = k.Y[:, bass.ds(b * TPB + c, 1), :].rearrange("p a d -> p (a d)")
                    tt(y, k.bank[3][:, 0:D], y, ALU.add).then_inc(q["done"], 1)

                def pair(b, hg, before, behind):
                    for (u, _, _, c), f, last in steps(b, hg, before, behind):
                        col = lambda a: a[:, bass.ds(b * (TPB * H) + hg * HG + c * H, HG)]
                        g = b * NG + hg
                        if c == 1 and behind and isinstance(behind[1], int) and behind[1] == 0:
                            w("gate", u)
                            load_x(f[1])
                        for l in range(1, NLEV):
                            w("Yps", u, LV, l)
                            tt(cols(flat(step[:, l - 1, c]), l, 0).rearrange("p (h n) s -> p h n s", h=HG),
                               packed(0, l).rearrange("p (h n) s -> p h n s", h=HG),
                               across(lev[:, l - 1, :].rearrange("p (n s) -> p n s", s=1 << l), HG), ALU.mult).then_inc(q["Yp"], 1)
                            if l == 1 and last:
                                gate_y(last)
                            elif l == 3 and f:
                                square_qk(f)
                            elif l == 4:
                                if f:
                                    norm_qk(f)
                                if last:
                                    add_y(last)
                            elif l == 5 and c == 1:
                                w("KS", g)
                                tt(lamq, bank3(3), over(col(lam), DV), ALU.mult)
                                dve.drain()
                                tt(lamq, lamq, over(col(nbeta), DV), ALU.mult)
                                dve.drain()
                                w("bv", u)
                                tt(v[:, 1], v[:, 1], lamq, ALU.add).then_inc(q["R1"], 1)
                                dve.drain()
                        if f:
                            mask_products(f)
                        if c == 1:
                            w("QS", g)
                            tt(lamq, bank3(3), over(col(lam), DV), ALU.mult)
                            dve.drain()
                            w("Ops", u)
                            tt(O[:, 1], bank3(1), lamq, ALU.add).then_inc(q["O"], 1)
                        else:
                            w("delta", u)
                            tt(wdelta, delta[:, 0], over(col(dlast), DV), ALU.mult).then_inc(q["wdelta"], 1)
                            w("Ops", u)
                            vv.tensor_copy(O[:, 0], bank3(1)).then_inc(q["O"], 1)
                        w("osq", u)
                        vv.tensor_reduce(os_[:, c], sq[:, c].rearrange("p h d -> p (h d)").rearrange("p (h d) -> p h d", h=HG), AXX, ALU.add)
                        dve.drain()
                        vv.tensor_scalar(os_[:, c], os_[:, c], 1.0 / DV, 1e-5, ALU.mult, ALU.add).then_inc(q["osum"], 1)
                        if f:
                            level0(f)

                f = FIRST
                load_x(0)
                square_qk(f)
                norm_qk(f)
                mask_products(f)
                level0(f)
                pairs(dve, pair)
                gate_y(FINAL)
                add_y(FINAL)


def delta_prologue(k, p, m):
    nc, H, TH = k.nc, 16, NT * 16
    wab, al = p.sb("wab", [P, 2 * H]), p.sb("alog_dtbias", [P, 2, H])
    with Part(k) as own:
        wide = {n: own.sb("plain_" + n, [P, s]) for n, s in (("q", 1024), ("k", 1024), ("v", 2048))}
        z, e, u, l, r = (own.sb(n, [P, NT, H]) for n in ("z", "e", "u", "l", "r"))
        names = ("small", "taps", "plain", "rest", "ab", "z", "exped", "u", "logged", "alog", "g", "cum", "cum_read")
        q = {n: own.sem(n) for n in names}
        ab = k.bank[0].rearrange("p (t h) -> p t h", h=2 * H)
        g3 = m["g"][:].rearrange("p (t h) -> p t h", h=H)
        with nc.Block() as block:
            @block.sync
            def _(sp):
                sp.dma_start(wab[:], k.dram["l0a_wab"]).then_inc(q["small"], 16)
                sp.dma_start(al[:], k.dram["l0a_alog_dt"].partition_broadcast(P)).then_inc(q["small"], 16)
                sp.dma_start(m["tri"][:], k.dram["l0a_tri"]).then_inc(q["small"], 16)
                for n in "qkv":
                    sp.dma_start(m["w" + n][:], k.dram[f"l0a_conv{n}"].partition_broadcast(P)).then_inc(q["taps"], 16)
                    sp.dma_start(wide[n][:], k.dram[f"l0a_w{n}"]).then_inc(q["plain"], 16)
                sp.dma_start(m["wg"][:], k.dram["l0a_wg"]).then_inc(q["rest"], 16)
                sp.dma_start(m["wout"][:], k.dram["l0a_wout"]).then_inc(q["rest"], 16)
                sp.dma_start(m["lev"][:], k.dram["l0a_levels"]).then_inc(q["rest"], 16)
                sp.dma_start(m["lev0"][:], k.dram["l0a_level0"]).then_inc(q["rest"], 16)
                sp.dma_start(m["nw"][:], k.dram["l0a_normw"].partition_broadcast(P)).then_inc(q["rest"], 16)
                sp.wait_ge(q["rest"], 80)

            @block.tensor
            def _(pe):
                pe.wait_ge(q["small"], 48)
                for t in range(NT):
                    i = nc.tensor.matmul(ab[:, t, :], k.HT[:, t // TPB, PAD + t % TPB * P:PAD + (t % TPB + 1) * P], wab[:],
                                         start=True, stop=True)
                i.then_inc(q["ab"], 1)
                pe.wait_ge(q["g"], 1)
                nc.tensor.matmul(k.bank[1][:, 0:TH], m["tri"][:, 0, :], m["g"][:], start=True, stop=True)
                nc.tensor.matmul(k.bank[2][:, 0:TH], m["tri"][:, 1, :], m["g"][:], start=True, stop=True).then_inc(q["cum"], 1)

            @block.scalar
            def _(act):
                a = nc.scalar.activation
                act.wait_ge(q["small"], 48)
                a(al[:, 0, :], al[:, 0, :], ACT.Exp).then_inc(q["alog"], 1)
                act.wait_ge(q["z"], 1)
                a(e[:], z[:], ACT.Abs)
                act.drain()
                a(e[:], e[:], ACT.Exp, scale=-1.0)
                a(r[:], ab[:, :, H:], ACT.Exp, scale=-1.0).then_inc(q["exped"], 1)
                act.wait_ge(q["u"], 1)
                a(l[:], u[:], ACT.Ln).then_inc(q["logged"], 1)
                act.wait_ge(q["cum"], 1)
                a(m["lam"][:], k.bank[1][:, 0:TH], ACT.Exp)
                a(m["dlast"][:], k.bank[2][:, 0:TH], ACT.Exp)
                act.drain()

            @block.vector
            def _(dve):
                v = nc.vector
                dve.wait_ge(q["ab"], 1)
                dve.wait_ge(q["alog"], 1)
                v.tensor_tensor(z[:], ab[:, :, 0:H], across(al[:, 1, :], NT), ALU.add).then_inc(q["z"], 1)
                dve.wait_ge(q["exped"], 1)
                v.tensor_scalar_add(u[:], e[:], 1.0).then_inc(q["u"], 1)
                v.tensor_scalar_max(z[:], z[:], 0.0)
                v.tensor_scalar_add(r[:], r[:], 1.0)
                dve.drain()
                v.scalar_tensor_tensor(out=e[:], in0=u[:], scalar=-1.0, in1=e[:], op0=ALU.add, op1=ALU.subtract)
                dve.wait_ge(q["logged"], 1)
                dve.drain()
                v.tensor_tensor(l[:], l[:], e[:], ALU.subtract)
                dve.drain()
                v.tensor_add(z[:], z[:], l[:])
                dve.drain()
                v.scalar_tensor_tensor(out=g3, in0=z[:], scalar=-1.0, in1=across(al[:, 0, :], NT), op0=ALU.mult,
                                       op1=ALU.mult).then_inc(q["g"], 1)
                v.reciprocal(r[:], r[:])
                dve.drain()
                v.tensor_scalar(m["nbeta"][:].rearrange("p (t h) -> p t h", h=H), r[:], -2.0, None, ALU.mult)
                dve.wait_ge(q["taps"], 48)
                dve.wait_ge(q["plain"], 48)
                for n in "qkv":
                    w = m["w" + n]
                    v.tensor_tensor(w[:], w[:], across(wide[n][:], 4), ALU.mult)
                dve.drain()


def lay_out_mamba(i, d, np):
    E, N, R = 2 * D, 64, D // 16
    rows = lambda a: a.reshape(2, P, *a.shape[1:]).swapaxes(0, 1)
    d["l3a_ln1"] = np.stack([i["L3_attn_ln1_w"], i["L3_attn_ln1_b"]])
    d["l3a_ln2"] = np.stack([i["L3_attn_ln2_w"], i["L3_attn_ln2_b"]])
    for m in (1, 2):
        g = lambda n: i[f"L3_attn_m{m}_{n}"]
        d[f"l3a_win{m}"] = g("W_in").T
        d[f"l3a_conv{m}"] = np.concatenate([rows(g("conv_w")), rows(g("conv_b"))[:, :, None],
                                            rows(g("dt_b"))[:, :, None], rows(g("D"))[:, :, None]], 2)
        xp = g("W_xp")
        bm, cm = xp[R:R + N], xp[R + N:]
        d[f"l3a_wxp{m}"] = by_blocks(np.concatenate([bm, bm, cm, cm, bm, cm, xp[:R]]).T)
        d[f"l3a_wdt{m}"] = g("W_dt").T
        d[f"l3a_alog{m}"] = rows(g("A_log"))
        d[f"l3a_wout{m}"] = by_blocks(g("W_out").T)
    e = np.eye(N, dtype=np.float32)
    z = np.zeros((N, N), np.float32)
    d["l3a_sel"] = np.stack([np.concatenate([e, e]), np.concatenate([e, z]), np.concatenate([z, e])], 1)




def bi_mamba(k):
    nc = k.nc
    with Part(k) as p:
        affine = p.sb("ln1", [P, 2, D])
        load_one(k, p, affine, k.dram["l3a_ln1"].partition_broadcast(P))
        normalise(k, src=k.H, affine=affine)
    with Part(k) as p:
        mem = mamba_memories(p)
        for m in (1, 2):
            mamba_inputs(k, m, mem)
            mamba_scan(k, m, mem)
            mamba_output(k, m, mem)
    with Part(k) as p:
        affine = p.sb("ln2", [P, 2, D])
        load_one(k, p, affine, k.dram["l3a_ln2"].partition_broadcast(P))
        add_norm_to_input(k, p, affine)


def load_one(k, p, dst, src):
    loaded = p.sem("loaded")
    with k.nc.Block() as block:
        @block.sync
        def _(sp):
            sp.dma_start(dst[:], src).then_inc(loaded, 16)
            sp.wait_ge(loaded, 16)


def add_norm_to_input(k, p, affine):
    nc = k.nc
    stats, mv = p.sb("stats", [P, NT, 6]), p.sb("meanvar", [P, NT, 2])
    rstd, half = p.sb("rstd", [P, NT]), p.sb("minus_half", [P, NT])
    var_ready, rstd_ready = p.sem("var"), p.sem("rstd")
    with nc.Block() as block:
        @block.gpsimd
        def _(pool):
            nc.gpsimd.memset(half[:], -0.5)
            pool.drain()
            pool.wait_ge(var_ready, 1)
            nc.gpsimd.tensor_tensor(rstd[:], rstd[:], half[:], ALU.pow).then_inc(rstd_ready, 1)

        @block.vector
        def _(dve):
            layer_norm_steps(nc, dve, k.Y, k.Y, stats, mv, rstd, var_ready, (rstd_ready, 1))
            nc.vector.tensor_tensor(k.Y[:], k.Y[:], across(affine[:, 0, :], NT), ALU.mult)
            dve.drain()
            nc.vector.tensor_tensor(k.Y[:], k.Y[:], across(affine[:, 1, :], NT), ALU.add)
            dve.drain()
            nc.vector.tensor_add(k.Y[:], k.Y[:], k.H[:])
            dve.drain()


SN, SE = 64, 2
SCH = 512
SNC = B * T // SCH
CPAD = 3


def mamba_memories(p):
    m = {}
    m["xp"] = p.sb("xp_padded", [P, B, CPAD + T])
    m["xc"] = p.sb("xc", [P, SE, B * T])
    m["sz"] = p.sb("silu_z", [P, SE, B * T])
    m["dt"] = p.sb("dt", [P, SE, B * T])
    m["dtx"] = p.sb("dtx", [P, SE, B * T])
    for n in ("hm_b", "hm_c", "lo"):
        m[n] = p.sb("bc_" + n, [P, B * T], BF16)
    m["A"] = p.sb("A", [P, SE, SN])
    m["sel"] = p.sb("selectors", [P, 3, SN], BF16)
    m["self"] = p.sb("selectors_f32", [P, 3, SN])
    m["cw"] = p.sb("conv_and_biases", [P, SE, 7])
    m["wout"] = p.sb("w_out", [P, SE, D])
    return m


def mamba_inputs(k, m, mem):
    nc, R = k.nc, D // 16
    xp, xc, sz, dt, dtx = (mem[n] for n in ("xp", "xc", "sz", "dt", "dtx"))
    cw = mem["cw"]
    with Part(k) as p:
        win, wxp = p.sb("w_in", [P, 4 * P]), p.sb("w_xp", [P, SE, 3 * P + R])
        wdt = p.sb("w_dt", [R, 2 * P])
        dtlo = p.sb("dt_low", [R, B * T])
        tmp = [p.sb(f"tmp{n}", [P, SCH]) for n in range(3)]
        hi, mid = p.sb("high", [P, SCH], BF16), p.sb("middle", [P, SCH], BF16)
        r1, r2 = p.sb("rest1", [P, SCH]), p.sb("rest2", [P, SCH])
        names = ("loaded", "proj", "xp_out", "z_out", "conved", "xc_ready", "bc", "bc_read", "dtlo", "dtlo_ready", "dtp",
                 "absd", "exped", "u_ready", "logged", "dt_done", "src_ready", "a_ready")
        q = {n: p.sem(n) for n in names}
        xsrc = xp[:, :, CPAD:]
        with nc.Block() as block:
            @block.sync
            def _(sp):
                for dst, n in ((win, "win"), (cw, "conv"), (wxp, "wxp"), (wdt, "wdt"), (mem["A"], "alog"), (mem["wout"], "wout")):
                    sp.dma_start(dst[:], k.dram[f"l3a_{n}{m}"]).then_inc(q["loaded"], 16)
                sp.dma_start(mem["self"][:], k.dram["l3a_sel"]).then_inc(q["loaded"], 16)

            @block.tensor
            def _(pe):
                pe.wait_ge(q["loaded"], 112)
                pe.wait_ge(q["src_ready"], 1)
                for blk in (0, 1, 2, 3):
                    if blk == 2:
                        pe.wait_ge(q["xp_out"], 4)
                    if blk == 3:
                        pe.wait_ge(q["xp_out"], 8)
                    for c in range(SNC):
                        nc.tensor.matmul(k.bank[blk % 2 * 4 + c].rearrange("p (b t) -> p b t", b=2), win[:, blk * P:(blk + 1) * P],
                                         k.HT[:, 2 * c:2 * c + 2, PAD:], start=True, stop=True).then_inc(q["proj"], 1)
                pe.wait_ge(q["xc_ready"], 2)
                for c in range(SNC):
                    for n, (lo, w) in enumerate(((0, P), (P, P), (2 * P, P), (3 * P, R))):
                        pe.wait_ge(*((q["z_out"], 4) if c == 0 else (q["bc_read"], 4 * c)))
                        for e in range(SE):
                            i = nc.tensor.matmul(k.bank[n][0:w, :], wxp[:, e, lo:lo + w], xc[:, e, c * SCH:(c + 1) * SCH],
                                                 start=e == 0, stop=e == SE - 1)
                        i.then_inc(q["bc"], 1)
                pe.wait_ge(q["dtlo_ready"], SNC)
                pe.wait_ge(q["z_out"], 8)
                for c in range(SNC):
                    for e in range(SE):
                        if c:
                            pe.wait_ge(q["dt_done"], (c - 1) * SE + e + 1)
                        nc.tensor.matmul(k.bank[4 + e], wdt[:, e * P:(e + 1) * P], dtlo[:, c * SCH:(c + 1) * SCH],
                                         start=True, stop=True).then_inc(q["dtp"], 1)

            @block.scalar
            def _(act):
                act.wait_ge(q["loaded"], 112)
                for blk in (0, 1):
                    if blk == 1:
                        act.wait_ge(q["conved"], 1)
                    for c in range(SNC):
                        act.wait_ge(q["proj"], blk * 4 + c + 1)
                        nc.scalar.activation(xsrc[:, 2 * c:2 * c + 2, :], k.bank[blk * 4 + c].rearrange("p (b t) -> p b t", b=2),
                                             ACT.Copy).then_inc(q["xp_out"], 1)
                for blk in (0, 1):
                    for c in range(SNC):
                        act.wait_ge(q["proj"], 8 + blk * 4 + c + 1)
                        nc.scalar.activation(sz[:, blk, c * SCH:(c + 1) * SCH], k.bank[blk * 4 + c], ACT.Silu).then_inc(q["z_out"], 1)
                for e in range(SE):
                    act.wait_ge(q["conved"], e + 1)
                    nc.scalar.activation(xc[:, e, :], xc[:, e, :], ACT.Silu, bias=cw[:, e, 4:5]).then_inc(q["xc_ready"], 1)
                nc.scalar.activation(mem["A"][:], mem["A"][:], ACT.Exp).then_inc(q["a_ready"], 1)
                for c in range(SNC):
                    for e in range(SE):
                        n = c * SE + e
                        act.wait_ge(q["dtp"], n + 1)
                        if n:
                            act.wait_ge(q["dt_done"], n)
                        nc.scalar.activation(tmp[0][:], k.bank[4 + e], ACT.Abs, bias=cw[:, e, 5:6])
                        act.drain()
                        nc.scalar.activation(tmp[0][:], tmp[0][:], ACT.Exp, scale=-1.0).then_inc(q["exped"], 1)
                        act.wait_ge(q["u_ready"], n + 1)
                        nc.scalar.activation(tmp[2][:], tmp[1][:], ACT.Ln).then_inc(q["logged"], 1)

            @block.vector
            def _(dve):
                v = nc.vector
                if m == 2:
                    v.tensor_copy(dtx[:, 0, :].rearrange("p (b t) -> p b t", b=B), k.HT[:, :, PAD + T - 1:PAD - 1:-1])
                    dve.drain()
                    v.tensor_copy(k.HT[:, :, PAD:], dtx[:, 0, :].rearrange("p (b t) -> p b t", b=B))
                    dve.drain()
                v.memset(xp[:, :, 0:CPAD], 0.0).then_inc(q["src_ready"], 1)
                dve.wait_ge(q["loaded"], 112)
                v.tensor_copy(mem["sel"][:], mem["self"][:])
                dve.drain()
                for e in range(SE):
                    dve.wait_ge(q["xp_out"], 4 * e + 4)
                    o = xc[:, e, :].rearrange("p (b t) -> p b t", b=B)
                    v.tensor_scalar(o, xp[:, :, 0:T], cw[:, e, 0:1], None, ALU.mult)
                    for j in range(1, 4):
                        dve.drain()
                        i = v.scalar_tensor_tensor(out=o, in0=xp[:, :, j:j + T], scalar=cw[:, e, j:j + 1], in1=o,
                                                   op0=ALU.mult, op1=ALU.add)
                    i.then_inc(q["conved"], 1)
                dve.wait_ge(q["a_ready"], 1)
                v.tensor_scalar(mem["A"][:], mem["A"][:], -1.0, None, ALU.mult)
                for c in range(SNC):
                    cols = slice(c * SCH, (c + 1) * SCH)
                    for n, name in enumerate(("hm_b", "hm_c")):
                        dve.wait_ge(q["bc"], c * 4 + n + 1)
                        v.tensor_copy(hi[:], k.bank[n])
                        dve.drain()
                        v.tensor_copy(mem[name][0:64, cols], hi[0:64, :])
                        v.tensor_tensor(mem[name][64:128, cols], k.bank[n][64:128, :], hi[64:128, :], ALU.subtract)
                        dve.drain()
                        v.engine_nop().then_inc(q["bc_read"], 1)
                    dve.wait_ge(q["bc"], c * 4 + 3)
                    v.tensor_copy(hi[:], k.bank[2])
                    dve.drain()
                    v.tensor_tensor(r1[:], k.bank[2], hi[:], ALU.subtract).then_inc(q["bc_read"], 1)
                    dve.drain()
                    v.tensor_copy(mid[:], r1[:])
                    dve.drain()
                    v.tensor_tensor(mem["lo"][:, cols], r1[:], mid[:], ALU.subtract)
                    dve.wait_ge(q["bc"], c * 4 + 4)
                    v.tensor_copy(dtlo[:, cols], k.bank[3][0:R, :]).then_inc(q["bc_read"], 1)
                    dve.drain()
                    v.engine_nop().then_inc(q["dtlo_ready"], 1)
                for c in range(SNC):
                    for e in range(SE):
                        n = c * SE + e
                        o = dt[:, e, c * SCH:(c + 1) * SCH]
                        dve.wait_ge(q["exped"], n + 1)
                        v.tensor_scalar_add(tmp[1][:], tmp[0][:], 1.0).then_inc(q["u_ready"], 1)
                        v.tensor_scalar(o, k.bank[4 + e], cw[:, e, 5:6], 0.0, ALU.add, ALU.max)
                        dve.drain()
                        v.scalar_tensor_tensor(out=r1[:], in0=tmp[1][:], scalar=-1.0, in1=tmp[0][:], op0=ALU.add, op1=ALU.subtract)
                        dve.drain()
                        dve.wait_ge(q["logged"], n + 1)
                        v.tensor_tensor(r2[:], tmp[2][:], r1[:], ALU.subtract)
                        dve.drain()
                        v.tensor_add(o, o, r2[:])
                        dve.drain()
                        v.tensor_tensor(dtx[:, e, c * SCH:(c + 1) * SCH], o, xc[:, e, c * SCH:(c + 1) * SCH],
                                        ALU.mult).then_inc(q["dt_done"], 1)
                dve.drain()
                for e in range(SE):
                    v.tensor_scalar(xc[:, e, :], xc[:, e, :], cw[:, e, 6:7], None, ALU.mult)
                dve.drain()


def mamba_scan(k, m, mem):
    NS = 4
    nc = k.nc
    xc, sz, dt, dtx = (mem[n] for n in ("xc", "sz", "dt", "dtx"))
    with Part(k) as p:
        dA = p.sb("dA", [P, NS, SE, SCH])
        dBx = p.sb("dBx", [P, NS, SE, SCH])
        h = p.sb("h", [P, 2, SE, SCH])
        hc = p.sb("hc", [P, 2, SE, SCH])
        bsb = p.sb("b_row", [P, NS, SCH])
        zero = p.sb("zero", [P, SCH], BF16)
        names = ("zeroed", "b_ready", "c_ready", "bsb_ready", "da_ready", "dbx_ready",
                 "scanned", "through_pool", "hc_ready", "hc_free", "y_ready", "y_read")
        q = {n: p.sem(n) for n in names}
        sel = mem["sel"]
        BBANK, LEAD = (2, 3, 6, 7), NS - 1

        def onto_all(ap):
            return ap.to_broadcast([P, P])

        with nc.Block() as block:
            @block.tensor
            def _(pe):
                pe.wait_ge(q["zeroed"], 1)

                def row(c, n, part, which, bank, free, ready):
                    cols = bass.ds(c * SCH, SCH)
                    pe.wait_ge(q[free], c * SN + n + 1)
                    nc.tensor.matmul(k.bank[bank], onto_all(sel[:, 0, bass.ds(n, 1)]), mem[part][:, cols], start=True, stop=False)
                    nc.tensor.matmul(k.bank[bank], onto_all(sel[:, which, bass.ds(n, 1)]), mem["lo"][:, cols],
                                     start=False, stop=True).then_inc(q[ready], 1)

                def b_row(c, n, s):
                    row(c, n, "hm_b", 1, BBANK[s], "bsb_ready", "b_ready")

                def c_row(c, n, s):
                    row(c, n, "hm_c", 2, 4 + s, "hc_ready", "c_ready")

                def add_up(c, n, s):
                    pe.wait_ge(q["hc_ready"], c * SN + n + 3)
                    for e in range(SE):
                        i = nc.tensor.matmul(k.bank[e], k.ident[:], hc[:, s, e, :], start=False, stop=False)
                    i.then_inc(q["hc_free"], 1)

                with pe.Fori(0, SNC) as c:
                    for n in range(LEAD):
                        b_row(c, n, n)
                    c_row(c, 0, 0)
                    pe.wait_ge(q["y_read"], c + 1)
                    for e in range(SE):
                        nc.tensor.matmul(k.bank[e], zero[:, 0:P], zero[:], start=True, stop=False)

                    def step(n, s):
                        b_row(c, n + LEAD, (s + LEAD) % NS)
                        c_row(c, n + 1, (s + 1) % 2)
                        add_up(c, n, s % 2)

                    with pe.Fori(0, SN // NS - 1) as n4:
                        for s in range(NS):
                            step(n4 * NS + s, s)
                    step(SN - NS, 0)
                    for n in range(SN - LEAD, SN):
                        if n + 1 < SN:
                            c_row(c, n + 1, (n + 1) % 2)
                        add_up(c, n, n % 2)
                    for e in range(SE):
                        i = nc.tensor.matmul(k.bank[e], k.ident[:], xc[:, e, bass.ds(c * SCH, SCH)], start=False, stop=True)
                    i.then_inc(q["y_ready"], 1)

            @block.scalar
            def _(act):
                act.wait_ge(q["zeroed"], 1)
                nc.scalar.activation(bsb[:, 0, 0:1], bsb[:, 0, 0:1], ACT.Exp)
                act.drain()
                with act.Fori(0, SNC) as c:
                    with act.Fori(0, SN // NS) as n4:
                        for s in range(NS):
                            n = n4 * NS + s
                            it = c * SN + n
                            act.wait_ge(q["scanned"], it + 1)
                            for e in range(SE):
                                d3 = dt[:, e, bass.ds(c * SCH, SCH)].rearrange("p (b t) -> p b t", t=T)
                                i = nc.scalar.activation(dA[:, s, e, :].rearrange("p (b t) -> p b t", t=T)[:, :, 1:], d3[:, :, 1:],
                                                         ACT.Exp, scale=mem["A"][:, e, bass.ds(n, 1)])
                            i.then_inc(q["da_ready"], 1)
                            act.wait_ge(q["b_ready"], it + 1)
                            act.wait_ge(q["dbx_ready"], it + 1)
                            nc.scalar.activation(bsb[:, s, :], k.bank[BBANK[s]], ACT.Copy).then_inc(q["bsb_ready"], 1)

            @block.gpsimd
            def _(pool):
                nc.gpsimd.memset(zero[:], 0.0)
                nc.gpsimd.memset(bsb[:], 0.0)
                nc.gpsimd.memset(dA[:], 0.0).then_inc(q["zeroed"], 1)
                for n, slots in (("bsb_ready", NS), ("dbx_ready", NS), ("scanned", NS), ("hc_ready", 2), ("hc_free", 2)):
                    pool.sem_inc(q[n], slots)
                pool.sem_inc(q["y_read"], 1)
                with pool.Fori(0, SNC) as c:
                    with pool.Fori(0, SN // NS) as n4:
                        for s in range(NS):
                            it = c * SN + n4 * NS + s
                            pool.wait_ge(q["bsb_ready"], it + NS + 1)
                            pool.wait_ge(q["scanned"], it + 1)
                            pool.sem_inc(q["through_pool"], 1)
                            nc.gpsimd.tensor_tensor(dBx[:, s], dtx[:, :, bass.ds(c * SCH, SCH)], across(bsb[:, s, :], SE),
                                                    ALU.mult).then_inc(q["dbx_ready"], 1)

            @block.vector
            def _(dve):
                v = nc.vector

                def scan(c, n, s):
                    it = c * SN + n
                    dve.wait_ge(q["da_ready"], it + 1)
                    dve.wait_ge(q["dbx_ready"], it + NS + 1)
                    dve.wait_ge(q["hc_ready"], it + 1)
                    flat = lambda a: a.rearrange("p e t -> p (e t)")
                    v.tensor_tensor_scan(flat(h[:, s % 2]), flat(dA[:, s]), flat(dBx[:, s]), 0.0, ALU.mult,
                                         ALU.add).then_inc(q["scanned"], 1)

                def times_c(c, n, s):
                    it = c * SN + n
                    dve.wait_ge(q["c_ready"], it + 1)
                    dve.wait_ge(q["hc_free"], it + 1)
                    dve.wait_ge(q["scanned"], it + NS + 1)
                    v.tensor_tensor(hc[:, s], h[:, s], across(k.bank[4 + s], SE), ALU.mult).then_inc(q["hc_ready"], 1)

                with dve.Fori(0, SNC) as c:
                    scan(c, 0, 0)
                    with dve.Fori(0, SN // NS - 1) as n4:
                        for s in range(NS):
                            scan(c, n4 * NS + s + 1, (s + 1) % NS)
                            times_c(c, n4 * NS + s, s % 2)
                    for n in range(SN - NS, SN):
                        if n + 1 < SN:
                            scan(c, n + 1, (n + 1) % NS)
                        times_c(c, n, n % 2)
                    dve.wait_ge(q["y_ready"], c + 1)
                    for e in range(SE):
                        z = sz[:, e, bass.ds(c * SCH, SCH)]
                        i = v.tensor_tensor(z, k.bank[e], z, ALU.mult)
                    i.then_inc(q["y_read"], 1)


def mamba_output(k, m, mem):
    nc = k.nc
    sz, xc = mem["sz"], mem["xc"]
    with Part(k) as p:
        gated_ready, out = p.sem("gated_ready"), p.sem("out")
        with nc.Block() as block:
            @block.tensor
            def _(pe):
                pe.wait_ge(gated_ready, 1)
                for t in range(NT):
                    for e in range(SE):
                        i = nc.tensor.matmul(k.bank[t // 4][:, t % 4 * D:(t % 4 + 1) * D], xc[:, e, t * P:(t + 1) * P],
                                             mem["wout"][:, e, :], start=e == 0, stop=e == SE - 1)
                    if t % 4 == 3:
                        i.then_inc(out, 1)

            @block.vector
            def _(dve):
                v = nc.vector
                for e in range(SE):
                    src = sz[:, e, :].rearrange("p (b t) -> p b t", t=T)
                    if m == 2:
                        src = src[:, :, ::-1]
                    v.tensor_copy(xc[:, e, :].rearrange("p (b t) -> p b t", t=T), src)
                dve.drain()
                v.engine_nop().then_inc(gated_ready, 1)
                for g in range(4):
                    dve.wait_ge(out, g + 1)
                    y, o = k.Y[:, 4 * g:4 * g + 4, :], k.bank[g].rearrange("p (t d) -> p t d", d=D)
                    if m == 1:
                        v.tensor_copy(y, o)
                    else:
                        v.tensor_tensor(y, o, y, ALU.add)
                dve.drain()


def blocks():
    return [gated_delta, window_attn, plucker_attn, ffn_ternary, flash_attn, ffn_experts, bi_mamba, ffn_int8]


def build_program(nc, dram, todo=None):
    with ExitStack() as ctx:
        k = Core(nc, dram, ctx)
        load_residual(k)
        todo = blocks() if todo is None else todo
        for n, block in enumerate(todo):
            normalise(k, add_y=n > 0)
            block(k)
        normalise(k, add_y=True, make_ht=False)
        store_residual(k)


def tokens_first(a):
    a = a.reshape(-1, P, a.shape[-1])
    return a.transpose(1, 0, 2)


def by_blocks(a):
    return a.reshape(-1, P, a.shape[-1]).transpose(1, 0, 2)


def laid_out(i):
    import numpy as np
    d = {}
    d["x"] = tokens_first(i["L0_attn_x"].reshape(-1, D))
    d["ident"] = np.eye(P, dtype=np.float32)
    d["iota8"] = np.arange(8, dtype=np.float32)
    d["l1f_w12"] = np.stack([i["L1_ffn_w1_w"].T, i["L1_ffn_w2_w"].T], 1)
    d["l1f_sc"] = np.stack([i[f"L1_ffn_{n}_s"].reshape(4, P).T for n in ("w1", "w2", "h1", "h2")], 1)
    d["l1f_wh"] = np.stack([by_blocks(i[f"L1_ffn_{n}_w"].T) for n in ("h1", "h2")], 1)
    d["l1f_w3"] = by_blocks(i["L1_ffn_w3_w"].T)
    d["l1f_s3"] = i["L1_ffn_w3_s"]
    d["l2f_gw"], d["l2f_gb"] = i["L2_ffn_gate_W"], i["L2_ffn_gate_b"]
    d["l2f_ew"] = i["L2_ffn_expert_W"].transpose(1, 0, 2).reshape(D, -1)
    d["l2f_eb"] = i["L2_ffn_expert_b"].reshape(1, -1)
    d["l3f_wgu"] = np.concatenate([i["L3_ffn_w_gate"].T, i["L3_ffn_w_up"].T], 1)
    d["l3f_wd"] = by_blocks(i["L3_ffn_w_down"].T).reshape(P, -1)
    for lay_out in (lay_out_delta, lay_out_window, lay_out_plucker, lay_out_flash, lay_out_mamba):
        lay_out(i, d, np)
    return {n: np.ascontiguousarray(a) for n, a in d.items()}


def kernel(**inputs):
    import numpy as np
    import concourse.bacc as bacc
    from concourse.bass_utils import run_bass_kernel_spmd

    arrays = laid_out({n: np.asarray(a) for n, a in inputs.items()})
    nc = bacc.Bacc("TRN2", target_bir_lowering=False, num_devices=1)
    dram = {n: nc.dram_tensor(f"in_{n}", a.shape, mybir.dt.from_np(a.dtype), kind="ExternalInput").ap()
            for n, a in arrays.items()}
    dram["out"] = nc.dram_tensor("out_0", (P, NT, D), F32, kind="ExternalOutput").ap()
    build_program(nc, dram)
    r = run_bass_kernel_spmd(nc, [{f"in_{n}": a for n, a in arrays.items()}], core_ids=[0])
    return r.results[0]["out_0"].transpose(1, 0, 2).reshape(B, T, D)
```

```python
from contextlib import ExitStack

import concourse.bass as bass
from concourse import mybir

F32 = mybir.dt.float32
BF16 = mybir.dt.bfloat16
I32 = mybir.dt.int32
ALU = mybir.AluOpType
ACT = mybir.ActivationFunctionType
AXX = mybir.AxisListType.X

P = 128
B, T, D = 8, 256, 128
NT = B * T // P
TPB = T // P
PAD = 4
LNEPS = 1e-5


class Core:

    def __init__(self, nc, dram, ctx):
        self.nc, self.dram, self.parts, self.cleared = nc, dram, 0, []
        sb = lambda name, shape, dt=F32: ctx.enter_context(nc.sbuf_tensor(name, shape, dt))
        self.banks = ctx.enter_context(nc.psum_tensor("banks", [P, 8, 512], F32))
        self.bank = [self.banks[:, i, :] for i in range(8)]
        self.X = sb("residual", [P, NT, D])
        self.Y = sb("block_out", [P, NT, D])
        self.HT = sb("norm_featmajor", [P, B, PAD + T])
        self.H = sb("norm", [P, NT, D])
        self.ident = sb("ident", [P, P])


class Part:

    def __init__(self, k):
        self.k, self.nc, self.ctx, self.sems = k, k.nc, ExitStack(), []
        k.parts += 1
        self.id = k.parts

    def __enter__(self):
        return self

    def sb(self, name, shape, dt=F32):
        return self.ctx.enter_context(self.nc.sbuf_tensor(f"{name}_{self.id}", shape, dt))

    def sem(self, name):
        self.sems.append(self.nc.alloc_semaphore(f"{name}_{self.id}"))
        return self.sems[-1]

    def __exit__(self, *a):
        if a[0] is None:
            for s in self.k.cleared:
                self.nc.release_semaphore(s)
            for s in self.sems:
                self.nc.gpsimd.sem_clear(s)
            self.k.cleared = self.sems
        return self.ctx.__exit__(*a)


def over(ap, n):
    return ap.unsqueeze(len(ap.shape)).to_broadcast([*ap.shape, n])


def across(ap, n):
    return ap.unsqueeze(1).to_broadcast([ap.shape[0], n, *ap.shape[1:]])


def load_residual(k):
    nc = k.nc
    with Part(k) as p:
        loaded = p.sem("loaded")
        with nc.Block() as block:
            @block.sync
            def _(sp):
                sp.dma_start(k.X[:], k.dram["x"]).then_inc(loaded, 16)
                sp.dma_start(k.ident[:], k.dram["ident"]).then_inc(loaded, 16)
                sp.wait_ge(loaded, 32)

            @block.vector
            def _(dve):
                nc.vector.memset(k.HT[:], 0.0)


def store_residual(k):
    nc = k.nc
    with Part(k) as p:
        stored = p.sem("stored")
        with nc.Block() as block:
            @block.sync
            def _(sp):
                sp.dma_start(k.dram["out"], k.X[:]).then_inc(stored, 16)
                sp.wait_ge(stored, 16)


def layer_norm_steps(nc, dve, src, stats, mv, rstd, var_ready, rstd_ready, r, apply):
    HALF = NT // 2
    for half in range(2):
        tiles = range(half * HALF, (half + 1) * HALF)
        for t in tiles:
            nc.vector.bn_stats(stats[:, t, :], src[:, t, :])
        dve.drain()
        for t in tiles:
            nc.vector.bn_aggr(mv[:, t, :], stats[:, t, :])
        dve.drain()
        cols = slice(half * HALF, (half + 1) * HALF)
        nc.vector.tensor_scalar_add(rstd[:, cols], mv[:, cols, 1], LNEPS).then_inc(var_ready, 1)
    for half in range(2):
        dve.wait_ge(rstd_ready, 2 * r + half + 1)
        for t in range(half * HALF, (half + 1) * HALF):
            apply(t)


def normalise(k, add_y=False, make_ht=True, src=None, affine=None, norm=True, meanwhile=None):
    nc = k.nc
    src = k.X if src is None else src
    rounds = int(add_y) + int(make_ht and norm)
    with Part(k) as p:
        stats = p.sb("stats", [P, NT, 6])
        mv = p.sb("meanvar", [P, NT, 2])
        rstd = p.sb("rstd", [P, NT])
        half = p.sb("minus_half", [P, NT])
        H = k.H
        var_ready, rstd_ready = p.sem("var"), p.sem("rstd")
        tile_ready, h_ready, turned = p.sem("tile"), p.sem("h"), p.sem("turned")
        turn_from = H if norm else src
        early = norm and affine is None
        with nc.Block() as block:
            if meanwhile is not None:
                @block.sync
                def _(sp):
                    meanwhile(sp)

            @block.gpsimd
            def _(pool):
                nc.gpsimd.memset(half[:], -0.5)
                pool.drain()
                for n in range(2 * rounds):
                    cols = slice(n % 2 * NT // 2, (n % 2 + 1) * NT // 2)
                    pool.wait_ge(var_ready, n + 1)
                    nc.gpsimd.tensor_tensor(rstd[:, cols], rstd[:, cols], half[:, cols], ALU.pow).then_inc(rstd_ready, 1)

            @block.vector
            def _(dve):
                def into_h(x):
                    return lambda t: nc.vector.tensor_scalar(H[:, t, :], x[:, t, :], mv[:, t, 0:1], rstd[:, t:t + 1],
                                                             ALU.subtract, ALU.mult)

                r = 0
                if add_y:
                    layer_norm_steps(nc, dve, k.Y, stats, mv, rstd, var_ready, rstd_ready, r, into_h(k.Y))
                    r += 1
                    dve.drain()
                    nc.vector.tensor_add(k.X[:], k.X[:], H[:])
                    dve.drain()
                if make_ht and norm:
                    layer_norm_steps(nc, dve, src, stats, mv, rstd, var_ready, rstd_ready, r,
                                     lambda t: into_h(src)(t).then_inc(tile_ready, 1))
                    if affine is not None:
                        dve.drain()
                        nc.vector.tensor_tensor(H[:], H[:], across(affine[:, 0, :], NT), ALU.mult)
                        dve.drain()
                        nc.vector.tensor_tensor(H[:], H[:], across(affine[:, 1, :], NT), ALU.add)
                        dve.drain()
                if not early:
                    nc.vector.engine_nop().then_inc(h_ready, 1)

            if make_ht:
                @block.tensor
                def _(pe):
                    if not early:
                        pe.wait_ge(h_ready, 1)
                    for t in range(NT):
                        if early:
                            pe.wait_ge(tile_ready, t + 1)
                        i = nc.tensor.transpose(k.bank[t // 4][:, t % 4 * P:(t % 4 + 1) * P], turn_from[:, t, :], k.ident[:])
                        if t % 4 == 3:
                            i.then_inc(turned, 1)

                @block.scalar
                def _(act):
                    for g in range(4):
                        act.wait_ge(turned, g + 1)
                        nc.scalar.activation(k.HT[:, 2 * g:2 * g + 2, PAD:PAD + T],
                                             k.bank[g][:].rearrange("p (b t) -> p b t", b=2), ACT.Copy)
                    act.drain()


def ffn_ternary(k, add_y):
    nc, HID, CH = k.nc, 512, 512
    KB, NCH = HID // P, B * T // CH
    bpc = CH // T
    with Part(k) as p:
        w12 = p.sb("w12", [P, 2, HID])
        wh = p.sb("wh", [P, 2, KB, HID])
        w3 = p.sb("w3", [P, KB, D])
        sc = p.sb("scales", [P, 4, KB])
        s3 = p.sb("s3", [P, D])
        gate = p.sb("gate", [P, KB, CH])
        hid = [p.sb(f"hid{i}", [P, KB, CH]) for i in range(3)]
        loaded, w3_loaded = p.sem("loaded"), p.sem("w3_loaded")
        pair, gated, prod = p.sem("pair"), p.sem("gated"), p.sem("prod")
        lin = [p.sem("lin1"), p.sem("lin2")]
        gelu = [p.sem("gelu1"), p.sem("gelu2")]
        down, out = p.sem("down"), p.sem("out")
        def weights(sp):
            sp.dma_start(w12[:], k.dram["l1f_w12"]).then_inc(loaded, 16)
            sp.dma_start(sc[:], k.dram["l1f_sc"]).then_inc(loaded, 16)
            sp.dma_start(wh[:], k.dram["l1f_wh"]).then_inc(loaded, 16)
            sp.dma_start(w3[:], k.dram["l1f_w3"]).then_inc(w3_loaded, 16)
            sp.dma_start(s3[:], k.dram["l1f_s3"].partition_broadcast(P)).then_inc(w3_loaded, 16)

        normalise(k, add_y, meanwhile=weights)
        with nc.Block() as block:
            @block.tensor
            def _(pe):
                pe.wait_ge(loaded, 48)
                pe.wait_ge(w3_loaded, 32)
                with pe.Fori(0, NCH) as c:
                    x = k.HT[:, bass.ds(c * bpc, bpc), PAD:PAD + T]
                    pe.wait_ge(out, c + 1)
                    for ob in range(KB):
                        for j in range(2):
                            i = nc.tensor.matmul(k.bank[4 * j + ob][:].rearrange("p (b t) -> p b t", b=bpc),
                                                 w12[:, j, ob * P:(ob + 1) * P], x, start=True, stop=True)
                        i.then_inc(pair, 1)
                    for l in range(2):
                        pe.wait_ge(*((prod, c * KB + KB) if l == 0 else (gelu[0], c * KB + KB)))
                        for ob in range(KB):
                            for kb in range(KB):
                                i = nc.tensor.matmul(k.bank[4 * l + ob][:], wh[:, l, kb, ob * P:(ob + 1) * P],
                                                     hid[l][:, kb, :], start=kb == 0, stop=kb == KB - 1)
                            i.then_inc(lin[l], 1)
                    pe.wait_ge(gelu[1], c * KB + KB)
                    for tt in range(CH // P):
                        for kb in range(KB):
                            i = nc.tensor.matmul(k.bank[0][:, tt * D:(tt + 1) * D], hid[2][:, kb, tt * P:(tt + 1) * P],
                                                 w3[:, kb, :], start=kb == 0, stop=kb == KB - 1)
                    i.then_inc(down, 1)

            @block.scalar
            def _(act):
                act.wait_ge(loaded, 48)
                with act.Fori(0, NCH) as c:
                    for ob in range(KB):
                        act.wait_ge(pair, c * KB + ob + 1)
                        nc.scalar.activation(gate[:, ob, :], k.bank[ob][:], ACT.Silu,
                                             scale=sc[:, 0, ob:ob + 1]).then_inc(gated, 1)
                    for l in range(2):
                        for ob in range(KB):
                            act.wait_ge(lin[l], c * KB + ob + 1)
                            nc.scalar.activation(hid[l + 1][:, ob, :], k.bank[4 * l + ob][:], ACT.Gelu,
                                                 scale=sc[:, 2 + l, ob:ob + 1]).then_inc(gelu[l], 1)

            @block.vector
            def _(dve):
                dve.sem_inc(out, 1)
                dve.wait_ge(w3_loaded, 32)
                dve.wait_ge(loaded, 48)
                with dve.Fori(0, NCH) as c:
                    for ob in range(KB):
                        dve.wait_ge(gated, c * KB + ob + 1)
                        nc.vector.scalar_tensor_tensor(out=hid[0][:, ob, :], in0=k.bank[4 + ob][:],
                                                       scalar=sc[:, 1, ob:ob + 1], in1=gate[:, ob, :],
                                                       op0=ALU.mult, op1=ALU.mult).then_inc(prod, 1)
                    dve.wait_ge(down, c + 1)
                    nc.vector.tensor_tensor(k.Y[:, bass.ds(c * (CH // P), CH // P), :],
                                            k.bank[0][:].rearrange("p (t d) -> p t d", d=D),
                                            across(s3[:], CH // P), ALU.mult).then_inc(out, 1)


def ffn_int8(k, add_y):
    nc, HID, CH = k.nc, 384, 512
    KB, NCH = HID // P, B * T // CH
    bpc = CH // T
    NW = 2 * HID + KB * D
    with Part(k) as p:
        wi = p.sb("w_int", [P, NW], I32)
        w = p.sb("w", [P, NW])
        gate = p.sb("gate", [P, KB, CH])
        hid = p.sb("hid", [P, KB, CH])
        loaded, scaled = p.sem("loaded"), p.sem("scaled")
        pair, gated, prod, down, out = p.sem("pair"), p.sem("gated"), p.sem("prod"), p.sem("down"), p.sem("out")
        def weights(sp):
            sp.dma_start(wi[:, 0:2 * HID], k.dram["l3f_wgu"]).then_inc(loaded, 16)
            sp.dma_start(wi[:, 2 * HID:], k.dram["l3f_wd"]).then_inc(loaded, 16)

        normalise(k, add_y, meanwhile=weights)
        with nc.Block() as block:
            @block.tensor
            def _(pe):
                pe.wait_ge(scaled, 1)
                with pe.Fori(0, NCH) as c:
                    x = k.HT[:, bass.ds(c * bpc, bpc), PAD:PAD + T]
                    pe.wait_ge(out, c + 1)
                    for ob in range(KB):
                        for j in range(2):
                            i = nc.tensor.matmul(k.bank[KB * j + ob][:].rearrange("p (b t) -> p b t", b=bpc),
                                                 w[:, j * HID + ob * P:j * HID + (ob + 1) * P], x,
                                                 start=True, stop=True)
                        i.then_inc(pair, 1)
                    pe.wait_ge(prod, c * KB + KB)
                    for tt in range(CH // P):
                        for kb in range(KB):
                            i = nc.tensor.matmul(k.bank[6][:, tt * D:(tt + 1) * D], hid[:, kb, tt * P:(tt + 1) * P],
                                                 w[:, 2 * HID + kb * D:2 * HID + (kb + 1) * D],
                                                 start=kb == 0, stop=kb == KB - 1)
                    i.then_inc(down, 1)

            @block.scalar
            def _(act):
                with act.Fori(0, NCH) as c:
                    for ob in range(KB):
                        act.wait_ge(pair, c * KB + ob + 1)
                        nc.scalar.activation(gate[:, ob, :], k.bank[ob][:], ACT.Silu).then_inc(gated, 1)

            @block.vector
            def _(dve):
                dve.sem_inc(out, 1)
                dve.wait_ge(loaded, 32)
                nc.vector.tensor_scalar(w[:], wi[:], 1.0 / 127.0, None, ALU.mult).then_inc(scaled, 1)
                with dve.Fori(0, NCH) as c:
                    for ob in range(KB):
                        dve.wait_ge(gated, c * KB + ob + 1)
                        nc.vector.tensor_tensor(hid[:, ob, :], k.bank[KB + ob][:], gate[:, ob, :],
                                                ALU.mult).then_inc(prod, 1)
                    dve.wait_ge(down, c + 1)
                    nc.vector.tensor_copy(k.Y[:, bass.ds(c * (CH // P), CH // P), :],
                                          k.bank[6][:].rearrange("p (t d) -> p t d", d=D)).then_inc(out, 1)


def ffn_experts(k, add_y):
    nc, E, TOPK, EPS, THRES = k.nc, 8, 2, 1e-4, 0.1
    with Part(k) as p:
        gw, gb = p.sb("gate_w", [P, E]), p.sb("gate_b", [P, E])
        ew, eb = p.sb("expert_w", [P, E * D]), p.sb("expert_b", [1, E * D])
        iota, ones = p.sb("iota", [P, E]), p.sb("ones", [1, P])
        xb = p.sb("x_batch", [P, 2, T])
        S, M, W, V = (p.sb(n, [P, NT, E]) for n in ("score", "mask", "weight", "tmp"))
        r = p.sb("row", [P, NT])
        loaded, xb_ready = p.sem("loaded"), p.sem("xb_ready")
        gates, exped, clipped = p.sem("gates"), p.sem("exped"), p.sem("clipped")
        experts, mixed, ones_ready = p.sem("experts"), p.sem("mixed"), p.sem("ones")
        sc3 = k.bank[0][:, 0:NT * E].rearrange("p (t e) -> p t e", e=E)
        def weights(sp):
            sp.dma_start(gw[:], k.dram["l2f_gw"]).then_inc(loaded, 16)
            sp.dma_start(gb[:], k.dram["l2f_gb"].partition_broadcast(P)).then_inc(loaded, 16)
            sp.dma_start(ew[:], k.dram["l2f_ew"]).then_inc(loaded, 16)
            sp.dma_start(eb[:], k.dram["l2f_eb"]).then_inc(loaded, 16)
            sp.dma_start(iota[:], k.dram["iota8"].partition_broadcast(P)).then_inc(loaded, 16)

        normalise(k, add_y, meanwhile=weights)
        with nc.Block() as block:
            @block.gpsimd
            def _(pool):
                nc.gpsimd.memset(ones[:], 1.0).then_inc(ones_ready, 1)

            @block.tensor
            def _(pe):
                pe.wait_ge(loaded, 80)
                pe.wait_ge(ones_ready, 1)
                for t in range(NT):
                    i = nc.tensor.matmul(sc3[:, t, :], k.HT[:, t // TPB, PAD + t % TPB * P:PAD + (t % TPB + 1) * P],
                                         gw[:], start=True, stop=True)
                i.then_inc(gates, 1)
                with pe.Fori(0, B // 2) as bb:
                    pe.wait_ge(xb_ready, bb + 1)
                    for s in range(2):
                        for t in range(TPB):
                            u = 2 * s + t
                            pe.wait_ge(mixed, bb * 4 + u + 1)
                            for h in range(2):
                                o = k.bank[2 * u + h][:]
                                nc.tensor.matmul(o, ones[:], eb[:, h * 512:(h + 1) * 512], start=True, stop=False)
                                i = nc.tensor.matmul(o, xb[:, s, t * P:(t + 1) * P], ew[:, h * 512:(h + 1) * 512],
                                                     start=False, stop=True)
                            i.then_inc(experts, 1)

            @block.scalar
            def _(act):
                act.wait_ge(clipped, 1)
                nc.scalar.activation(W[:], S[:], ACT.Exp).then_inc(exped, 1)

            @block.vector
            def _(dve):
                v = nc.vector
                dve.sem_inc(mixed, 4)
                dve.wait_ge(loaded, 80)
                dve.wait_ge(gates, 1)
                v.tensor_tensor(S[:], sc3, across(gb[:], NT), ALU.add)
                dve.drain()
                v.tensor_scalar_max(S[:], S[:], EPS)
                dve.drain()
                v.tensor_reduce(r[:], S[:], AXX, ALU.max)
                dve.drain()
                v.tensor_tensor(S[:], S[:], over(r[:], E), ALU.subtract).then_inc(clipped, 1)
                dve.wait_ge(exped, 1)
                v.tensor_reduce(r[:], W[:], AXX, ALU.add)
                dve.drain()
                v.reciprocal(r[:], r[:])
                dve.drain()
                v.tensor_tensor(W[:], W[:], over(r[:], E), ALU.mult)
                dve.drain()
                v.tensor_copy(S[:], W[:])
                v.memset(M[:], 0.0)
                for _ in range(TOPK):
                    dve.drain()
                    v.tensor_reduce(r[:], S[:], AXX, ALU.max)
                    dve.drain()
                    v.tensor_tensor(V[:], S[:], over(r[:], E), ALU.is_equal)
                    dve.drain()
                    v.scalar_tensor_tensor(out=V[:], in0=V[:], scalar=-100.0, in1=across(iota[:], NT),
                                           op0=ALU.mult, op1=ALU.add)
                    dve.drain()
                    v.tensor_reduce(r[:], V[:], AXX, ALU.min)
                    dve.drain()
                    v.tensor_tensor(V[:], V[:], over(r[:], E), ALU.is_equal)
                    dve.drain()
                    v.tensor_add(M[:], M[:], V[:])
                    v.scalar_tensor_tensor(out=S[:], in0=V[:], scalar=-2.0, in1=S[:], op0=ALU.mult, op1=ALU.add)
                dve.drain()
                v.scalar_tensor_tensor(out=W[:], in0=W[:], scalar=THRES, in1=M[:], op0=ALU.max, op1=ALU.mult)
                dve.drain()
                v.tensor_reduce(r[:], W[:], AXX, ALU.add)
                dve.drain()
                v.reciprocal(r[:], r[:])
                dve.drain()
                v.scalar_tensor_tensor(out=W[:], in0=W[:], scalar=1.0 / TOPK, in1=over(r[:], E),
                                       op0=ALU.mult, op1=ALU.mult)
                dve.drain()
                with dve.Fori(0, B // 2) as bb:
                    v.tensor_copy(xb[:], k.HT[:, bass.ds(bb * 2, 2), PAD:PAD + T]).then_inc(xb_ready, 1)
                    for s in range(2):
                        for t in range(TPB):
                            u = 2 * s + t
                            dve.wait_ge(experts, bb * 4 + u + 1)
                            y = k.Y[:, bb * 4 + u, :]
                            for e in range(E):
                                o = k.bank[2 * u + e // 4][:, e % 4 * D:(e % 4 + 1) * D]
                                c = W[:, bb * 4 + u, e:e + 1]
                                if e == 0:
                                    i = v.tensor_scalar(y, o, c, None, ALU.mult)
                                else:
                                    i = v.scalar_tensor_tensor(out=y, in0=o, scalar=c, in1=y,
                                                               op0=ALU.mult, op1=ALU.add)
                                if e < E - 1:
                                    dve.drain()
                            i.then_inc(mixed, 1)


def lay_out_flash(i, d, np):
    for n in "qkv":
        d[f"l2a_w{n}"] = i[f"L2_attn_W{n}"]
    d["l2a_wo"] = by_blocks(i["L2_attn_Wo"])
    d["l2a_forget"] = np.tile(np.array([-3e38, 0, 0, 0], np.float32), 4)
    d["l2a_keep"] = np.tile(np.array([0, 1, 1, 1], np.float32), 4)


def flash_attn(k, add_y):
    nc, H, DK, NJ = k.nc, 16, 64, 4
    C = H * DK
    CB = C // P
    HG = 4
    units = [(g, t) for g in range(H // HG) for t in range(TPB)]
    NU = len(units)
    with Part(k) as p:
        w = {n: p.sb("w" + n, [P, C]) for n in "qkv"}
        wo = p.sb("wo", [P, CB, D])
        forget, keep = p.sb("forget", [P, 16]), p.sb("keep", [P, 16])
        xb = p.sb("x_batch", [P, T])
        qk2 = p.sb("qk_featmajor", [P, 2, 2, CB, T])
        v2 = p.sb("v", [P, 2, TPB, C])
        S = p.sb("probs", [P, 2, HG, T])
        SW = p.sb("weighted", [P, 2, HG, T])
        PT = p.sb("weighted_keymajor", [P, 2, HG * TPB, P])
        O = p.sb("heads_out", [P, TPB, C])
        OT = p.sb("heads_out_featmajor", [P, CB, T])
        bm, m, al, ls, rs, f = (p.sb(n, [P, 2, 16]) for n in ("bm", "m", "alpha", "l", "rowsum", "f"))
        loaded, xb_ready = p.sem("loaded"), p.sem("xb_ready")
        proj, projected = p.sem("proj"), p.sem("projected")
        scores, shifted, exped = p.sem("scores"), p.sem("shifted"), p.sem("exped")
        w_ready, weighted, turned, pt_ready = p.sem("w_ready"), p.sem("weighted"), p.sem("turned"), p.sem("pt_ready")
        heads, heads_out = p.sem("heads"), p.sem("heads_out")
        o_turned, ot_ready, final, done = p.sem("o_turned"), p.sem("ot_ready"), p.sem("final"), p.sem("done")

        qk_flat = [qk2[:, n].rearrange("p a c t -> p (a c t)") for n in range(2)]
        v_flat = [v2[:, n].rearrange("p a c -> p (a c)") for n in range(2)]
        dest = lambda slot, n: (qk_flat if n < 8 else v_flat)[slot][:, n % 8 * 512:(n % 8 + 1) * 512]
        FILLS = ((0, 1), (2, 3), (4, 5), (6, 7), (8,), (9,), (10,), (11,))

        def batches(eng, batch):
            with eng.Fori(0, B // 2 - 1) as i:
                batch(2 * i, 0, 2 * i + 1)
                batch(2 * i + 1, 1, 2 * i + 2)
            batch(B - 2, 0, B - 1)
            batch(B - 1, 1, None)

        def weights(sp):
            for n in "qkv":
                sp.dma_start(w[n][:], k.dram[f"l2a_w{n}"]).then_inc(loaded, 16)
            sp.dma_start(forget[:], k.dram["l2a_forget"].partition_broadcast(P)).then_inc(loaded, 16)
            sp.dma_start(keep[:], k.dram["l2a_keep"].partition_broadcast(P)).then_inc(loaded, 16)
            sp.dma_start(wo[:], k.dram["l2a_wo"]).then_inc(loaded, 16)

        normalise(k, add_y, meanwhile=weights)
        with nc.Block() as block:
            @block.tensor
            def _(pe):
                pe.wait_ge(loaded, 96)

                def project(b, slot, n):
                    if n == 0:
                        pe.wait_ge(xb_ready, b + 1)
                    if n > 0 or not isinstance(b, int) or b > 0:
                        pe.wait_ge(projected, b * 12 + n)
                    o = k.bank[7]
                    if n < 8:
                        for h in range(2):
                            c = n % 4 * 2 + h
                            i = nc.tensor.matmul(o[:, h * T:(h + 1) * T], w["qk"[n // 4]][:, c * P:(c + 1) * P], xb[:],
                                                 start=True, stop=True)
                    else:
                        t, h = (n - 8) // 2, (n - 8) % 2
                        i = nc.tensor.matmul(o, xb[:, t * P:(t + 1) * P], w["v"][:, h * 512:(h + 1) * 512],
                                             start=True, stop=True)
                    i.then_inc(proj, 1)

                def score(b, slot, u):
                    g, t = units[u]
                    s = u % 2
                    if u == 0:
                        pe.wait_ge(projected, b * 12 + 8)
                    pe.wait_ge(shifted, b * NU + u + 1)
                    for h in range(HG):
                        c, r = (g * HG + h) // 2, (g * HG + h) % 2 * DK
                        i = nc.tensor.matmul(k.bank[2 * s + h % 2][:, h // 2 * T:(h // 2 + 1) * T],
                                             qk2[r:r + DK, slot, 0, c, t * P:(t + 1) * P], qk2[r:r + DK, slot, 1, c, :],
                                             start=True, stop=True)
                    i.then_inc(scores, 1)

                def turn(b, u):
                    s = u % 2
                    pe.wait_ge(weighted, b * NU + u + 3)
                    pe.wait_ge(pt_ready, b * NU + u + 1)
                    for h in range(HG):
                        for kt in range(TPB):
                            n = h * TPB + kt
                            i = nc.tensor.transpose(k.bank[4 + n // 4][:, n % 4 * P:(n % 4 + 1) * P],
                                                    SW[:, s, h, kt * P:(kt + 1) * P], k.ident[:])
                    i.then_inc(turned, 1)

                def values(b, slot, u):
                    g, t = units[u]
                    s = u % 2
                    pe.wait_ge(pt_ready, b * NU + u + 2)
                    pe.wait_ge(heads_out, b * NU + u + 1)
                    if u == 0:
                        pe.wait_ge(done, b + 1)
                        pe.wait_ge(projected, b * 12 + 12)
                    for h in range(HG):
                        hd = g * HG + h
                        at = h % 2 * 2 + h // 2
                        for kt in range(TPB):
                            i = nc.tensor.matmul(k.bank[6][:, h * DK:(h + 1) * DK], PT[:, s, at * TPB + kt, :],
                                                 v2[:, slot, kt, hd * DK:(hd + 1) * DK], start=kt == 0, stop=kt == TPB - 1)
                    i.then_inc(heads, 1)

                def batch(b, slot, behind):
                    more = behind is not None
                    for u in range(NU):
                        if more:
                            project(behind, 1 - slot, FILLS[u][0])
                        if u + 2 < NU:
                            score(b, slot, u + 2)
                        elif more:
                            score(behind, 1 - slot, u + 2 - NU)
                        if more and len(FILLS[u]) > 1:
                            project(behind, 1 - slot, FILLS[u][1])
                        turn(b, u)
                        if u > 0:
                            values(b, slot, u - 1)
                    values(b, slot, NU - 1)
                    pe.wait_ge(pt_ready, b * NU + NU + 1)
                    pe.wait_ge(heads_out, b * NU + NU + 1)
                    if more:
                        pe.wait_ge(projected, behind * 12 + 12)
                    for c in range(CB):
                        for t in range(TPB):
                            n = c * TPB + t
                            i = nc.tensor.transpose(k.bank[4 + n // 4][:, n % 4 * P:(n % 4 + 1) * P],
                                                    O[:, t, c * P:(c + 1) * P], k.ident[:])
                            if n % 4 == 3:
                                i.then_inc(o_turned, 1)
                    pe.wait_ge(ot_ready, b * 4 + 4)
                    for t in range(TPB):
                        for c in range(CB):
                            i = nc.tensor.matmul(k.bank[6][:, t * D:(t + 1) * D], OT[:, c, t * P:(t + 1) * P],
                                                 wo[:, c, :], start=c == 0, stop=c == CB - 1)
                    i.then_inc(final, 1)

                for n in range(12):
                    project(0, 0, n)
                score(0, 0, 0)
                score(0, 0, 1)
                batches(pe, batch)

            @block.scalar
            def _(act):
                act.sem_inc(pt_ready, 1)
                act.sem_inc(heads_out, 1)

                def read_out(b, slot, n):
                    act.wait_ge(proj, b * 12 + n + 1)
                    nc.scalar.activation(dest(slot, n), k.bank[7], ACT.Copy).then_inc(projected, 1)

                def evacuate(b, u):
                    s = u % 2
                    act.wait_ge(turned, b * NU + u + 3)
                    for h in range(2):
                        i = nc.scalar.activation(PT[:, s, 4 * h:4 * h + 4, :],
                                                 k.bank[4 + h][:].rearrange("p (a q) -> p a q", q=P), ACT.Copy)
                    i.then_inc(pt_ready, 1)

                def out(b, u):
                    g, t = units[u]
                    act.wait_ge(heads, b * NU + u + 1)
                    nc.scalar.activation(O[:, t, g * HG * DK:(g + 1) * HG * DK], k.bank[6][:, 0:HG * DK],
                                         ACT.Copy).then_inc(heads_out, 1)

                def batch(b, slot, behind):
                    for u in range(NU):
                        s = u % 2
                        act.wait_ge(shifted, b * NU + u + 3)
                        nc.scalar.activation(al[:, s, :], al[:, s, :], ACT.Exp, scale=DK ** -0.5)
                        nc.scalar.activation(S[:, s], S[:, s], ACT.Exp, scale=DK ** -0.5).then_inc(exped, 1)
                        if u > 0:
                            evacuate(b, u - 1)
                        if behind is not None:
                            for n in FILLS[u]:
                                read_out(behind, 1 - slot, n)
                        if u > 1:
                            out(b, u - 2)
                    evacuate(b, NU - 1)
                    out(b, NU - 2)
                    out(b, NU - 1)
                    for n in range(4):
                        act.wait_ge(o_turned, b * 4 + n + 1)
                        nc.scalar.activation(OT[:, 2 * n:2 * n + 2, :], k.bank[4 + n][:].rearrange("p (c t) -> p c t", t=T),
                                             ACT.Copy).then_inc(ot_ready, 1)
                    act.wait_ge(final, b + 1)
                    nc.scalar.activation(k.Y[:, bass.ds(b * TPB, TPB), :],
                                         k.bank[6][:, 0:TPB * D].rearrange("p (t d) -> p t d", d=D), ACT.Copy).then_inc(done, 1)

                for n in range(12):
                    read_out(0, 0, n)
                batches(act, batch)

            @block.gpsimd
            def _(pool):
                pool.sem_inc(weighted, 2)
                with pool.Fori(0, B) as b:
                    for u in range(NU):
                        s = u % 2
                        pool.wait_ge(w_ready, b * NU + u + 1)
                        pool.wait_ge(turned, b * NU + u + 1)
                        nc.gpsimd.tensor_tensor(SW[:, s].rearrange("p h (j t) -> p (h j) t", j=NJ),
                                                S[:, s].rearrange("p h (j t) -> p (h j) t", j=NJ),
                                                over(f[:, s, :], T // NJ), ALU.mult).then_inc(weighted, 1)

            @block.vector
            def _(dve):
                vv = nc.vector
                dve.sem_inc(shifted, 2)
                dve.sem_inc(turned, 2)
                dve.sem_inc(done, 1)
                dve.wait_ge(loaded, 96)

                def shift(b, u):
                    s = u % 2
                    dve.wait_ge(scores, b * NU + u + 1)
                    for h in range(2):
                        vv.tensor_reduce(bm[:, s, 8 * h:8 * h + 8], k.bank[2 * s + h][:].rearrange("p (a t) -> p a t", a=8),
                                         AXX, ALU.max)
                    dve.drain()
                    vv.tensor_tensor_scan(m[:, s, :], forget[:], bm[:, s, :], 0.0, ALU.add, ALU.max)
                    dve.drain()
                    vv.tensor_tensor(al[:, s, 1:16], m[:, s, 0:15], m[:, s, 1:16], ALU.subtract)
                    dve.drain()
                    vv.memset(al[:, s, 0:1], 0.0)
                    dve.drain()
                    vv.tensor_tensor(al[:, s, :], al[:, s, :], keep[:], ALU.mult)
                    dve.wait_ge(weighted, b * NU + u + 1)
                    for h in range(2):
                        i = vv.tensor_tensor(S[:, s, 2 * h:2 * h + 2, :].rearrange("p h (j t) -> p (h j) t", j=NJ),
                                             k.bank[2 * s + h][:].rearrange("p (a t) -> p a t", a=8),
                                             over(m[:, s, 8 * h:8 * h + 8], T // NJ), ALU.subtract)
                    i.then_inc(shifted, 1)

                def weigh(b, u):
                    s = u % 2
                    dve.wait_ge(exped, b * NU + u + 1)
                    vv.tensor_reduce(rs[:, s, :], S[:, s].rearrange("p h (j t) -> p (h j) t", j=NJ), AXX, ALU.add)
                    vv.tensor_tensor(al[:, s, :], al[:, s, :], keep[:], ALU.mult)
                    dve.drain()
                    vv.tensor_tensor_scan(ls[:, s, :], al[:, s, :], rs[:, s, :], 0.0, ALU.mult, ALU.add)
                    dve.drain()
                    vv.reciprocal(f[:, s, :], ls[:, s, :])
                    dve.drain()
                    f4 = f[:, s, :].rearrange("p (h j) -> p h j", j=NJ)
                    a4 = al[:, s, :].rearrange("p (h j) -> p h j", j=NJ)
                    vv.tensor_tensor(f4[:, :, 0:3], f4[:, :, 0:3], a4[:, :, 1:4], ALU.mult)
                    for j in (2, 1, 0):
                        dve.drain()
                        i = vv.tensor_tensor(f4[:, :, j], f4[:, :, j], f4[:, :, j + 1], ALU.mult)
                    i.then_inc(w_ready, 1)

                def load_x(b):
                    vv.tensor_copy(xb[:], k.HT[:, bass.ds(b, 1), PAD:PAD + T].rearrange("p a t -> p (a t)")).then_inc(xb_ready, 1)

                def batch(b, slot, behind):
                    if behind is not None:
                        dve.wait_ge(proj, b * 12 + 12)
                        load_x(behind)
                    for u in range(NU):
                        if u + 1 < NU:
                            shift(b, u + 1)
                        elif behind is not None:
                            shift(behind, 0)
                        weigh(b, u)

                load_x(0)
                shift(0, 0)
                batches(dve, batch)


def lay_out_plucker(i, d, np):
    wq = [i["L1_attn_W1_q"].T, i["L1_attn_W2_q"].T]
    d["l1a_wx"] = np.concatenate([wq[0][:D], wq[1][:D], i["L1_attn_W1_k"].T, i["L1_attn_W2_k"].T,
                                  i["L1_attn_Wv"].T], 1)
    d["l1a_wprev"] = np.concatenate([wq[0][D:], wq[1][D:]], 1)
    d["l1a_wo"] = i["L1_attn_Wo"].T
    d["l1a_bias"] = np.stack([i["L1_attn_bv"], i["L1_attn_bo"]])
    d["causal"] = np.triu(np.ones((P, P), np.float32))


def plucker_attn(k, add_y):
    nc, H, LC = k.nc, 16, 6
    DH, SLOT = D // H, 32
    G = H // 4
    PAIRS = [(0, slice(1, 4), slice(0, 3)), (1, slice(2, 4), slice(3, 5)), (2, slice(3, 4), slice(5, 6))]
    JSIGN = [1.0, -1.0, 1.0, 1.0, -1.0, 1.0]
    with Part(k) as p:
        wx, wprev, wo = p.sb("wx", [P, 4 * 64 + D]), p.sb("wprev", [P, 2 * 64]), p.sb("wo", [P, D])
        bias = p.sb("bias", [P, 2, D])
        causal = p.sb("causal", [P, P])
        xb = p.sb("x_batch", [P, 1 + T])
        pts = p.sb("points", [P, TPB, 2, 2, H, 4])
        v = p.sb("v_and_one", [P, TPB, H, DH + 1])
        ln, ln2 = p.sb("lines", [P, TPB * 2, H, LC]), p.sb("lines2", [P, TPB * 2, H, LC])
        nrm, half = p.sb("norms", [P, TPB * 2, H]), p.sb("minus_half", [P, TPB * 2, H])
        qk = p.sb("lines_padded", [P, 2, TPB, H, SLOT])
        qkT = p.sb("lines_featmajor", [P, 2, G, T])
        E = p.sb("probs", [P, 2, 4, T + P])
        rsum = p.sb("rsum", [P, TPB, H])
        O = p.sb("heads_out", [P, TPB, H, DH])
        OT = p.sb("heads_out_featmajor", [P, T])
        loaded, xb_ready, proj = p.sem("loaded"), p.sem("xb_ready"), p.sem("proj")
        sq_ready, norm_ready, lines_ready = p.sem("sq_ready"), p.sem("norm_ready"), p.sem("lines_ready")
        turned, t_act, t_dve = p.sem("turned"), p.sem("t_act"), p.sem("t_dve")
        scores, exped, masked, heads = p.sem("scores"), p.sem("exped"), p.sem("masked"), p.sem("heads")
        o_ready, o_turned, ot_ready, final, done = (p.sem(n) for n in ("o_ready", "o_turned", "ot_ready", "final", "done"))
        zeroed, v_ready = p.sem("zeroed"), p.sem("v_ready")
        oview = k.bank[6][:, 0:TPB * H * (DH + 1)].rearrange("p (t h c) -> p t h c", t=TPB, h=H)
        def weights(sp):
            sp.dma_start(wx[:], k.dram["l1a_wx"]).then_inc(loaded, 16)
            sp.dma_start(wprev[:], k.dram["l1a_wprev"]).then_inc(loaded, 16)
            sp.dma_start(wo[:], k.dram["l1a_wo"]).then_inc(loaded, 16)
            sp.dma_start(bias[:], k.dram["l1a_bias"].partition_broadcast(P)).then_inc(loaded, 16)
            sp.dma_start(causal[:], k.dram["causal"]).then_inc(loaded, 16)

        normalise(k, add_y, meanwhile=weights)
        with nc.Block() as block:
            @block.tensor
            def _(pe):
                pe.wait_ge(loaded, 80)

                def out_of(pe, b, g):
                    s = g % 2
                    pe.wait_ge(masked, b * G + g + 1)
                    for r in range(4):
                        h = 4 * g + r
                        nc.tensor.matmul(oview[:, 0, h, :], E[:, s, r, 0:P], v[:, 0, h, :], start=True, stop=True)
                        nc.tensor.matmul(oview[:, 1, h, :], E[:, s, r, P:2 * P], v[:, 0, h, :], start=True, stop=False)
                        i = nc.tensor.matmul(oview[:, 1, h, :], E[:, s, r, T:T + P], v[:, 1, h, :], start=False, stop=True)
                    i.then_inc(heads, 1)

                def project(pe, b):
                    pe.wait_ge(xb_ready, b + 1)
                    for t in range(TPB):
                        o = k.bank[4 + t]
                        nc.tensor.matmul(o[:, 0:384], xb[:, 1 + t * P:1 + (t + 1) * P], wx[:], start=True, stop=False)
                        i = nc.tensor.matmul(o[:, 0:128], xb[:, t * P:(t + 1) * P], wprev[:], start=False, stop=True)
                    i.then_inc(proj, 1)

                def batch(pe, b, behind):
                    pe.wait_ge(lines_ready, b + 1)
                    for n in range(4):
                        for g in range(G):
                            i = nc.tensor.transpose(k.bank[n][:, g * P:(g + 1) * P],
                                                    qk[:, n // 2, n % 2, 4 * g:4 * g + 4, :].rearrange("p h c -> p (h c)"),
                                                    k.ident[:])
                        i.then_inc(turned, 1)
                    pe.wait_ge(t_act, b * 2 + 2)
                    pe.wait_ge(t_dve, b * 2 + 2)
                    for g in range(G):
                        if g > 0:
                            pe.wait_ge(exped, b * G + g)
                        for kt in range(TPB):
                            for r in range(4):
                                rows = slice(SLOT * r, SLOT * (r + 1))
                                i = nc.tensor.matmul(k.bank[r][:, kt * T:kt * T + (T - kt * P)],
                                                     qkT[rows, 1, g, kt * P:(kt + 1) * P], qkT[rows, 0, g, kt * P:T],
                                                     start=True, stop=True)
                        i.then_inc(scores, 1)
                        if g > 0:
                            out_of(pe, b, g - 1)
                        elif behind is not None:
                            pe.wait_ge(v_ready, b + 1)
                            project(pe, behind)
                    out_of(pe, b, G - 1)
                    pe.wait_ge(o_ready, b + 1)
                    for t in range(TPB):
                        i = nc.tensor.transpose(k.bank[7][:, t * P:(t + 1) * P],
                                                O[:, t].rearrange("p h c -> p (h c)"), k.ident[:])
                    i.then_inc(o_turned, 1)
                    pe.wait_ge(ot_ready, b + 1)
                    for t in range(TPB):
                        i = nc.tensor.matmul(k.bank[7][:, 256 + t * D:256 + (t + 1) * D], OT[:, t * P:(t + 1) * P], wo[:],
                                             start=True, stop=True)
                    i.then_inc(final, 1)

                project(pe, 0)
                with pe.Fori(0, B - 1) as b:
                    batch(pe, b, b + 1)
                batch(pe, B - 1, None)

            @block.scalar
            def _(act):
                with act.Fori(0, B) as b:
                    for n in (0, 2):
                        act.wait_ge(turned, b * 4 + n + 1)
                        nc.scalar.activation(qkT[:, n // 2, :, 0:P], k.bank[n].rearrange("p (g t) -> p g t", g=G),
                                             ACT.Copy).then_inc(t_act, 1)
                    for g in range(G):
                        s = g % 2
                        act.wait_ge(scores, b * G + g + 1)
                        if g > 1:
                            act.wait_ge(heads, b * G + g - 1)
                        nc.scalar.activation(E[:, s], k.banks[:, 0:4, 0:T + P], ACT.Exp, scale=LC ** -0.5).then_inc(exped, 1)
                    act.wait_ge(o_turned, b + 1)
                    nc.scalar.activation(OT[:], k.bank[7][:, 0:T], ACT.Copy).then_inc(ot_ready, 1)

            @block.gpsimd
            def _(pool):
                nc.gpsimd.memset(half[:], -0.5)
                nc.gpsimd.memset(qk[:], 0.0)
                nc.gpsimd.memset(v[:], 1.0).then_inc(zeroed, 1)
                pool.wait_ge(loaded, 80)
                pool.drain()
                with pool.Fori(0, B) as b:
                    pool.wait_ge(sq_ready, b + 1)
                    nc.gpsimd.tensor_tensor(nrm[:], nrm[:], half[:], ALU.pow).then_inc(norm_ready, 1)

            @block.vector
            def _(dve):
                vv = nc.vector
                dve.wait_ge(loaded, 80)
                dve.wait_ge(zeroed, 1)
                def points(b):
                    vv.tensor_copy(xb[:], k.HT[:, bass.ds(b, 1), PAD - 1:PAD + T].rearrange("p a t -> p (a t)")).then_inc(xb_ready, 1)
                    dve.wait_ge(proj, b + 1)
                    for t in range(TPB):
                        vv.tensor_copy(pts[:, t].rearrange("p a b h c -> p (a b h c)"), k.bank[4 + t][:, 0:256])
                    dve.drain()
                    pv = pts[:].rearrange("p t a b h c -> p (t a) b h c")
                    for i0, js, cs in PAIRS:
                        n = js.stop - js.start
                        one = [pv[:, :, a, :, i0:i0 + 1].to_broadcast([P, 4, H, n]) for a in range(2)]
                        many = [pv[:, :, a, :, js] for a in range(2)]
                        vv.tensor_tensor(ln[:, :, :, cs], one[0], many[1], ALU.mult)
                        vv.tensor_tensor(ln2[:, :, :, cs], one[1], many[0], ALU.mult)
                    dve.drain()

                def norms(b):
                    vv.tensor_tensor(ln[:], ln[:], ln2[:], ALU.subtract)
                    dve.drain()
                    vv.tensor_tensor(ln2[:], ln[:], ln[:], ALU.mult)
                    dve.drain()
                    vv.tensor_reduce(nrm[:], ln2[:], AXX, ALU.add)
                    dve.drain()
                    vv.tensor_scalar_max(nrm[:], nrm[:], 1e-24).then_inc(sq_ready, 1)

                def lines(b):
                    dve.wait_ge(norm_ready, b + 1)
                    lq = ln[:].rearrange("p (t a) h c -> p t a h c", a=2)
                    nq = nrm[:].rearrange("p (t a) h -> p t a h", a=2)
                    for t in range(TPB):
                        vv.tensor_tensor(qk[:, 0, t, :, 0:LC], lq[:, t, 0], over(nq[:, t, 0, :], LC), ALU.mult)
                    for c in range(LC):
                        i = vv.scalar_tensor_tensor(out=qk[:, 1, :, :, c], in0=lq[:, :, 1, :, 5 - c], scalar=JSIGN[c],
                                                    in1=nq[:, :, 1, :], op0=ALU.mult, op1=ALU.mult)
                    i.then_inc(lines_ready, 1)

                def batch(b, behind):
                    for t in range(TPB):
                        i = vv.tensor_tensor(v[:, t, :, 0:DH], k.bank[4 + t][:, 256:384].rearrange("p (h c) -> p h c", h=H),
                                             bias[:, 0, :].rearrange("p (h c) -> p h c", h=H), ALU.add)
                    i.then_inc(v_ready, 1)
                    for n in (1, 3):
                        dve.wait_ge(turned, b * 4 + n + 1)
                        vv.tensor_copy(qkT[:, n // 2, :, P:T], k.bank[n].rearrange("p (g t) -> p g t", g=G)).then_inc(t_dve, 1)
                    for g, front in enumerate((points, norms, lines, None)):
                        dve.wait_ge(exped, b * G + g + 1)
                        for c in (0, T):
                            at = E[:, g % 2, :, c:c + P]
                            i = vv.tensor_tensor(at, at, across(causal[:], 4), ALU.mult)
                        i.then_inc(masked, 1)
                        if front and behind is not None:
                            front(behind)
                    dve.wait_ge(heads, b * G + G)
                    vv.reciprocal(rsum[:], oview[:, :, :, DH])
                    dve.drain()
                    for t in range(TPB):
                        i = vv.tensor_tensor(O[:, t], oview[:, t, :, 0:DH], over(rsum[:, t, :], DH), ALU.mult)
                    i.then_inc(o_ready, 1)
                    dve.wait_ge(final, b + 1)
                    vv.tensor_tensor(k.Y[:, bass.ds(b * TPB, TPB), :], k.bank[7][:, 256:512].rearrange("p (t d) -> p t d", d=D),
                                     across(bias[:, 1, :], TPB), ALU.add).then_inc(done, 1)

                points(0)
                norms(0)
                lines(0)
                with dve.Fori(0, B - 1) as b:
                    batch(b, b + 1)
                batch(B - 1, None)


def lay_out_window(i, d, np):
    half = 32
    swap = lambda a: np.concatenate([a[..., half:], a[..., :half]], -1)
    HID = 341
    for l in range(2):
        d[f"l0f_wqkv{l}"] = i["L0_ffn_wqkv"][l]
        qk = np.stack([i["L0_ffn_q_scale"][l], i["L0_ffn_k_scale"][l]])
        d[f"l0f_qks{l}"] = np.stack([qk, swap(qk)], 1)
        d[f"l0f_wo{l}"] = by_blocks(i["L0_ffn_wo"][l])
        d[f"l0f_ln{l}"] = np.stack([i["L0_ffn_ln_g"][l], i["L0_ffn_ln_b"][l]])
        pad = lambda a: np.concatenate([a, np.zeros((3 * P - HID,) + a.shape[1:], a.dtype)])
        w1, b1 = i["L0_ffn_w1"][l], i["L0_ffn_b1"][l]
        d[f"l0f_w1{l}"] = np.stack([pad(w1[:, n * HID:(n + 1) * HID].T).T for n in range(2)], 1)
        d[f"l0f_b1{l}"] = np.stack([pad(b1[n * HID:(n + 1) * HID]).reshape(3, P).T for n in range(2)], 1)
        d[f"l0f_w2{l}"] = by_blocks(pad(i["L0_ffn_w2"][l]))
        d[f"l0f_b2{l}"] = i["L0_ffn_b2"][l]
    hi = np.arange(0, 64, 2, dtype=np.float32)
    inv = (np.float32(1.0) / np.float32(10000.0) ** (hi / np.float32(64))).astype(np.float32)
    t = np.arange(T, dtype=np.float32)
    fr = (t[:, None] * inv[None, :]).astype(np.float32)
    base = ((hi + np.float32(0.4 * 64)) / np.float32(1.4 * 64)).astype(np.float32)
    power = ((t - T // 2) / np.float32(32.0)).astype(np.float32)
    sc = (base[None, :] ** power[:, None]).astype(np.float32)
    tw = lambda a: np.concatenate([a, a], -1)
    cos, sin, sc = tw(np.cos(fr)), tw(np.sin(fr)), tw(sc)
    sin[:, :half] *= -1
    tab = np.stack([cos * sc, sin * sc, cos / sc, sin / sc], 1).reshape(T, 2, 2, 64)
    d["l0f_rot"] = tab.reshape(TPB, P, 2, 2, 64).transpose(1, 0, 2, 3, 4)
    q, j0, j1 = np.arange(P), np.arange(P), np.arange(64, 256)
    ok = lambda q, j: (q[:, None] >= j[None, :]) & (q[:, None] <= j[None, :] + 64)
    band = np.concatenate([ok(q, j0), ok(q + P, j1)], 1)
    d["l0f_band"] = np.where(band, 0.0, -1e30).astype(np.float32)
    d["l0f_shift"] = np.stack([np.eye(P, k=1, dtype=np.float32), np.zeros((P, P), np.float32)], 1)
    d["l0f_shift"][P - 1, 1, 0] = 1.0


def window_attn(k, add_y):
    for l in range(2):
        window_attention_layer(k, l, add_y)
        window_ffn_layer(k, l)


def shift_tokens(k, shifted, affine, l):
    nc, HALF = k.nc, D // 2
    with Part(k) as p:
        mats = p.sb("shift", [P, 2, P])
        loaded, moved = p.sem("loaded"), p.sem("moved")
        with nc.Block() as block:
            @block.sync
            def _(sp):
                sp.dma_start(mats[:], k.dram["l0f_shift"]).then_inc(loaded, 16)
                sp.dma_start(affine[:], k.dram[f"l0f_ln{l}"].partition_broadcast(P)).then_inc(loaded, 16)
                sp.wait_ge(loaded, 32)

            @block.tensor
            def _(pe):
                pe.wait_ge(loaded, 32)
                for n in range(2):
                    o = k.bank[n].rearrange("p (b t d) -> p b t d", t=TPB, d=HALF)
                    y = k.Y[:, 8 * n:8 * n + 8, HALF:].rearrange("p (b t) d -> p b t d", t=TPB)
                    nc.tensor.matmul(k.bank[n].rearrange("p (b d) -> p b d", d=HALF), mats[:, 0, :], k.Y[:, 8 * n:8 * n + 8, HALF:],
                                     start=True, stop=False)
                    nc.tensor.matmul(o[:, :, 1, :], mats[:, 1, :], y[:, :, 0, :], start=False, stop=True).then_inc(moved, 1)

            @block.vector
            def _(dve):
                nc.vector.tensor_copy(shifted[:, :, 0:HALF], k.Y[:, :, 0:HALF])
                for n in range(2):
                    dve.wait_ge(moved, n + 1)
                    nc.vector.tensor_copy(shifted[:, 8 * n:8 * n + 8, HALF:], k.bank[n].rearrange("p (a d) -> p a d", d=HALF))


def window_attention_layer(k, l, add_y):
    nc, H, DK, HALF = k.nc, 8, 64, 32
    CB, HG, NU, W0, W1 = H * DK // P, 4, 2, P, 192
    with Part(k) as p:
        wqkv, wo = p.sb("wqkv", [P, 3 * 512]), p.sb("wo", [P, CB, D])
        qks, rot, tab = p.sb("qk_scales", [P, 2, 2, DK]), p.sb("rotary", [P, TPB, 2, 2, DK]), p.sb("table", [P, TPB, 2, 2, DK])
        band = p.sb("band", [P, W0 + W1])
        xb = p.sb("x_batch", [P, T])
        sq = p.sb("squares", [P, TPB, 2, 512])
        ss, half = p.sb("norms", [P, TPB, 2, H]), p.sb("minus_half", [P, TPB * 2 * H])
        qn, qr, qk = (p.sb(n, [P, TPB, 2, H, DK]) for n in ("qk_normed", "qk_turned_part", "qk_rotated"))
        raw = p.sb("qkv_ahead", [P, TPB, 3, 512])
        v = p.sb("v", [P, TPB, 512])
        qkT = p.sb("qk_featmajor", [P, 2, CB, T])
        S = p.sb("scores", [P, 2, HG, W0 + W1])
        E = p.sb("probs", [P, 2, HG, W0 + T])
        mx, rs = p.sb("rowmax", [P, 2, HG, TPB]), p.sb("rowsum", [P, 2, HG, TPB])
        ET = p.sb("probs_keymajor", [P, NU, HG * 3, P])
        TB = (4, 0)
        O = p.sb("heads_out", [P, TPB, 512])
        OT = p.sb("heads_out_featmajor", [P, CB, T])
        names = ("loaded", "zeroed", "xb_ready", "proj", "squared", "ss_ready", "norm_ready", "normed", "turned_part",
                 "v_moved", "read_out", "y_added",
                 "rotated", "turned", "t_act", "t_dve", "scores", "maxed", "exped", "p_turned", "pt_act", "pt_dve", "heads",
                 "heads_out", "o_turned", "ot_ready", "final", "s_read")
        q = {n: p.sem(n) for n in names}
        hout = k.bank[7].rearrange("p (t h d) -> p t h d", t=TPB, h=HG)

        def weights(sp):
            sp.dma_start(wqkv[:], k.dram[f"l0f_wqkv{l}"]).then_inc(q["loaded"], 16)
            sp.dma_start(wo[:], k.dram[f"l0f_wo{l}"]).then_inc(q["loaded"], 16)
            sp.dma_start(qks[:], k.dram[f"l0f_qks{l}"].partition_broadcast(P)).then_inc(q["loaded"], 16)
            sp.dma_start(rot[:], k.dram["l0f_rot"]).then_inc(q["loaded"], 16)
            sp.dma_start(band[:], k.dram["l0f_band"]).then_inc(q["loaded"], 16)

        if l == 0:
            normalise(k, add_y, meanwhile=weights)
            with nc.Block() as block:
                @block.vector
                def _(dve):
                    nc.vector.tensor_copy(k.Y[:], k.H[:])
        else:
            normalise(k, src=k.Y, norm=False, meanwhile=weights)
        with nc.Block() as block:
            @block.tensor
            def _(pe):
                pe.wait_ge(q["loaded"], 80)

                def score(b, u):
                    for h in range(HG):
                        hd = HG * u + h
                        rows, c = slice(hd % 2 * DK, (hd % 2 + 1) * DK), hd // 2
                        nc.tensor.matmul(k.bank[h][:, 0:W0], qkT[rows, 0, c, 0:P], qkT[rows, 1, c, 0:P], start=True, stop=True)
                        nc.tensor.matmul(k.bank[h][:, W0:W0 + W1], qkT[rows, 0, c, P:T], qkT[rows, 1, c, DK:T],
                                         start=True, stop=True).then_inc(q["scores"], 1)

                def turn(b, u):
                    pe.wait_ge(q["exped"], b * NU + u + 1)
                    for n in range(HG * 3):
                        i = nc.tensor.transpose(k.bank[TB[u] + n // 4][:, n % 4 * P:(n % 4 + 1) * P],
                                                E[:, u, n // 3, n % 3 * P:(n % 3 + 1) * P], k.ident[:])
                        if n % 4 == 3:
                            i.then_inc(q["p_turned"], 1)

                def heads_of(b, u):
                    pe.wait_ge(q["pt_act"], (b * NU + u) * 2 + 2)
                    pe.wait_ge(q["pt_dve"], b * NU + u + 1)
                    pe.wait_ge(q["heads_out"], b * NU + u + 1)
                    for h in range(HG):
                        vh = slice((HG * u + h) * DK, (HG * u + h + 1) * DK)
                        nc.tensor.matmul(hout[:, 0, h, :], ET[:, u, 3 * h, :], v[:, 0, vh], start=True, stop=True)
                        nc.tensor.matmul(hout[:, 1, h, :], ET[:, u, 3 * h + 1, :], v[:, 0, vh], start=True, stop=False)
                        i = nc.tensor.matmul(hout[:, 1, h, :], ET[:, u, 3 * h + 2, :], v[:, 1, vh], start=False, stop=True)
                    i.then_inc(q["heads"], 1)

                def project(b, t):
                    if t == 0:
                        pe.wait_ge(q["xb_ready"], b + 1)
                    else:
                        pe.wait_ge(q["read_out"], b * TPB + t)
                    for n in range(3):
                        i = nc.tensor.matmul(k.bank[4 + n][:], xb[:, t * P:(t + 1) * P], wqkv[:, n * 512:(n + 1) * 512],
                                             start=True, stop=True)
                    i.then_inc(q["proj"], 1)

                def batch(b, behind):
                    pe.wait_ge(q["rotated"], b + 1)
                    pe.wait_ge(q["y_added"], b + 1)
                    for n in range(4):
                        for c in range(CB):
                            i = nc.tensor.transpose(k.bank[n][:, c * P:(c + 1) * P],
                                                    qk[:, n % 2, n // 2].rearrange("p h d -> p (h d)")[:, c * P:(c + 1) * P],
                                                    k.ident[:])
                        i.then_inc(q["turned"], 1)
                    if behind is not None:
                        project(behind, 0)
                    pe.wait_ge(q["t_act"], b * 2 + 2)
                    pe.wait_ge(q["t_dve"], b * 2 + 2)
                    score(b, 0)
                    if behind is not None:
                        project(behind, 1)
                        pe.wait_ge(q["read_out"], behind * TPB + 2)
                    pe.wait_ge(q["s_read"], b * NU + 1)
                    score(b, 1)
                    turn(b, 0)
                    pe.wait_ge(q["s_read"], b * NU + NU)
                    turn(b, 1)
                    pe.wait_ge(q["v_moved"], b + 1)
                    heads_of(b, 0)
                    heads_of(b, 1)
                    pe.wait_ge(q["heads_out"], b * NU + NU + 1)
                    for n in range(CB * TPB):
                        c, t = n // TPB, n % TPB
                        i = nc.tensor.transpose(k.bank[n // 4][:, n % 4 * P:(n % 4 + 1) * P], O[:, t, c * P:(c + 1) * P],
                                                k.ident[:])
                    i.then_inc(q["o_turned"], 1)
                    pe.wait_ge(q["ot_ready"], b + 1)
                    for t in range(TPB):
                        for c in range(CB):
                            i = nc.tensor.matmul(k.bank[2][:, t * D:(t + 1) * D], OT[:, c, t * P:(t + 1) * P], wo[:, c, :],
                                                 start=c == 0, stop=c == CB - 1)
                    i.then_inc(q["final"], 1)

                for t in range(TPB):
                    project(0, t)
                with pe.Fori(0, B - 1) as b:
                    batch(b, b + 1)
                batch(B - 1, None)

            @block.scalar
            def _(act):
                def read_out(b, t):
                    act.wait_ge(q["proj"], b * TPB + t + 1)
                    nc.scalar.activation(raw[:, t], k.banks[:, 4:7, :], ACT.Copy).then_inc(q["read_out"], 1)

                def batch(b, behind):
                    if not isinstance(b, int) or b > 0:
                        act.wait_ge(q["heads"], b * NU)
                    act.wait_ge(q["read_out"], b * TPB + TPB)
                    nc.scalar.activation(v[:], raw[:, :, 2, :], ACT.Copy).then_inc(q["v_moved"], 1)
                    for n in (0, 2):
                        act.wait_ge(q["turned"], b * 4 + n + 1)
                        nc.scalar.activation(qkT[:, n // 2, :, 0:P], k.bank[n].rearrange("p (c t) -> p c t", c=CB),
                                             ACT.Copy).then_inc(q["t_act"], 1)
                    if behind is not None:
                        act.wait_ge(q["v_moved"], b + 1)
                        act.wait_ge(q["rotated"], b + 1)
                        for t in range(TPB):
                            read_out(behind, t)
                    for u in range(NU):
                        act.wait_ge(q["maxed"], b * NU + u + 1)
                        for h in range(HG):
                            for t in range(TPB):
                                src = S[:, u, h, 0:W0] if t == 0 else S[:, u, h, W0:]
                                dst = E[:, u, h, 0:W0] if t == 0 else E[:, u, h, W0 + T - W1:]
                                i = nc.scalar.activation(dst, src, ACT.Exp, scale=8.0, bias=mx[:, u, h, t:t + 1],
                                                         accum_out=rs[:, u, h, t:t + 1])
                        i.then_inc(q["exped"], 1)
                    for u in range(NU):
                        for n in (0, 1):
                            act.wait_ge(q["p_turned"], (b * NU + u) * 3 + n + 1)
                            nc.scalar.activation(ET[:, u, 4 * n:4 * n + 4, :], k.bank[TB[u] + n].rearrange("p (a t) -> p a t", t=P),
                                                 ACT.Copy).then_inc(q["pt_act"], 1)
                    act.wait_ge(q["o_turned"], b + 1)
                    for n in range(2):
                        i = nc.scalar.activation(OT[:, 2 * n:2 * n + 2, :], k.bank[n].rearrange("p (c t) -> p c t", t=T), ACT.Copy)
                    i.then_inc(q["ot_ready"], 1)

                for t in range(TPB):
                    read_out(0, t)
                batch(0, 1)
                with act.Fori(1, B - 1) as b:
                    batch(b, b + 1)
                batch(B - 1, None)

            @block.gpsimd
            def _(pool):
                g = nc.gpsimd
                g.memset(half[:], -0.5)
                g.memset(E[:], 0.0).then_inc(q["zeroed"], 1)
                pool.wait_ge(q["loaded"], 80)
                for t in range(TPB):
                    for a in range(2):
                        g.tensor_tensor(tab[:, t, a], rot[:, t, a], qks[:, a], ALU.mult)
                pool.drain()
                with pool.Fori(0, B) as b:
                    for t in range(TPB):
                        pool.wait_ge(q["read_out"], b * TPB + t + 1)
                        g.tensor_tensor(sq[:, t], raw[:, t, 0:2, :], raw[:, t, 0:2, :], ALU.mult).then_inc(q["squared"], 1)
                    pool.wait_ge(q["ss_ready"], b + 1)
                    flat = ss[:].rearrange("p t a h -> p (t a h)")
                    g.tensor_tensor(flat, flat, half[:], ALU.pow).then_inc(q["norm_ready"], 1)
                    for t in range(TPB):
                        pool.wait_ge(q["normed"], b * TPB + t + 1)
                        for a in range(2):
                            g.tensor_tensor(qk[:, t, a], qn[:, t, a], across(tab[:, t, a, 0, :], H), ALU.mult).then_inc(q["turned_part"], 1)

            @block.vector
            def _(dve):
                vv = nc.vector
                dve.sem_inc(q["heads_out"], 1)
                dve.sem_inc(q["y_added"], 1)
                dve.wait_ge(q["zeroed"], 1)
                dve.wait_ge(q["loaded"], 80)
                def load_x(b):
                    x = lambda lo, at: k.HT[lo:lo + 64, bass.ds(b, 1), at:at + T].rearrange("p a t -> p (a t)")
                    vv.tensor_copy(xb[0:64, :], x(0, PAD))
                    vv.tensor_copy(xb[64:128, :], x(64, PAD - 1))
                    dve.drain()
                    vv.engine_nop().then_inc(q["xb_ready"], 1)

                def norms(b, t):
                    dve.wait_ge(q["squared"], b * TPB + t + 1)
                    vv.tensor_reduce(ss[:, t], sq[:, t].rearrange("p a (h d) -> p a h d", d=DK), AXX, ALU.add)
                    if t == TPB - 1:
                        dve.drain()
                        vv.tensor_scalar_max(ss[:], ss[:], 1e-24).then_inc(q["ss_ready"], 1)

                def normalised(b):
                    dve.wait_ge(q["norm_ready"], b + 1)
                    for t in range(TPB):
                        for a in range(2):
                            i = vv.tensor_tensor(qn[:, t, a], raw[:, t, a].rearrange("p (h d) -> p h d", d=DK),
                                                 over(ss[:, t, a, :], DK), ALU.mult)
                        i.then_inc(q["normed"], 1)
                    dve.drain()

                def rotated(b):
                    for t in range(TPB):
                        for a in range(2):
                            for lo in (0, HALF):
                                vv.tensor_tensor(qr[:, t, a, :, lo:lo + HALF], qn[:, t, a, :, HALF - lo:DK - lo],
                                                 across(tab[:, t, a, 1, lo:lo + HALF], H), ALU.mult)
                    dve.drain()
                    for t in range(TPB):
                        for a in range(2):
                            dve.wait_ge(q["turned_part"], (b * TPB + t) * 2 + a + 1)
                            i = vv.tensor_add(qk[:, t, a], qk[:, t, a], qr[:, t, a])
                    i.then_inc(q["rotated"], 1)

                def banded(b, u):
                    for h in range(HG):
                        dve.wait_ge(q["scores"], (b * NU + u) * HG + h + 1)
                        i = vv.tensor_tensor(S[:, u, h, :], k.bank[h][:, 0:W0 + W1], band[:], ALU.add)
                    i.then_inc(q["s_read"], 1)
                    dve.drain()
                    vv.tensor_reduce(mx[:, u, :, 0], S[:, u, :, 0:W0], AXX, ALU.max)
                    vv.tensor_reduce(mx[:, u, :, 1], S[:, u, :, W0:], AXX, ALU.max)
                    dve.drain()
                    vv.tensor_scalar(mx[:, u], mx[:, u], -8.0, None, ALU.mult).then_inc(q["maxed"], 1)

                def copy_turned(b, u):
                    dve.wait_ge(q["p_turned"], (b * NU + u) * 3 + 3)
                    vv.tensor_copy(ET[:, u, 8:12, :], k.bank[TB[u] + 2].rearrange("p (a t) -> p a t", t=P)).then_inc(q["pt_dve"], 1)

                def out(b, u):
                    dve.wait_ge(q["heads"], b * NU + u + 1)
                    vv.reciprocal(rs[:, u], rs[:, u])
                    dve.drain()
                    for t in range(TPB):
                        i = vv.tensor_tensor(O[:, t, u * 256:(u + 1) * 256].rearrange("p (h d) -> p h d", d=DK),
                                             hout[:, t], over(rs[:, u, :, t], DK), ALU.mult)
                    i.then_inc(q["heads_out"], 1)

                def batch(b, behind):
                    if behind is not None:
                        load_x(behind)
                    for n in (1, 3):
                        dve.wait_ge(q["turned"], b * 4 + n + 1)
                        vv.tensor_copy(qkT[:, n // 2, :, P:T], k.bank[n].rearrange("p (c t) -> p c t", c=CB)).then_inc(q["t_dve"], 1)
                    for u in range(NU):
                        banded(b, u)
                        if behind is not None:
                            norms(behind, u)
                    for u in range(NU):
                        copy_turned(b, u)
                    out(b, 0)
                    if behind is not None:
                        normalised(behind)
                    out(b, 1)
                    if behind is not None:
                        rotated(behind)
                    dve.wait_ge(q["final"], b + 1)
                    y = k.Y[:, bass.ds(b * TPB, TPB), :]
                    vv.tensor_tensor(y, k.bank[2][:, 0:TPB * D].rearrange("p (t d) -> p t d", d=D), y, ALU.add).then_inc(q["y_added"], 1)
                    dve.drain()

                load_x(0)
                for t in range(TPB):
                    norms(0, t)
                normalised(0)
                rotated(0)
                with dve.Fori(0, B - 1) as b:
                    batch(b, b + 1)
                batch(B - 1, None)


def window_ffn_layer(k, l):
    nc, KB, CH = k.nc, 3, 512
    NCH, bpc = B * T // CH, CH // T
    with Part(k) as p:
        w1, b1 = p.sb("w1", [P, 2, KB * P]), p.sb("b1", [P, 2, KB])
        w2, b2 = p.sb("w2", [P, KB, D]), p.sb("b2", [P, D])
        gate, hid = p.sb("gate", [P, KB, CH]), p.sb("hid", [P, KB, CH])
        shifted, affine = p.sb("shifted", [P, NT, D]), p.sb("affine", [P, 2, D])
        loaded, pair, gated, prod, down, out = (p.sem(n) for n in ("loaded", "pair", "gated", "prod", "down", "out"))

        def weights(sp):
            sp.dma_start(w1[:], k.dram[f"l0f_w1{l}"]).then_inc(loaded, 16)
            sp.dma_start(b1[:], k.dram[f"l0f_b1{l}"]).then_inc(loaded, 16)
            sp.dma_start(w2[:], k.dram[f"l0f_w2{l}"]).then_inc(loaded, 16)
            sp.dma_start(b2[:], k.dram[f"l0f_b2{l}"].partition_broadcast(P)).then_inc(loaded, 16)

        shift_tokens(k, shifted, affine, l)
        normalise(k, src=shifted, affine=affine, meanwhile=weights)
        with nc.Block() as block:
            @block.tensor
            def _(pe):
                pe.wait_ge(loaded, 64)
                with pe.Fori(0, NCH) as c:
                    x = k.HT[:, bass.ds(c * bpc, bpc), PAD:PAD + T]
                    pe.wait_ge(out, c + 1)
                    for ob in range(KB):
                        for j in range(2):
                            i = nc.tensor.matmul(k.bank[KB * j + ob].rearrange("p (b t) -> p b t", b=bpc),
                                                 w1[:, j, ob * P:(ob + 1) * P], x, start=True, stop=True)
                        i.then_inc(pair, 1)
                    pe.wait_ge(prod, c * KB + KB)
                    for tt in range(CH // P):
                        for kb in range(KB):
                            i = nc.tensor.matmul(k.bank[6][:, tt * D:(tt + 1) * D], hid[:, kb, tt * P:(tt + 1) * P],
                                                 w2[:, kb, :], start=kb == 0, stop=kb == KB - 1)
                    i.then_inc(down, 1)

            @block.scalar
            def _(act):
                act.wait_ge(loaded, 64)
                with act.Fori(0, NCH) as c:
                    for ob in range(KB):
                        act.wait_ge(pair, c * KB + ob + 1)
                        nc.scalar.activation(gate[:, ob, :], k.bank[KB + ob], ACT.Gelu, bias=b1[:, 1, ob:ob + 1]).then_inc(gated, 1)

            @block.vector
            def _(dve):
                dve.sem_inc(out, 1)
                dve.wait_ge(loaded, 64)
                nc.vector.tensor_tensor(k.Y[:], k.Y[:], across(b2[:], NT), ALU.add)
                dve.drain()
                with dve.Fori(0, NCH) as c:
                    for ob in range(KB):
                        dve.wait_ge(gated, c * KB + ob + 1)
                        nc.vector.scalar_tensor_tensor(out=hid[:, ob, :], in0=k.bank[ob], scalar=b1[:, 0, ob:ob + 1],
                                                       in1=gate[:, ob, :], op0=ALU.add, op1=ALU.mult).then_inc(prod, 1)
                    dve.wait_ge(down, c + 1)
                    y = k.Y[:, bass.ds(c * (CH // P), CH // P), :]
                    nc.vector.tensor_tensor(y, k.bank[6].rearrange("p (t d) -> p t d", d=D), y, ALU.add).then_inc(out, 1)


def lay_out_delta(i, d, np):
    for n in "qkv":
        d[f"l0a_w{n}"] = i[f"L0_attn_w_{n}"]
        d[f"l0a_conv{n}"] = i[f"L0_attn_conv_{n}"].T
    d["l0a_wg"] = i["L0_attn_w_g"]
    d["l0a_wab"] = np.concatenate([i["L0_attn_w_a"], i["L0_attn_w_b"]], 1)
    d["l0a_wout"] = by_blocks(i["L0_attn_w_out"])
    d["l0a_alog_dt"] = np.stack([i["L0_attn_A_log"], i["L0_attn_dt_bias"]])
    d["l0a_normw"] = i["L0_attn_norm_w"]
    r = np.arange(P)
    row, col = r[:, None], r[None, :]
    f = lambda a: a.astype(np.float32)
    d["l0a_tri"] = np.stack([f(row <= col), f(row > col), f(row >= col)], 1)
    lev = []
    for e in range(7):
        s = 1 << e
        lev.append(f((row // (2 * s) == col // (2 * s)) & (row // s % 2 == 1) & (col // s % 2 == 0)) + f(row == col))
    d["l0a_level0"] = np.stack([lev[0], lev[0].T], 1)
    d["l0a_levels"] = np.stack([lev[e][:, r // (1 << e) % 2 == 0] for e in range(1, 7)], 1)


def gated_delta(k, add_y):
    normalise(k, add_y)
    nc, H, DK, DV, HG = k.nc, 16, 64, 128, 4
    NG = H // HG
    KD, VD = H * DK, H * DV
    NLEV = 7
    TH = NT * H
    with Part(k) as p:
        wq, wk, wv = p.sb("wq", [P, 4, KD]), p.sb("wk", [P, 4, KD]), p.sb("wv", [P, 4, VD])
        wg, wout = p.sb("wg", [P, VD]), p.sb("wout", [P, H, D])
        tri, lev0, nw = p.sb("tri", [P, 3, P]), p.sb("level0", [P, 2, P]), p.sb("norm_w", [P, DV])
        lev = p.sb("levels", [P, NLEV - 1, P // 2])
        g, nbeta, lam, dlast = (p.sb(n, [P, TH]) for n in ("g", "minus_beta", "lam", "decay_to_end"))
        half = p.sb("minus_half", [P, 2 * HG])
        delta_prologue(k, p, dict(wq=wq, wk=wk, wv=wv, wg=wg, wout=wout, tri=tri, lev=lev, lev0=lev0, nw=nw, g=g, nbeta=nbeta,
                                  lam=lam, dlast=dlast))
        xb = p.sb("x_batch", [P, 3 + T])
        C2 = lambda name, shape, parts=P: p.sb(name, [parts, TPB, *shape])
        qk, v, gate = C2("qk", [2 * HG, DK]), C2("v", [HG, DV]), C2("gate", [HG, DV])
        sq = C2("squares", [2 * HG, DK])
        ss, os_ = C2("qk_norms", [2 * HG]), C2("o_norms", [HG])
        qkT = p.sb("qk_featmajor", [DK, TPB, 2 * HG, P])
        G2 = lambda name: C2(name, [HG, P])
        rD, Dm, Ds, A, AT, Pm, PT, Tm, TT = (G2(n) for n in ("g_masked", "decay", "decay_strict", "A", "A_turned",
                                                             "QK", "QK_turned", "inv", "inv_turned"))
        step = p.sb("steps", [P, NLEV - 1, TPB, HG, P])
        delta, O, yT = Ds, A, PT
        wdelta, lamq, S = Pm[:, 0], Pm[:, 1], k.H[0:DK, 0:HG, :]
        names = ("xb", "qk", "v", "gate", "rD", "Dps", "Dexp", "Ds", "Dm", "qk_silu", "v_silu", "gate_silu", "ss", "ssr",
                 "qkn", "turned", "qkT", "G", "A0", "A", "P", "APt", "AT", "PTr", "T1", "bv", "gatew",
                 "Yps", "Yp", "Tps", "TTps", "T", "TT", "KS", "R1", "QS", "dps", "delta", "wdelta", "Sps", "S",
                 "Ops", "O", "osq", "osum", "orstd", "y", "yT_ps", "yT", "fin", "done", "through_pe", "through_pool")
        q = {n: p.sem(n) for n in names}
        flat = lambda a: a.rearrange("p h t -> p (h t)")

        def cols(a, l, odd):
            return a.rearrange("p (n two s) -> p n two s", two=2, s=1 << l)[:, :, odd, :]

        def packed(c, l):
            return k.bank[c][:, 0:HG * P // 2].rearrange("p (n s) -> p n s", s=1 << l)

        def pairs(eng, pair):
            def batch(b, before, behind):
                pair(b, 0, before, (b, 1))
                with eng.Fori(1, NG - 1) as hg:
                    pair(b, hg, (b, hg - 1), (b, hg + 1))
                pair(b, NG - 1, (b, NG - 2), behind)

            batch(0, None, (1, 0))
            with eng.Fori(1, B - 1) as b:
                batch(b, (b - 1, NG - 1), (b + 1, 0))
            batch(B - 1, (B - 2, NG - 1), None)

        def steps(b, hg, before, behind):
            u = (b * NG + hg) * 2
            yield (u, b, hg, 0), (u + 1, b, hg, 1), before and (u - 1, *before, 1)
            yield (u + 1, b, hg, 1), behind and (u + 2, *behind, 0), (u, b, hg, 0)

        LV = NLEV - 1
        FIRST, FINAL = (0, 0, 0, 0), (2 * B * NG - 1, B - 1, NG - 1, 1)

        with nc.Block() as block:
            @block.tensor
            def _(pe):
                mm, tr = nc.tensor.matmul, nc.tensor.transpose
                w = lambda n, u, per=1, j=1: pe.wait_ge(q[n], u * per + j)
                hd = lambda bank, h: k.bank[bank][:, h * P:(h + 1) * P]

                def project_qk(f, n):
                    u, b, hg, c = f
                    for j in range(4):
                        i = mm(k.bank[4][:, n * 256:(n + 1) * 256], xb[:, c * P + j:c * P + j + P],
                               (wq, wk)[n][:, j, bass.ds(hg * 256, 256)], start=j == 0, stop=j == 3)
                    if n == 1:
                        i.then_inc(q["qk"], 1)

                def project_v(f, taps):
                    u, b, hg, c = f
                    for j in taps:
                        i = mm(k.bank[5], xb[:, c * P + j:c * P + j + P], wv[:, j, bass.ds(hg * 512, 512)],
                               start=j == 0, stop=j == 3)
                    if j == 3:
                        i.then_inc(q["v"], 1)

                def project_gate(f):
                    u, b, hg, c = f
                    mm(k.bank[6], xb[:, 3 + c * P:3 + c * P + P], wg[:, bass.ds(hg * 512, 512)],
                       start=True, stop=True).then_inc(q["gate"], 1)

                def decays(f):
                    w("rD", f[0])
                    mm(k.bank[7], tri[:, 0, :], flat(rD[:, f[3]]), start=True, stop=True).then_inc(q["Dps"], 1)

                def turn_qk(f):
                    u, b, hg, c = f
                    w("v_silu", u)
                    w("qkn", u)
                    pe.sem_inc(q["through_pe"], 1)
                    for n in range(2 * HG):
                        i = tr(k.bank[4 + n // HG][0:DK, n % HG * P:(n % HG + 1) * P], qk[:, c, n, :], k.ident[:])
                    i.then_inc(q["turned"], 1)

                def kk(f):
                    u, b, hg, c = f
                    w("gate_silu", u)
                    w("qkT", u)
                    for h in range(HG):
                        mm(hd(6, h), qkT[:, c, HG + h, :], qkT[:, c, HG + h, :], start=True, stop=True)

                def qk_products(f):
                    u, b, hg, c = f
                    w("Dexp", u)
                    for h in range(HG):
                        i = mm(hd(7, h), qkT[:, c, h, :], qkT[:, c, HG + h, :], start=True, stop=True)
                    i.then_inc(q["G"], 1)

                def turn_ap(f):
                    u, b, hg, c = f
                    w("P", u)
                    w("A", u)
                    for n, a in enumerate((A, Pm)):
                        for h in range(HG):
                            i = tr(hd(4 + n, h), a[:, c, h, :], k.ident[:])
                    i.then_inc(q["APt"], 1)

                def level_step(bk, l):
                    u, b, hg, c = bk
                    if l > 1:
                        w("T", u, LV - 1, l - 1)
                    for h in range(HG):
                        i = mm(k.bank[0][:, h * 64:(h + 1) * 64], AT[:, c, h, :], cols(Tm[:, c, h, :], l, 0), start=True, stop=True)
                    i.then_inc(q["Yps"], 1)

                def level_inverse(bk, l):
                    u, b, hg, c = bk
                    if l > 1:
                        w("TT", u, LV, l - 1)
                    w("Yp", u, LV, l)
                    if l < LV:
                        for h in range(HG):
                            i = mm(k.bank[1][:, h * 64:(h + 1) * 64], TT[:, c, h, :],
                                   cols(step[:, l - 1, c, h, :], l, 0), start=True, stop=True)
                        i.then_inc(q["Tps"], 1)
                    for h in range(HG):
                        i = mm(k.bank[2][:, h * 64:(h + 1) * 64], step[:, l - 1, c, h, :],
                               cols(TT[:, c, h, :], l, 1), start=True, stop=True)
                    i.then_inc(q["TTps"], 1)

                def turn_y(last):
                    u, b, hg, c = last
                    w("y", u)
                    for h in range(HG):
                        i = tr(hd(3, h), O[:, c, h, :], k.ident[:])
                    i.then_inc(q["yT_ps"], 1)

                def out(last):
                    u, b, hg, c = last
                    w("yT", u)
                    for h in range(HG):
                        i = mm(k.bank[3][:, 0:D], yT[:, c, h, :], wout[:, bass.ds(hg * HG + h, 1), :].rearrange("p a d -> p (a d)"),
                               start=h == 0, stop=h == HG - 1)
                    i.then_inc(q["fin"], 1)

                def front_first(f):
                    if f[3] == 0:
                        w("xb", f[1])
                    project_qk(f, 0)

                def pair(b, hg, before, behind):
                    for bk, f, last in steps(b, hg, before, behind):
                        u, _, _, c = bk
                        g = b * NG + hg
                        if f:
                            w("AT", u)
                            front_first(f)
                        w("PTr", u)
                        w("T1", u)
                        level_step(bk, 1)
                        if f:
                            project_qk(f, 1)
                        level_inverse(bk, 1)
                        if f:
                            decays(f)
                        level_step(bk, 2)
                        if f:
                            project_v(f, [0])
                        level_inverse(bk, 2)
                        if c == 1:
                            w("S", g)
                        if last:
                            turn_y(last)
                        level_step(bk, 3)
                        if f:
                            project_v(f, [1])
                        level_inverse(bk, 3)
                        if f:
                            project_v(f, [2, 3])
                        level_step(bk, 4)
                        if f:
                            project_gate(f)
                        level_inverse(bk, 4)
                        if last:
                            out(last)
                        level_step(bk, 5)
                        if last:
                            w("done", u - 1)
                        if c == 1:
                            for h in range(HG):
                                i = mm(hd(3, h), qkT[:, 1, HG + h, :], S[:, h, :], start=True, stop=True)
                            i.then_inc(q["KS"], 1)
                        if f:
                            turn_qk(f)
                        level_inverse(bk, 5)
                        level_step(bk, 6)
                        if f:
                            kk(f)
                            qk_products(f)
                        level_inverse(bk, 6)
                        if c == 1:
                            w("R1", g)
                            for h in range(HG):
                                i = mm(hd(3, h), qkT[:, 1, h, :], S[:, h, :], start=True, stop=True)
                            i.then_inc(q["QS"], 1)
                        else:
                            w("bv", u)
                        w("TT", u, LV, LV)
                        for h in range(HG):
                            i = mm(hd(0, h), TT[:, c, h, :], v[:, c, h, :], start=True, stop=True)
                        i.then_inc(q["dps"], 1)
                        w("delta", u)
                        for h in range(HG):
                            i = mm(hd(1, h), PT[:, c, h, :], delta[:, c, h, :], start=True, stop=True)
                        i.then_inc(q["Ops"], 1)
                        if f:
                            turn_ap(f)
                        if c == 0:
                            w("wdelta", g)
                            for h in range(HG):
                                i = mm(k.bank[3][0:DK, h * DV:(h + 1) * DV], qk[:, 0, HG + h, :], wdelta[:, h, :], start=True, stop=True)
                            i.then_inc(q["Sps"], 1)

                f = FIRST
                front_first(f)
                project_qk(f, 1)
                decays(f)
                project_v(f, range(4))
                project_gate(f)
                turn_qk(f)
                kk(f)
                qk_products(f)
                turn_ap(f)
                pairs(pe, pair)
                turn_y(FINAL)
                out(FINAL)

            @block.scalar
            def _(act):
                w = lambda n, u, per=1, j=1: act.wait_ge(q[n], u * per + j)

                def copy(dst, src):
                    return nc.scalar.activation(dst, src, ACT.Copy)

                def silu(f, n, dst, src):
                    w(n, f[0])
                    nc.scalar.activation(dst[:, f[3]].rearrange("p h d -> p (h d)"), k.bank[src], ACT.Silu).then_inc(q[n + "_silu"], 1)

                def exp_decays(f):
                    w("Dps", f[0])
                    nc.scalar.activation(flat(Dm[:, f[3]]), k.bank[7], ACT.Exp).then_inc(q["Dexp"], 1)

                def copy_qkT(f):
                    w("turned", f[0])
                    copy(flat(qkT[:, f[3], 0:HG]), k.bank[4][0:DK, :])
                    copy(flat(qkT[:, f[3], HG:]), k.bank[5][0:DK, :]).then_inc(q["qkT"], 1)

                def copy_ap(f):
                    w("APt", f[0])
                    copy(flat(AT[:, f[3]]), k.bank[4]).then_inc(q["AT"], 1)
                    copy(flat(PT[:, f[3]]), k.bank[5]).then_inc(q["PTr"], 1)

                def copy_y(last):
                    u, b, hg, c = last
                    w("yT_ps", u)
                    copy(flat(yT[:, c]), k.bank[3]).then_inc(q["yT"], 1)

                def pair(b, hg, before, behind):
                    for (u, _, _, c), f, last in steps(b, hg, before, behind):
                        for l in range(1, NLEV):
                            if l < LV:
                                w("Tps", u, LV - 1, l)
                                copy(cols(flat(Tm[:, c]), l, 0), packed(1, l)).then_inc(q["T"], 1)
                            w("TTps", u, LV, l)
                            copy(cols(flat(TT[:, c]), l, 1), packed(2, l)).then_inc(q["TT"], 1)
                            if l == 1 and f:
                                silu(f, "qk", qk, 4)
                            elif l == 2:
                                if f:
                                    exp_decays(f)
                                if last:
                                    copy_y(last)
                            elif l == 4 and f:
                                silu(f, "v", v, 5)
                                silu(f, "gate", gate, 6)
                                copy_qkT(f)
                        w("dps", u)
                        copy(flat(delta[:, c]), k.bank[0]).then_inc(q["delta"], 1)
                        if f:
                            copy_ap(f)
                        w("O", u, 1, 3)
                        nc.scalar.activation(sq[:, c].rearrange("p h d -> p (h d)"), flat(O[:, c]), ACT.Square).then_inc(q["osq"], 1)
                        if c == 0:
                            w("Sps", b * NG + hg)
                            copy(flat(S), k.bank[3][0:DK, :]).then_inc(q["S"], 1)

                f = FIRST
                silu(f, "qk", qk, 4)
                exp_decays(f)
                silu(f, "v", v, 5)
                silu(f, "gate", gate, 6)
                copy_qkT(f)
                copy_ap(f)
                pairs(act, pair)
                copy_y(FINAL)

            @block.gpsimd
            def _(pool):
                tt = nc.gpsimd.tensor_tensor
                w = lambda n, u, per=1, j=1: pool.wait_ge(q[n], u * per + j)
                nc.gpsimd.memset(half[:], -0.5)
                pool.drain()

                def alone():
                    pool.sem_inc(q["through_pool"], 1)

                def front(f):
                    u, b, hg, c = f
                    col = lambda a: a[:, bass.ds(b * (TPB * H) + hg * HG + c * H, HG)]
                    w("O", u, 1, 1)
                    alone()
                    tt(rD[:, c], across(tri[:, 1, :], HG), over(col(g), P), ALU.mult).then_inc(q["rD"], 1)
                    tt(Ds[:, c], across(tri[:, 1, :], HG), over(col(nbeta), P), ALU.mult)
                    w("ss", u)
                    tt(ss[:, c], ss[:, c], half[:], ALU.pow).then_inc(q["ssr"], 1)
                    pool.drain()
                    w("Dexp", u)
                    tt(Ds[:, c], Dm[:, c], Ds[:, c], ALU.mult).then_inc(q["Ds"], 1)
                    pool.drain()
                    tt(Dm[:, c], Dm[:, c], across(tri[:, 2, :], HG), ALU.mult).then_inc(q["Dm"], 1)
                    w("v_silu", u)
                    alone()
                    tt(v[:, c], v[:, c], over(col(nbeta), DV), ALU.mult).then_inc(q["bv"], 1)
                    w("gate_silu", u)
                    tt(gate[:, c], gate[:, c], across(nw[:], HG), ALU.mult).then_inc(q["gatew"], 1)
                    w("A0", u)
                    tt(A[:, c], A[:, c], across(k.ident[:], HG), ALU.add).then_inc(q["A"], 1)

                def pair(b, hg, before, behind):
                    for (u, _, _, c), f, last in steps(b, hg, before, behind):
                        if f:
                            front(f)
                        w("osum", u)
                        tt(os_[:, c], os_[:, c], half[:, 0:HG], ALU.pow).then_inc(q["orstd"], 1)

                front(FIRST)
                pairs(pool, pair)

            @block.vector
            def _(dve):
                vv = nc.vector
                tt = vv.tensor_tensor
                w = lambda n, u, per=1, j=1: dve.wait_ge(q[n], u * per + j)
                bank3 = lambda n: k.bank[n].rearrange("p (h t) -> p h t", h=HG)
                vv.memset(k.Y[:], 0.0)
                every = LV * TPB * HG
                vv.tensor_copy(step[:].rearrange("p l c h t -> p (l c h) t"), across(k.ident[:], every))
                dve.drain()
                dve.sem_inc(q["O"], 2)

                def load_x(b):
                    vv.tensor_copy(xb[:], k.HT[:, bass.ds(b, 1), PAD - 3:].rearrange("p a t -> p (a t)")).then_inc(q["xb"], 1)

                def square_qk(f):
                    u, b, hg, c = f
                    w("qk_silu", u)
                    tt(sq[:, c], qk[:, c], qk[:, c], ALU.mult)
                    dve.drain()
                    vv.tensor_reduce(ss[:, c], sq[:, c], AXX, ALU.add)
                    dve.drain()
                    vv.tensor_scalar_add(ss[:, c], ss[:, c], 1e-6).then_inc(q["ss"], 1)

                def norm_qk(f):
                    u, b, hg, c = f
                    w("ssr", u)
                    vv.tensor_scalar(ss[:, c, 0:HG], ss[:, c, 0:HG], DK ** -0.5, None, ALU.mult)
                    dve.drain()
                    tt(qk[:, c], qk[:, c], over(ss[:, c, :], DK), ALU.mult).then_inc(q["qkn"], 1)

                def mask_products(f):
                    u, b, hg, c = f
                    w("G", u)
                    w("Ds", u)
                    tt(A[:, c], bank3(6), Ds[:, c], ALU.mult).then_inc(q["A0"], 1)
                    w("Dm", u)
                    tt(Pm[:, c], bank3(7), Dm[:, c], ALU.mult).then_inc(q["P"], 1)

                def level0(f):
                    u, b, hg, c = f
                    w("A", u)
                    tt(Tm[:, c], A[:, c], across(lev0[:, 0, :], HG), ALU.mult)
                    w("AT", u)
                    tt(TT[:, c], AT[:, c], across(lev0[:, 1, :], HG), ALU.mult).then_inc(q["T1"], 1)

                def gate_y(last):
                    u, b, hg, c = last
                    w("orstd", u)
                    vv.tensor_scalar(os_[:, c], os_[:, c], -1.0, None, ALU.mult)
                    dve.drain()
                    tt(O[:, c], O[:, c], over(os_[:, c, :], DV), ALU.mult)
                    dve.drain()
                    w("gatew", u)
                    tt(O[:, c], O[:, c], gate[:, c], ALU.mult).then_inc(q["y"], 1)

                def add_y(last):
                    u, b, hg, c = last
                    w("fin", u)
                    y = k.Y[:, bass.ds(b * TPB + c, 1), :].rearrange("p a d -> p (a d)")
                    tt(y, k.bank[3][:, 0:D], y, ALU.add).then_inc(q["done"], 1)

                def pair(b, hg, before, behind):
                    for (u, _, _, c), f, last in steps(b, hg, before, behind):
                        col = lambda a: a[:, bass.ds(b * (TPB * H) + hg * HG + c * H, HG)]
                        g = b * NG + hg
                        if c == 1 and behind and isinstance(behind[1], int) and behind[1] == 0:
                            w("gate", u)
                            load_x(f[1])
                        for l in range(1, NLEV):
                            w("Yps", u, LV, l)
                            tt(cols(flat(step[:, l - 1, c]), l, 0).rearrange("p (h n) s -> p h n s", h=HG),
                               packed(0, l).rearrange("p (h n) s -> p h n s", h=HG),
                               across(lev[:, l - 1, :].rearrange("p (n s) -> p n s", s=1 << l), HG), ALU.mult).then_inc(q["Yp"], 1)
                            if l == 1 and last:
                                gate_y(last)
                            elif l == 3 and f:
                                square_qk(f)
                            elif l == 4:
                                if f:
                                    norm_qk(f)
                                if last:
                                    add_y(last)
                            elif l == 5 and c == 1:
                                w("KS", g)
                                tt(lamq, bank3(3), over(col(lam), DV), ALU.mult)
                                dve.drain()
                                tt(lamq, lamq, over(col(nbeta), DV), ALU.mult)
                                dve.drain()
                                w("bv", u)
                                tt(v[:, 1], v[:, 1], lamq, ALU.add).then_inc(q["R1"], 1)
                                dve.drain()
                        if f:
                            mask_products(f)
                        if c == 1:
                            w("QS", g)
                            tt(lamq, bank3(3), over(col(lam), DV), ALU.mult)
                            dve.drain()
                            w("Ops", u)
                            tt(O[:, 1], bank3(1), lamq, ALU.add).then_inc(q["O"], 1)
                        else:
                            w("delta", u)
                            tt(wdelta, delta[:, 0], over(col(dlast), DV), ALU.mult).then_inc(q["wdelta"], 1)
                            w("Ops", u)
                            vv.tensor_copy(O[:, 0], bank3(1)).then_inc(q["O"], 1)
                        if f:
                            level0(f)
                        w("osq", u)
                        squares = sq[:, c].rearrange("p h d -> p (h d)").rearrange("p (h d) -> p h d", h=HG)
                        vv.tensor_reduce(os_[:, c], squares, AXX, ALU.add)
                        dve.drain()
                        vv.tensor_scalar(os_[:, c], os_[:, c], 1.0 / DV, 1e-5, ALU.mult, ALU.add).then_inc(q["osum"], 1)

                f = FIRST
                load_x(0)
                square_qk(f)
                norm_qk(f)
                mask_products(f)
                level0(f)
                pairs(dve, pair)
                gate_y(FINAL)
                add_y(FINAL)


def delta_prologue(k, p, m):
    nc, H, TH = k.nc, 16, NT * 16
    wab, al = p.sb("wab", [P, 2 * H]), p.sb("alog_dtbias", [P, 2, H])
    with Part(k) as own:
        wide = {n: own.sb("plain_" + n, [P, s]) for n, s in (("q", 1024), ("k", 1024), ("v", 2048))}
        z, e, u, l, r = (own.sb(n, [P, NT, H]) for n in ("z", "e", "u", "l", "r"))
        names = ("small", "taps", "plain", "rest", "ab", "z", "exped", "u", "logged", "alog", "g", "cum")
        q = {n: own.sem(n) for n in names}
        ab = k.bank[0].rearrange("p (t h) -> p t h", h=2 * H)
        g3 = m["g"][:].rearrange("p (t h) -> p t h", h=H)
        with nc.Block() as block:
            @block.sync
            def _(sp):
                sp.dma_start(wab[:], k.dram["l0a_wab"]).then_inc(q["small"], 16)
                sp.dma_start(al[:], k.dram["l0a_alog_dt"].partition_broadcast(P)).then_inc(q["small"], 16)
                sp.dma_start(m["tri"][:], k.dram["l0a_tri"]).then_inc(q["small"], 16)
                for n in "qkv":
                    sp.dma_start(m["w" + n][:], k.dram[f"l0a_conv{n}"].partition_broadcast(P)).then_inc(q["taps"], 16)
                    sp.dma_start(wide[n][:], k.dram[f"l0a_w{n}"]).then_inc(q["plain"], 16)
                sp.dma_start(m["wg"][:], k.dram["l0a_wg"]).then_inc(q["rest"], 16)
                sp.dma_start(m["wout"][:], k.dram["l0a_wout"]).then_inc(q["rest"], 16)
                sp.dma_start(m["lev"][:], k.dram["l0a_levels"]).then_inc(q["rest"], 16)
                sp.dma_start(m["lev0"][:], k.dram["l0a_level0"]).then_inc(q["rest"], 16)
                sp.dma_start(m["nw"][:], k.dram["l0a_normw"].partition_broadcast(P)).then_inc(q["rest"], 16)
                sp.wait_ge(q["rest"], 80)

            @block.tensor
            def _(pe):
                pe.wait_ge(q["small"], 48)
                for t in range(NT):
                    i = nc.tensor.matmul(ab[:, t, :], k.HT[:, t // TPB, PAD + t % TPB * P:PAD + (t % TPB + 1) * P], wab[:],
                                         start=True, stop=True)
                i.then_inc(q["ab"], 1)
                pe.wait_ge(q["g"], 1)
                nc.tensor.matmul(k.bank[1][:, 0:TH], m["tri"][:, 0, :], m["g"][:], start=True, stop=True)
                nc.tensor.matmul(k.bank[2][:, 0:TH], m["tri"][:, 1, :], m["g"][:], start=True, stop=True).then_inc(q["cum"], 1)

            @block.scalar
            def _(act):
                a = nc.scalar.activation
                act.wait_ge(q["small"], 48)
                a(al[:, 0, :], al[:, 0, :], ACT.Exp).then_inc(q["alog"], 1)
                act.wait_ge(q["z"], 1)
                a(e[:], z[:], ACT.Abs)
                act.drain()
                a(e[:], e[:], ACT.Exp, scale=-1.0)
                a(r[:], ab[:, :, H:], ACT.Exp, scale=-1.0).then_inc(q["exped"], 1)
                act.wait_ge(q["u"], 1)
                a(l[:], u[:], ACT.Ln).then_inc(q["logged"], 1)
                act.wait_ge(q["cum"], 1)
                a(m["lam"][:], k.bank[1][:, 0:TH], ACT.Exp)
                a(m["dlast"][:], k.bank[2][:, 0:TH], ACT.Exp)
                act.drain()

            @block.vector
            def _(dve):
                v = nc.vector
                dve.wait_ge(q["ab"], 1)
                dve.wait_ge(q["alog"], 1)
                v.tensor_tensor(z[:], ab[:, :, 0:H], across(al[:, 1, :], NT), ALU.add).then_inc(q["z"], 1)
                dve.wait_ge(q["exped"], 1)
                v.tensor_scalar_add(u[:], e[:], 1.0).then_inc(q["u"], 1)
                v.tensor_scalar_max(z[:], z[:], 0.0)
                v.tensor_scalar_add(r[:], r[:], 1.0)
                dve.drain()
                v.scalar_tensor_tensor(out=e[:], in0=u[:], scalar=-1.0, in1=e[:], op0=ALU.add, op1=ALU.subtract)
                dve.wait_ge(q["logged"], 1)
                dve.drain()
                v.tensor_tensor(l[:], l[:], e[:], ALU.subtract)
                dve.drain()
                v.tensor_add(z[:], z[:], l[:])
                dve.drain()
                v.scalar_tensor_tensor(out=g3, in0=z[:], scalar=-1.0, in1=across(al[:, 0, :], NT), op0=ALU.mult,
                                       op1=ALU.mult).then_inc(q["g"], 1)
                v.reciprocal(r[:], r[:])
                dve.drain()
                v.tensor_scalar(m["nbeta"][:].rearrange("p (t h) -> p t h", h=H), r[:], -2.0, None, ALU.mult)
                dve.wait_ge(q["taps"], 48)
                dve.wait_ge(q["plain"], 48)
                for n in "qkv":
                    w = m["w" + n]
                    v.tensor_tensor(w[:], w[:], across(wide[n][:], 4), ALU.mult)
                dve.drain()


def lay_out_mamba(i, d, np):
    E, N, R = 2 * D, 64, D // 16
    rows = lambda a: a.reshape(2, P, *a.shape[1:]).swapaxes(0, 1)
    d["l3a_ln1"] = np.stack([i["L3_attn_ln1_w"], i["L3_attn_ln1_b"]])
    d["l3a_ln2"] = np.stack([i["L3_attn_ln2_w"], i["L3_attn_ln2_b"]])
    for m in (1, 2):
        g = lambda n: i[f"L3_attn_m{m}_{n}"]
        d[f"l3a_win{m}"] = g("W_in").T
        d[f"l3a_conv{m}"] = np.concatenate([rows(g("conv_w")), rows(g("conv_b"))[:, :, None],
                                            rows(g("dt_b"))[:, :, None], rows(g("D"))[:, :, None]], 2)
        xp = g("W_xp")
        bm, cm = xp[R:R + N], xp[R + N:]
        d[f"l3a_wxp{m}"] = by_blocks(np.concatenate([bm, bm, cm, cm, bm, cm, xp[:R]]).T)
        d[f"l3a_wdt{m}"] = g("W_dt").T
        d[f"l3a_alog{m}"] = rows(g("A_log"))
        d[f"l3a_wout{m}"] = by_blocks(g("W_out").T)
    e = np.eye(N, dtype=np.float32)
    z = np.zeros((N, N), np.float32)
    d["l3a_sel"] = np.stack([np.concatenate([e, e]), np.concatenate([e, z]), np.concatenate([z, e])], 1)




def bi_mamba(k, add_y):
    with Part(k) as own:
        affine = own.sb("ln1_ln2", [P, 2, 2, D])
        loaded = own.sem("loaded")

        def weights(sp):
            for n in range(2):
                sp.dma_start(affine[:, n], k.dram[f"l3a_ln{n + 1}"].partition_broadcast(P)).then_inc(loaded, 16)
            sp.wait_ge(loaded, 32)

        normalise(k, add_y, meanwhile=weights)
        normalise(k, src=k.H, affine=affine[:, 0])
        with Part(k) as p:
            mem = mamba_memories(p)
            for m in (1, 2):
                mamba_inputs(k, m, mem)
                mamba_scan(k, m, mem)
                mamba_output(k, m, mem)
        with Part(k) as p:
            add_norm_to_input(k, p, affine[:, 1])


def add_norm_to_input(k, p, affine):
    nc = k.nc
    stats, mv = p.sb("stats", [P, NT, 6]), p.sb("meanvar", [P, NT, 2])
    rstd, half = p.sb("rstd", [P, NT]), p.sb("minus_half", [P, NT])
    var_ready, rstd_ready = p.sem("var"), p.sem("rstd")
    with nc.Block() as block:
        @block.gpsimd
        def _(pool):
            nc.gpsimd.memset(half[:], -0.5)
            pool.drain()
            for n in range(2):
                cols = slice(n * NT // 2, (n + 1) * NT // 2)
                pool.wait_ge(var_ready, n + 1)
                nc.gpsimd.tensor_tensor(rstd[:, cols], rstd[:, cols], half[:, cols], ALU.pow).then_inc(rstd_ready, 1)

        @block.vector
        def _(dve):
            layer_norm_steps(nc, dve, k.Y, stats, mv, rstd, var_ready, rstd_ready, 0,
                             lambda t: nc.vector.tensor_scalar(k.Y[:, t, :], k.Y[:, t, :], mv[:, t, 0:1], rstd[:, t:t + 1],
                                                               ALU.subtract, ALU.mult))
            dve.drain()
            nc.vector.tensor_tensor(k.Y[:], k.Y[:], across(affine[:, 0, :], NT), ALU.mult)
            dve.drain()
            nc.vector.tensor_tensor(k.Y[:], k.Y[:], across(affine[:, 1, :], NT), ALU.add)
            dve.drain()
            nc.vector.tensor_add(k.Y[:], k.Y[:], k.H[:])
            dve.drain()


SN, SE = 64, 2
SCH = 512
SNC = B * T // SCH
CPAD = 3


def mamba_memories(p):
    m = {}
    m["xp"] = p.sb("xp_padded", [P, B, CPAD + T])
    m["xc"] = p.sb("xc", [P, SE, B * T])
    m["sz"] = p.sb("silu_z", [P, SE, B * T])
    m["dt"] = p.sb("dt", [P, SE, B * T])
    m["dtx"] = p.sb("dtx", [P, SE, B * T])
    for n in ("hm_b", "hm_c", "lo"):
        m[n] = p.sb("bc_" + n, [P, B * T], BF16)
    m["A"] = p.sb("A", [P, SE, SN])
    m["sel"] = p.sb("selectors", [P, 3, SN], BF16)
    m["self"] = p.sb("selectors_f32", [P, 3, SN])
    m["cw"] = p.sb("conv_and_biases", [P, SE, 7])
    m["wout"] = p.sb("w_out", [P, SE, D])
    return m


def mamba_inputs(k, m, mem):
    nc, R = k.nc, D // 16
    xp, xc, sz, dt, dtx = (mem[n] for n in ("xp", "xc", "sz", "dt", "dtx"))
    cw = mem["cw"]
    with Part(k) as p:
        win, wxp = p.sb("w_in", [P, 4 * P]), p.sb("w_xp", [P, SE, 3 * P + R])
        wdt = p.sb("w_dt", [R, 2 * P])
        dtlo = p.sb("dt_low", [R, B * T])
        en, u = p.sb("exp_minus_abs", [P, SE, B * T]), p.sb("one_plus", [P, SE, B * T])
        hi, mid = p.sb("high", [P, SCH], BF16), p.sb("middle", [P, SCH], BF16)
        r1 = p.sb("rest", [P, SCH])
        names = ("loaded", "proj", "xp_out", "z_out", "conved", "xc_ready", "bc", "bc_read", "dtlo_ready", "dtp",
                 "exped", "u_ready", "logged", "src_ready", "a_ready")
        q = {n: p.sem(n) for n in names}
        xsrc = xp[:, :, CPAD:]
        with nc.Block() as block:
            @block.sync
            def _(sp):
                for dst, n in ((win, "win"), (cw, "conv"), (wxp, "wxp"), (wdt, "wdt"), (mem["A"], "alog"), (mem["wout"], "wout")):
                    sp.dma_start(dst[:], k.dram[f"l3a_{n}{m}"]).then_inc(q["loaded"], 16)
                sp.dma_start(mem["self"][:], k.dram["l3a_sel"]).then_inc(q["loaded"], 16)

            @block.tensor
            def _(pe):
                pe.wait_ge(q["loaded"], 112)
                pe.wait_ge(q["src_ready"], 1)
                for blk in (0, 1, 2, 3):
                    if blk == 2:
                        pe.wait_ge(q["xp_out"], 4)
                    if blk == 3:
                        pe.wait_ge(q["xp_out"], 8)
                    for c in range(SNC):
                        nc.tensor.matmul(k.bank[blk % 2 * 4 + c].rearrange("p (b t) -> p b t", b=2), win[:, blk * P:(blk + 1) * P],
                                         k.HT[:, 2 * c:2 * c + 2, PAD:], start=True, stop=True).then_inc(q["proj"], 1)
                pe.wait_ge(q["xc_ready"], 2)
                pe.wait_ge(q["z_out"], 8)
                for c in range(SNC):
                    for n, (lo, w) in enumerate(((0, P), (P, P), (2 * P, P), (3 * P, R))):
                        if c > 1:
                            pe.wait_ge(q["bc_read"], 4 * (c - 2) + n + 1)
                        for e in range(SE):
                            i = nc.tensor.matmul(k.bank[c % 2 * 4 + n][0:w, :], wxp[:, e, lo:lo + w], xc[:, e, c * SCH:(c + 1) * SCH],
                                                 start=e == 0, stop=e == SE - 1)
                        i.then_inc(q["bc"], 1)
                pe.wait_ge(q["dtlo_ready"], SNC)
                for e in range(SE):
                    for c in range(SNC):
                        i = nc.tensor.matmul(k.bank[4 - 4 * e + c], wdt[:, e * P:(e + 1) * P], dtlo[:, c * SCH:(c + 1) * SCH],
                                             start=True, stop=True)
                    i.then_inc(q["dtp"], 1)

            @block.scalar
            def _(act):
                act.wait_ge(q["loaded"], 112)
                for blk in (0, 1):
                    if blk == 1:
                        act.wait_ge(q["conved"], 1)
                    for c in range(SNC):
                        act.wait_ge(q["proj"], blk * 4 + c + 1)
                        nc.scalar.activation(xsrc[:, 2 * c:2 * c + 2, :], k.bank[blk * 4 + c].rearrange("p (b t) -> p b t", b=2),
                                             ACT.Copy).then_inc(q["xp_out"], 1)
                for blk in (0, 1):
                    for c in range(SNC):
                        act.wait_ge(q["proj"], 8 + blk * 4 + c + 1)
                        nc.scalar.activation(sz[:, blk, c * SCH:(c + 1) * SCH], k.bank[blk * 4 + c], ACT.Silu).then_inc(q["z_out"], 1)
                for e in range(SE):
                    act.wait_ge(q["conved"], e + 1)
                    nc.scalar.activation(xc[:, e, :], xc[:, e, :], ACT.Silu, bias=cw[:, e, 4:5]).then_inc(q["xc_ready"], 1)
                nc.scalar.activation(mem["A"][:], mem["A"][:], ACT.Exp).then_inc(q["a_ready"], 1)
                for e in range(SE):
                    act.wait_ge(q["dtp"], e + 1)
                    nc.scalar.activation(en[:, e, :].rearrange("p (c t) -> p c t", t=SCH), k.banks[:, 4 - 4 * e:8 - 4 * e, :],
                                         ACT.Abs, bias=cw[:, e, 5:6])
                act.drain()
                for e in range(SE):
                    nc.scalar.activation(en[:, e, :], en[:, e, :], ACT.Exp, scale=-1.0).then_inc(q["exped"], 1)
                for e in range(SE):
                    act.wait_ge(q["u_ready"], e + 1)
                    nc.scalar.activation(dtx[:, e, :], u[:, e, :], ACT.Ln).then_inc(q["logged"], 1)

            @block.vector
            def _(dve):
                v = nc.vector
                if m == 2:
                    v.tensor_copy(dtx[:, 0, :].rearrange("p (b t) -> p b t", b=B), k.HT[:, :, PAD + T - 1:PAD - 1:-1])
                    dve.drain()
                    v.tensor_copy(k.HT[:, :, PAD:], dtx[:, 0, :].rearrange("p (b t) -> p b t", b=B))
                    dve.drain()
                v.memset(xp[:, :, 0:CPAD], 0.0).then_inc(q["src_ready"], 1)
                dve.wait_ge(q["loaded"], 112)
                v.tensor_copy(mem["sel"][:], mem["self"][:])
                dve.drain()
                for e in range(SE):
                    dve.wait_ge(q["xp_out"], 4 * e + 4)
                    o = xc[:, e, :].rearrange("p (b t) -> p b t", b=B)
                    v.tensor_scalar(o, xp[:, :, 0:T], cw[:, e, 0:1], None, ALU.mult)
                    for j in range(1, 4):
                        dve.drain()
                        i = v.scalar_tensor_tensor(out=o, in0=xp[:, :, j:j + T], scalar=cw[:, e, j:j + 1], in1=o,
                                                   op0=ALU.mult, op1=ALU.add)
                    i.then_inc(q["conved"], 1)
                dve.wait_ge(q["a_ready"], 1)
                v.tensor_scalar(mem["A"][:], mem["A"][:], -1.0, None, ALU.mult)
                for c in range(SNC):
                    cols = slice(c * SCH, (c + 1) * SCH)
                    for n, name in enumerate(("hm_b", "hm_c")):
                        dve.wait_ge(q["bc"], c * 4 + n + 1)
                        bank = k.bank[c % 2 * 4 + n]
                        v.tensor_copy(hi[:], bank)
                        dve.drain()
                        v.tensor_copy(mem[name][0:64, cols], hi[0:64, :])
                        v.tensor_tensor(mem[name][64:128, cols], bank[64:128, :], hi[64:128, :], ALU.subtract)
                        dve.drain()
                        v.engine_nop().then_inc(q["bc_read"], 1)
                    dve.wait_ge(q["bc"], c * 4 + 3)
                    bank = k.bank[c % 2 * 4 + 2]
                    v.tensor_copy(hi[:], bank)
                    dve.drain()
                    v.tensor_tensor(r1[:], bank, hi[:], ALU.subtract).then_inc(q["bc_read"], 1)
                    dve.drain()
                    v.tensor_copy(mid[:], r1[:])
                    dve.drain()
                    v.tensor_tensor(mem["lo"][:, cols], r1[:], mid[:], ALU.subtract)
                    dve.wait_ge(q["bc"], c * 4 + 4)
                    v.tensor_copy(dtlo[:, cols], k.bank[c % 2 * 4 + 3][0:R, :]).then_inc(q["bc_read"], 1)
                    dve.drain()
                    v.engine_nop().then_inc(q["dtlo_ready"], 1)
                for e in range(SE):
                    dve.wait_ge(q["exped"], e + 1)
                    v.tensor_scalar_add(u[:, e, :], en[:, e, :], 1.0).then_inc(q["u_ready"], 1)
                dve.drain()
                for e in range(SE):
                    v.tensor_scalar(dt[:, e, :].rearrange("p (c t) -> p c t", t=SCH), k.banks[:, 4 - 4 * e:8 - 4 * e, :],
                                    cw[:, e, 5:6], 0.0, ALU.add, ALU.max)
                    v.scalar_tensor_tensor(out=en[:, e, :], in0=u[:, e, :], scalar=-1.0, in1=en[:, e, :],
                                           op0=ALU.add, op1=ALU.subtract)
                for e in range(SE):
                    dve.drain()
                    dve.wait_ge(q["logged"], e + 1)
                    v.tensor_tensor(en[:, e, :], dtx[:, e, :], en[:, e, :], ALU.subtract)
                    dve.drain()
                    v.tensor_add(dt[:, e, :], dt[:, e, :], en[:, e, :])
                    dve.drain()
                    v.tensor_tensor(dtx[:, e, :], dt[:, e, :], xc[:, e, :], ALU.mult)
                dve.drain()
                for e in range(SE):
                    v.tensor_scalar(xc[:, e, :], xc[:, e, :], cw[:, e, 6:7], None, ALU.mult)
                dve.drain()


def mamba_scan(k, m, mem):
    NS = 4
    nc = k.nc
    xc, sz, dt, dtx = (mem[n] for n in ("xc", "sz", "dt", "dtx"))
    with Part(k) as p:
        dA = p.sb("dA", [P, NS, SE, SCH])
        dBx = p.sb("dBx", [P, NS, SE, SCH])
        h = p.sb("h", [P, 2, SE, SCH])
        hc = p.sb("hc", [P, 2, SE, SCH])
        bsb = p.sb("b_row", [P, NS, SCH])
        zero = p.sb("zero", [P, SCH], BF16)
        names = ("zeroed", "b_ready", "c_ready", "bsb_ready", "da_ready", "dbx_ready",
                 "scanned", "through_pool", "hc_ready", "hc_free", "y_ready", "y_read")
        q = {n: p.sem(n) for n in names}
        sel = mem["sel"]
        BBANK, LEAD = (2, 3, 6, 7), NS - 1

        def onto_all(ap):
            return ap.to_broadcast([P, P])

        with nc.Block() as block:
            @block.tensor
            def _(pe):
                pe.wait_ge(q["zeroed"], 1)

                def row(c, n, part, which, bank, free, ready):
                    cols = bass.ds(c * SCH, SCH)
                    pe.wait_ge(q[free], c * SN + n + 1)
                    nc.tensor.matmul(k.bank[bank], onto_all(sel[:, 0, bass.ds(n, 1)]), mem[part][:, cols], start=True, stop=False)
                    nc.tensor.matmul(k.bank[bank], onto_all(sel[:, which, bass.ds(n, 1)]), mem["lo"][:, cols],
                                     start=False, stop=True).then_inc(q[ready], 1)

                def b_row(c, n, s):
                    row(c, n, "hm_b", 1, BBANK[s], "bsb_ready", "b_ready")

                def c_row(c, n, s):
                    row(c, n, "hm_c", 2, 4 + s, "hc_ready", "c_ready")

                def add_up(c, n, s):
                    pe.wait_ge(q["hc_ready"], c * SN + n + 3)
                    for e in range(SE):
                        i = nc.tensor.matmul(k.bank[e], k.ident[:], hc[:, s, e, :], start=False, stop=False)
                    i.then_inc(q["hc_free"], 1)

                with pe.Fori(0, SNC) as c:
                    for n in range(LEAD):
                        b_row(c, n, n)
                    c_row(c, 0, 0)
                    pe.wait_ge(q["y_read"], c + 1)
                    for e in range(SE):
                        nc.tensor.matmul(k.bank[e], zero[:, 0:P], zero[:], start=True, stop=False)

                    def step(n, s):
                        b_row(c, n + LEAD, (s + LEAD) % NS)
                        c_row(c, n + 1, (s + 1) % 2)
                        add_up(c, n, s % 2)

                    with pe.Fori(0, SN // NS - 1) as n4:
                        for s in range(NS):
                            step(n4 * NS + s, s)
                    step(SN - NS, 0)
                    for n in range(SN - LEAD, SN):
                        if n + 1 < SN:
                            c_row(c, n + 1, (n + 1) % 2)
                        add_up(c, n, n % 2)
                    for e in range(SE):
                        i = nc.tensor.matmul(k.bank[e], k.ident[:], xc[:, e, bass.ds(c * SCH, SCH)], start=False, stop=True)
                    i.then_inc(q["y_ready"], 1)

            @block.scalar
            def _(act):
                act.wait_ge(q["zeroed"], 1)
                nc.scalar.activation(bsb[:, 0, 0:1], bsb[:, 0, 0:1], ACT.Exp)
                act.drain()
                with act.Fori(0, SNC) as c:
                    with act.Fori(0, SN // NS) as n4:
                        for s in range(NS):
                            n = n4 * NS + s
                            it = c * SN + n
                            act.wait_ge(q["scanned"], it + 1)
                            for e in range(SE):
                                d3 = dt[:, e, bass.ds(c * SCH, SCH)].rearrange("p (b t) -> p b t", t=T)
                                i = nc.scalar.activation(dA[:, s, e, :].rearrange("p (b t) -> p b t", t=T)[:, :, 1:], d3[:, :, 1:],
                                                         ACT.Exp, scale=mem["A"][:, e, bass.ds(n, 1)])
                            i.then_inc(q["da_ready"], 1)
                            act.wait_ge(q["b_ready"], it + 1)
                            act.wait_ge(q["dbx_ready"], it + 1)
                            nc.scalar.activation(bsb[:, s, :], k.bank[BBANK[s]], ACT.Copy).then_inc(q["bsb_ready"], 1)

            @block.gpsimd
            def _(pool):
                nc.gpsimd.memset(zero[:], 0.0)
                nc.gpsimd.memset(bsb[:], 0.0)
                nc.gpsimd.memset(dA[:], 0.0).then_inc(q["zeroed"], 1)
                for n, slots in (("bsb_ready", NS), ("dbx_ready", NS), ("scanned", NS), ("hc_ready", 2), ("hc_free", 2)):
                    pool.sem_inc(q[n], slots)
                pool.sem_inc(q["y_read"], 1)
                with pool.Fori(0, SNC) as c:
                    with pool.Fori(0, SN // NS) as n4:
                        for s in range(NS):
                            it = c * SN + n4 * NS + s
                            pool.wait_ge(q["bsb_ready"], it + NS + 1)
                            pool.wait_ge(q["scanned"], it + 1)
                            pool.sem_inc(q["through_pool"], 1)
                            nc.gpsimd.tensor_tensor(dBx[:, s], dtx[:, :, bass.ds(c * SCH, SCH)], across(bsb[:, s, :], SE),
                                                    ALU.mult).then_inc(q["dbx_ready"], 1)

            @block.vector
            def _(dve):
                v = nc.vector

                def scan(c, n, s):
                    it = c * SN + n
                    dve.wait_ge(q["da_ready"], it + 1)
                    dve.wait_ge(q["dbx_ready"], it + NS + 1)
                    dve.wait_ge(q["hc_ready"], it + 1)
                    flat = lambda a: a.rearrange("p e t -> p (e t)")
                    v.tensor_tensor_scan(flat(h[:, s % 2]), flat(dA[:, s]), flat(dBx[:, s]), 0.0, ALU.mult,
                                         ALU.add).then_inc(q["scanned"], 1)

                def times_c(c, n, s):
                    it = c * SN + n
                    dve.wait_ge(q["c_ready"], it + 1)
                    dve.wait_ge(q["hc_free"], it + 1)
                    dve.wait_ge(q["scanned"], it + NS + 1)
                    v.tensor_tensor(hc[:, s], h[:, s], across(k.bank[4 + s], SE), ALU.mult).then_inc(q["hc_ready"], 1)

                with dve.Fori(0, SNC) as c:
                    scan(c, 0, 0)
                    with dve.Fori(0, SN // NS - 1) as n4:
                        for s in range(NS):
                            scan(c, n4 * NS + s + 1, (s + 1) % NS)
                            times_c(c, n4 * NS + s, s % 2)
                    for n in range(SN - NS, SN):
                        if n + 1 < SN:
                            scan(c, n + 1, (n + 1) % NS)
                        times_c(c, n, n % 2)
                    dve.wait_ge(q["y_ready"], c + 1)
                    for e in range(SE):
                        z = sz[:, e, bass.ds(c * SCH, SCH)]
                        i = v.tensor_tensor(z, k.bank[e], z, ALU.mult)
                    i.then_inc(q["y_read"], 1)


def mamba_output(k, m, mem):
    nc = k.nc
    sz, xc = mem["sz"], mem["xc"]
    with Part(k) as p:
        gated_ready, out = p.sem("gated_ready"), p.sem("out")
        with nc.Block() as block:
            @block.tensor
            def _(pe):
                pe.wait_ge(gated_ready, 1)
                for t in range(NT):
                    for e in range(SE):
                        i = nc.tensor.matmul(k.bank[t // 4][:, t % 4 * D:(t % 4 + 1) * D], xc[:, e, t * P:(t + 1) * P],
                                             mem["wout"][:, e, :], start=e == 0, stop=e == SE - 1)
                    if t % 4 == 3:
                        i.then_inc(out, 1)

            @block.vector
            def _(dve):
                v = nc.vector
                for e in range(SE):
                    src = sz[:, e, :].rearrange("p (b t) -> p b t", t=T)
                    if m == 2:
                        src = src[:, :, ::-1]
                    v.tensor_copy(xc[:, e, :].rearrange("p (b t) -> p b t", t=T), src)
                dve.drain()
                v.engine_nop().then_inc(gated_ready, 1)
                for g in range(4):
                    dve.wait_ge(out, g + 1)
                    y, o = k.Y[:, 4 * g:4 * g + 4, :], k.bank[g].rearrange("p (t d) -> p t d", d=D)
                    if m == 1:
                        v.tensor_copy(y, o)
                    else:
                        v.tensor_tensor(y, o, y, ALU.add)
                dve.drain()


def blocks():
    return [gated_delta, window_attn, plucker_attn, ffn_ternary, flash_attn, ffn_experts, bi_mamba, ffn_int8]


def build_program(nc, dram, todo=None):
    with ExitStack() as ctx:
        k = Core(nc, dram, ctx)
        load_residual(k)
        todo = blocks() if todo is None else todo
        for n, block in enumerate(todo):
            block(k, add_y=n > 0)
        normalise(k, add_y=True, make_ht=False)
        store_residual(k)


def tokens_first(a):
    a = a.reshape(-1, P, a.shape[-1])
    return a.transpose(1, 0, 2)


def by_blocks(a):
    return a.reshape(-1, P, a.shape[-1]).transpose(1, 0, 2)


def laid_out(i):
    import numpy as np
    d = {}
    d["x"] = tokens_first(i["L0_attn_x"].reshape(-1, D))
    d["ident"] = np.eye(P, dtype=np.float32)
    d["iota8"] = np.arange(8, dtype=np.float32)
    d["l1f_w12"] = np.stack([i["L1_ffn_w1_w"].T, i["L1_ffn_w2_w"].T], 1)
    d["l1f_sc"] = np.stack([i[f"L1_ffn_{n}_s"].reshape(4, P).T for n in ("w1", "w2", "h1", "h2")], 1)
    d["l1f_wh"] = np.stack([by_blocks(i[f"L1_ffn_{n}_w"].T) for n in ("h1", "h2")], 1)
    d["l1f_w3"] = by_blocks(i["L1_ffn_w3_w"].T)
    d["l1f_s3"] = i["L1_ffn_w3_s"]
    d["l2f_gw"], d["l2f_gb"] = i["L2_ffn_gate_W"], i["L2_ffn_gate_b"]
    d["l2f_ew"] = i["L2_ffn_expert_W"].transpose(1, 0, 2).reshape(D, -1)
    d["l2f_eb"] = i["L2_ffn_expert_b"].reshape(1, -1)
    d["l3f_wgu"] = np.concatenate([i["L3_ffn_w_gate"].T, i["L3_ffn_w_up"].T], 1)
    d["l3f_wd"] = by_blocks(i["L3_ffn_w_down"].T).reshape(P, -1)
    for lay_out in (lay_out_delta, lay_out_window, lay_out_plucker, lay_out_flash, lay_out_mamba):
        lay_out(i, d, np)
    return {n: np.ascontiguousarray(a) for n, a in d.items()}


def kernel(**inputs):
    import numpy as np
    import concourse.bacc as bacc
    from concourse.bass_utils import run_bass_kernel_spmd

    arrays = laid_out({n: np.asarray(a) for n, a in inputs.items()})
    nc = bacc.Bacc("TRN2", target_bir_lowering=False, num_devices=1)
    dram = {n: nc.dram_tensor(f"in_{n}", a.shape, mybir.dt.from_np(a.dtype), kind="ExternalInput").ap()
            for n, a in arrays.items()}
    dram["out"] = nc.dram_tensor("out_0", (P, NT, D), F32, kind="ExternalOutput").ap()
    build_program(nc, dram)
    r = run_bass_kernel_spmd(nc, [{f"in_{n}": a for n, a in arrays.items()}], core_ids=[0])
    return r.results[0]["out_0"].transpose(1, 0, 2).reshape(B, T, D)
```
